# Optimizing a Trainium2 kernel written in Bass

```python
import numpy as np
import jax
import jax.numpy as jnp

def _softmax(x, axis=-1):
    return jax.nn.softmax(x, axis=axis)

def _gelu(x):
    return jax.nn.gelu(x, approximate=True)

def _silu(x):
    return jax.nn.silu(x)

def _sigmoid(x):
    return jax.nn.sigmoid(x)

def _layernorm(x, axis=-1, eps=1e-05):
    m = jnp.mean(x, axis=axis, keepdims=True)
    v = jnp.var(x, axis=axis, keepdims=True)
    return (x - m) / jnp.sqrt(v + eps)

def _scatter_add(tgt, idx, src, axis=0):
    return tgt.at[idx].add(src)

def _segment_sum(src, seg, n):
    return jax.ops.segment_sum(src, seg, n)
kernel_name = 'mk_decoder_preln_d2_seqx_r8_45b320'

def setup_inputs(seed: int=0):
    np.random.seed(seed)
    _w = jnp.asarray

    def _rec_inputs():
        import jax
        import jax.numpy as jnp
        _rk = jax.random.key(seed)
        x = 7.22e-05 + 1 * jax.random.normal(jax.random.fold_in(_rk, 1), (1, 1024, 128), jnp.float32)
        _lenS = 1024 - jax.random.randint(jax.random.fold_in(_rk, 7), (1,), 0, max(1, 1024 // 4) + 1, jnp.int32)
        _lenS2 = 6404 - jax.random.randint(jax.random.fold_in(_rk, 8), (1,), 0, max(1, 6404 // 4) + 1, jnp.int32)
        _ctx_768P = jax.random.normal(jax.random.fold_in(_rk, 11), (1, 16, 96), jnp.float32)
        _ctx_768c = jax.random.dirichlet(jax.random.fold_in(_rk, 511), 0.3 * jnp.ones((16,), jnp.float32), (1, 6404))
        _ctx_768t = jnp.einsum('bsk,bkd->bsd', _ctx_768c, _ctx_768P)
        _ctx_768t = _ctx_768t * jax.lax.rsqrt(jnp.mean(jnp.square(_ctx_768t)) + 1e-12) * 0.953939
        ctx_768 = -0.000191848 + 0.999787 * (_ctx_768t + 0.3 * jax.random.normal(jax.random.fold_in(_rk, 611), (1, 6404, 96), jnp.float32))
        _validS = jnp.arange(1024)[None, :] < _lenS[:, None]
        _validS2 = jnp.arange(6404)[None, :] < _lenS2[:, None]
        _causal = jnp.tril(jnp.ones((1024, 1024), dtype=bool))
        mask_BxS_bf1 = jnp.ones((1, 1024), dtype=bool)
        mask_BxS2_bf1 = jnp.ones((1, 6404), dtype=bool)
        return (x, ctx_768, mask_BxS_bf1, mask_BxS2_bf1)
    x, ctx_768, mask_BxS_bf1, mask_BxS2_bf1 = _rec_inputs()

    def _L0_attn_setup():
        import jax, jax.numpy as jnp
        import numpy as np
        B, L, D_MODEL = (4, 256, 128)
        EXPAND = 2
        D_INNER = EXPAND * D_MODEL
        D_STATE = 16
        D_CONV = 4
        DT_RANK = (D_MODEL + 15) // 16
        EPS = 1e-05

        def _rmsnorm(x, w):
            return x * jax.lax.rsqrt(jnp.mean(x * x, axis=-1, keepdims=True) + EPS) * w

        def _causal_depthwise_conv(x, w, b):
            xp = jnp.pad(x, ((0, 0), (0, 0), (D_CONV - 1, 0)))
            y = jax.lax.conv_general_dilated(xp, w[:, None, :], window_strides=(1,), padding='VALID', dimension_numbers=('NCH', 'OIH', 'NCH'), feature_group_count=D_INNER)
            return y + b[None, :, None]

        def _selective_scan(u, delta, A, Bm, Cm, D):

            def step(s, inp):
                d_t, B_t, C_t, u_t = inp
                dA = jnp.exp(d_t[..., None] * A)
                dBu = d_t[..., None] * B_t[:, None, :] * u_t[..., None]
                s = s * dA + dBu
                y = jnp.einsum('bds,bs->bd', s, C_t)
                return (s, y)
            s0 = jnp.zeros((u.shape[0], D_INNER, D_STATE), u.dtype)
            xs = (delta.swapaxes(0, 1), Bm.swapaxes(0, 1), Cm.swapaxes(0, 1), u.swapaxes(0, 1))
            _, ys = jax.lax.scan(step, s0, xs)
            return ys.swapaxes(0, 1) + u * D
        key = jax.random.key(seed)
        ks = jax.random.split(key, 10)
        s = 0.02
        return {'x': jax.random.normal(ks[0], (B, L, D_MODEL), jnp.float32), 'norm_w': jnp.ones((D_MODEL,), jnp.float32), 'in_proj_w': jax.random.normal(ks[1], (2 * D_INNER, D_MODEL), jnp.float32) * s, 'conv_w': jax.random.normal(ks[2], (D_INNER, D_CONV), jnp.float32) * s, 'conv_b': jnp.zeros((D_INNER,), jnp.float32), 'x_proj_w': jax.random.normal(ks[3], (DT_RANK + 2 * D_STATE, D_INNER), jnp.float32) * s, 'dt_proj_w': jax.random.normal(ks[4], (D_INNER, DT_RANK), jnp.float32) * s, 'dt_proj_b': jnp.log(jnp.expm1(jnp.full((D_INNER,), 0.01, jnp.float32))), 'A_log': jnp.log(jnp.broadcast_to(jnp.arange(1, D_STATE + 1, dtype=jnp.float32), (D_INNER, D_STATE))), 'D': jnp.ones((D_INNER,), jnp.float32), 'out_proj_w': jax.random.normal(ks[5], (D_MODEL, D_INNER), jnp.float32) * s}
    _L0_attn_all = _L0_attn_setup()
    _L0_attn_in = {k: v for k, v in _L0_attn_all.items() if k in ('norm_w', 'in_proj_w', 'conv_w', 'conv_b', 'x_proj_w', 'dt_proj_w', 'dt_proj_b', 'A_log', 'D', 'out_proj_w')}
    del _L0_attn_all

    def _L0_xattn_setup():
        import jax, jax.numpy as jnp
        import numpy as np
        B, LQ, LK = (4, 256, 256)
        D1, D2, H = (128, 96, 128)
        key = jax.random.key(seed)
        ks = jax.random.split(key, 9)
        s1, s2, sh = (1.0 / np.sqrt(D1), 1.0 / np.sqrt(D2), 1.0 / np.sqrt(H))
        return {'query': jax.random.normal(ks[0], (B, LQ, D1), jnp.float32), 'key': jax.random.normal(ks[1], (B, LK, D2), jnp.float32), 'value': jax.random.normal(ks[2], (B, LK, D2), jnp.float32), 'Wq': jax.random.normal(ks[3], (D1, H), jnp.float32) * s1, 'bq': jax.random.normal(ks[4], (H,), jnp.float32) * s1, 'Wk': jax.random.normal(ks[5], (D2, H), jnp.float32) * s2, 'bk': jax.random.normal(ks[6], (H,), jnp.float32) * s2, 'Wv': jax.random.normal(ks[7], (D2, H), jnp.float32) * s2, 'bv': jax.random.normal(ks[8], (H,), jnp.float32) * s2}
    _L0_xattn_all = _L0_xattn_setup()
    _L0_xattn_in = {k: v for k, v in _L0_xattn_all.items() if k in ('Wq', 'bq', 'Wk', 'bk', 'Wv', 'bv')}
    del _L0_xattn_all

    def _L0_ffn_setup():
        import jax, jax.numpy as jnp
        import numpy as np
        THRESHOLD = 0.1
        key = jax.random.key(seed)
        k1, k2, k3 = jax.random.split(key, 3)
        B, S, D, E = (4, 512, 128, 8)
        inputs = jax.random.normal(k1, (B, S, D), dtype=jnp.float32)
        gate_w = jax.random.normal(k2, (D, E), dtype=jnp.float32) * 0.02
        gate_b = jnp.zeros((E,), dtype=jnp.float32)
        expert_w = jax.random.normal(k3, (E, D, D), dtype=jnp.float32) * 0.02
        expert_b = jnp.zeros((E, D), dtype=jnp.float32)
        return {'inputs': inputs, 'gate_w': gate_w, 'gate_b': gate_b, 'expert_w': expert_w, 'expert_b': expert_b}
    _L0_ffn_all = _L0_ffn_setup()
    _L0_ffn_in = {k: v for k, v in _L0_ffn_all.items() if k in ('gate_w', 'gate_b', 'expert_w', 'expert_b')}
    del _L0_ffn_all

    def _L1_attn_setup():
        import jax, jax.numpy as jnp
        import numpy as np
        KEY_DIM = 128
        SCALE = KEY_DIM ** (-0.5)
        key = jax.random.key(seed)
        k1, k2, k3, k4 = jax.random.split(key, 4)
        B, S, E = (4, 256, 128)
        x = jax.random.normal(k1, (B, S, E), dtype=jnp.float32)
        WQ = jax.random.normal(k2, (KEY_DIM, E), dtype=jnp.float32) * E ** (-0.5)
        WK = jax.random.normal(k3, (KEY_DIM, E), dtype=jnp.float32) * E ** (-0.5)
        WV = jax.random.normal(k4, (KEY_DIM, E), dtype=jnp.float32) * E ** (-0.5)
        return {'x': x, 'WQ': WQ, 'WK': WK, 'WV': WV}
    _L1_attn_all = _L1_attn_setup()
    _L1_attn_in = {k: v for k, v in _L1_attn_all.items() if k in ('WQ', 'WK', 'WV')}
    del _L1_attn_all

    def _L1_xattn_setup():
        import jax, jax.numpy as jnp
        import numpy as np
        B, T, DT, G, DV = (16, 64, 128, 72, 96)
        H, DH = (4, 32)
        INNER = H * DH
        HID = 4 * DT
        N_STATE = 64
        K_TOP = 32

        def layernorm(x, g, b, eps=1e-05):
            m = x.mean(-1, keepdims=True)
            v = x.var(-1, keepdims=True)
            return (x - m) * jax.lax.rsqrt(v + eps) * g + b

        def s4d(x, log_dt, A_re, A_im, C_re, C_im, D_skip):
            Bb, L, D = x.shape
            dt = jnp.exp(log_dt)
            A = A_re + 1j * A_im
            C = C_re + 1j * C_im
            dtA = dt[:, None] * A
            dC = C * (jnp.exp(dtA) - 1.0) / A
            powers = jnp.exp(dtA[:, :, None] * jnp.arange(L))
            K = 2.0 * jnp.einsum('dn,dnl->dl', dC, powers).real
            n = 2 * L
            Kf = jnp.fft.rfft(K, n=n, axis=-1)
            xf = jnp.fft.rfft(x, n=n, axis=1)
            y = jnp.fft.irfft(xf * Kf.T[None], n=n, axis=1)[:, :L]
            return y + x * D_skip
        key = jax.random.key(seed)
        ks = jax.random.split(key, 16)
        s = 0.02
        inp = {'x_text': jax.random.normal(ks[0], (B, T, DT), jnp.float32), 'x_vision': jax.random.normal(ks[1], (B, G, DV), jnp.float32), 'text_mask': jnp.ones((B, T), bool), 'vision_mask': jnp.ones((B, G), bool), 'Wq': jax.random.normal(ks[2], (DT, INNER), jnp.float32) * s, 'Wk': jax.random.normal(ks[3], (DV, INNER), jnp.float32) * s, 'Wv': jax.random.normal(ks[4], (DV, DT), jnp.float32) * s, 'W_film_in': jax.random.normal(ks[5], (DT, 2 * DT), jnp.float32) * s, 'b_film_in': jnp.zeros((2 * DT,), jnp.float32), 'W_film_out': jax.random.normal(ks[6], (DT, 2 * DT), jnp.float32) * s, 'b_film_out': jnp.zeros((2 * DT,), jnp.float32), 'g_norm_in': jnp.ones((DT,), jnp.float32), 'b_norm_in': jnp.zeros((DT,), jnp.float32), 'g_norm_out': jnp.ones((DT,), jnp.float32), 'b_norm_out': jnp.zeros((DT,), jnp.float32), 'g_ffn': jnp.ones((DT,), jnp.float32), 'b_ffn': jnp.zeros((DT,), jnp.float32), 'W1': jax.random.normal(ks[7], (DT, HID), jnp.float32) * s, 'b1': jnp.zeros((HID,), jnp.float32), 'W2': jax.random.normal(ks[8], (HID, DT), jnp.float32) * s, 'b2': jnp.zeros((DT,), jnp.float32), 'log_dt': jnp.log(0.001) + jax.random.uniform(ks[9], (DT,), jnp.float32) * (jnp.log(0.1) - jnp.log(0.001)), 'A_re': -0.5 * jnp.ones((DT, N_STATE), jnp.float32), 'A_im': jnp.tile(jnp.pi * jnp.arange(N_STATE, dtype=jnp.float32), (DT, 1)), 'C_re': jax.random.normal(ks[10], (DT, N_STATE), jnp.float32) * 0.5 ** 0.5, 'C_im': jax.random.normal(ks[11], (DT, N_STATE), jnp.float32) * 0.5 ** 0.5, 'D_skip': jax.random.normal(ks[12], (DT,), jnp.float32), 'mod_gate': jnp.array(0.5, jnp.float32)}
        return inp
    _L1_xattn_all = _L1_xattn_setup()
    _L1_xattn_in = {k: v for k, v in _L1_xattn_all.items() if k in ('Wq', 'Wk', 'Wv', 'W_film_in', 'b_film_in', 'W_film_out', 'b_film_out', 'g_norm_in', 'b_norm_in', 'g_norm_out', 'b_norm_out', 'g_ffn', 'b_ffn', 'W1', 'b1', 'W2', 'b2', 'log_dt', 'A_re', 'A_im', 'C_re', 'C_im', 'D_skip', 'mod_gate')}
    del _L1_xattn_all

    def _L1_ffn_setup():
        import jax, jax.numpy as jnp
        import numpy as np
        DIM = 128
        NQ = 16
        NKV = 4
        HD = DIM // NQ
        HID = 256
        E = 8
        B, S = (1, 128)
        EPS = 1e-06

        def rmsnorm(x, w):
            ms = jnp.mean(x * x, axis=-1, keepdims=True)
            return w * (x * jax.lax.rsqrt(ms + EPS))

        def rope_tables(seq_len, head_dim):
            inv_freq = 1.0 / 10000.0 ** (jnp.arange(0, head_dim, 2, dtype=jnp.float32) / head_dim)
            t = jnp.arange(seq_len, dtype=jnp.float32)
            freqs = jnp.einsum('i,j->ij', t, inv_freq)
            return (jnp.cos(freqs), jnp.sin(freqs))

        def apply_rope(x, cos, sin):
            c = cos[None, :, None, :]
            s = sin[None, :, None, :]
            half = x.shape[-1] // 2
            x1, x2 = (x[..., :half], x[..., half:])
            return jnp.concatenate([x1 * c - x2 * s, x1 * s + x2 * c], axis=-1)

        def _forward(x, ln1_w, ln2_w, Wq, bq, Wk, bk, Wv, bv, qn_w, kn_w, Wg, bg, Wo, bo, Wr, br, W1, b1, W2, b2):
            batch, seq, _ = x.shape
            cos, sin = rope_tables(seq, HD)
            h = rmsnorm(x, ln1_w)
            q = (h @ Wq + bq).reshape(batch, seq, NQ, HD)
            k = (h @ Wk + bk).reshape(batch, seq, NKV, HD)
            v = (h @ Wv + bv).reshape(batch, seq, NKV, HD)
            q = rmsnorm(apply_rope(q, cos, sin), qn_w)
            k = rmsnorm(apply_rope(k, cos, sin), kn_w)
            rep = NQ // NKV
            k = jnp.repeat(k, rep, axis=2)
            v = jnp.repeat(v, rep, axis=2)
            scores = jnp.einsum('bthd,bshd->bhts', q, k) / np.sqrt(HD)
            causal = jnp.tril(jnp.ones((seq, seq), dtype=bool))
            scores = jnp.where(causal[None, None], scores, -jnp.inf)
            attn = jax.nn.softmax(scores, axis=-1)
            out = jnp.einsum('bhts,bshd->bthd', attn, v)
            gate = jax.nn.sigmoid(out @ Wg + bg)
            out = (out * gate).reshape(batch, seq, DIM)
            x = x + out @ Wo + bo
            h2 = rmsnorm(x, ln2_w)
            logits = h2 @ Wr + br
            top1 = jnp.argmax(logits, axis=-1).reshape(-1)
            xt = h2.reshape(-1, DIM)
            u = jnp.einsum('td,edf->tef', xt, W1) + b1
            u1, u2 = (u[..., :HID], u[..., HID:])
            act = u1 * jax.nn.sigmoid(u2)
            y_all = jnp.einsum('teh,ehd->ted', act, W2) + b2
            y = jnp.take_along_axis(y_all, top1[:, None, None], axis=1)[:, 0, :]
            return x + y.reshape(batch, seq, DIM)
        key = jax.random.key(seed)
        ks = jax.random.split(key, 20)
        sc = lambda fan_in: 1.0 / np.sqrt(fan_in)
        d = {}
        d['x'] = jax.random.normal(ks[0], (B, S, DIM), dtype=jnp.float32)
        d['ln1_w'] = jnp.ones((DIM,), jnp.float32)
        d['ln2_w'] = jnp.ones((DIM,), jnp.float32)
        d['Wq'] = jax.random.normal(ks[1], (DIM, DIM), jnp.float32) * sc(DIM)
        d['bq'] = jnp.zeros((DIM,), jnp.float32)
        d['Wk'] = jax.random.normal(ks[2], (DIM, HD * NKV), jnp.float32) * sc(DIM)
        d['bk'] = jnp.zeros((HD * NKV,), jnp.float32)
        d['Wv'] = jax.random.normal(ks[3], (DIM, HD * NKV), jnp.float32) * sc(DIM)
        d['bv'] = jnp.zeros((HD * NKV,), jnp.float32)
        d['qn_w'] = jnp.ones((HD,), jnp.float32)
        d['kn_w'] = jnp.ones((HD,), jnp.float32)
        d['Wg'] = jax.random.normal(ks[4], (HD, HD), jnp.float32) * sc(HD)
        d['bg'] = jnp.zeros((HD,), jnp.float32)
        d['Wo'] = jax.random.normal(ks[5], (DIM, DIM), jnp.float32) * sc(DIM)
        d['bo'] = jnp.zeros((DIM,), jnp.float32)
        d['Wr'] = jax.random.normal(ks[6], (DIM, E), jnp.float32) * sc(DIM)
        d['br'] = jnp.zeros((E,), jnp.float32)
        d['W1'] = jax.random.normal(ks[7], (E, DIM, 2 * HID), jnp.float32) * sc(DIM)
        d['b1'] = jnp.zeros((E, 2 * HID), jnp.float32)
        d['W2'] = jax.random.normal(ks[8], (E, HID, DIM), jnp.float32) * sc(HID)
        d['b2'] = jnp.zeros((E, DIM), jnp.float32)
        return d
    _L1_ffn_all = _L1_ffn_setup()
    _L1_ffn_in = {k: v for k, v in _L1_ffn_all.items() if k in ('ln1_w', 'ln2_w', 'Wq', 'bq', 'Wk', 'bk', 'Wv', 'bv', 'qn_w', 'kn_w', 'Wg', 'bg', 'Wo', 'bo', 'Wr', 'br', 'W1', 'b1', 'W2', 'b2')}
    del _L1_ffn_all
    return {'x': x, 'ctx_768': ctx_768, 'mask_BxS_bf1': mask_BxS_bf1, 'mask_BxS2_bf1': mask_BxS2_bf1, 'L0_attn_norm_w': _L0_attn_in['norm_w'], 'L0_attn_in_proj_w': _L0_attn_in['in_proj_w'], 'L0_attn_conv_w': _L0_attn_in['conv_w'], 'L0_attn_conv_b': _L0_attn_in['conv_b'], 'L0_attn_x_proj_w': _L0_attn_in['x_proj_w'], 'L0_attn_dt_proj_w': _L0_attn_in['dt_proj_w'], 'L0_attn_dt_proj_b': _L0_attn_in['dt_proj_b'], 'L0_attn_A_log': _L0_attn_in['A_log'], 'L0_attn_D': _L0_attn_in['D'], 'L0_attn_out_proj_w': _L0_attn_in['out_proj_w'], 'L0_xattn_Wq': _L0_xattn_in['Wq'], 'L0_xattn_bq': _L0_xattn_in['bq'], 'L0_xattn_Wk': _L0_xattn_in['Wk'], 'L0_xattn_bk': _L0_xattn_in['bk'], 'L0_xattn_Wv': _L0_xattn_in['Wv'], 'L0_xattn_bv': _L0_xattn_in['bv'], 'L0_ffn_gate_w': _L0_ffn_in['gate_w'], 'L0_ffn_gate_b': _L0_ffn_in['gate_b'], 'L0_ffn_expert_w': _L0_ffn_in['expert_w'], 'L0_ffn_expert_b': _L0_ffn_in['expert_b'], 'L1_attn_WQ': _L1_attn_in['WQ'], 'L1_attn_WK': _L1_attn_in['WK'], 'L1_attn_WV': _L1_attn_in['WV'], 'L1_xattn_Wq': _L1_xattn_in['Wq'], 'L1_xattn_Wk': _L1_xattn_in['Wk'], 'L1_xattn_Wv': _L1_xattn_in['Wv'], 'L1_xattn_W_film_in': _L1_xattn_in['W_film_in'], 'L1_xattn_b_film_in': _L1_xattn_in['b_film_in'], 'L1_xattn_W_film_out': _L1_xattn_in['W_film_out'], 'L1_xattn_b_film_out': _L1_xattn_in['b_film_out'], 'L1_xattn_g_norm_in': _L1_xattn_in['g_norm_in'], 'L1_xattn_b_norm_in': _L1_xattn_in['b_norm_in'], 'L1_xattn_g_norm_out': _L1_xattn_in['g_norm_out'], 'L1_xattn_b_norm_out': _L1_xattn_in['b_norm_out'], 'L1_xattn_g_ffn': _L1_xattn_in['g_ffn'], 'L1_xattn_b_ffn': _L1_xattn_in['b_ffn'], 'L1_xattn_W1': _L1_xattn_in['W1'], 'L1_xattn_b1': _L1_xattn_in['b1'], 'L1_xattn_W2': _L1_xattn_in['W2'], 'L1_xattn_b2': _L1_xattn_in['b2'], 'L1_xattn_log_dt': _L1_xattn_in['log_dt'], 'L1_xattn_A_re': _L1_xattn_in['A_re'], 'L1_xattn_A_im': _L1_xattn_in['A_im'], 'L1_xattn_C_re': _L1_xattn_in['C_re'], 'L1_xattn_C_im': _L1_xattn_in['C_im'], 'L1_xattn_D_skip': _L1_xattn_in['D_skip'], 'L1_xattn_mod_gate': _L1_xattn_in['mod_gate'], 'L1_ffn_ln1_w': _L1_ffn_in['ln1_w'], 'L1_ffn_ln2_w': _L1_ffn_in['ln2_w'], 'L1_ffn_Wq': _L1_ffn_in['Wq'], 'L1_ffn_bq': _L1_ffn_in['bq'], 'L1_ffn_Wk': _L1_ffn_in['Wk'], 'L1_ffn_bk': _L1_ffn_in['bk'], 'L1_ffn_Wv': _L1_ffn_in['Wv'], 'L1_ffn_bv': _L1_ffn_in['bv'], 'L1_ffn_qn_w': _L1_ffn_in['qn_w'], 'L1_ffn_kn_w': _L1_ffn_in['kn_w'], 'L1_ffn_Wg': _L1_ffn_in['Wg'], 'L1_ffn_bg': _L1_ffn_in['bg'], 'L1_ffn_Wo': _L1_ffn_in['Wo'], 'L1_ffn_bo': _L1_ffn_in['bo'], 'L1_ffn_Wr': _L1_ffn_in['Wr'], 'L1_ffn_br': _L1_ffn_in['br'], 'L1_ffn_W1': _L1_ffn_in['W1'], 'L1_ffn_b1': _L1_ffn_in['b1'], 'L1_ffn_W2': _L1_ffn_in['W2'], 'L1_ffn_b2': _L1_ffn_in['b2']}

def reference(x, ctx_768, mask_BxS_bf1, mask_BxS2_bf1, L0_attn_norm_w, L0_attn_in_proj_w, L0_attn_conv_w, L0_attn_conv_b, L0_attn_x_proj_w, L0_attn_dt_proj_w, L0_attn_dt_proj_b, L0_attn_A_log, L0_attn_D, L0_attn_out_proj_w, L0_xattn_Wq, L0_xattn_bq, L0_xattn_Wk, L0_xattn_bk, L0_xattn_Wv, L0_xattn_bv, L0_ffn_gate_w, L0_ffn_gate_b, L0_ffn_expert_w, L0_ffn_expert_b, L1_attn_WQ, L1_attn_WK, L1_attn_WV, L1_xattn_Wq, L1_xattn_Wk, L1_xattn_Wv, L1_xattn_W_film_in, L1_xattn_b_film_in, L1_xattn_W_film_out, L1_xattn_b_film_out, L1_xattn_g_norm_in, L1_xattn_b_norm_in, L1_xattn_g_norm_out, L1_xattn_b_norm_out, L1_xattn_g_ffn, L1_xattn_b_ffn, L1_xattn_W1, L1_xattn_b1, L1_xattn_W2, L1_xattn_b2, L1_xattn_log_dt, L1_xattn_A_re, L1_xattn_A_im, L1_xattn_C_re, L1_xattn_C_im, L1_xattn_D_skip, L1_xattn_mod_gate, L1_ffn_ln1_w, L1_ffn_ln2_w, L1_ffn_Wq, L1_ffn_bq, L1_ffn_Wk, L1_ffn_bk, L1_ffn_Wv, L1_ffn_bv, L1_ffn_qn_w, L1_ffn_kn_w, L1_ffn_Wg, L1_ffn_bg, L1_ffn_Wo, L1_ffn_bo, L1_ffn_Wr, L1_ffn_br, L1_ffn_W1, L1_ffn_b1, L1_ffn_W2, L1_ffn_b2):
    import jax
    import jax.numpy as jnp

    def _L0_attn_ref(x, norm_w, in_proj_w, conv_w, conv_b, x_proj_w, dt_proj_w, dt_proj_b, A_log, D, out_proj_w):
        import jax, jax.numpy as jnp
        import numpy as np
        B, L, D_MODEL = (4, 256, 128)
        EXPAND = 2
        D_INNER = EXPAND * D_MODEL
        D_STATE = 16
        D_CONV = 4
        DT_RANK = (D_MODEL + 15) // 16
        EPS = 1e-05

        def _rmsnorm(x, w):
            return x * jax.lax.rsqrt(jnp.mean(x * x, axis=-1, keepdims=True) + EPS) * w

        def _causal_depthwise_conv(x, w, b):
            xp = jnp.pad(x, ((0, 0), (0, 0), (D_CONV - 1, 0)))
            y = jax.lax.conv_general_dilated(xp, w[:, None, :], window_strides=(1,), padding='VALID', dimension_numbers=('NCH', 'OIH', 'NCH'), feature_group_count=D_INNER)
            return y + b[None, :, None]

        def _selective_scan(u, delta, A, Bm, Cm, D):

            def step(s, inp):
                d_t, B_t, C_t, u_t = inp
                dA = jnp.exp(d_t[..., None] * A)
                dBu = d_t[..., None] * B_t[:, None, :] * u_t[..., None]
                s = s * dA + dBu
                y = jnp.einsum('bds,bs->bd', s, C_t)
                return (s, y)
            s0 = jnp.zeros((u.shape[0], D_INNER, D_STATE), u.dtype)
            xs = (delta.swapaxes(0, 1), Bm.swapaxes(0, 1), Cm.swapaxes(0, 1), u.swapaxes(0, 1))
            _, ys = jax.lax.scan(step, s0, xs)
            return ys.swapaxes(0, 1) + u * D
        h = _rmsnorm(x, norm_w)
        xz = jnp.einsum('bld,ed->ble', h, in_proj_w)
        xi, z = jnp.split(xz, 2, axis=-1)
        xi = _causal_depthwise_conv(xi.swapaxes(1, 2), conv_w, conv_b).swapaxes(1, 2)
        xi = jax.nn.silu(xi)
        x_dbl = jnp.einsum('bld,ed->ble', xi, x_proj_w)
        dt, Bm, Cm = jnp.split(x_dbl, [DT_RANK, DT_RANK + D_STATE], axis=-1)
        delta = jax.nn.softplus(jnp.einsum('blr,dr->bld', dt, dt_proj_w) + dt_proj_b)
        A = -jnp.exp(A_log)
        y = _selective_scan(xi, delta, A, Bm, Cm, D)
        y = y * jax.nn.silu(z)
        out = jnp.einsum('bld,ed->ble', y, out_proj_w)
        return out + x

    def _L0_xattn_ref(query, key, value, Wq, bq, Wk, bk, Wv, bv):
        import jax, jax.numpy as jnp
        import numpy as np
        B, LQ, LK = (4, 256, 256)
        D1, D2, H = (128, 96, 128)
        q = jnp.einsum('bqd,dh->bqh', query, Wq) + bq
        k = jnp.einsum('bkd,dh->bkh', key, Wk) + bk
        v = jnp.einsum('bkd,dh->bkh', value, Wv) + bv
        scores = jnp.einsum('bqh,bkh->bqk', q, k)
        weights = jax.nn.softmax(scores, axis=-1)
        return jnp.einsum('bqk,bkh->bqh', weights, v)

    def _L0_ffn_ref(inputs, gate_w, gate_b, expert_w, expert_b):
        import jax, jax.numpy as jnp
        import numpy as np
        THRESHOLD = 0.1
        d = inputs.shape[-1]
        x = inputs.reshape(-1, d)
        gate_logits = jax.nn.softmax(x @ gate_w + gate_b, axis=-1)
        selected = (gate_logits >= THRESHOLD).astype(x.dtype)
        weights = gate_logits * selected
        wsum = jnp.sum(weights, axis=-1, keepdims=True)
        weights = weights / jnp.where(wsum == 0, jnp.ones_like(wsum), wsum)
        E = expert_w.shape[0]
        out = jnp.zeros((x.shape[0], expert_w.shape[-1]), dtype=x.dtype)
        for e in range(E):
            out = out + weights[:, e:e + 1] * (x @ expert_w[e] + expert_b[e])
        return out.reshape(*inputs.shape[:-1], out.shape[-1])

    def _L1_attn_ref(x, WQ, WK, WV):
        import jax, jax.numpy as jnp
        import numpy as np
        KEY_DIM = 128
        SCALE = KEY_DIM ** (-0.5)
        q = jnp.einsum('bse,ke->bsk', x, WQ)
        k = jnp.einsum('bse,ke->bsk', x, WK)
        v = jnp.einsum('bse,ve->bsv', x, WV)
        scores = jnp.einsum('bsk,btk->bst', q, k) * SCALE
        masked = jnp.where(jnp.tril(scores) == 0, -jnp.inf, scores)
        attn = jax.nn.softmax(masked, axis=-1)
        return jnp.einsum('bst,btv->bsv', attn, v)

    def _L1_xattn_ref(x_text, x_vision, text_mask, vision_mask, Wq, Wk, Wv, W_film_in, b_film_in, W_film_out, b_film_out, g_norm_in, b_norm_in, g_norm_out, b_norm_out, g_ffn, b_ffn, W1, b1, W2, b2, log_dt, A_re, A_im, C_re, C_im, D_skip, mod_gate):
        import jax, jax.numpy as jnp
        import numpy as np
        B, T, DT, G, DV = (16, 64, 128, 72, 96)
        H, DH = (4, 32)
        INNER = H * DH
        HID = 4 * DT
        N_STATE = 64
        K_TOP = 32

        def layernorm(x, g, b, eps=1e-05):
            m = x.mean(-1, keepdims=True)
            v = x.var(-1, keepdims=True)
            return (x - m) * jax.lax.rsqrt(v + eps) * g + b

        def s4d(x, log_dt, A_re, A_im, C_re, C_im, D_skip):
            Bb, L, D = x.shape
            dt = jnp.exp(log_dt)
            A = A_re + 1j * A_im
            C = C_re + 1j * C_im
            dtA = dt[:, None] * A
            dC = C * (jnp.exp(dtA) - 1.0) / A
            powers = jnp.exp(dtA[:, :, None] * jnp.arange(L))
            K = 2.0 * jnp.einsum('dn,dnl->dl', dC, powers).real
            n = 2 * L
            Kf = jnp.fft.rfft(K, n=n, axis=-1)
            xf = jnp.fft.rfft(x, n=n, axis=1)
            y = jnp.fft.irfft(xf * Kf.T[None], n=n, axis=1)[:, :L]
            return y + x * D_skip
        Bb, Tt, D = x_text.shape
        Gg = x_vision.shape[1]
        Q = (x_text @ Wq).reshape(Bb, Tt, H, DH)
        K = (x_vision @ Wk).reshape(Bb, Gg, H, DH)
        scores = jnp.einsum('bthd,bghd->bhtg', Q, K) / np.sqrt(DH).astype(np.float32)
        scores = jnp.where(vision_mask[:, None, None, :], scores, -jnp.inf)
        topv, topi = jax.lax.top_k(scores, K_TOP)
        probs = jax.nn.softmax(topv, axis=-1)
        bi = jnp.arange(Bb)[:, None, None, None]
        hi = jnp.arange(H)[None, :, None, None]
        ti = jnp.arange(Tt)[None, None, :, None]
        attn = jnp.zeros_like(scores).at[bi, hi, ti, topi].set(probs)
        attn_mean = attn.mean(axis=1)
        V = x_vision @ Wv
        c_t = jnp.einsum('btg,bgd->btd', attn_mean, V)
        c_t = c_t * text_mask[..., None]
        x = layernorm(x_text, g_norm_in, b_norm_in)
        scale_in, shift_in = jnp.split(c_t @ W_film_in + b_film_in, 2, axis=-1)
        x = x * (1.0 + mod_gate * scale_in) + mod_gate * shift_in
        y = s4d(x, log_dt, A_re, A_im, C_re, C_im, D_skip)
        scale_out, shift_out = jnp.split(c_t @ W_film_out + b_film_out, 2, axis=-1)
        y = y * (1.0 + mod_gate * scale_out) + mod_gate * shift_out
        xt = x_text + y
        h = layernorm(xt, g_ffn, b_ffn)
        h = jax.nn.gelu(h @ W1 + b1, approximate=False) @ W2 + b2
        xt = xt + h
        return layernorm(xt, g_norm_out, b_norm_out)

    def _L1_ffn_ref(x, ln1_w, ln2_w, Wq, bq, Wk, bk, Wv, bv, qn_w, kn_w, Wg, bg, Wo, bo, Wr, br, W1, b1, W2, b2):
        import jax, jax.numpy as jnp
        import numpy as np
        DIM = 128
        NQ = 16
        NKV = 4
        HD = DIM // NQ
        HID = 256
        E = 8
        B, S = (1, 128)
        EPS = 1e-06

        def rmsnorm(x, w):
            ms = jnp.mean(x * x, axis=-1, keepdims=True)
            return w * (x * jax.lax.rsqrt(ms + EPS))

        def rope_tables(seq_len, head_dim):
            inv_freq = 1.0 / 10000.0 ** (jnp.arange(0, head_dim, 2, dtype=jnp.float32) / head_dim)
            t = jnp.arange(seq_len, dtype=jnp.float32)
            freqs = jnp.einsum('i,j->ij', t, inv_freq)
            return (jnp.cos(freqs), jnp.sin(freqs))

        def apply_rope(x, cos, sin):
            c = cos[None, :, None, :]
            s = sin[None, :, None, :]
            half = x.shape[-1] // 2
            x1, x2 = (x[..., :half], x[..., half:])
            return jnp.concatenate([x1 * c - x2 * s, x1 * s + x2 * c], axis=-1)

        def _forward(x, ln1_w, ln2_w, Wq, bq, Wk, bk, Wv, bv, qn_w, kn_w, Wg, bg, Wo, bo, Wr, br, W1, b1, W2, b2):
            batch, seq, _ = x.shape
            cos, sin = rope_tables(seq, HD)
            h = rmsnorm(x, ln1_w)
            q = (h @ Wq + bq).reshape(batch, seq, NQ, HD)
            k = (h @ Wk + bk).reshape(batch, seq, NKV, HD)
            v = (h @ Wv + bv).reshape(batch, seq, NKV, HD)
            q = rmsnorm(apply_rope(q, cos, sin), qn_w)
            k = rmsnorm(apply_rope(k, cos, sin), kn_w)
            rep = NQ // NKV
            k = jnp.repeat(k, rep, axis=2)
            v = jnp.repeat(v, rep, axis=2)
            scores = jnp.einsum('bthd,bshd->bhts', q, k) / np.sqrt(HD)
            causal = jnp.tril(jnp.ones((seq, seq), dtype=bool))
            scores = jnp.where(causal[None, None], scores, -jnp.inf)
            attn = jax.nn.softmax(scores, axis=-1)
            out = jnp.einsum('bhts,bshd->bthd', attn, v)
            gate = jax.nn.sigmoid(out @ Wg + bg)
            out = (out * gate).reshape(batch, seq, DIM)
            x = x + out @ Wo + bo
            h2 = rmsnorm(x, ln2_w)
            logits = h2 @ Wr + br
            top1 = jnp.argmax(logits, axis=-1).reshape(-1)
            xt = h2.reshape(-1, DIM)
            u = jnp.einsum('td,edf->tef', xt, W1) + b1
            u1, u2 = (u[..., :HID], u[..., HID:])
            act = u1 * jax.nn.sigmoid(u2)
            y_all = jnp.einsum('teh,ehd->ted', act, W2) + b2
            y = jnp.take_along_axis(y_all, top1[:, None, None], axis=1)[:, 0, :]
            return x + y.reshape(batch, seq, DIM)
        return _forward(x, ln1_w, ln2_w, Wq, bq, Wk, bk, Wv, bv, qn_w, kn_w, Wg, bg, Wo, bo, Wr, br, W1, b1, W2, b2)
    x = x + _L0_attn_ref(_layernorm(x, axis=-1), L0_attn_norm_w, L0_attn_in_proj_w, L0_attn_conv_w, L0_attn_conv_b, L0_attn_x_proj_w, L0_attn_dt_proj_w, L0_attn_dt_proj_b, L0_attn_A_log, L0_attn_D, L0_attn_out_proj_w)
    x = x + _L0_xattn_ref(_layernorm(x, axis=-1), ctx_768, ctx_768, L0_xattn_Wq, L0_xattn_bq, L0_xattn_Wk, L0_xattn_bk, L0_xattn_Wv, L0_xattn_bv)
    x = x + _L0_ffn_ref(_layernorm(x, axis=-1), L0_ffn_gate_w, L0_ffn_gate_b, L0_ffn_expert_w, L0_ffn_expert_b)
    x = x + _L1_attn_ref(_layernorm(x, axis=-1), L1_attn_WQ, L1_attn_WK, L1_attn_WV)
    x = x + _L1_xattn_ref(_layernorm(x, axis=-1), ctx_768, mask_BxS_bf1, mask_BxS2_bf1, L1_xattn_Wq, L1_xattn_Wk, L1_xattn_Wv, L1_xattn_W_film_in, L1_xattn_b_film_in, L1_xattn_W_film_out, L1_xattn_b_film_out, L1_xattn_g_norm_in, L1_xattn_b_norm_in, L1_xattn_g_norm_out, L1_xattn_b_norm_out, L1_xattn_g_ffn, L1_xattn_b_ffn, L1_xattn_W1, L1_xattn_b1, L1_xattn_W2, L1_xattn_b2, L1_xattn_log_dt, L1_xattn_A_re, L1_xattn_A_im, L1_xattn_C_re, L1_xattn_C_im, L1_xattn_D_skip, L1_xattn_mod_gate)
    x = x + _L1_ffn_ref(_layernorm(x, axis=-1), L1_ffn_ln1_w, L1_ffn_ln2_w, L1_ffn_Wq, L1_ffn_bq, L1_ffn_Wk, L1_ffn_bk, L1_ffn_Wv, L1_ffn_bv, L1_ffn_qn_w, L1_ffn_kn_w, L1_ffn_Wg, L1_ffn_bg, L1_ffn_Wo, L1_ffn_bo, L1_ffn_Wr, L1_ffn_br, L1_ffn_W1, L1_ffn_b1, L1_ffn_W2, L1_ffn_b2)
    return x

_drawn_inputs = setup_inputs


def setup_inputs(seed=0):
    import zlib

    import numpy as np

    out = dict(_drawn_inputs(seed))
    spreads = {'L0_attn_norm_w': (1.0, 0.6),
     'L0_attn_conv_b': (0.0, 0.8),
     'L0_attn_dt_proj_b': (-4.600166320800781, 0.6),
     'L0_attn_D': (1.0, 0.6),
     'L0_ffn_gate_b': (0.0, 2.0),
     'L0_ffn_expert_b': (0.0, 2.0),
     'L1_xattn_b_film_in': (0.0, 0.8),
     'L1_xattn_b_film_out': (0.0, 2.0),
     'L1_xattn_g_norm_in': (1.0, 0.6),
     'L1_xattn_b_norm_in': (0.0, 0.8),
     'L1_xattn_g_norm_out': (1.0, 0.6),
     'L1_xattn_b_norm_out': (0.0, 0.8),
     'L1_xattn_g_ffn': (1.0, 0.6),
     'L1_xattn_b_ffn': (0.0, 2.0),
     'L1_xattn_b1': (0.0, 2.0),
     'L1_xattn_b2': (0.0, 2.0),
     'L1_xattn_A_re': (-0.5, 0.6),
     'L1_ffn_ln1_w': (1.0, 0.6),
     'L1_ffn_ln2_w': (1.0, 0.6),
     'L1_ffn_bq': (0.0, 2.0),
     'L1_ffn_bk': (0.0, 2.0),
     'L1_ffn_bv': (0.0, 0.651),
     'L1_ffn_qn_w': (1.0, 0.6),
     'L1_ffn_kn_w': (1.0, 0.6),
     'L1_ffn_bg': (0.0, 2.0),
     'L1_ffn_bo': (0.0, 0.628),
     'L1_ffn_br': (0.0, 0.624),
     'L1_ffn_b1': (0.0, 2.0),
     'L1_ffn_b2': (0.0, 1.582)}
    factors = {'L0_attn_in_proj_w': 8.0,
     'L0_attn_conv_w': 8.0,
     'L0_attn_x_proj_w': 8.0,
     'L0_attn_dt_proj_w': 8.0,
     'L0_attn_A_log': 8.0,
     'L0_attn_out_proj_w': 8.0,
     'L0_xattn_bk': 200.0,
     'L1_xattn_Wq': 23.35,
     'L1_xattn_Wk': 24.041,
     'L1_xattn_Wv': 4.166,
     'L1_xattn_W_film_in': 13.693,
     'L1_xattn_W_film_out': 17.617,
     'L1_xattn_W1': 9.72,
     'L1_xattn_W2': 2.697,
     'L0_xattn_bq': 4.089,
     'L0_xattn_bv': 8.0,
     'L0_ffn_gate_w': 8.0,
     'L0_ffn_expert_w': 7.815,
     'L1_attn_WQ': 5.817,
     'L1_attn_WK': 5.412,
     'L1_xattn_C_im': 2.841,
     'L1_ffn_Wq': 6.253,
     'L1_ffn_Wk': 4.843,
     'L1_ffn_Wg': 8.0,
     'L1_ffn_Wo': 3.5}
    for name, (base, spread) in spreads.items():
        noise = np.random.default_rng([zlib.crc32(name.encode()), seed]).standard_normal(out[name].shape)
        drawn = base * np.exp(spread * noise) if base else spread * noise
        out[name] = jnp.asarray(drawn.astype(out[name].dtype))
    for name, factor in factors.items():
        out[name] = (out[name] * factor).astype(out[name].dtype)
    return out
```

```python
from contextlib import ExitStack

import numpy as np

import concourse.bass as bass
from concourse import mybir

ALU = mybir.AluOpType
ACT = mybir.ActivationFunctionType
F32 = mybir.dt.float32
BF16 = mybir.dt.bfloat16
U8 = mybir.dt.uint8
AX = mybir.AxisListType.X

P = 128
S = 1024
D = 128
NT = S // P
S2 = 6404
DC = 96
HALF = 512
LN_EPS = 1e-5
NEG = -1e30


def recycle(nc, used):
    nc.clear_and_free_semaphores(list(used))
    used.clear()
    nc.all_engine_barrier()


class Memory:

    used = []

    def __init__(self, nc, ctx, name):
        self.nc, self.ctx, self.name = nc, ctx, name

    def sb(self, name, shape, dt=F32):
        return self.ctx.enter_context(self.nc.sbuf_tensor(f"{self.name}_{name}", shape, dt))

    def sem(self, name):
        handle = self.nc.alloc_semaphore(f"{self.name}_{name}")
        self.used.append(handle)
        return handle


def chained(eng, sem):
    count = [0]

    def link(ins):
        count[0] += 1
        ins.then_inc(sem, 1)
        eng.wait_ge(sem, count[0])

    return link


def wait_in_loop(eng, sem, value, passed):
    eng.wait_ge(sem, value)
    eng.sem_inc(passed, 1)


def normalise(dve, link, x, stats, mv, rstd, var_ready, root_ready, xn, ready, second_eps=None,
              second=None):
    for i in range(NT):
        ins = dve.bn_stats(stats[:, i, :], x[:, i, :])
    link(ins)
    for i in range(NT):
        ins = dve.bn_aggr(mv[:, i, :], stats[:, i, :])
    link(ins)
    ins = dve.tensor_scalar(rstd[:, :, 0], mv[:, :, 1], LN_EPS, None, ALU.add)
    n = 1
    if second is not None:
        n = 2
        ins = dve.tensor_scalar(rstd[:, :, 1], mv[:, :, 1], 1.0 + second_eps, LN_EPS * second_eps,
                                ALU.mult, ALU.add)
    ins.then_inc(var_ready, 1)
    dve.wait_ge(root_ready, 1)
    link(dve.reciprocal(rstd[:, :, 0:n], rstd[:, :, 0:n]))
    for k, dst in enumerate((xn, second)[:n]):
        for i in range(NT):
            ins = dve.tensor_scalar(dst[:, i, :], x[:, i, :], mv[:, i, 0:1], rstd[:, i, k:k + 1],
                                    ALU.subtract, ALU.mult)
            if k == n - 1:
                ins.then_inc(ready, 1)


def root(act, rstd, n, var_ready, root_ready):
    act.wait_ge(var_ready, 1)
    act.activation(rstd[:, :, 0:n], rstd[:, :, 0:n], ACT.Sqrt).then_inc(root_ready, 1)


def transpose_tiles(pe, src, ident, banks, ready, done):
    for i in range(NT):
        pe.wait_ge(ready, i + 1)
        pe.transpose(banks[:, i // 4, (i % 4) * P:(i % 4 + 1) * P], src[:, i, :],
                     ident).then_inc(done, 1)



def load_constants(nc, g, t, m):
    loaded = m.sem("loaded")
    consts = m.sem("consts")
    with nc.Block() as block:
        @block.sync
        def _(sp):
            sp.dma_start(g["x"][:], t["x"].rearrange("(i p) d -> p i d", p=P)).then_inc(loaded, 16)
            sp.dma_start(g["ident"][:], t["ident"]).then_inc(loaded, 16)
            sp.wait_ge(loaded, 32)

        @block.vector
        def _(dve):
            dve.memset(g["ones"][:], 1.0).then_inc(consts, 1)
            dve.wait_ge(consts, 1)


def store_output(nc, g, t, m):
    stored = m.sem("stored")
    with nc.Block() as block:
        @block.sync
        def _(sp):
            sp.dma_start(t["out"].rearrange("(i p) d -> p i d", p=P), g["x"][:]).then_inc(stored, 16)
            sp.wait_ge(stored, 16)



def mamba(nc, g, t, m):
    DI, NS, DR = 2 * D, 16, D // 16
    NC = DI // P
    ps = g["psum"]
    w_in = m.sb("w_in", [P, 2 * DI])
    norm_w = m.sb("norm_w", [P, 1])
    conv_w = m.sb("conv_w", [P, NC, 4])
    conv_b = m.sb("conv_b", [P, NC])
    w_bcdt = m.sb("w_bcdt", [P, NC, 3 * 2 * NS + DR])
    w_dt = m.sb("w_dt", [DR, DI])
    dt_b = m.sb("dt_b", [P, NC])
    a_log = m.sb("a_log", [P, NC, NS])
    a_neg = m.sb("a_neg", [P, NC, NS])
    skip = m.sb("skip", [P, NC])
    w_out = m.sb("w_out", [P, NC, D])
    onehot = m.sb("onehot", [3 * 2 * NS, 2 * NS], BF16)
    onehot_f = m.sb("onehot_f", [3 * 2 * NS, 2 * NS])
    stats = m.sb("stats", [P, NT, 6])
    mv = m.sb("mv", [P, NT, 2])
    rstd = m.sb("rstd", [P, NT, 2])
    xn = m.sb("xn", [P, NT, D])
    h = m.sb("h", [P, NT, D])
    hT = m.sb("hT", [P, S])
    xi_pad = m.sb("xi_pad", [P, NC, S + 3])
    conv = m.sb("conv", [P, NC, S])
    xi = m.sb("xi", [P, NC, S])
    zs = m.sb("zs", [P, NC, S])
    dt_low = m.sb("dt_low", [DR, S])
    pre = m.sb("pre", [P, NC, S])
    soft = m.sb("soft", [P, NC, S])
    delta = m.sb("delta", [P, NC, S])
    du = m.sb("du", [P, NC, S])
    rest = m.sb("rest", [3 * 2 * NS, S])
    hi = m.sb("hi", [3 * 2 * NS, S], BF16)
    mid = m.sb("mid", [3 * 2 * NS, S], BF16)
    split = m.sb("split", [3 * 2 * NS, S], BF16)
    b_all = m.sb("b_all", [P, 2, S])
    decay = m.sb("decay", [P, 2, S])
    drive = m.sb("drive", [P, 2, S])
    state = m.sb("state", [P, 2, S])
    read = m.sb("read", [P, 2, S])
    y = m.sb("y", [P, NC, S])

    loaded = m.sem("loaded")
    chain = {e: m.sem(f"chain_{e}") for e in ("dve", "act")}
    h_ready, hT_psum, hT_ready, in_done, xi_copied, z_ready, conv_done, xi_ready = (
        m.sem(n) for n in ("h_ready", "hT_psum", "hT_ready", "in_done", "xi_copied", "z_ready",
                           "conv_done", "xi_ready"))
    bc_done, dt_copied, split_ready, dt_done, pre_ready, delta_ready, du_ready = (
        m.sem(n) for n in ("bc_done", "dt_copied", "split_ready", "dt_done", "pre_ready",
                           "delta_ready", "du_ready"))
    b_bcast, c_bcast, b_copied, decay_ready, drive_ready, scanned, read_ready, summed = (
        m.sem(n) for n in ("b_bcast", "c_bcast", "b_copied", "decay_ready", "drive_ready",
                           "scanned", "read_ready", "summed"))
    y_ready, out_done, abs_ready, a_ready = (m.sem(n) for n in ("y_ready", "out_done", "abs_ready", "a_ready"))
    var_ready, root_ready = m.sem("var_ready"), m.sem("root_ready")
    N_LOADS = 11
    BC, BC3 = 2 * NS, 3 * 2 * NS

    with nc.Block() as block:
        @block.sync
        def _(sp):
            for dst, src in ((w_in[:], t["L0_in_proj_T"]),
                             (norm_w[:], t["L0_attn_norm_w"].unsqueeze(1)),
                             (conv_w[:], t["L0_attn_conv_w"].rearrange("(c p) k -> p c k", p=P)),
                             (conv_b[:], t["L0_conv_b_T"]),
                             (w_bcdt[:], t["L0_bcdt_T"].rearrange("(c p) k -> p c k", p=P)),
                             (w_dt[:], t["L0_dt_proj_T"]),
                             (dt_b[:], t["L0_dt_b_T"]),
                             (a_log[:], t["L0_attn_A_log"].rearrange("(c p) n -> p c n", p=P)),
                             (skip[:], t["L0_D_T"]),
                             (w_out[:], t["L0_out_proj_T"].rearrange("(c p) k -> p c k", p=P)),
                             (onehot_f[:], t["onehot3"])):
                sp.dma_start(dst, src).then_inc(loaded, 16)

        @block.vector
        def _(dve):
            link = chained(dve, chain["dve"])
            link(dve.memset(xi_pad[:, :, 0:3], 0.0))
            normalise(dve, link, g["x"], stats, mv, rstd, var_ready, root_ready, xn, h_ready,
                      LN_EPS, h)
            dve.wait_ge(loaded, 16 * N_LOADS)
            link(dve.tensor_copy(onehot[:], onehot_f[:]))
            dve.wait_ge(xi_copied, 2 * NC)
            for c in range(NC):
                link(dve.tensor_scalar(conv[:, c, :], xi_pad[:, c, 0:S], conv_w[:, c, 0:1], None, ALU.mult))
                for k in range(1, 4):
                    ins = dve.scalar_tensor_tensor(out=conv[:, c, :], in0=xi_pad[:, c, k:k + S],
                                                   scalar=conv_w[:, c, k:k + 1], in1=conv[:, c, :],
                                                   op0=ALU.mult, op1=ALU.add)
                    if k < 3:
                        link(ins)
                ins.then_inc(conv_done, 1)
            dve.wait_ge(bc_done, 3)
            bc = ps[0:3 * BC, 0:2, :].rearrange("p b n -> p (b n)")
            link(dve.tensor_copy(hi[:], bc))
            link(dve.tensor_tensor(rest[:], bc, hi[:], ALU.subtract))
            link(dve.tensor_copy(mid[:], rest[:]))
            link(dve.tensor_tensor(rest[:], rest[:], mid[:], ALU.subtract))
            dve.tensor_copy(split[0:BC, :], hi[0:BC, :]).then_inc(split_ready, 1)
            dve.tensor_copy(split[BC:2 * BC, :], mid[BC:2 * BC, :]).then_inc(split_ready, 1)
            dve.tensor_copy(split[2 * BC:3 * BC, :], rest[2 * BC:3 * BC, :]).then_inc(split_ready, 1)
            dve.wait_ge(dt_done, 2 * NC)
            for c in range(NC):
                acc = ps[:, 4 + 2 * c:6 + 2 * c, :].rearrange("p b n -> p (b n)")
                link(dve.tensor_scalar(pre[:, c, :], acc, dt_b[:, c:c + 1], None, ALU.add))
            link(dve.tensor_scalar(soft[:], pre[:], -1.0, None, ALU.mult))
            dve.tensor_tensor(soft[:], soft[:], pre[:], ALU.min).then_inc(abs_ready, 1)
            dve.wait_ge(delta_ready, 1)
            link(dve.scalar_tensor_tensor(out=delta[:], in0=pre[:], scalar=0.0, in1=soft[:],
                                          op0=ALU.max, op1=ALU.add))
            dve.wait_ge(xi_ready, NC)
            dve.tensor_tensor(du[:], delta[:], xi[:], ALU.mult).then_inc(du_ready, 1)
            for s in range(NS):
                for c in range(NC):
                    n = NC * s + c
                    dve.wait_ge(decay_ready, n + 1)
                    dve.wait_ge(drive_ready, n + 1)
                    dve.tensor_tensor_scan(state[:, c, :], decay[:, c, :], drive[:, c, :], 0.0,
                                           ALU.mult, ALU.add).then_inc(scanned, 1)
                    dve.wait_ge(scanned, n + 1)
                    dve.wait_ge(c_bcast, s + 1)
                    if n >= 2:
                        dve.wait_ge(summed, n - 1)
                    dve.tensor_tensor(read[:, c, :], state[:, c, :],
                                      ps[:, 2:4, :].rearrange("p b n -> p (b n)"),
                                      ALU.mult).then_inc(read_ready, 1)
            dve.wait_ge(summed, NC * NS)
            dve.wait_ge(z_ready, 2 * NC)
            for c in range(NC):
                acc = ps[:, 4 + 2 * c:6 + 2 * c, :].rearrange("p b n -> p (b n)")
                link(dve.scalar_tensor_tensor(out=y[:, c, :], in0=xi[:, c, :], scalar=skip[:, c:c + 1],
                                              in1=acc, op0=ALU.mult, op1=ALU.add))
                dve.tensor_tensor(y[:, c, :], y[:, c, :], zs[:, c, :], ALU.mult).then_inc(y_ready, 1)
            link(dve.tensor_tensor(g["x"][:], g["x"][:], xn[:], ALU.add))
            dve.wait_ge(out_done, NT)
            dve.tensor_tensor(g["x"][:], g["x"][:],
                              ps[:, 0:2, :].rearrange("p b (i d) -> p (b i) d", d=D), ALU.add)

        @block.tensor
        def _(pe):
            transpose_tiles(pe, h, g["ident"][:], ps, h_ready, hT_psum)
            pe.wait_ge(loaded, 16 * N_LOADS)
            pe.wait_ge(hT_ready, 2)
            for e in range(2 * NC):
                for n in range(2):
                    bank = (4 + 2 * e + n) % 8
                    pe.matmul(ps[:, bank, :], w_in[:, e * P:(e + 1) * P], hT[:, n * HALF:(n + 1) * HALF],
                              start=True, stop=True).then_inc(in_done, 1)
            pe.wait_ge(xi_ready, NC)
            pe.wait_ge(z_ready, 2 * NC)
            for n in range(2):
                for c in range(NC):
                    last = pe.matmul(ps[0:3 * BC, n, :],
                                     w_bcdt[:, c, 0:BC3],
                                     xi[:, c, n * HALF:(n + 1) * HALF], start=c == 0, stop=c == NC - 1)
                last.then_inc(bc_done, 1)
                for c in range(NC):
                    last = pe.matmul(ps[0:DR, 2 + n, :], w_bcdt[:, c, BC3:BC3 + DR],
                                     xi[:, c, n * HALF:(n + 1) * HALF], start=c == 0, stop=c == NC - 1)
                last.then_inc(bc_done, 1)
            pe.wait_ge(dt_copied, 1)
            for c in range(NC):
                for n in range(2):
                    pe.matmul(ps[:, 4 + 2 * c + n, :], w_dt[:, c * P:(c + 1) * P],
                              dt_low[:, n * HALF:(n + 1) * HALF], start=True, stop=True).then_inc(dt_done, 1)
            pe.wait_ge(split_ready, 3)
            pe.wait_ge(abs_ready, 1)

            def broadcast(row, banks, done):
                sel = onehot[:, row:row + 1].to_broadcast([3 * BC, P])
                for n in range(2):
                    last = pe.matmul(ps[:, banks + n, :], sel, split[:, n * HALF:(n + 1) * HALF],
                                     start=True, stop=True)
                last.then_inc(done, 1)

            def add_state(n):
                c = n % NC
                pe.wait_ge(read_ready, n + 1)
                for q in range(2):
                    last = pe.matmul(ps[:, 4 + 2 * c + q, :], g["ident"][:],
                                     read[:, c, q * HALF:(q + 1) * HALF],
                                     start=n < NC, stop=n >= NC * (NS - 1))
                last.then_inc(summed, 1)

            for s in range(NS):
                if s >= 1:
                    pe.wait_ge(b_copied, s)
                broadcast(s, 0, b_bcast)
                if s >= 1:
                    pe.wait_ge(read_ready, NC * s)
                broadcast(NS + s, 2, c_bcast)
                if s >= 1:
                    for c in range(NC):
                        add_state(NC * (s - 1) + c)
            for c in range(NC):
                add_state(NC * (NS - 1) + c)
            pe.wait_ge(y_ready, NC)
            for i in range(NT):
                for c in range(NC):
                    last = pe.matmul(ps[:, i // 4, (i % 4) * D:(i % 4 + 1) * D],
                                     y[:, c, i * P:(i + 1) * P], w_out[:, c, :],
                                     start=c == 0, stop=c == NC - 1)
                last.then_inc(out_done, 1)

        @block.scalar
        def _(act):
            link = chained(act, chain["act"])
            root(act, rstd, 2, var_ready, root_ready)
            act.wait_ge(loaded, 16 * N_LOADS)
            link(act.activation(a_neg[:], a_log[:], ACT.Exp))
            link(act.mul(a_neg[:], a_neg[:], -1.0))
            for n in range(2):
                act.wait_ge(hT_psum, 4 * (n + 1))
                act.activation(hT[:, n * HALF:(n + 1) * HALF], ps[:, n, :], ACT.Copy,
                               scale=norm_w[:, 0:1]).then_inc(hT_ready, 1)
            for e in range(2 * NC):
                for n in range(2):
                    act.wait_ge(in_done, 2 * e + n + 1)
                    bank = (4 + 2 * e + n) % 8
                    if e < NC:
                        act.activation(xi_pad[:, e, 3 + n * HALF:3 + (n + 1) * HALF], ps[:, bank, :],
                                       ACT.Copy).then_inc(xi_copied, 1)
                    else:
                        act.activation(zs[:, e - NC, n * HALF:(n + 1) * HALF], ps[:, bank, :],
                                       ACT.Silu).then_inc(z_ready, 1)
            for c in range(NC):
                act.wait_ge(conv_done, c + 1)
                act.activation(xi[:, c, :], conv[:, c, :], ACT.Silu,
                               bias=conv_b[:, c:c + 1]).then_inc(xi_ready, 1)
            act.wait_ge(bc_done, 4)
            act.activation(dt_low[:], ps[0:DR, 2:4, :].rearrange("p b n -> p (b n)"),
                           ACT.Copy).then_inc(dt_copied, 1)
            act.wait_ge(abs_ready, 1)
            link(act.activation(soft[:], soft[:], ACT.Exp))
            act.activation(soft[:], soft[:], ACT.Ln, bias=1.0).then_inc(delta_ready, 1)
            act.wait_ge(du_ready, 1)
            for s in range(NS):
                act.wait_ge(b_bcast, s + 1)
                if s >= 2:
                    act.wait_ge(drive_ready, NC * (s - 1))
                act.activation(b_all[:, s % 2, :], ps[:, 0:2, :].rearrange("p b n -> p (b n)"),
                               ACT.Copy).then_inc(b_copied, 1)
                for c in range(NC):
                    n = NC * s + c
                    if n >= 2:
                        act.wait_ge(scanned, n - 1)
                    act.activation(decay[:, c, :], delta[:, c, :], ACT.Exp,
                                   scale=a_neg[:, c, s:s + 1]).then_inc(decay_ready, 1)

        @block.gpsimd
        def _(pool):
            pool.wait_ge(du_ready, 1)
            for s in range(NS):
                pool.wait_ge(b_copied, s + 1)
                for c in range(NC):
                    n = NC * s + c
                    if n >= 2:
                        pool.wait_ge(scanned, n - 1)
                    pool.tensor_tensor(drive[:, c, :], du[:, c, :], b_all[:, s % 2, :],
                                       ALU.mult).then_inc(drive_ready, 1)



KT = -(-S2 // P)
K_LAST = S2 - (KT - 1) * P
CHUNK = 2 * HALF
N_CHUNK = -(-S2 // CHUNK)


def cross_attention(nc, g, t, m):
    CA = DC + 1
    ps = g["psum"]
    ctx_T = m.sb("ctx_T", [CA, S2])
    w_q = m.sb("w_q", [P, D])
    b_q = m.sb("b_q", [P, 1])
    w_k = m.sb("w_k", [P, CA])
    w_v = m.sb("w_v", [CA, D + 1])
    stats = m.sb("stats", [P, NT, 6])
    mv = m.sb("mv", [P, NT, 2])
    rstd = m.sb("rstd", [P, NT, 1])
    xn = m.sb("xn", [P, NT, D])
    xT = m.sb("xT", [P, S])
    qT = m.sb("qT", [P, S])
    qc = m.sb("qc", [CA, S])
    qc_shifted = m.sb("qc_shifted", [CA, S])
    tops = m.sb("tops", [P, NT, N_CHUNK])
    top = m.sb("top", [P, NT])
    minus_top = m.sb("minus_top", [P, NT, CA])
    prob = m.sb("prob", [P, 3, S])
    summed_c = m.sb("summed_c", [CA, S])
    share = m.sb("share", [P, NT])

    loaded, ctx_loaded, ones_set = m.sem("loaded"), m.sem("ctx_loaded"), m.sem("ones_set")
    chain_dve, chain_pool = m.sem("chain_dve"), m.sem("chain_pool")
    var_ready, root_ready, xn_ready, xT_psum, xT_ready = (
        m.sem(n) for n in ("var_ready", "root_ready", "xn_ready", "xT_psum", "xT_ready"))
    q_done, q_ready, qc_done, qc_ready, score_done, max_read, top_ready = (
        m.sem(n) for n in ("q_done", "q_ready", "qc_done", "qc_ready", "score_done", "max_read",
                           "top_ready"))
    shift_done, shift_ready, prob_psum, prob_ready, pv_done, sum_ready, out_done = (
        m.sem(n) for n in ("shift_done", "shift_ready", "prob_psum", "prob_ready", "pv_done",
                           "sum_ready", "out_done"))
    N_LOADS, N_CTX = 5, 3
    ctx = g["ctx_rows"]

    def chunk_cols(c):
        return range(c * CHUNK, min((c + 1) * CHUNK, S2), HALF)

    def pair(n):
        return ps[:, n:n + 2, :].rearrange("p b n -> p (b n)")

    with nc.Block() as block:
        @block.sync
        def _(sp):
            sp.dma_start(w_q[:], t["L0_xattn_Wq"]).then_inc(loaded, 16)
            sp.dma_start(b_q[:], t["L0_xattn_bq"].unsqueeze(1)).then_inc(loaded, 16)
            sp.dma_start(w_k[:, 0:DC], t["L0_Wk_T"]).then_inc(loaded, 16)
            sp.dma_start(w_k[:, DC:CA], t["L0_xattn_bk"].unsqueeze(1)).then_inc(loaded, 16)
            sp.dma_start(ctx_T[0:DC, :], t["ctx_T"]).then_inc(loaded, 16)
            full = (KT - 1) * P
            sp.dma_start(ctx[:, 0:KT - 1, 0:DC],
                         t["ctx"][0:full, :].rearrange("(k p) c -> p k c", p=P)).then_inc(ctx_loaded, 16)
            sp.dma_start(ctx[0:K_LAST, KT - 1, 0:DC], t["ctx"][full:S2, :]).then_inc(ctx_loaded, 16)
            sp.wait_ge(ones_set, 1)
            sp.dma_start(w_v[0:DC, 0:D], t["L0_xattn_Wv"]).then_inc(ctx_loaded, 16)
            sp.dma_start(w_v[DC:CA, 0:D], t["L0_xattn_bv"].unsqueeze(0)).then_inc(ctx_loaded, 16)

        @block.gpsimd
        def _(pool):
            link = chained(pool, chain_pool)
            link(pool.memset(w_v[:], 0.0))
            link(pool.memset(w_v[DC:CA, D:D + 1], 1.0))
            link(pool.memset(ctx_T[DC:CA, :], 1.0))
            link(pool.memset(ctx[:, :, DC:CA], 1.0))
            pool.memset(minus_top[:], 0.0).then_inc(ones_set, 1)

        @block.vector
        def _(dve):
            link = chained(dve, chain_dve)
            normalise(dve, link, g["x"], stats, mv, rstd, var_ready, root_ready, xn, xn_ready)
            dve.wait_ge(ones_set, 1)
            for i in range(NT):
                for c in range(N_CHUNK):
                    n = N_CHUNK * i + c
                    dve.wait_ge(score_done, n + 1)
                    width = min(CHUNK, S2 - c * CHUNK)
                    dve.reduce_max(tops[:, i, c:c + 1], pair(2 * (n % 4))[:, 0:width],
                                   AX).then_inc(max_read, 1)
            dve.wait_ge(max_read, NT * N_CHUNK)
            link(dve.reduce_max(top[:], tops[:], AX))
            dve.tensor_scalar(minus_top[:, :, DC], top[:], -1.0, None, ALU.mult).then_inc(top_ready, 1)
            dve.wait_ge(pv_done, KT)
            dve.tensor_copy(summed_c[:], pair(6)[0:CA, :]).then_inc(sum_ready, 1)
            for i in range(NT):
                dve.wait_ge(out_done, i + 1)
                bank = ps[:, i % 2, :]
                link(dve.reciprocal(share[:, i:i + 1], bank[:, D:D + 1]))
                dve.scalar_tensor_tensor(out=g["x"][:, i, :], in0=bank[:, 0:D], scalar=share[:, i:i + 1],
                                         in1=g["x"][:, i, :], op0=ALU.mult, op1=ALU.add).then_inc(sum_ready, 1)

        @block.tensor
        def _(pe):
            transpose_tiles(pe, xn, g["ident"][:], ps, xn_ready, xT_psum)
            pe.wait_ge(loaded, 16 * N_LOADS)
            for n in range(2):
                pe.wait_ge(xT_ready, n + 1)
                pe.matmul(ps[:, 2 + n, :], w_q[:], xT[:, n * HALF:(n + 1) * HALF],
                          start=True, stop=True).then_inc(q_done, 1)
            for n in range(2):
                pe.wait_ge(q_ready, n + 1)
                pe.matmul(ps[0:CA, 4 + n, :], w_k[:], qT[:, n * HALF:(n + 1) * HALF],
                          start=True, stop=True).then_inc(qc_done, 1)
            pe.wait_ge(ones_set, 1)
            pe.wait_ge(qc_ready, 2)
            for i in range(NT):
                for c in range(N_CHUNK):
                    n = N_CHUNK * i + c
                    if n >= 4:
                        pe.wait_ge(max_read, n - 3)
                    for b, k in enumerate(chunk_cols(c)):
                        width = min(HALF, S2 - k)
                        last = pe.matmul(ps[:, 2 * (n % 4) + b, 0:width], qc[:, i * P:(i + 1) * P],
                                         ctx_T[:, k:k + width], start=True, stop=True)
                    last.then_inc(score_done, 1)
            pe.wait_ge(top_ready, 1)
            for n in range(2):
                pe.matmul(ps[0:CA, n, :], w_k[:], qT[:, n * HALF:(n + 1) * HALF], start=True, stop=False)
                for q in range(4):
                    last = pe.matmul(ps[0:CA, n, q * P:(q + 1) * P], minus_top[:, 4 * n + q, :],
                                     g["ident"][:], start=False, stop=q == 3)
                last.then_inc(shift_done, 1)
            pe.wait_ge(ctx_loaded, 16 * 4)

            def weighted(k):
                rows = P if k < KT - 1 else K_LAST
                pe.wait_ge(prob_ready, k + 1)
                for n in range(2):
                    last = pe.matmul(ps[0:CA, 6 + n, :], ctx[0:rows, k, :],
                                     prob[0:rows, k % 3, n * HALF:(n + 1) * HALF],
                                     start=k == 0, stop=k == KT - 1)
                last.then_inc(pv_done, 1)

            pe.wait_ge(shift_ready, 2)
            for k in range(KT):
                rows = P if k < KT - 1 else K_LAST
                if k >= 3:
                    pe.wait_ge(prob_ready, k - 2)
                for n in range(2):
                    last = pe.matmul(ps[0:rows, 2 * (k % 3) + n, :], ctx_T[:, k * P:k * P + rows],
                                     qc_shifted[:, n * HALF:(n + 1) * HALF], start=True, stop=True)
                last.then_inc(prob_psum, 1)
                if k >= 1:
                    weighted(k - 1)
            weighted(KT - 1)
            pe.wait_ge(sum_ready, 1)
            for i in range(NT):
                if i >= 2:
                    pe.wait_ge(sum_ready, i)
                pe.matmul(ps[:, i % 2, 0:D + 1], summed_c[:, i * P:(i + 1) * P], w_v[:],
                          start=True, stop=True).then_inc(out_done, 1)

        @block.scalar
        def _(act):
            root(act, rstd, 1, var_ready, root_ready)
            act.wait_ge(loaded, 16 * N_LOADS)
            for n in range(2):
                act.wait_ge(xT_psum, 4 * (n + 1))
                act.activation(xT[:, n * HALF:(n + 1) * HALF], ps[:, n, :], ACT.Copy).then_inc(xT_ready, 1)
            for n in range(2):
                act.wait_ge(q_done, n + 1)
                act.activation(qT[:, n * HALF:(n + 1) * HALF], ps[:, 2 + n, :], ACT.Identity,
                               bias=b_q[:, 0:1]).then_inc(q_ready, 1)
            for n in range(2):
                act.wait_ge(qc_done, n + 1)
                act.activation(qc[:, n * HALF:(n + 1) * HALF], ps[0:CA, 4 + n, :],
                               ACT.Copy).then_inc(qc_ready, 1)
            for n in range(2):
                act.wait_ge(shift_done, n + 1)
                act.activation(qc_shifted[:, n * HALF:(n + 1) * HALF], ps[0:CA, n, :],
                               ACT.Copy).then_inc(shift_ready, 1)
            for k in range(KT):
                rows = P if k < KT - 1 else K_LAST
                act.wait_ge(prob_psum, k + 1)
                if k >= 3:
                    act.wait_ge(pv_done, k - 2)
                act.activation(prob[0:rows, k % 3, :], pair(2 * (k % 3))[0:rows, :],
                               ACT.Exp).then_inc(prob_ready, 1)



def threshold_experts(nc, g, t, m):
    NE = 8
    THRESHOLD = 0.1
    ps = g["psum"]
    w_e = m.sb("w_e", [P, NE, D])
    b_e = m.sb("b_e", [1, NE * D])
    w_g = m.sb("w_g", [P, NE])
    b_g = m.sb("b_g", [1, NE])
    stats = m.sb("stats", [P, NT, 6])
    mv = m.sb("mv", [P, NT, 2])
    rstd = m.sb("rstd", [P, NT, 1])
    xn = m.sb("xn", [P, NT, D])
    xT = m.sb("xT", [P, S])
    gates = m.sb("gates", [P, NT, NE])
    kept = m.sb("kept", [P, NT, NE])
    best = m.sb("best", [P, NT])
    total = m.sb("total", [P, NT])
    none = m.sb("none", [P, NT])
    scaled = m.sb("scaled", [P, 2, NE, D])
    mixed = m.sb("mixed", [P, 2, D])

    loaded, chain_dve = m.sem("loaded"), m.sem("chain_dve")
    var_ready, root_ready, xn_ready, xT_psum, xT_ready = (
        m.sem(n) for n in ("var_ready", "root_ready", "xn_ready", "xT_psum", "xT_ready"))
    gate_done, shifted, exp_ready, expert_done, scaled_ready = (
        m.sem(n) for n in ("gate_done", "shifted", "exp_ready", "expert_done", "scaled_ready"))
    N_LOADS = 4

    def spread(v):
        return v.unsqueeze(2).to_broadcast([P, NT, NE])

    with nc.Block() as block:
        @block.sync
        def _(sp):
            sp.dma_start(w_e[:], t["L0_ffn_expert_w"].rearrange("e p d -> p e d")).then_inc(loaded, 16)
            sp.dma_start(b_e[:], t["L0_ffn_expert_b"].rearrange("e d -> (e d)").unsqueeze(0)).then_inc(loaded, 16)
            sp.dma_start(w_g[:], t["L0_ffn_gate_w"]).then_inc(loaded, 16)
            sp.dma_start(b_g[:], t["L0_ffn_gate_b"].unsqueeze(0)).then_inc(loaded, 16)

        @block.vector
        def _(dve):
            link = chained(dve, chain_dve)
            normalise(dve, link, g["x"], stats, mv, rstd, var_ready, root_ready, xn, xn_ready)
            dve.wait_ge(gate_done, 1)
            logits = ps[:, 6, 0:NT * NE].rearrange("p (i e) -> p i e", e=NE)
            link(dve.reduce_max(best[:], logits, AX))
            dve.tensor_tensor(gates[:], logits, spread(best[:]), ALU.subtract).then_inc(shifted, 1)
            dve.wait_ge(exp_ready, 1)
            link(dve.reduce_sum(total[:], gates[:], AX))
            link(dve.reciprocal(total[:], total[:]))
            link(dve.tensor_tensor(gates[:], gates[:], spread(total[:]), ALU.mult))
            link(dve.scalar_tensor_tensor(out=kept[:], in0=gates[:], scalar=THRESHOLD, in1=gates[:],
                                          op0=ALU.is_ge, op1=ALU.mult))
            link(dve.reduce_sum(total[:], kept[:], AX))
            link(dve.tensor_scalar(none[:], total[:], 0.0, None, ALU.is_equal))
            link(dve.tensor_tensor(total[:], total[:], none[:], ALU.add))
            link(dve.reciprocal(total[:], total[:]))
            link(dve.tensor_tensor(kept[:], kept[:], spread(total[:]), ALU.mult))
            for i in range(NT):
                dve.wait_ge(expert_done, i + 1)
                b = 2 * (i % 3)
                out = ps[:, b:b + 2, :].rearrange("p b (e d) -> p (b e) d", d=D)
                dve.tensor_tensor(scaled[:, i % 2, :, :], out,
                                  kept[:, i, :].unsqueeze(2).to_broadcast([P, NE, D]),
                                  ALU.mult).then_inc(scaled_ready, 1)
                dve.wait_ge(scaled_ready, i + 1)
                link(dve.reduce_sum(mixed[:, i % 2, :], scaled[:, i % 2, :, :].rearrange("p e d -> p d e"), AX))
                link(dve.tensor_tensor(g["x"][:, i, :], g["x"][:, i, :], mixed[:, i % 2, :], ALU.add))

        @block.tensor
        def _(pe):
            transpose_tiles(pe, xn, g["ident"][:], ps, xn_ready, xT_psum)
            pe.wait_ge(loaded, 16 * N_LOADS)
            for i in range(NT):
                pe.wait_ge(xT_ready, i // 4 + 1)
                cols = slice(i * NE, (i + 1) * NE)
                pe.matmul(ps[:, 6, cols], xT[:, i * P:(i + 1) * P], w_g[:], start=True, stop=False)
                last = pe.matmul(ps[:, 6, cols], g["ones"][:, 0:P], b_g[:], start=False, stop=True)
            last.then_inc(gate_done, 1)
            for i in range(NT):
                if i >= 3:
                    pe.wait_ge(scaled_ready, i - 2)
                for h in range(2):
                    bank = ps[:, 2 * (i % 3) + h, :]
                    pe.matmul(bank, xT[:, i * P:(i + 1) * P],
                              w_e[:, 4 * h:4 * h + 4, :].rearrange("p e d -> p (e d)"), start=True, stop=False)
                    last = pe.matmul(bank, g["ones"][:, 0:P], b_e[:, h * HALF:(h + 1) * HALF],
                                     start=False, stop=True)
                last.then_inc(expert_done, 1)

        @block.scalar
        def _(act):
            root(act, rstd, 1, var_ready, root_ready)
            for n in range(2):
                act.wait_ge(xT_psum, 4 * (n + 1))
                act.activation(xT[:, n * HALF:(n + 1) * HALF], ps[:, n, :], ACT.Copy).then_inc(xT_ready, 1)
            act.wait_ge(shifted, 1)
            act.activation(gates[:], gates[:], ACT.Exp).then_inc(exp_ready, 1)



def causal_attention(nc, g, t, m):
    SCALE = float(D) ** -0.5
    ps = g["psum"]
    w = m.sb("w", [P, 3, D])
    tri_f = m.sb("tri_f", [P, P])
    stats = m.sb("stats", [P, NT, 6])
    mv = m.sb("mv", [P, NT, 2])
    rstd = m.sb("rstd", [P, NT, 1])
    xn = m.sb("xn", [P, NT, D])
    xT = m.sb("xT", [P, S])
    qT = m.sb("qT", [P, S])
    kT = m.sb("kT", [P, S])
    v = m.sb("v", [P, NT, D])
    penalty = m.sb("penalty", [P, S])
    score = m.sb("score", [P, 2, S])
    low = m.sb("low", [P, NT])
    total = m.sb("total", [P, NT])
    share = m.sb("share", [P, NT])
    pT = m.sb("pT", [P, 2, S])

    loaded, chain_dve = m.sem("loaded"), m.sem("chain_dve")
    var_ready, root_ready, xn_ready, xT_psum, xT_ready = (
        m.sem(n) for n in ("var_ready", "root_ready", "xn_ready", "xT_psum", "xT_ready"))
    qkv_done, qkv_ready, score_done, low_ready, exp_ready, pT_psum, pT_ready, out_done, added = (
        m.sem(n) for n in ("qkv_done", "qkv_ready", "score_done", "low_ready", "exp_ready",
                           "pT_psum", "pT_ready", "out_done", "added"))
    N_LOADS = 4

    def wide(b, n):
        return ps[:, b:b + 2, :].rearrange("p b n -> p (b n)")[:, 0:n]

    with nc.Block() as block:
        @block.sync
        def _(sp):
            for k, name in enumerate(("L1_WQ_T", "L1_WK_T", "L1_WV_T")):
                sp.dma_start(w[:, k, :], t[name]).then_inc(loaded, 16)
            sp.dma_start(tri_f[:], t["above_diagonal"]).then_inc(loaded, 16)

        @block.vector
        def _(dve):
            link = chained(dve, chain_dve)
            normalise(dve, link, g["x"], stats, mv, rstd, var_ready, root_ready, xn, xn_ready)
            def finish(i):
                dve.wait_ge(exp_ready, i + 1)
                link(dve.reciprocal(share[:, i:i + 1], total[:, i:i + 1]))
                dve.wait_ge(out_done, i + 1)
                dve.scalar_tensor_tensor(out=g["x"][:, i, :], in0=ps[:, 6 + i % 2, 0:D],
                                         scalar=share[:, i:i + 1], in1=g["x"][:, i, :],
                                         op0=ALU.mult, op1=ALU.add).then_inc(added, 1)

            for i in range(NT):
                n = (i + 1) * P
                b = 2 * (i % 2)
                dve.wait_ge(score_done, i + 1)
                link(dve.tensor_scalar(penalty[:, 0:n], wide(b, n), 0.0, NEG, ALU.is_equal, ALU.mult))
                if i >= 2:
                    dve.wait_ge(pT_psum, i - 1)
                link(dve.tensor_tensor(score[:, i % 2, 0:n], wide(b, n), penalty[:, 0:n], ALU.add))
                link(dve.reduce_max(low[:, i:i + 1], score[:, i % 2, 0:n], AX))
                dve.tensor_scalar(low[:, i:i + 1], low[:, i:i + 1], -SCALE, None,
                                  ALU.mult).then_inc(low_ready, 1)
                if i >= 1:
                    finish(i - 1)
            finish(NT - 1)

        @block.tensor
        def _(pe):
            transpose_tiles(pe, xn, g["ident"][:], ps, xn_ready, xT_psum)
            pe.wait_ge(loaded, 16 * N_LOADS)
            pe.wait_ge(xT_ready, 2)
            for k in range(2):
                for n in range(2):
                    last = pe.matmul(ps[:, 2 + 2 * k + n, :], w[:, k, :], xT[:, n * HALF:(n + 1) * HALF],
                                     start=True, stop=True)
                last.then_inc(qkv_done, 1)
            for i in range(NT):
                last = pe.matmul(ps[:, 6 + i // 4, (i % 4) * D:(i % 4 + 1) * D], xT[:, i * P:(i + 1) * P],
                                 w[:, 2, :], start=True, stop=True)
            last.then_inc(qkv_done, 1)

            def scores(i):
                n = (i + 1) * P
                if i >= 2:
                    pe.wait_ge(low_ready, i - 1)
                for k in range(0, n, HALF):
                    width = min(HALF, n - k)
                    bank = 2 * (i % 2) + k // HALF
                    last = pe.matmul(ps[:, bank, 0:width], qT[:, i * P:(i + 1) * P], kT[:, k:k + width],
                                     start=True, stop=k + width < n)
                a = (i % 4) * P
                pe.matmul(ps[:, bank, a:a + P], g["ident"][:], tri_f[:], start=False,
                          stop=True).then_inc(score_done, 1)

            def values(i):
                n = i + 1
                pe.wait_ge(exp_ready, i + 1)
                if i >= 1:
                    pe.wait_ge(pT_ready, i)
                for k in range(n):
                    last = pe.transpose(ps[:, 4 + k // 4, (k % 4) * P:(k % 4 + 1) * P],
                                        score[:, i % 2, k * P:(k + 1) * P], g["ident"][:])
                last.then_inc(pT_psum, 1)
                if i >= 2:
                    pe.wait_ge(added, i - 1)
                pe.wait_ge(pT_ready, i + 1)
                for k in range(n):
                    last = pe.matmul(ps[:, 6 + i % 2, 0:D], pT[:, i % 2, k * P:(k + 1) * P], v[:, k, :],
                                     start=k == 0, stop=k == n - 1)
                last.then_inc(out_done, 1)

            pe.wait_ge(qkv_ready, 3)
            scores(0)
            for i in range(1, NT):
                scores(i)
                values(i - 1)
            values(NT - 1)

        @block.scalar
        def _(act):
            root(act, rstd, 1, var_ready, root_ready)
            for n in range(2):
                act.wait_ge(xT_psum, 4 * (n + 1))
                act.activation(xT[:, n * HALF:(n + 1) * HALF], ps[:, n, :], ACT.Copy).then_inc(xT_ready, 1)
            for k, dst in enumerate((qT[:], kT[:], v[:].rearrange("p i d -> p (i d)"))):
                act.wait_ge(qkv_done, k + 1)
                act.activation(dst, wide(2 + 2 * k, S), ACT.Copy).then_inc(qkv_ready, 1)

            def exps(i):
                n = (i + 1) * P
                act.wait_ge(low_ready, i + 1)
                act.activation(score[:, i % 2, 0:n], score[:, i % 2, 0:n], ACT.Exp, scale=SCALE,
                               bias=low[:, i:i + 1], accum_out=total[:, i:i + 1]).then_inc(exp_ready, 1)

            def copy_out(i):
                n = (i + 1) * P
                act.wait_ge(pT_psum, i + 1)
                if i >= 2:
                    act.wait_ge(out_done, i - 1)
                act.activation(pT[:, i % 2, 0:n], wide(4, n), ACT.Copy).then_inc(pT_ready, 1)

            exps(0)
            for i in range(1, NT):
                exps(i)
                copy_out(i - 1)
            copy_out(NT - 1)



NH, DH = 4, 32
TOP = 32
MASKED = 2.0 ** 50
GONE = -3e38
UNITS = [(c, min(CHUNK, S2 - c)) for c in range(0, S2, CHUNK)]


def segments(width):
    n = -(-width // 171)
    edges = [round(k * width / n) for k in range(n + 1)]
    return list(zip(edges[:-1], edges[1:]))


N_SEG = sum(len(segments(w)) for _, w in UNITS)


def film_context(nc, g, t, m):
    a = {"qa": m.sb("qa", [P, NT, NH, P], BF16), "qb": m.sb("qb", [P, NT, NH, P], BF16),
         "ka": m.sb("ka", [P, NH, S2], BF16), "kb": m.sb("kb", [P, NH, S2], BF16),
         "top": m.sb("top", [P, NT * NH, TOP]), "flags": m.sb("flags", [P, NT * NH])}
    for part in (split_heads, search_top, search_general, weigh_context):
        with ExitStack() as ctx:
            part(nc, g, t, Memory(nc, ctx, part.__name__), a)


def split_heads(nc, g, t, m, a):
    ps = g["psum"]
    qa, qb, ka, kb = a["qa"], a["qb"], a["ka"], a["kb"]
    ROW = 3 * DH
    RING = 3
    w_q = m.sb("w_q", [P, NH, P])
    w_k = m.sb("w_k", [DC, NH, P])
    ctx_T = m.sb("ctx_T", [DC, RING, CHUNK])
    mask = m.sb("mask", [ROW + 1, S2], U8)
    stats = m.sb("stats", [P, NT, 6])
    mv = m.sb("mv", [P, NT, 2])
    rstd = m.sb("rstd", [P, NT, 1])
    xT = m.sb("xT", [P, S])
    q = m.sb("q", [P, S])
    hi = m.sb("hi", [P, S], BF16)
    mid = m.sb("mid", [P, S], BF16)
    rest = m.sb("rest", [P, 2, S])
    k_mid = m.sb("k_mid", [2 * DH, 2, S], BF16)

    loaded, mask_loaded = m.sem("loaded"), m.sem("mask_loaded")
    ctx_loaded = [m.sem(f"ctx_loaded_{r}") for r in range(RING)]
    chain_dve, chain_pool = m.sem("chain_dve"), m.sem("chain_pool")
    var_ready, root_ready, xn_ready, xT_psum, xT_ready = (
        m.sem(n) for n in ("var_ready", "root_ready", "xn_ready", "xT_psum", "xT_ready"))
    q_done, q_ready, q_split, k_done, k_hi, k_rest, k_mids, k_low = (
        m.sem(n) for n in ("q_done", "q_ready", "q_split", "k_done", "k_hi", "k_rest", "k_mids", "k_low"))
    xn = g["xn"]

    def pair(n):
        return ps[:, 2 * n:2 * n + 2, :].rearrange("p b n -> p (b n)")

    units = [(h, c, w) for c, w in UNITS for h in range(NH)]
    with nc.Block() as block:
        @block.sync
        def _(sp):
            sp.dma_start(w_q[:], t["L1_Wq_rep"].rearrange("p (h c) -> p h c", c=P)).then_inc(loaded, 16)
            sp.dma_start(w_k[:], t["L1_Wk_rep"].rearrange("p (h c) -> p h c", c=P)).then_inc(loaded, 16)
            sp.dma_start(mask[ROW:ROW + 1, :], t["vision_mask"]).then_inc(mask_loaded, 16)
            for u, (c, w) in enumerate(UNITS):
                if u >= RING:
                    sp.wait_ge(k_done, NH * (u - RING + 1))
                sp.dma_start(ctx_T[:, u % RING, 0:w], t["ctx_T"][:, c:c + w]).then_inc(ctx_loaded[u % RING], 16)

        @block.vector
        def _(dve):
            link = chained(dve, chain_dve)
            normalise(dve, link, g["x"], stats, mv, rstd, var_ready, root_ready, xn, xn_ready)
            for h in range(NH):
                dve.wait_ge(q_ready, h + 1)
                link(dve.tensor_copy(hi[:], q[:]))
                link(dve.tensor_tensor(rest[:, 0, :], q[:], hi[:], ALU.subtract))
                link(dve.tensor_copy(mid[:], rest[:, 0, :]))

                def rows(x):
                    return x.rearrange("p (i c) -> p i c", c=P)

                for k, src in enumerate((hi, mid, hi, mid)):
                    part = slice(k * DH, (k + 1) * DH)
                    dve.tensor_copy(qa[part, :, h, :], rows(src[part, :]))
                for k, src in enumerate((hi, mid)):
                    part = slice(k * DH, (k + 1) * DH)
                    dve.tensor_copy(qb[part, :, h, :], rows(src[part, :]))
                part = slice(2 * DH, 3 * DH)
                last = dve.tensor_tensor(qb[part, :, h, :], rows(rest[part, 0, :]), rows(mid[part, :]),
                                         ALU.subtract)
                link(last)
                dve.engine_nop().then_inc(q_split, 1)
            for n, (h, c, w) in enumerate(units):
                dve.wait_ge(k_hi, 2 * (n + 1))
                if n >= 2:
                    dve.wait_ge(k_low, n - 1)
                dve.tensor_tensor(rest[:, n % 2, 0:w], pair(n % 4)[:, 0:w], ka[:, h, c:c + w],
                                  ALU.subtract).then_inc(k_rest, 1)
                dve.wait_ge(k_rest, n + 1)
                dve.tensor_copy(k_mid[:, n % 2, 0:w], rest[0:2 * DH, n % 2, 0:w])
                dve.tensor_copy(ka[2 * DH:P, h, c:c + w], rest[2 * DH:P, n % 2, 0:w]).then_inc(k_mids, 1)

        @block.tensor
        def _(pe):
            transpose_tiles(pe, xn, g["ident"][:], ps, xn_ready, xT_psum)
            pe.wait_ge(loaded, 32)
            pe.wait_ge(xT_ready, 2)
            for h in range(NH):
                if h >= 2:
                    pe.wait_ge(q_ready, h - 1)
                for n in range(2):
                    last = pe.matmul(ps[:, 4 + 2 * (h % 2) + n, :], w_q[:, h, :],
                                     xT[:, n * HALF:(n + 1) * HALF], start=True, stop=True)
                last.then_inc(q_done, 1)
            pe.wait_ge(q_ready, NH)
            for n, (h, c, w) in enumerate(units):
                u = n // NH
                pe.wait_ge(ctx_loaded[u % RING], 16 * (u // RING + 1))
                if n >= 4:
                    pe.wait_ge(k_rest, n - 3)
                for b in range(0, w, HALF):
                    cols = min(HALF, w - b)
                    last = pe.matmul(ps[:, 2 * (n % 4) + b // HALF, 0:cols], w_k[:, h, :],
                                     ctx_T[:, u % RING, b:b + cols], start=True, stop=True)
                last.then_inc(k_done, 1)

        @block.scalar
        def _(act):
            root(act, rstd, 1, var_ready, root_ready)
            for n in range(2):
                act.wait_ge(xT_psum, 4 * (n + 1))
                act.activation(xT[:, n * HALF:(n + 1) * HALF], ps[:, n, :], ACT.Copy).then_inc(xT_ready, 1)
            for h in range(NH):
                act.wait_ge(q_done, h + 1)
                if h >= 1:
                    act.wait_ge(q_split, h)
                act.activation(q[:], pair(2 + h % 2), ACT.Copy,
                               scale=float(DH) ** -0.5).then_inc(q_ready, 1)
            part = slice(2 * DH, 3 * DH)
            for n, (h, c, w) in enumerate(units):
                act.wait_ge(k_done, n + 1)
                act.activation(ka[:, h, c:c + w], pair(n % 4)[:, 0:w], ACT.Copy).then_inc(k_hi, 1)
                act.activation(kb[part, h, c:c + w], pair(n % 4)[part, 0:w], ACT.Copy).then_inc(k_hi, 1)

        @block.gpsimd
        def _(pool):
            link = chained(pool, chain_pool)
            link(pool.memset(qb[ROW:ROW + 1, :, :, :], 1.0))
            pool.wait_ge(mask_loaded, 16)
            for h in range(NH):
                link(pool.tensor_scalar(kb[ROW:ROW + 1, h, :], mask[ROW:ROW + 1, :], 1.0, MASKED,
                                        ALU.subtract, ALU.mult))
            for n, (h, c, w) in enumerate(units):
                pool.wait_ge(k_mids, n + 1)
                pool.tensor_tensor(kb[0:2 * DH, h, c:c + w], rest[0:2 * DH, n % 2, 0:w],
                                   k_mid[:, n % 2, 0:w], ALU.subtract).then_inc(k_low, 1)


def score_unit(pe, a, ps, bank, tile, h, c, w):
    ROWS = 3 * DH + 1
    for b in range(0, w, HALF):
        cols = min(HALF, w - b)
        out = ps[:, bank + b // HALF, 0:cols]
        pe.matmul(out, a["qa"][:, tile, h, :], a["ka"][:, h, c + b:c + b + cols], start=True, stop=False)
        last = pe.matmul(out, a["qb"][0:ROWS, tile, h, :], a["kb"][0:ROWS, h, c + b:c + b + cols],
                         start=False, stop=True)
    return last


def search_top(nc, g, t, m, a):
    ps = g["psum"]
    kept = m.sb("kept", [P, 2, N_SEG, 8])
    best = m.sb("best", [P, 2, TOP])
    eighth = m.sb("eighth", [P, 2])
    score_done, searched, found, chain_dve, passed = (
        m.sem(n) for n in ("score_done", "searched", "found", "chain_dve", "passed"))
    NU = len(UNITS)
    STEPS = NH * NU

    with nc.Block() as block:
        @block.tensor
        def _(pe):
            def tile_units(i, first):
                for h in range(NH):
                    for u, (c, w) in enumerate(UNITS):
                        n = h * NU + u
                        if not first or n >= 4:
                            pe.wait_ge(searched, i * STEPS + n - 3)
                        score_unit(pe, a, ps, 2 * (n % 4), i, h, c, w).then_inc(score_done, 1)

            tile_units(0, True)
            with pe.Fori(1, NT) as i:
                tile_units(i, False)

        @block.vector
        def _(dve):
            def tile_search(i):
                dve.sem_clear(chain_dve)
                link = chained(dve, chain_dve)
                for h in range(NH):
                    k = h % 2
                    s = 0
                    for u, (c, w) in enumerate(UNITS):
                        n = h * NU + u
                        wait_in_loop(dve, score_done, i * STEPS + n + 1, passed)
                        bank = 2 * (n % 4)
                        flat = ps[:, bank:bank + 2, :].rearrange("p b n -> p (b n)")
                        for lo, hi in segments(w):
                            last = dve.max(kept[:, k, s, :], flat[:, lo:hi])
                            s += 1
                        if u < NU - 1:
                            last.then_inc(searched, 1)
                    last.then_inc(searched, 1)
                    wait_in_loop(dve, searched, i * STEPS + (h + 1) * NU, passed)
                    all_kept = kept[:, k, :, :].rearrange("p s e -> p (s e)")
                    link(dve.reduce_max(eighth[:, k:k + 1], kept[:, k, :, 7], AX))
                    for r in range(TOP // 8):
                        eight = best[:, k, 8 * r:8 * r + 8]
                        link(dve.max(eight, all_kept))
                        if r < TOP // 8 - 1:
                            link(dve.match_replace(all_kept, eight, all_kept, GONE))
                    link(dve.tensor_copy(a["top"][:, bass.ds(i * NH + h, 1), :], best[:, k:k + 1, :]))
                    dve.tensor_tensor(a["flags"][:, bass.ds(i * NH + h, 1)], eighth[:, k:k + 1],
                                      best[:, k, TOP - 1:TOP], ALU.is_gt).then_inc(found, 1)

            with dve.Fori(0, NT) as i:
                tile_search(i)
            dve.wait_ge(found, NT * NH)


def search_general(nc, g, t, m, a):
    ps = g["psum"]
    full = m.sb("full", [P, S2])
    best = m.sb("best", [P, TOP])
    column = m.sb("column", [P, 1])
    count = m.sb("count", [1, NT * NH], mybir.dt.int32)
    ones_set, counted, count_ready, score_done, copied, chain_dve, passed, passed_pe = (
        m.sem(n) for n in ("ones_set", "counted", "count_ready", "score_done", "copied", "chain_dve",
                           "passed", "passed_pe"))
    NU = len(UNITS)

    with nc.Block() as block:
        @block.tensor
        def _(pe):
            pe.wait_ge(ones_set, 1)
            pe.matmul(ps[0:1, 7, 0:NT * NH], column[:], a["flags"][:], start=True,
                      stop=True).then_inc(counted, 1)
            pe.wait_ge(count_ready, 1)
            with pe.Fori(0, NT) as i:
                for h in range(NH):
                    flagged = pe.value_load(count[0:1, bass.ds(i * NH + h, 1)])
                    base = i * NH * NU + h * NU
                    with pe.If(flagged > 0):
                        for u, (c, w) in enumerate(UNITS):
                            bank = 2 * (u % 2)
                            wait_in_loop(pe, copied, base + 1 + max(u - 1, 0), passed_pe)
                            score_unit(pe, a, ps, bank, i, h, c, w).then_inc(score_done, 1)
                    with pe.Else():
                        pe.sem_inc(score_done, NU)

        @block.vector
        def _(dve):
            dve.memset(column[:], 1.0).then_inc(ones_set, 1)
            dve.wait_ge(counted, 1)
            dve.tensor_copy(count[:], ps[0:1, 7, 0:NT * NH]).then_inc(count_ready, 1)
            dve.wait_ge(count_ready, 1)
            dve.engine_nop().then_inc(copied, 1)
            with dve.Fori(0, NT) as i:
                for h in range(NH):
                    flagged = dve.value_load(count[0:1, bass.ds(i * NH + h, 1)])
                    units = i * NH * NU + h * NU
                    with dve.If(flagged > 0):
                        for u, (c, w) in enumerate(UNITS):
                            bank = 2 * (u % 2)
                            wait_in_loop(dve, score_done, units + u + 1, passed)
                            dve.tensor_copy(full[:, c:c + w],
                                            ps[:, bank:bank + 2, :].rearrange("p b n -> p (b n)")[:, 0:w]
                                            ).then_inc(copied, 1)
                        wait_in_loop(dve, copied, units + NU + 1, passed)
                        dve.sem_clear(chain_dve)
                        link = chained(dve, chain_dve)
                        for r in range(TOP // 8):
                            eight = best[:, 8 * r:8 * r + 8]
                            link(dve.max(eight, full[:]))
                            if r < TOP // 8 - 1:
                                link(dve.match_replace(full[:], eight, full[:], GONE))
                        link(dve.tensor_copy(a["top"][:, bass.ds(i * NH + h, 1), :], best[:].unsqueeze(1)))
                    with dve.Else():
                        dve.sem_inc(copied, NU)


def weigh_context(nc, g, t, m, a):
    ps = g["psum"]
    NJ = NT * NH
    shifted = m.sb("shifted", [P, NJ, TOP])
    total = m.sb("total", [P, NJ])
    bias = m.sb("bias", [P, NJ])
    least = m.sb("least", [P, NJ])
    e = m.sb("e", [P, 2, NH, CHUNK // 2])
    w = e
    mean = m.sb("mean", [P, 2, CHUNK // 2])
    half_sum = m.sb("half_sum", [P, 2, CHUNK // 2])
    mean_T = m.sb("mean_T", [P, 2, CHUNK // 2])
    mask8 = m.sb("mask8", [P, NT], U8)
    mask = m.sb("mask", [P, NT])
    w_v = m.sb("w_v", [DC, D])
    c_tok = m.sb("c_tok", [P, NT, DC])
    c_ctx = m.sb("c_ctx", [DC, S])
    loaded, chain_dve, chain_act = m.sem("loaded"), m.sem("chain_dve"), m.sem("chain_act")
    top_shifted, summed, bias_ready, mask_ready = (
        m.sem(n) for n in ("top_shifted", "summed", "bias_ready", "mask_ready"))
    score_done, e_ready, w_ready, half_ready, mean_ready, mT_psum, mT_ready, pv_done = (
        m.sem(n) for n in ("score_done", "e_ready", "w_ready", "half_ready", "mean_ready", "mT_psum",
                           "mT_ready", "pv_done"))
    tok_ready, cc_psum, cc_ready, c_done, exp_done, least_ready = (
        m.sem(n) for n in ("tok_ready", "cc_psum", "cc_ready", "c_done", "exp_done", "least_ready"))
    chunks = [(c, min(HALF, S2 - c)) for c in range(0, S2, HALF)]
    NCH = len(chunks)

    def tiles(w):
        return [(b, min(P, w - b)) for b in range(0, w, P)]

    with nc.Block() as block:
        @block.sync
        def _(sp):
            sp.dma_start(mask8[:], t["text_mask"].rearrange("(i p) -> p i", p=P),
                         allow_slow_non_contiguous=True).then_inc(loaded, 16)
            sp.dma_start(w_v[:], t["L1_xattn_Wv"]).then_inc(loaded, 16)

        @block.vector
        def _(dve):
            link = chained(dve, chain_dve)
            top = a["top"]
            dve.tensor_tensor(shifted[:], top[:], top[:, :, 0:1].to_broadcast([P, NJ, TOP]),
                              ALU.subtract).then_inc(top_shifted, 1)
            dve.wait_ge(exp_done, 1)
            dve.reduce_sum(total[:], shifted[:], AX).then_inc(summed, 1)
            dve.wait_ge(bias_ready, 1)
            link(dve.tensor_tensor(bias[:], total[:], top[:, :, 0], ALU.add))
            link(dve.tensor_scalar(bias[:], bias[:], -1.0, None, ALU.mult))
            dve.tensor_tensor(least[:], top[:, :, TOP - 1], bias[:], ALU.add).then_inc(bias_ready, 1)
            dve.wait_ge(loaded, 32)
            dve.tensor_copy(mask[:], mask8[:]).then_inc(mask_ready, 1)
            dve.wait_ge(least_ready, 1)
            for i in range(NT):
                for u, (c, wd) in enumerate(chunks):
                    n = i * NCH + u
                    k = n % 2
                    dve.wait_ge(e_ready, NH * (n + 1))
                    for h in range(NH):
                        j = i * NH + h
                        dve.scalar_tensor_tensor(out=w[:, k, h, 0:wd], in0=e[:, k, h, 0:wd],
                                                 scalar=least[:, j:j + 1], in1=e[:, k, h, 0:wd],
                                                 op0=ALU.is_ge, op1=ALU.mult).then_inc(w_ready, 1)
                    dve.wait_ge(w_ready, NH * (n + 1))
                    if n >= 2:
                        dve.wait_ge(mean_ready, n - 1)
                    dve.tensor_tensor(half_sum[:, k, 0:wd], w[:, k, 0, 0:wd], w[:, k, 1, 0:wd],
                                      ALU.add).then_inc(half_ready, 1)

        @block.gpsimd
        def _(pool):
            link = chained(pool, m.sem("chain_pool"))
            for i in range(NT):
                for u, (c, wd) in enumerate(chunks):
                    n = i * NCH + u
                    k = n % 2
                    pool.wait_ge(w_ready, NH * (n + 1))
                    if n >= 2:
                        pool.wait_ge(mT_psum, n - 1)
                    link(pool.tensor_tensor(mean[:, k, 0:wd], w[:, k, 2, 0:wd], w[:, k, 3, 0:wd], ALU.add))
                    pool.wait_ge(half_ready, n + 1)
                    pool.tensor_tensor(mean[:, k, 0:wd], mean[:, k, 0:wd], half_sum[:, k, 0:wd],
                                       ALU.add).then_inc(mean_ready, 1)

        @block.tensor
        def _(pe):
            ctx = g["ctx_rows"]

            def weighted(n):
                i, u = divmod(n, NCH)
                c, wd = chunks[u]
                pe.wait_ge(mean_ready, n + 1)
                if n >= 1:
                    pe.wait_ge(mT_ready, n)
                for b, r in tiles(wd):
                    last = pe.transpose(ps[0:r, 5, b:b + P], mean[:, n % 2, b:b + r], g["ident"][:])
                last.then_inc(mT_psum, 1)

            def add_context(n):
                i, u = divmod(n, NCH)
                c, wd = chunks[u]
                pe.wait_ge(mT_ready, n + 1)
                if u == 0 and i >= 2:
                    pe.wait_ge(tok_ready, i - 1)
                for b, r in tiles(wd):
                    last = pe.matmul(ps[:, 6 + i % 2, 0:DC], mean_T[0:r, n % 2, b:b + P],
                                     ctx[0:r, (c + b) // P, 0:DC], start=c + b == 0, stop=c + b + r == S2)
                last.then_inc(pv_done, 1)

            for n in range(NT * NCH):
                i, u = divmod(n, NCH)
                c, wd = chunks[u]
                for h in range(NH):
                    q = NH * n + h
                    if q >= 5:
                        pe.wait_ge(e_ready, q - 4)
                    score_unit(pe, a, ps, q % 5, i, h, c, wd).then_inc(score_done, 1)
                if n >= 1:
                    weighted(n - 1)
                if n >= 2:
                    add_context(n - 2)
            weighted(NT * NCH - 1)
            add_context(NT * NCH - 2)
            add_context(NT * NCH - 1)
            for i in range(NT):
                pe.wait_ge(tok_ready, NT)
                last = pe.transpose(ps[0:DC, i // 4, (i % 4) * P:(i % 4 + 1) * P], c_tok[:, i, :],
                                    g["ident"][:])
            last.then_inc(cc_psum, 1)
            pe.wait_ge(cc_ready, 1)
            pe.wait_ge(loaded, 32)
            for n in range(2):
                pe.matmul(ps[:, 2 + n, :], w_v[:], c_ctx[:, n * HALF:(n + 1) * HALF],
                          start=True, stop=True).then_inc(c_done, 1)

        @block.scalar
        def _(act):
            act.wait_ge(top_shifted, 1)
            act.activation(shifted[:], shifted[:], ACT.Exp).then_inc(exp_done, 1)
            act.wait_ge(summed, 1)
            act.activation(total[:], total[:], ACT.Ln, scale=float(NH)).then_inc(bias_ready, 1)
            act.wait_ge(bias_ready, 2)
            act.activation(least[:], least[:], ACT.Exp).then_inc(least_ready, 1)
            act.wait_ge(mask_ready, 1)

            def copy_mean(n):
                i, u = divmod(n, NCH)
                wd = chunks[u][1]
                r = min(P, wd)
                act.wait_ge(mT_psum, n + 1)
                if n >= 2:
                    act.wait_ge(pv_done, n - 1)
                last = None
                full = wd // P * P
                if full:
                    last = act.activation(mean_T[:, n % 2, 0:full], ps[:, 5, 0:full], ACT.Copy)
                if wd - full:
                    last = act.activation(mean_T[0:wd - full, n % 2, full:full + P],
                                          ps[0:wd - full, 5, full:full + P], ACT.Copy)
                last.then_inc(mT_ready, 1)

            def copy_context(i):
                act.wait_ge(pv_done, NCH * (i + 1))
                act.activation(c_tok[:, i, :], ps[:, 6 + i % 2, 0:DC], ACT.Copy,
                               scale=mask[:, i:i + 1]).then_inc(tok_ready, 1)

            for n in range(NT * NCH):
                i, u = divmod(n, NCH)
                c, wd = chunks[u]
                if n >= 2:
                    act.wait_ge(mean_ready, n - 1)
                for h in range(NH):
                    q = NH * n + h
                    j = i * NH + h
                    act.wait_ge(score_done, q + 1)
                    act.activation(e[:, n % 2, h, 0:wd], ps[:, q % 5, 0:wd], ACT.Exp,
                                   bias=bias[:, j:j + 1]).then_inc(e_ready, 1)
                if n >= 1:
                    copy_mean(n - 1)
                if u == 3 and i >= 1:
                    copy_context(i - 1)
            copy_mean(NT * NCH - 1)
            copy_context(NT - 1)
            act.wait_ge(cc_psum, 1)
            act.activation(c_ctx[:], ps[0:DC, 0:2, :].rearrange("p b n -> p (b n)"),
                           ACT.Copy).then_inc(cc_ready, 1)
            for n in range(2):
                act.wait_ge(c_done, n + 1)
                last = act.activation(g["c_T"][:, n * HALF:(n + 1) * HALF], ps[:, 2 + n, :], ACT.Copy)



NF = 2 * S


def film_s4d_ffn(nc, g, t, m):
    a = {"dft": m.sb("dft", [P, NT, NF]), "k_tok": m.sb("k_tok", [P, NT, D]),
         "u": m.sb("u", [P, NT, D]), "y": m.sb("y", [P, NT, D]), "dft_loaded": m.sem("dft_loaded"),
         "gate": m.sb("gate", [P, 1])}
    for part in (s4d_kernel, film_in, convolve, film_out_ffn):
        with ExitStack() as ctx:
            part(nc, g, t, Memory(nc, ctx, part.__name__), a)


ROUND = 1.5 * 2.0 ** 23
TURN = 6.2831850


def s4d_kernel(nc, g, t, m, a):
    NS = 64
    NJ = NT
    GROUP = 16
    NG = D // GROUP
    ps = g["psum"]
    names = ("log_dt", "a_re", "a_im", "c_re", "c_im")
    raw = {n: m.sb(n, [P, D]) for n in names}
    dt_, ar, ai, turns, half = (m.sb(n, [P, D]) for n in ("dt", "ar", "ai", "turns", "half"))
    tanh, grow, er, ei, nr, ni, qr, qi, inv, tmp = (
        m.sb(n, [P, D]) for n in ("tanh", "grow", "er", "ei", "nr", "ni", "qr", "qi", "inv", "tmp"))
    angle = m.sb("angle", [P, 3, D])
    rounded = m.sb("rounded", [P, 3, D])
    on_c, on_s = m.sb("on_c", [P, D]), m.sb("on_s", [P, D])
    index = m.sb("index", [P, P + NJ])
    quarter = m.sb("quarter", [P, 1])
    j_angle, j_round = m.sb("j_angle", [P, 2, D, NJ]), m.sb("j_round", [P, 2, D, NJ])
    j_decay = m.sb("j_decay", [P, D, NJ])
    left = m.sb("left", [P, D, NJ])
    i_angle, i_round, i_decay = (m.sb(n, [P, 2, GROUP, P]) for n in ("i_angle", "i_round", "i_decay"))
    d_skip = m.sb("d_skip", [1, D])

    loaded, chain_dve = m.sem("loaded"), m.sem("chain_dve")
    dt_ready, parts_ready, small_ready, small_done, j_ready, j_done = (
        m.sem(n) for n in ("dt_ready", "parts_ready", "small_ready", "small_done", "j_ready", "j_done"))
    left_ready, i_ready, sin_done, grown, decayed, powers, k_psum, k_ready = (
        m.sem(n) for n in ("left_ready", "i_ready", "sin_done", "grown", "decayed", "powers",
                           "k_psum", "k_ready"))
    N_LOADS = len(names) + 3

    with nc.Block() as block:
        @block.sync
        def _(sp):
            sp.dma_start(raw["log_dt"][:], t["L1_xattn_log_dt"].unsqueeze(0).to_broadcast([P, D])
                         ).then_inc(loaded, 16)
            for n in names[1:]:
                sp.dma_start(raw[n][:], t[f"s4d_{n}"]).then_inc(loaded, 16)
            sp.dma_start(index[:], t["s4d_index"]).then_inc(loaded, 16)
            sp.dma_start(quarter[:], t["s4d_quarter"]).then_inc(loaded, 16)
            sp.dma_start(d_skip[:], t["L1_xattn_D_skip"].unsqueeze(0)).then_inc(loaded, 16)
            for j in range(NT):
                sp.dma_start(a["dft"][:, j, :], t["dft"][j * P:(j + 1) * P, :]).then_inc(a["dft_loaded"], 16)

        @block.vector
        def _(dve):
            link = chained(dve, chain_dve)

            def tt(out, x, y, op):
                link(dve.tensor_tensor(out, x, y, op))

            dve.wait_ge(dt_ready, 1)
            tt(ar[:], dt_[:], raw["a_re"][:], ALU.mult)
            tt(ai[:], dt_[:], raw["a_im"][:], ALU.mult)
            dve.tensor_scalar(turns[:], ai[:], 1.0 / (2.0 * np.pi), None, ALU.mult).then_inc(parts_ready, 1)
            dve.wait_ge(parts_ready, 1)
            link(dve.tensor_scalar(angle[:, 0, :], turns[:], 0.25, None, ALU.add))
            link(dve.tensor_scalar(angle[:, 1, :], turns[:], 1.0, None, ALU.mult))
            link(dve.tensor_scalar(angle[:, 2, :], turns[:], 0.5, None, ALU.mult))
            link(dve.tensor_scalar(rounded[:], angle[:], ROUND, None, ALU.add))
            link(dve.tensor_scalar(rounded[:], rounded[:], ROUND, None, ALU.subtract))
            dve.tensor_tensor(angle[:], angle[:], rounded[:], ALU.subtract).then_inc(small_ready, 1)
            dve.wait_ge(small_done, 2)
            link(dve.tensor_scalar(tmp[:], tanh[:], -1.0, 1.0, ALU.mult, ALU.add))
            link(dve.reciprocal(tmp[:], tmp[:]))
            link(dve.scalar_tensor_tensor(out=grow[:], in0=tanh[:], scalar=2.0, in1=tmp[:],
                                          op0=ALU.mult, op1=ALU.mult))
            cos_b, sin_b, sin_half = angle[:, 0, :], angle[:, 1, :], angle[:, 2, :]
            tt(er[:], grow[:], cos_b, ALU.mult)
            link(dve.scalar_tensor_tensor(out=tmp[:], in0=sin_half, scalar=-2.0, in1=sin_half,
                                          op0=ALU.mult, op1=ALU.mult))
            tt(er[:], er[:], tmp[:], ALU.add)
            link(dve.scalar_tensor_tensor(out=ei[:], in0=grow[:], scalar=1.0, in1=sin_b,
                                          op0=ALU.add, op1=ALU.mult))
            cr, ci, re, im = raw["c_re"][:], raw["c_im"][:], raw["a_re"][:], raw["a_im"][:]
            tt(nr[:], cr, er[:], ALU.mult)
            tt(tmp[:], ci, ei[:], ALU.mult)
            tt(nr[:], nr[:], tmp[:], ALU.subtract)
            tt(ni[:], cr, ei[:], ALU.mult)
            tt(tmp[:], ci, er[:], ALU.mult)
            tt(ni[:], ni[:], tmp[:], ALU.add)
            tt(inv[:], re, re, ALU.mult)
            tt(tmp[:], im, im, ALU.mult)
            tt(inv[:], inv[:], tmp[:], ALU.add)
            link(dve.reciprocal(inv[:], inv[:]))
            tt(qr[:], nr[:], re, ALU.mult)
            tt(tmp[:], ni[:], im, ALU.mult)
            tt(qr[:], qr[:], tmp[:], ALU.add)
            tt(qr[:], qr[:], inv[:], ALU.mult)
            tt(qi[:], ni[:], re, ALU.mult)
            tt(tmp[:], nr[:], im, ALU.mult)
            tt(qi[:], qi[:], tmp[:], ALU.subtract)
            tt(qi[:], qi[:], inv[:], ALU.mult)
            link(dve.tensor_scalar(on_c[0:NS, :], qr[0:NS, :], 2.0, None, ALU.mult))
            link(dve.tensor_scalar(on_s[0:NS, :], qi[0:NS, :], -2.0, None, ALU.mult))
            link(dve.tensor_scalar(on_c[NS:P, :], qi[NS:P, :], -2.0, None, ALU.mult))
            link(dve.tensor_scalar(on_s[NS:P, :], qr[NS:P, :], -2.0, None, ALU.mult))

            def over(x, n):
                return x.unsqueeze(2).to_broadcast([P, x.shape[1], n])

            j_index = index[:, P:P + NJ].unsqueeze(1).to_broadcast([P, D, NJ])
            tt(j_angle[:, 1, :, :], over(turns[:], NJ), j_index, ALU.mult)
            link(dve.tensor_scalar(j_angle[:, 0, :, :], j_angle[:, 1, :, :], 0.25, None, ALU.add))
            link(dve.tensor_scalar(j_round[:], j_angle[:], ROUND, None, ALU.add))
            link(dve.tensor_scalar(j_round[:], j_round[:], ROUND, None, ALU.subtract))
            tt(j_angle[:], j_angle[:], j_round[:], ALU.subtract)
            dve.tensor_tensor(j_decay[:], over(ar[:], NJ), j_index, ALU.mult).then_inc(j_ready, 1)
            dve.wait_ge(j_done, 2)
            tt(left[:], j_angle[:, 0, :, :], over(on_c[:], NJ), ALU.mult)
            tt(j_angle[:, 1, :, :], j_angle[:, 1, :, :], over(on_s[:], NJ), ALU.mult)
            tt(left[:], left[:], j_angle[:, 1, :, :], ALU.add)
            dve.tensor_tensor(left[:], left[:], j_decay[:], ALU.mult).then_inc(left_ready, 1)
            def power(q):
                dve.wait_ge(sin_done, q + 1)
                dve.wait_ge(decayed, q + 1)
                dve.tensor_tensor(i_angle[:, q % 2], i_angle[:, q % 2], i_decay[:, q % 2],
                                  ALU.mult).then_inc(powers, 1)

            i_index = index[:, 0:P].unsqueeze(1).to_broadcast([P, GROUP, P])
            for q in range(NG):
                k = q % 2
                group = slice(q * GROUP, (q + 1) * GROUP)
                if q >= 2:
                    dve.wait_ge(k_psum, q - 1)
                tt(i_angle[:, k], over(turns[:, group], P), i_index, ALU.mult)
                link(dve.tensor_scalar(i_round[:, k], i_angle[:, k], quarter[:, 0:1], ROUND,
                                       ALU.add, ALU.add))
                link(dve.tensor_scalar(i_round[:, k], i_round[:, k], ROUND, None, ALU.subtract))
                dve.scalar_tensor_tensor(out=i_angle[:, k], in0=i_angle[:, k], scalar=quarter[:, 0:1],
                                         in1=i_round[:, k], op0=ALU.add, op1=ALU.subtract).then_inc(i_ready, 1)
                if q >= 1:
                    power(q - 1)

            power(NG - 1)
            dve.wait_ge(k_ready, 1)
            link(dve.tensor_tensor(a["k_tok"][0:1, 0, :], a["k_tok"][0:1, 0, :], d_skip[:], ALU.add))

        @block.gpsimd
        def _(pool):
            pool.wait_ge(parts_ready, 1)
            i_index = index[:, 0:P].unsqueeze(1).to_broadcast([P, GROUP, P])
            for q in range(NG):
                group = slice(q * GROUP, (q + 1) * GROUP)
                if q >= 2:
                    pool.wait_ge(powers, q - 1)
                pool.tensor_tensor(i_decay[:, q % 2], ar[:, group].unsqueeze(2).to_broadcast([P, GROUP, P]),
                                   i_index, ALU.mult).then_inc(grown, 1)

        @block.scalar
        def _(act):
            act.wait_ge(loaded, 16 * N_LOADS)
            act.activation(dt_[:], raw["log_dt"][:], ACT.Exp).then_inc(dt_ready, 1)
            act.wait_ge(parts_ready, 1)
            act.activation(tanh[:], ar[:], ACT.Tanh, scale=0.5).then_inc(small_done, 1)
            act.wait_ge(small_ready, 1)
            act.activation(angle[:], angle[:], ACT.Sin, scale=TURN).then_inc(small_done, 1)
            act.wait_ge(j_ready, 1)
            act.activation(j_angle[:], j_angle[:], ACT.Sin, scale=TURN).then_inc(j_done, 1)
            act.activation(j_decay[:], j_decay[:], ACT.Exp).then_inc(j_done, 1)
            for q in range(0, NG, 2):
                for k in range(2):
                    act.wait_ge(i_ready, q + k + 1)
                    act.activation(i_angle[:, k], i_angle[:, k], ACT.Sin, scale=TURN).then_inc(sin_done, 1)
                for k in range(2):
                    act.wait_ge(grown, q + k + 1)
                    act.activation(i_decay[:, k], i_decay[:, k], ACT.Exp).then_inc(decayed, 1)
            act.wait_ge(k_psum, NG)
            act.activation(a["k_tok"][:], ps[:, 0:2, :].rearrange("p b (d j) -> p j (b d)", j=NJ),
                           ACT.Copy).then_inc(k_ready, 1)

        @block.tensor
        def _(pe):
            pe.wait_ge(left_ready, 1)
            for q in range(NG):
                pe.wait_ge(powers, q + 1)
                for c in range(GROUP):
                    d = q * GROUP + c
                    last = pe.matmul(ps[:, d // 64, (d % 64) * NJ:(d % 64 + 1) * NJ], i_angle[:, q % 2, c, :],
                                     left[:, d, :], start=True, stop=True)
                last.then_inc(k_psum, 1)


def broadcast_row(name, t):
    return t[name].unsqueeze(0).to_broadcast([P, D])


def film(pe, g, w_f, b_f, ps, done):
    for i in range(NT):
        out = ps[:, i // 2, (i % 2) * 2 * D:(i % 2 + 1) * 2 * D]
        pe.matmul(out, g["c_T"][:, i * P:(i + 1) * P], w_f[:], start=True, stop=False)
        last = pe.matmul(out, g["ones"][:, 0:P], b_f[:], start=False, stop=True)
    last.then_inc(done, 1)


def film_apply(dve, link, ps, gate, x, scale, out):
    film_psum = ps[:, 0:4, :].rearrange("p b (i s d) -> p (b i) s d", s=2, d=D)
    link(dve.tensor_scalar(scale[:], film_psum[:, :, 0, :], gate[:, 0:1], 1.0, ALU.mult, ALU.add))
    link(dve.tensor_tensor(out, x, scale[:], ALU.mult))
    return dve.scalar_tensor_tensor(out=out, in0=film_psum[:, :, 1, :], scalar=gate[:, 0:1], in1=out,
                                    op0=ALU.mult, op1=ALU.add)


def film_in(nc, g, t, m, a):
    ps = g["psum"]
    gain, shift = m.sb("gain", [P, D]), m.sb("shift", [P, D])
    w_f, b_f = m.sb("w_f", [P, 2 * D]), m.sb("b_f", [1, 2 * D])
    stats = m.sb("stats", [P, NT, 6])
    mv = m.sb("mv", [P, NT, 2])
    rstd = m.sb("rstd", [P, NT, 1])
    scale = m.sb("scale", [P, NT, D])
    loaded, chain_dve, var_ready, root_ready, normed, film_done = (
        m.sem(n) for n in ("loaded", "chain_dve", "var_ready", "root_ready", "normed", "film_done"))
    N_LOADS = 5

    def tiles(v):
        return v.unsqueeze(1).to_broadcast([P, NT, D])

    with nc.Block() as block:
        @block.sync
        def _(sp):
            sp.dma_start(gain[:], broadcast_row("L1_xattn_g_norm_in", t)).then_inc(loaded, 16)
            sp.dma_start(shift[:], broadcast_row("L1_xattn_b_norm_in", t)).then_inc(loaded, 16)
            sp.dma_start(w_f[:], t["L1_xattn_W_film_in"]).then_inc(loaded, 16)
            sp.dma_start(b_f[:], t["L1_xattn_b_film_in"].unsqueeze(0)).then_inc(loaded, 16)
            sp.dma_start(a["gate"][:], t["mod_gate"].to_broadcast([P, 1])).then_inc(loaded, 16)

        @block.vector
        def _(dve):
            link = chained(dve, chain_dve)
            u = a["u"]
            normalise(dve, link, g["xn"], stats, mv, rstd, var_ready, root_ready, u, normed)
            dve.wait_ge(normed, NT)
            dve.wait_ge(loaded, 16 * N_LOADS)
            link(dve.tensor_tensor(u[:], u[:], tiles(gain[:]), ALU.mult))
            link(dve.tensor_tensor(u[:], u[:], tiles(shift[:]), ALU.add))
            dve.wait_ge(film_done, 1)
            link(film_apply(dve, link, ps, a["gate"], u[:], scale, u[:]))

        @block.scalar
        def _(act):
            root(act, rstd, 1, var_ready, root_ready)

        @block.tensor
        def _(pe):
            pe.wait_ge(loaded, 16 * N_LOADS)
            film(pe, g, w_f, b_f, ps, film_done)


def convolve(nc, g, t, m, a):
    ps = g["psum"]
    dft = a["dft"]
    kf = m.sb("kf", [P, NF])
    yf = m.sb("yf", [P, NF])
    cross = m.sb("cross", [P, S])
    ends = m.sb("ends", [P, 2])
    yt = m.sb("yt", [P, NF // P, D])
    sign = m.sb("sign", [1, S])
    sign_loaded, kf_done, kf_ready, uf_done, yf_ready, yt_psum, yt_ready, patched, y_done, chain_dve = (
        m.sem(n) for n in ("sign_loaded", "kf_done", "kf_ready", "uf_done", "yf_ready", "yt_psum",
                           "yt_ready", "patched", "y_done", "chain_dve"))

    def banks(b, n):
        return ps[:, b:b + n, :].rearrange("p b n -> p (b n)")

    with nc.Block() as block:
        @block.sync
        def _(sp):
            sp.dma_start(sign[:], t["alternating"]).then_inc(sign_loaded, 16)

        @block.tensor
        def _(pe):
            pe.wait_ge(a["dft_loaded"], 16 * NT)
            for src, first, done in ((a["k_tok"], 0, kf_done), (a["u"], 4, uf_done)):
                for n in range(4):
                    for j in range(NT):
                        last = pe.matmul(ps[:, first + n, :], src[:, j, :], dft[:, j, n * HALF:(n + 1) * HALF],
                                         start=j == 0, stop=j == NT - 1)
                    last.then_inc(done, 1)
            for f in range(NF // P):
                pe.wait_ge(yf_ready, 1)
                pe.wait_ge(kf_ready, 4)
                pe.transpose(ps[:, f // 4, (f % 4) * P:(f % 4 + 1) * P], yf[:, f * P:(f + 1) * P],
                             g["ident"][:]).then_inc(yt_psum, 1)
            pe.wait_ge(patched, 1)
            pe.wait_ge(yt_ready, 4)
            for b in range(NT):
                for f in range(NF // P):
                    cols = (f // NT) * S + b * P
                    last = pe.matmul(ps[:, 4 + b // 4, (b % 4) * D:(b % 4 + 1) * D],
                                     dft[:, f % NT, cols:cols + P], yt[:, f, :],
                                     start=f == 0, stop=f == NF // P - 1)
            last.then_inc(y_done, 1)

        @block.scalar
        def _(act):
            for n in range(4):
                act.wait_ge(kf_done, n + 1)
                act.activation(kf[:, n * HALF:(n + 1) * HALF], ps[:, n, :], ACT.Copy,
                               scale=2.0 / NF).then_inc(kf_ready, 1)
            for n in range(4):
                act.wait_ge(yt_psum, 4 * (n + 1))
                act.activation(yt[:, 4 * n:4 * n + 4, :], ps[:, n, :].rearrange("p (f d) -> p f d", d=D),
                               ACT.Copy).then_inc(yt_ready, 1)
            act.wait_ge(y_done, 1)
            act.activation(a["y"][:], banks(4, 2).rearrange("p (i d) -> p i d", d=D), ACT.Copy)

        @block.vector
        def _(dve):
            link = chained(dve, chain_dve)
            dve.wait_ge(kf_ready, 4)
            dve.wait_ge(uf_done, 4)
            ur, ui, kr, ki = banks(4, 2), banks(6, 2), kf[:, 0:S], kf[:, S:NF]
            link(dve.scalar_tensor_tensor(out=ends[:], in0=banks(4, 4)[:, 0:NF:S], scalar=0.5,
                                          in1=kf[:, 0:NF:S], op0=ALU.mult, op1=ALU.mult))
            link(dve.tensor_tensor(yf[:, 0:S], ur, kr, ALU.mult))
            link(dve.tensor_tensor(cross[:], ui, ki, ALU.mult))
            link(dve.tensor_tensor(yf[:, 0:S], yf[:, 0:S], cross[:], ALU.subtract))
            link(dve.tensor_tensor(yf[:, S:NF], ur, ki, ALU.mult))
            link(dve.tensor_tensor(cross[:], ui, kr, ALU.mult))
            link(dve.tensor_tensor(yf[:, S:NF], yf[:, S:NF], cross[:], ALU.add))
            dve.tensor_copy(yf[:, 0:NF:S], ends[:]).then_inc(yf_ready, 1)
            link(dve.memset(dft[:, :, S:S + 1], 0.0))
            dve.wait_ge(sign_loaded, 16)
            dve.tensor_copy(dft[0:1, 0, S:NF], sign[:]).then_inc(patched, 1)


def film_out_ffn(nc, g, t, m, a):
    HID = 4 * D
    NH_ = HID // P
    ps = g["psum"]
    w_f, b_f = m.sb("w_f", [P, 2 * D]), m.sb("b_f", [1, 2 * D])
    w1, b1 = m.sb("w1", [P, HID]), m.sb("b1", [P, NH_])
    w2, b2 = m.sb("w2", [P, NH_, D]), m.sb("b2", [1, D])
    g_ffn, b_ffn = m.sb("g_ffn", [P, 1]), m.sb("b_ffn", [P, 1])
    gain, shift = m.sb("gain", [P, D]), m.sb("shift", [P, D])
    scale = m.sb("scale", [P, NT, D])
    xt = m.sb("xt", [P, NT, D])
    h = m.sb("h", [P, NT, D])
    hT = m.sb("hT", [P, S])
    act_T = m.sb("act_T", [P, NH_, S])
    norm = [{n: m.sb(f"{n}{k}", s) for n, s in (("stats", [P, NT, 6]), ("mv", [P, NT, 2]), ("rstd", [P, NT, 1]))}
            for k in range(2)]
    var_ready = [m.sem(f"var_ready{k}") for k in range(2)]
    root_ready = [m.sem(f"root_ready{k}") for k in range(2)]
    loaded, chain_dve, film_done, h_ready, hT_psum, hT_ready, u_done, act_ready, out_done, normed = (
        m.sem(n) for n in ("loaded", "chain_dve", "film_done", "h_ready", "hT_psum", "hT_ready",
                           "u_done", "act_ready", "out_done", "normed"))
    N_LOADS = 10

    def tiles(v):
        return v.unsqueeze(1).to_broadcast([P, NT, D])

    with nc.Block() as block:
        @block.sync
        def _(sp):
            for dst, src in ((w_f[:], t["L1_xattn_W_film_out"]),
                             (b_f[:], t["L1_xattn_b_film_out"].unsqueeze(0)),
                             (w1[:], t["L1_xattn_W1"]),
                             (b1[:], t["L1_b1_T"]),
                             (w2[:], t["L1_xattn_W2"].rearrange("(q p) d -> p q d", p=P)),
                             (b2[:], t["L1_xattn_b2"].unsqueeze(0)),
                             (g_ffn[:], t["L1_xattn_g_ffn"].unsqueeze(1)),
                             (b_ffn[:], t["L1_xattn_b_ffn"].unsqueeze(1)),
                             (gain[:], broadcast_row("L1_xattn_g_norm_out", t)),
                             (shift[:], broadcast_row("L1_xattn_b_norm_out", t))):
                sp.dma_start(dst, src).then_inc(loaded, 16)

        @block.vector
        def _(dve):
            link = chained(dve, chain_dve)
            dve.wait_ge(film_done, 1)
            link(film_apply(dve, link, ps, a["gate"], a["y"][:], scale, xt[:]))
            link(dve.tensor_tensor(xt[:], xt[:], g["xn"][:], ALU.add))
            normalise(dve, link, xt, norm[0]["stats"], norm[0]["mv"], norm[0]["rstd"], var_ready[0],
                      root_ready[0], h, h_ready)
            dve.wait_ge(out_done, 1)
            link(dve.tensor_tensor(xt[:], xt[:], ps[:, 4:6, :].rearrange("p b (i d) -> p (b i) d", d=D),
                                   ALU.add))
            normalise(dve, link, xt, norm[1]["stats"], norm[1]["mv"], norm[1]["rstd"], var_ready[1],
                      root_ready[1], h, normed)
            dve.wait_ge(normed, NT)
            link(dve.tensor_tensor(h[:], h[:], tiles(gain[:]), ALU.mult))
            link(dve.tensor_tensor(h[:], h[:], tiles(shift[:]), ALU.add))
            link(dve.tensor_tensor(g["x"][:], g["x"][:], h[:], ALU.add))

        @block.scalar
        def _(act):
            root(act, norm[0]["rstd"], 1, var_ready[0], root_ready[0])
            act.wait_ge(loaded, 16 * N_LOADS)
            for n in range(2):
                act.wait_ge(hT_psum, 4 * (n + 1))
                act.activation(hT[:, n * HALF:(n + 1) * HALF], ps[:, n, :], ACT.Identity,
                               scale=g_ffn[:, 0:1], bias=b_ffn[:, 0:1]).then_inc(hT_ready, 1)
            for q in range(NH_):
                act.wait_ge(u_done, q + 1)
                b = 2 * ((q + 1) % 4)
                act.activation(act_T[:, q, :], ps[:, b:b + 2, :].rearrange("p b n -> p (b n)"),
                               ACT.Gelu, bias=b1[:, q:q + 1]).then_inc(act_ready, 1)
            root(act, norm[1]["rstd"], 1, var_ready[1], root_ready[1])

        @block.tensor
        def _(pe):
            pe.wait_ge(loaded, 16 * N_LOADS)
            film(pe, g, w_f, b_f, ps, film_done)
            transpose_tiles(pe, h, g["ident"][:], ps, h_ready, hT_psum)
            pe.wait_ge(hT_ready, 2)
            for q in range(NH_):
                for n in range(2):
                    last = pe.matmul(ps[:, 2 * ((q + 1) % 4) + n, :], w1[:, q * P:(q + 1) * P],
                                     hT[:, n * HALF:(n + 1) * HALF], start=True, stop=True)
                last.then_inc(u_done, 1)
            pe.wait_ge(act_ready, NH_)
            for i in range(NT):
                out = ps[:, 4 + i // 4, (i % 4) * D:(i % 4 + 1) * D]
                for q in range(NH_):
                    pe.matmul(out, act_T[:, q, i * P:(i + 1) * P], w2[:, q, :], start=q == 0, stop=False)
                last = pe.matmul(out, g["ones"][:, 0:P], b2[:], start=False, stop=True)
            last.then_inc(out_done, 1)



HQ, HKV, HD = 16, 4, 8
HQK = HQ + HKV
PARTS9 = 9 * HD
SPLIT = PARTS9 + 3
OUT = HD + 1


def gqa_experts(nc, g, t, m):
    a = {"xn": m.sb("xn", [P, NT, D]), "o": m.sb("o", [P, NT, HQ, HD])}
    with ExitStack() as ctx:
        mm = Memory(nc, ctx, "gqa")
        a["split"] = mm.sb("split", [P, NT, HQK, SPLIT], BF16)
        a["v"] = mm.sb("v", [P, NT, HKV, OUT])
        with ExitStack() as inner:
            gqa_project(nc, g, t, Memory(nc, inner, "gqa_project"), a)
        with ExitStack() as inner:
            gqa_attend(nc, g, t, Memory(nc, inner, "gqa_attend"), a)
    with ExitStack() as ctx:
        gqa_output(nc, g, t, Memory(nc, ctx, "gqa_output"), a)
    recycle(nc, Memory.used)
    with ExitStack() as ctx:
        top_expert(nc, g, t, Memory(nc, ctx, "top_expert"), a)


def gqa_project(nc, g, t, m, a):
    ps = g["psum"]
    WQKV = (HQ + 2 * HKV) * HD
    w, bias = m.sb("w", [P, WQKV]), m.sb("bias", [1, WQKV])
    ln_w = m.sb("ln_w", [P, 1])
    cos, sin = m.sb("cos", [P, NT, HD // 2]), m.sb("sin", [P, NT, HD // 2])
    qn_w, kn_w = m.sb("qn_w", [P, HD]), m.sb("kn_w", [P, HD])
    stats, mv, rstd = m.sb("stats", [P, NT, 6]), m.sb("mv", [P, NT, 2]), m.sb("rstd", [P, NT, 2])
    h, hT = m.sb("h", [P, NT, D]), m.sb("hT", [P, S])
    qkv = m.sb("qkv", [P, NT, HQ + 2 * HKV, HD])
    turned = m.sb("turned", [P, NT, HQK, HD])
    half = m.sb("half", [P, NT, HQK, HD // 2])
    square = m.sb("square", [P, NT * HQK, HD])
    scale = m.sb("scale", [P, NT * HQK])
    eps = m.sb("eps", [P, 1])
    part = m.sb("part", [P, 3, NT, HQK, HD], BF16)
    rest = m.sb("rest", [P, NT, HQK, HD])

    loaded, chain_dve, var_ready, root_ready, h_ready, hT_psum, hT_ready = (
        m.sem(n) for n in ("loaded", "chain_dve", "var_ready", "root_ready", "h_ready", "hT_psum", "hT_ready"))
    qkv_done, qkv_ready, square_ready, scale_ready, parts_ready, stacked = (
        m.sem(n) for n in ("qkv_done", "qkv_ready", "square_ready", "scale_ready", "parts_ready", "stacked"))
    N_LOADS = 7

    with nc.Block() as block:
        @block.sync
        def _(sp):
            for dst, src in ((w[:], t["L1_Wqkv"]), (bias[:], t["L1_bqkv"]),
                             (ln_w[:], t["L1_ffn_ln1_w"].unsqueeze(1)),
                             (cos[:], t["rope_cos"].rearrange("(i p) c -> p i c", p=P)),
                             (sin[:], t["rope_sin"].rearrange("(i p) c -> p i c", p=P)),
                             (qn_w[:], t["L1_ffn_qn_w"].unsqueeze(0).to_broadcast([P, HD])),
                             (kn_w[:], t["L1_ffn_kn_w"].unsqueeze(0).to_broadcast([P, HD]))):
                sp.dma_start(dst, src).then_inc(loaded, 16)

        @block.vector
        def _(dve):
            link = chained(dve, chain_dve)
            link(dve.memset(eps[:], 1e-6))
            normalise(dve, link, g["x"], stats, mv, rstd, var_ready, root_ready, a["xn"], h_ready,
                      1e-6, h)
            dve.wait_ge(qkv_ready, 4)
            HH = HD // 2
            x1, x2 = qkv[:, :, 0:HQK, 0:HH], qkv[:, :, 0:HQK, HH:HD]
            c = cos[:].unsqueeze(2).to_broadcast([P, NT, HQK, HH])
            s = sin[:].unsqueeze(2).to_broadcast([P, NT, HQK, HH])
            for out, one, two, op in ((turned[:, :, :, 0:HH], (x1, c), (x2, s), ALU.subtract),
                                      (turned[:, :, :, HH:HD], (x1, s), (x2, c), ALU.add)):
                link(dve.tensor_tensor(out, *one, ALU.mult))
                link(dve.tensor_tensor(half[:], *two, ALU.mult))
                link(dve.tensor_tensor(out, out, half[:], op))
            flat = turned[:].rearrange("p i h c -> p (i h) c")
            link(dve.tensor_tensor(square[:], flat, flat, ALU.mult))
            dve.reduce_sum(scale[:], square[:], AX).then_inc(square_ready, 1)
            dve.wait_ge(scale_ready, 1)
            link(dve.reciprocal(scale[:], scale[:]))
            link(dve.tensor_tensor(flat, flat, scale[:].unsqueeze(2).to_broadcast([P, NT * HQK, HD]), ALU.mult))
            for w_n, lo, hi in ((qn_w, 0, HQ), (kn_w, HQ, HQK)):
                v = turned[:, :, lo:hi, :]
                link(dve.tensor_tensor(v, v, w_n[:].unsqueeze(1).unsqueeze(1).to_broadcast(
                    [P, NT, hi - lo, HD]), ALU.mult))
            link(dve.tensor_copy(part[:, 0], turned[:]))
            link(dve.tensor_tensor(rest[:], turned[:], part[:, 0], ALU.subtract))
            link(dve.tensor_copy(part[:, 1], rest[:]))
            dve.tensor_tensor(part[:, 2], rest[:], part[:, 1], ALU.subtract).then_inc(parts_ready, 1)
            dve.wait_ge(parts_ready, 1)
            for n in range(9):
                cols = slice(n * HD, (n + 1) * HD)
                dve.tensor_copy(a["split"][:, :, HQ:HQK, cols], part[:, n % 3, :, HQ:HQK, :])
                last = dve.tensor_copy(a["split"][:, :, 0:HQ, cols], part[:, n // 3, :, 0:HQ, :])
            last.then_inc(stacked, 1)
            dve.wait_ge(stacked, 1)

        @block.gpsimd
        def _(pool):
            link = chained(pool, m.sem("chain_pool"))
            link(pool.memset(a["split"][:, :, HQ:HQK, PARTS9:SPLIT], 1.0))
            link(pool.memset(a["v"][:, :, :, HD:OUT], 1.0))

        @block.scalar
        def _(act):
            root(act, rstd, 2, var_ready, root_ready)
            act.wait_ge(loaded, 16 * N_LOADS)
            for n in range(2):
                act.wait_ge(hT_psum, 4 * (n + 1))
                act.activation(hT[:, n * HALF:(n + 1) * HALF], ps[:, n, :], ACT.Copy,
                               scale=ln_w[:, 0:1]).then_inc(hT_ready, 1)
            for n in range(4):
                act.wait_ge(qkv_done, 2 * (n + 1))
                act.activation(qkv[:, 2 * n:2 * n + 2, :, :],
                               ps[:, 4 + n, 0:2 * WQKV].rearrange("p (i h c) -> p i h c", i=2, c=HD),
                               ACT.Copy).then_inc(qkv_ready, 1)
            act.wait_ge(qkv_ready, 4)
            act.activation(a["v"][:, :, :, 0:HD], qkv[:, :, HQK:, :], ACT.Copy)
            act.wait_ge(square_ready, 1)
            act.activation(scale[:], scale[:], ACT.Sqrt, scale=1.0 / HD, bias=eps[:, 0:1]).then_inc(scale_ready, 1)

        @block.tensor
        def _(pe):
            transpose_tiles(pe, h, g["ident"][:], ps, h_ready, hT_psum)
            pe.wait_ge(loaded, 16 * N_LOADS)
            for i in range(NT):
                pe.wait_ge(hT_ready, i // 4 + 1)
                out = ps[:, 4 + i // 2, (i % 2) * WQKV:(i % 2 + 1) * WQKV]
                pe.matmul(out, hT[:, i * P:(i + 1) * P], w[:], start=True, stop=False)
                pe.matmul(out, g["ones"][:, 0:P], bias[:], start=False, stop=True).then_inc(qkv_done, 1)


def gqa_attend(nc, g, t, m, a):
    SCALE = float(HD) ** -0.5
    ps = g["psum"]
    split = a["split"]
    ident = m.sb("ident", [P, P], BF16)
    above, below = m.sb("above", [P, P], BF16), m.sb("below", [P, P], BF16)
    masks_f = m.sb("masks_f", [P, 2, P])
    kT = m.sb("kT", [SPLIT, HKV, S], BF16)
    qT = m.sb("qT", [SPLIT, 2, S], BF16)
    sT = m.sb("sT", [SPLIT, 2, S], BF16)
    low = m.sb("low", [P, 2, NT])
    rest = m.sb("rest", [P, 2, NT])
    prob = m.sb("prob", [P, 2, NT, S])
    share = m.sb("share", [P, 2, NT])

    loaded, consts, chain_dve = m.sem("loaded"), m.sem("consts"), m.sem("chain_dve")
    k_psum, k_ready, q_psum, q_ready, score_done, max_read, shift_ready, s_psum, s_ready = (
        m.sem(n) for n in ("k_psum", "k_ready", "q_psum", "q_ready", "score_done", "max_read",
                           "shift_ready", "s_psum", "s_ready"))
    prob_psum, prob_ready, pv_done, o_ready = (
        m.sem(n) for n in ("prob_psum", "prob_ready", "pv_done", "o_ready"))

    def pair(n, cols):
        return ps[:, n:n + 2, :].rearrange("p b n -> p (b n)")[:, 0:cols]

    turned_bank = ps[0:SPLIT, 6, :].bitcast(BF16)

    with nc.Block() as block:
        @block.sync
        def _(sp):
            sp.dma_start(masks_f[:, 0, :], t["above_diagonal"]).then_inc(loaded, 16)
            sp.dma_start(masks_f[:, 1, :], t["below_diagonal"]).then_inc(loaded, 16)

        @block.tensor
        def _(pe):
            pe.wait_ge(consts, 3)

            def turn(head, rows, done):
                for i in range(NT):
                    last = pe.transpose(turned_bank[0:rows, i * P:(i + 1) * P], split[:, i, head, 0:rows],
                                        ident[:])
                last.then_inc(done, 1)

            def maxima(h):
                for i in range(NT):
                    n = NT * h + i
                    b = 2 * (n % 2)
                    if n >= 2:
                        pe.wait_ge(max_read, n - 1)
                    width = (i + 1) * P
                    for k in range(0, width, HALF):
                        w = min(HALF, width - k)
                        pe.matmul(ps[:, b + k // HALF, 0:w], qT[0:PARTS9, h % 2, i * P:(i + 1) * P],
                                  kT[0:PARTS9, h // (HQ // HKV), k:k + w], start=True, stop=k + w < width)
                    col = (i % 4) * P
                    pe.matmul(ps[:, b + i // 4, col:col + P], ident[:], above[:], start=False,
                              stop=True).then_inc(score_done, 1)

            def exponentials(h):
                for k in range(NT):
                    n = NT * h + k
                    if n >= 1:
                        pe.wait_ge(prob_ready, n)
                    width = S - k * P
                    for q in range(0, width, HALF):
                        w = min(HALF, width - q)
                        last = pe.matmul(ps[:, 4 + q // HALF, 0:w], kT[:, h // (HQ // HKV), k * P:(k + 1) * P],
                                         sT[:, h % 2, k * P + q:k * P + q + w], start=True, stop=q > 0)
                        if q == 0:
                            last = pe.matmul(ps[:, 4, 0:P], ident[:], below[:], start=False, stop=True)
                    last.then_inc(prob_psum, 1)

            def outputs(h):
                pe.wait_ge(prob_ready, NT * (h + 1))
                if h >= 1:
                    pe.wait_ge(o_ready, h)
                for i in range(NT):
                    for k in range(i + 1):
                        last = pe.matmul(ps[:, 7, i * 16:i * 16 + OUT],
                                         prob[:, h % 2, k, (i - k) * P:(i - k + 1) * P],
                                         a["v"][:, k, h // (HQ // HKV), :], start=k == 0, stop=k == i)
                last.then_inc(pv_done, 1)

            def turn_queries(h):
                if h >= 1:
                    pe.wait_ge(s_ready, h)
                turn(h, PARTS9, q_psum)

            for k in range(HKV):
                if k >= 1:
                    pe.wait_ge(k_ready, k)
                turn(HQ + k, SPLIT, k_psum)
            pe.wait_ge(k_ready, HKV)
            for h in range(HQ + 1):
                if h < HQ:
                    turn_queries(h)
                    pe.wait_ge(q_ready, h + 1)
                    maxima(h)
                if h >= 1:
                    exponentials(h - 1)
                    outputs(h - 1)
                if h < HQ:
                    pe.wait_ge(shift_ready, h + 1)
                    turn(h, SPLIT, s_psum)
                    pe.wait_ge(s_ready, h + 1)

        @block.vector
        def _(dve):
            link = chained(dve, chain_dve)
            dve.wait_ge(loaded, 32)
            dve.tensor_copy(ident[:], g["ident"][:]).then_inc(consts, 1)
            dve.tensor_copy(above[:], masks_f[:, 0, :]).then_inc(consts, 1)
            dve.tensor_copy(below[:], masks_f[:, 1, :]).then_inc(consts, 1)
            for h in range(HQ + 1):
                if h < HQ:
                    b = h % 2
                    for i in range(NT):
                        n = NT * h + i
                        dve.wait_ge(score_done, n + 1)
                        dve.tensor_reduce(low[:, b, i:i + 1], pair(2 * (n % 2), (i + 1) * P), AX, ALU.max,
                                          negate=True).then_inc(max_read, 1)
                    dve.wait_ge(max_read, NT * (h + 1))
                    parts = split[:, :, h, PARTS9:SPLIT]
                    link(dve.tensor_copy(parts[:, :, 0], low[:, b, :]))
                    link(dve.tensor_tensor(rest[:, b, :], low[:, b, :], parts[:, :, 0], ALU.subtract))
                    link(dve.tensor_copy(parts[:, :, 1], rest[:, b, :]))
                    dve.tensor_tensor(parts[:, :, 2], rest[:, b, :], parts[:, :, 1],
                                      ALU.subtract).then_inc(shift_ready, 1)
                if h >= 1:
                    b = (h - 1) % 2
                    dve.wait_ge(pv_done, h)
                    out = ps[:, 7, 0:NT * 16].rearrange("p (i c) -> p i c", c=16)
                    link(dve.reciprocal(share[:, b, :], out[:, :, HD]))
                    dve.tensor_tensor(a["o"][:, :, h - 1, :], out[:, :, 0:HD],
                                      share[:, b, :].unsqueeze(2).to_broadcast([P, NT, HD]),
                                      ALU.mult).then_inc(o_ready, 1)

        @block.scalar
        def _(act):
            for k in range(HKV):
                act.wait_ge(k_psum, k + 1)
                act.activation(kT[:, k, :], turned_bank, ACT.Copy).then_inc(k_ready, 1)
            for h in range(HQ + 1):
                if h < HQ:
                    act.wait_ge(q_psum, h + 1)
                    act.activation(qT[0:PARTS9, h % 2, :], turned_bank[0:PARTS9, :], ACT.Copy).then_inc(q_ready, 1)
                if h >= 1:
                    for k in range(NT):
                        n = NT * (h - 1) + k
                        act.wait_ge(prob_psum, n + 1)
                        if h >= 3 and k == 0:
                            act.wait_ge(pv_done, h - 2)
                        act.activation(prob[:, (h - 1) % 2, k, 0:S - k * P], pair(4, S - k * P), ACT.Exp,
                                       scale=SCALE).then_inc(prob_ready, 1)
                if h < HQ:
                    act.wait_ge(s_psum, h + 1)
                    act.activation(sT[:, h % 2, :], turned_bank, ACT.Copy).then_inc(s_ready, 1)


def gqa_output(nc, g, t, m, a):
    ps = g["psum"]
    w_g, b_g = m.sb("w_g", [P, D]), m.sb("b_g", [1, D])
    w_o, b_o = m.sb("w_o", [P, D]), m.sb("b_o", [1, D])
    oT, gT = m.sb("oT", [P, S]), m.sb("gT", [P, S])
    gate = m.sb("gate", [P, NT, D])
    gated = m.sb("gated", [P, NT, D])
    zeroed, loaded, chain_dve, oT_psum, oT_ready, gate_done, gate_ready, gated_ready, gT_psum, gT_ready, out_done = (
        m.sem(n) for n in ("zeroed", "loaded", "chain_dve", "oT_psum", "oT_ready", "gate_done",
                           "gate_ready", "gated_ready", "gT_psum", "gT_ready", "out_done"))
    N_LOADS = 3 + HQ
    o = a["o"][:].rearrange("p i h c -> p i (h c)")

    def wide(b):
        return ps[:, b:b + 2, :].rearrange("p b (i d) -> p (b i) d", d=D)

    with nc.Block() as block:
        @block.sync
        def _(sp):
            sp.dma_start(b_g[:], t["L1_bg_rep"]).then_inc(loaded, 16)
            sp.dma_start(w_o[:], t["L1_ffn_Wo"]).then_inc(loaded, 16)
            sp.dma_start(b_o[:], t["L1_ffn_bo"].unsqueeze(0)).then_inc(loaded, 16)
            sp.wait_ge(zeroed, 1)
            for h in range(HQ):
                sp.dma_start(w_g[h * HD:(h + 1) * HD, h * HD:(h + 1) * HD], t["L1_ffn_Wg"]).then_inc(loaded, 16)

        @block.gpsimd
        def _(pool):
            pool.memset(w_g[:], 0.0).then_inc(zeroed, 1)

        @block.tensor
        def _(pe):
            for i in range(NT):
                pe.transpose(ps[:, i // 4, (i % 4) * P:(i % 4 + 1) * P], o[:, i, :],
                             g["ident"][:]).then_inc(oT_psum, 1)
            pe.wait_ge(loaded, 16 * N_LOADS)
            for i in range(NT):
                pe.wait_ge(oT_ready, i // 4 + 1)
                out = ps[:, 2 + i // 4, (i % 4) * D:(i % 4 + 1) * D]
                pe.matmul(out, oT[:, i * P:(i + 1) * P], w_g[:], start=True, stop=False)
                pe.matmul(out, g["ones"][:, 0:P], b_g[:], start=False, stop=True).then_inc(gate_done, 1)
            transpose_tiles(pe, gated, g["ident"][:], ps[:, 4:6, :], gated_ready, gT_psum)
            for i in range(NT):
                pe.wait_ge(gT_ready, i // 4 + 1)
                out = ps[:, 6 + i // 4, (i % 4) * D:(i % 4 + 1) * D]
                pe.matmul(out, gT[:, i * P:(i + 1) * P], w_o[:], start=True, stop=False)
                last = pe.matmul(out, g["ones"][:, 0:P], b_o[:], start=False, stop=True)
            last.then_inc(out_done, 1)

        @block.scalar
        def _(act):
            for n in range(2):
                act.wait_ge(oT_psum, 4 * (n + 1))
                act.activation(oT[:, n * HALF:(n + 1) * HALF], ps[:, n, :], ACT.Copy).then_inc(oT_ready, 1)
            act.wait_ge(gate_done, NT)
            act.activation(gate[:], wide(2), ACT.Sigmoid).then_inc(gate_ready, 1)
            for n in range(2):
                act.wait_ge(gT_psum, 4 * (n + 1))
                act.activation(gT[:, n * HALF:(n + 1) * HALF], ps[:, 4 + n, :], ACT.Copy).then_inc(gT_ready, 1)

        @block.vector
        def _(dve):
            link = chained(dve, chain_dve)
            dve.wait_ge(gate_ready, 1)
            dve.tensor_tensor(gated[:], o, gate[:], ALU.mult).then_inc(gated_ready, NT)
            dve.wait_ge(out_done, 1)
            link(dve.tensor_tensor(a["xn"][:], a["xn"][:], wide(6), ALU.add))


def top_expert(nc, g, t, m, a):
    NE, HID = 8, 256
    ps = g["psum"]
    x1 = a["xn"]
    ln_w = m.sb("ln_w", [P, 1])
    w_r, b_r = m.sb("w_r", [P, NE]), m.sb("b_r", [1, NE])
    w1, b1 = m.sb("w1", [P, NE, 2 * HID]), m.sb("b1", [P, NE, 4])
    w2, b2 = m.sb("w2", [P, NE, 2, D]), m.sb("b2", [1, NE, D])
    order = m.sb("order", [P, NE])
    stats, mv = m.sb("stats", [P, NT, 6]), m.sb("mv", [P, NT, 2])
    scale = m.sb("scale", [P, NT])
    h, hT = m.sb("h", [P, NT, D]), m.sb("hT", [P, S])
    best = m.sb("best", [P, NT])
    rank = m.sb("rank", [P, NT, NE])
    own = m.sb("own", [P, NT, NE])
    sig = m.sb("sig", [P, 2, S])
    act_T = m.sb("act_T", [P, 2, 2, S])
    kept = m.sb("kept", [P, 2, NT, D])

    loaded, loaded_w, chain_dve, scale_sq, scale_ready, h_ready, hT_psum, hT_ready, logit_done = (
        m.sem(n) for n in ("loaded", "loaded_w", "chain_dve", "scale_sq", "scale_ready", "h_ready",
                           "hT_psum", "hT_ready", "logit_done"))
    u_done, sig_ready, act_ready, y_done, y_read, added, sum_ready = (
        m.sem(n) for n in ("u_done", "sig_ready", "act_ready", "y_done", "y_read", "added", "sum_ready"))
    N_LOADS = 4

    def pair(n):
        return ps[:, 2 * n:2 * n + 2, :].rearrange("p b n -> p (b n)")

    with nc.Block() as block:
        @block.sync
        def _(sp):
            sp.dma_start(ln_w[:], t["L1_ffn_ln2_w"].unsqueeze(1)).then_inc(loaded, 16)
            sp.dma_start(w_r[:], t["L1_ffn_Wr"]).then_inc(loaded, 16)
            sp.dma_start(b_r[:], t["L1_ffn_br"].unsqueeze(0)).then_inc(loaded, 16)
            sp.dma_start(order[:], t["order"]).then_inc(loaded, 16)
            sp.dma_start(b1[:], t["L1_eb1_T"].rearrange("(e q p) -> p e q", e=NE, p=P),
                         allow_slow_non_contiguous=True).then_inc(loaded_w, 16)
            sp.dma_start(w1[:], t["L1_ffn_W1"].rearrange("e p n -> p e n")).then_inc(loaded_w, 16)
            sp.dma_start(w2[:], t["L1_ffn_W2"].rearrange("e (q p) d -> p e q d", p=P)).then_inc(loaded_w, 16)
            sp.dma_start(b2[:], t["L1_ffn_b2"].unsqueeze(0)).then_inc(loaded_w, 16)

        @block.vector
        def _(dve):
            link = chained(dve, chain_dve)
            for i in range(NT):
                last = dve.bn_stats(stats[:, i, :], x1[:, i, :])
            link(last)
            for i in range(NT):
                last = dve.bn_aggr(mv[:, i, :], stats[:, i, :])
            link(last)
            link(dve.tensor_tensor(scale[:], mv[:, :, 0], mv[:, :, 0], ALU.mult))
            dve.scalar_tensor_tensor(out=scale[:], in0=scale[:], scalar=1e-6, in1=mv[:, :, 1],
                                     op0=ALU.add, op1=ALU.add).then_inc(scale_sq, 1)
            dve.wait_ge(scale_ready, 1)
            link(dve.reciprocal(scale[:], scale[:]))
            for i in range(NT):
                dve.tensor_scalar(h[:, i, :], x1[:, i, :], scale[:, i:i + 1], None,
                                  ALU.mult).then_inc(h_ready, 1)
            link(dve.tensor_tensor(g["x"][:], g["x"][:], x1[:], ALU.add))
            dve.wait_ge(logit_done, 1)
            dve.wait_ge(loaded, 16 * N_LOADS)
            logits = ps[:, 2, 0:NT * NE].rearrange("p (i e) -> p i e", e=NE)

            def spread(v):
                return v.unsqueeze(2).to_broadcast([P, NT, NE])

            link(dve.reduce_max(best[:], logits, AX))
            link(dve.tensor_tensor(rank[:], logits, spread(best[:]), ALU.is_equal))
            link(dve.tensor_tensor(rank[:], rank[:], order[:].unsqueeze(1).to_broadcast([P, NT, NE]), ALU.mult))
            link(dve.reduce_max(best[:], rank[:], AX))
            dve.tensor_tensor(own[:], rank[:], spread(best[:]), ALU.is_equal).then_inc(sum_ready, 1)
            dve.wait_ge(sum_ready, 1)

            def keep(e):
                dve.wait_ge(y_done, e + 1)
                if e >= 2:
                    dve.wait_ge(added, e - 1)
                dve.tensor_tensor(kept[:, e % 2], pair(3).rearrange("p (i d) -> p i d", d=D),
                                  own[:, :, e:e + 1].to_broadcast([P, NT, D]), ALU.mult).then_inc(y_read, 1)

            for e in range(NE):
                for q in range(2):
                    n = 2 * e + q
                    dve.wait_ge(u_done, 2 * n + 2)
                    dve.wait_ge(sig_ready, n + 1)
                    if e >= 2:
                        dve.wait_ge(y_done, e - 1)
                    dve.scalar_tensor_tensor(out=act_T[:, e % 2, q, :], in0=pair((2 * n + 1) % 3),
                                             scalar=b1[:, e, q:q + 1], in1=sig[:, q, :],
                                             op0=ALU.add, op1=ALU.mult).then_inc(act_ready, 1)
                if e >= 1:
                    keep(e - 1)
            keep(NE - 1)

        @block.gpsimd
        def _(pool):
            pool.wait_ge(sum_ready, 1)
            for e in range(NE):
                pool.wait_ge(y_read, e + 1)
                pool.tensor_tensor(g["x"][:], g["x"][:], kept[:, e % 2], ALU.add).then_inc(added, 1)
                pool.wait_ge(added, e + 1)

        @block.scalar
        def _(act):
            act.wait_ge(scale_sq, 1)
            act.activation(scale[:], scale[:], ACT.Sqrt).then_inc(scale_ready, 1)
            act.wait_ge(loaded, 16 * N_LOADS)
            for n in range(2):
                act.wait_ge(hT_psum, 4 * (n + 1))
                act.activation(hT[:, n * HALF:(n + 1) * HALF], ps[:, n, :], ACT.Copy,
                               scale=ln_w[:, 0:1]).then_inc(hT_ready, 1)
            act.wait_ge(loaded_w, 64)
            for e in range(NE):
                for q in range(2):
                    n = 2 * e + q
                    act.wait_ge(u_done, 2 * n + 1)
                    if n >= 2:
                        act.wait_ge(act_ready, n - 1)
                    act.activation(sig[:, q, :], pair((2 * n) % 3), ACT.Sigmoid,
                                   bias=b1[:, e, 2 + q:3 + q]).then_inc(sig_ready, 1)

        @block.tensor
        def _(pe):
            transpose_tiles(pe, h, g["ident"][:], ps, h_ready, hT_psum)
            pe.wait_ge(loaded, 16 * N_LOADS)
            for i in range(NT):
                pe.wait_ge(hT_ready, i // 4 + 1)
                out = ps[:, 2, i * NE:(i + 1) * NE]
                pe.matmul(out, hT[:, i * P:(i + 1) * P], w_r[:], start=True, stop=False)
                last = pe.matmul(out, g["ones"][:, 0:P], b_r[:], start=False, stop=True)
            last.then_inc(logit_done, 1)
            pe.wait_ge(loaded_w, 64)

            def expert_out(e):
                pe.wait_ge(act_ready, 2 * (e + 1))
                if e >= 1:
                    pe.wait_ge(y_read, e)
                for i in range(NT):
                    out = ps[:, 6 + i // 4, (i % 4) * D:(i % 4 + 1) * D]
                    for q in range(2):
                        pe.matmul(out, act_T[:, e % 2, q, i * P:(i + 1) * P], w2[:, e, q, :],
                                  start=q == 0, stop=False)
                    last = pe.matmul(out, g["ones"][:, 0:P], b2[:, e, :], start=False, stop=True)
                last.then_inc(y_done, 1)

            for e in range(NE):
                for q in range(2):
                    for k in (2 + q, q):
                        n = 2 * (2 * e + q) + (k < 2)
                        if n == 1:
                            pe.wait_ge(sum_ready, 1)
                        if n >= 3:
                            pe.wait_ge(sig_ready, (n - 3) // 2 + 1)
                            if (n - 3) % 2:
                                pe.wait_ge(act_ready, (n - 3) // 2 + 1)
                        for c in range(2):
                            last = pe.matmul(ps[:, 2 * (n % 3) + c, :], w1[:, e, k * P:(k + 1) * P],
                                             hT[:, c * HALF:(c + 1) * HALF], start=True, stop=True)
                        last.then_inc(u_done, 1)
                if e >= 1:
                    expert_out(e - 1)
            expert_out(NE - 1)



def shape_constants():
    onehot3 = np.tile(np.eye(32, dtype=np.float32), (3, 1))
    above = np.triu(np.full((P, P), NEG, np.float32), 1)
    turns = 2.0 * np.pi * (np.outer(np.arange(S), np.arange(S)) % NF) / NF
    dft = np.concatenate([np.cos(turns), -np.sin(turns)], 1)
    alternating = 1.0 - 2.0 * (np.arange(S) % 2)
    dft[:, S] = alternating
    index = np.concatenate([np.arange(P), P * np.arange(NT)]).astype(np.float32)
    quarter = np.where(np.arange(P) < P // 2, 0.25, 0.0).astype(np.float32).reshape(P, 1)
    freqs = np.outer(np.arange(S), 1.0 / 10000.0 ** (np.arange(0, HD, 2) / HD)).astype(np.float32)
    return {"rope_cos": np.cos(freqs), "rope_sin": np.sin(freqs), "below_diagonal": above.T,
            "order": np.tile(np.arange(8, 0, -1, dtype=np.float32), (P, 1)),
            "dft": dft.astype(np.float32), "alternating": alternating.astype(np.float32).reshape(1, S),
            "s4d_index": np.tile(index, (P, 1)), "s4d_quarter": quarter,
            "above_diagonal": above, "ident": np.eye(P, dtype=np.float32), "onehot3": onehot3}


def laid_out(a):
    w = {k: v for k, v in a.items() if k.startswith("L")}
    w["x"] = a["x"].reshape(S, D)
    w["ctx"] = a["ctx_768"].reshape(S2, DC)
    w["ctx_T"] = a["ctx_768"].reshape(S2, DC).T
    w["L0_in_proj_T"] = a["L0_attn_in_proj_w"].T
    w["L0_conv_b_T"] = a["L0_attn_conv_b"].reshape(2, P).T
    w["L0_dt_b_T"] = a["L0_attn_dt_proj_b"].reshape(2, P).T
    w["L0_D_T"] = a["L0_attn_D"].reshape(2, P).T
    xp = a["L0_attn_x_proj_w"]
    w["L0_bcdt_T"] = np.concatenate([xp[8:], xp[8:], xp[8:], xp[:8]], 0).T
    w["L0_dt_proj_T"] = a["L0_attn_dt_proj_w"].T
    w["L0_out_proj_T"] = a["L0_attn_out_proj_w"].T
    w["L0_Wk_T"] = a["L0_xattn_Wk"].T
    for k in ("WQ", "WK", "WV"):
        w[f"L1_{k}_T"] = a[f"L1_attn_{k}"].T
    w["L1_Wq_rep"] = np.concatenate([np.tile(a["L1_xattn_Wq"][:, 32 * h:32 * h + 32], 4) for h in range(4)], 1)
    w["L1_Wk_rep"] = np.concatenate([np.tile(a["L1_xattn_Wk"][:, 32 * h:32 * h + 32], 4) for h in range(4)], 1)
    w["vision_mask"] = a["mask_BxS2_bf1"].reshape(1, S2).view(np.uint8)
    w["text_mask"] = a["mask_BxS_bf1"].reshape(S).view(np.uint8)
    for n in ("A_re", "A_im", "C_re", "C_im"):
        w[f"s4d_{n.lower()}"] = np.tile(a[f"L1_xattn_{n}"].T, (2, 1))
    w["mod_gate"] = a["L1_xattn_mod_gate"].reshape(1, 1)
    w["L1_b1_T"] = a["L1_xattn_b1"].reshape(4, P).T
    w["L1_Wqkv"] = np.concatenate([a[f"L1_ffn_W{k}"] for k in "qkv"], 1)
    w["L1_bqkv"] = np.concatenate([a[f"L1_ffn_b{k}"] for k in "qkv"]).reshape(1, -1)
    w["L1_bg_rep"] = np.tile(a["L1_ffn_bg"], HQ).reshape(1, -1)
    w["L1_eb1_T"] = a["L1_ffn_b1"].reshape(-1)
    w.update(shape_constants())
    return w

PARTS = [mamba, cross_attention, threshold_experts, causal_attention, film_context, film_s4d_ffn,
         gqa_experts]



def decoder(nc, t):
    g = {}
    with ExitStack() as whole:
        g["psum"] = whole.enter_context(nc.psum_tensor("psum", [P, 8, HALF], F32))
        g["x"] = whole.enter_context(nc.sbuf_tensor("residual", [P, NT, D], F32))
        g["ident"] = whole.enter_context(nc.sbuf_tensor("ident", [P, P], F32))
        g["ones"] = whole.enter_context(nc.sbuf_tensor("ones", [1, HALF], F32))
        g["ctx_rows"] = whole.enter_context(nc.sbuf_tensor("ctx_rows", [P, KT, DC + 1], F32))
        g["xn"] = whole.enter_context(nc.sbuf_tensor("layer1_xn", [P, NT, D], F32))
        g["c_T"] = whole.enter_context(nc.sbuf_tensor("c_T", [P, S], F32))
        Memory.used.clear()
        for part in [load_constants] + PARTS + [store_output]:
            with ExitStack() as ctx:
                part(nc, g, t, Memory(nc, ctx, part.__name__))
            if part in (causal_attention, film_context, film_s4d_ffn):
                recycle(nc, Memory.used)


def kernel(**inputs):
    import numpy as _np
    import concourse.bacc as _bacc
    from concourse import mybir as _mybir
    from concourse.bass_utils import run_bass_kernel_spmd as _run

    nc = _bacc.Bacc("TRN2", target_bir_lowering=False, num_devices=1)
    arrays = {k: v for k, v in laid_out({k: _np.asarray(v) for k, v in inputs.items()}).items()}
    t = {}
    feeds = {}
    for name, a in arrays.items():
        a = _np.ascontiguousarray(a)
        feeds[f"in_{name}"] = a
        t[name] = nc.dram_tensor(f"in_{name}", a.shape, _mybir.dt.from_np(a.dtype), kind="ExternalInput").ap()
    t["out"] = nc.dram_tensor("out_0", (S, D), _mybir.dt.float32, kind="ExternalOutput").ap()
    decoder(nc, t)
    r = _run(nc, [feeds], core_ids=[0])
    return r.results[0]["out_0"].reshape(1, S, D)
```

```python
from contextlib import ExitStack

import numpy as np

import concourse.bass as bass
from concourse import mybir

ALU = mybir.AluOpType
ACT = mybir.ActivationFunctionType
F32 = mybir.dt.float32
BF16 = mybir.dt.bfloat16
U8 = mybir.dt.uint8
AX = mybir.AxisListType.X

P = 128
S = 1024
D = 128
NT = S // P
S2 = 6404
DC = 96
HALF = 512
LN_EPS = 1e-5
NEG = -1e30


def recycle(nc, used):
    nc.clear_and_free_semaphores(list(used))
    used.clear()
    nc.all_engine_barrier()


class Memory:

    used = []

    def __init__(self, nc, ctx, name):
        self.nc, self.ctx, self.name = nc, ctx, name

    def sb(self, name, shape, dt=F32):
        return self.ctx.enter_context(self.nc.sbuf_tensor(f"{self.name}_{name}", shape, dt))

    def sem(self, name):
        handle = self.nc.alloc_semaphore(f"{self.name}_{name}")
        self.used.append(handle)
        return handle


def chained(eng, sem):
    count = [0]

    def link(ins):
        count[0] += 1
        ins.then_inc(sem, 1)
        eng.wait_ge(sem, count[0])

    return link


def wait_in_loop(eng, sem, value, passed):
    eng.wait_ge(sem, value)
    eng.sem_inc(passed, 1)


def normalise(dve, link, x, stats, mv, rstd, var_ready, root_ready, xn, ready, second_eps=None,
              second=None):
    for i in range(NT):
        ins = dve.bn_stats(stats[:, i, :], x[:, i, :])
    link(ins)
    for i in range(NT):
        ins = dve.bn_aggr(mv[:, i, :], stats[:, i, :])
    link(ins)
    ins = dve.tensor_scalar(rstd[:, :, 0], mv[:, :, 1], LN_EPS, None, ALU.add)
    n = 1
    if second is not None:
        n = 2
        ins = dve.tensor_scalar(rstd[:, :, 1], mv[:, :, 1], 1.0 + second_eps, LN_EPS * second_eps,
                                ALU.mult, ALU.add)
    ins.then_inc(var_ready, 1)
    dve.wait_ge(root_ready, 1)
    link(dve.reciprocal(rstd[:, :, 0:n], rstd[:, :, 0:n]))
    for k, dst in enumerate((xn, second)[:n]):
        for i in range(NT):
            ins = dve.tensor_scalar(dst[:, i, :], x[:, i, :], mv[:, i, 0:1], rstd[:, i, k:k + 1],
                                    ALU.subtract, ALU.mult)
            if k == n - 1:
                ins.then_inc(ready, 1)


def root(act, rstd, n, var_ready, root_ready):
    act.wait_ge(var_ready, 1)
    act.activation(rstd[:, :, 0:n], rstd[:, :, 0:n], ACT.Sqrt).then_inc(root_ready, 1)


def transpose_tiles(pe, src, ident, banks, ready, done):
    for i in range(NT):
        pe.wait_ge(ready, i + 1)
        pe.transpose(banks[:, i // 4, (i % 4) * P:(i % 4 + 1) * P], src[:, i, :],
                     ident).then_inc(done, 1)



def load_constants(nc, g, t, m):
    loaded = m.sem("loaded")
    consts = m.sem("consts")
    with nc.Block() as block:
        @block.sync
        def _(sp):
            sp.dma_start(g["x"][:], t["x"].rearrange("(i p) d -> p i d", p=P)).then_inc(loaded, 16)
            sp.dma_start(g["ident"][:], t["ident"]).then_inc(loaded, 16)
            sp.wait_ge(loaded, 32)

        @block.vector
        def _(dve):
            dve.memset(g["ones"][:], 1.0).then_inc(consts, 1)
            dve.wait_ge(consts, 1)


def store_output(nc, g, t, m):
    stored = m.sem("stored")
    with nc.Block() as block:
        @block.sync
        def _(sp):
            sp.dma_start(t["out"].rearrange("(i p) d -> p i d", p=P), g["x"][:]).then_inc(stored, 16)
            sp.wait_ge(stored, 16)



def mamba(nc, g, t, m):
    DI, NS, DR = 2 * D, 16, D // 16
    NC = DI // P
    ps = g["psum"]
    w_in = m.sb("w_in", [P, 2 * DI])
    norm_w = m.sb("norm_w", [P, 1])
    conv_w = m.sb("conv_w", [P, NC, 4])
    conv_b = m.sb("conv_b", [P, NC])
    w_bcdt = m.sb("w_bcdt", [P, NC, 3 * 2 * NS + DR])
    w_dt = m.sb("w_dt", [DR, DI])
    dt_b = m.sb("dt_b", [P, NC])
    a_log = m.sb("a_log", [P, NC, NS])
    a_neg = m.sb("a_neg", [P, NC, NS])
    skip = m.sb("skip", [P, NC])
    w_out = m.sb("w_out", [P, NC, D])
    onehot = m.sb("onehot", [3 * 2 * NS, 2 * NS], BF16)
    onehot_f = m.sb("onehot_f", [3 * 2 * NS, 2 * NS])
    stats = m.sb("stats", [P, NT, 6])
    mv = m.sb("mv", [P, NT, 2])
    rstd = m.sb("rstd", [P, NT, 2])
    xn = m.sb("xn", [P, NT, D])
    h = m.sb("h", [P, NT, D])
    hT = m.sb("hT", [P, S])
    xi_pad = m.sb("xi_pad", [P, NC, S + 3])
    conv = m.sb("conv", [P, NC, S])
    xi = m.sb("xi", [P, NC, S])
    zs = m.sb("zs", [P, NC, S])
    dt_low = m.sb("dt_low", [DR, S])
    pre = m.sb("pre", [P, NC, S])
    soft = m.sb("soft", [P, NC, S])
    delta = m.sb("delta", [P, NC, S])
    du = m.sb("du", [P, NC, S])
    rest = m.sb("rest", [3 * 2 * NS, S])
    hi = m.sb("hi", [3 * 2 * NS, S], BF16)
    mid = m.sb("mid", [3 * 2 * NS, S], BF16)
    split = m.sb("split", [3 * 2 * NS, S], BF16)
    b_all = m.sb("b_all", [P, 2, S])
    decay = m.sb("decay", [P, 2, S])
    drive = m.sb("drive", [P, 2, S])
    state = m.sb("state", [P, 2, S])
    read = m.sb("read", [P, 2, S])
    y = m.sb("y", [P, NC, S])

    loaded = m.sem("loaded")
    chain = {e: m.sem(f"chain_{e}") for e in ("dve", "act")}
    h_ready, hT_psum, hT_ready, in_done, xi_copied, z_ready, conv_done, xi_ready = (
        m.sem(n) for n in ("h_ready", "hT_psum", "hT_ready", "in_done", "xi_copied", "z_ready",
                           "conv_done", "xi_ready"))
    bc_done, dt_copied, split_ready, dt_done, pre_ready, delta_ready, du_ready = (
        m.sem(n) for n in ("bc_done", "dt_copied", "split_ready", "dt_done", "pre_ready",
                           "delta_ready", "du_ready"))
    b_bcast, c_bcast, b_copied, decay_ready, drive_ready, scanned, read_ready, summed = (
        m.sem(n) for n in ("b_bcast", "c_bcast", "b_copied", "decay_ready", "drive_ready",
                           "scanned", "read_ready", "summed"))
    y_ready, out_done, abs_ready, a_ready = (m.sem(n) for n in ("y_ready", "out_done", "abs_ready", "a_ready"))
    var_ready, root_ready = m.sem("var_ready"), m.sem("root_ready")
    N_LOADS = 11
    BC, BC3 = 2 * NS, 3 * 2 * NS

    with nc.Block() as block:
        @block.sync
        def _(sp):
            for dst, src in ((w_in[:], t["L0_in_proj_T"]),
                             (norm_w[:], t["L0_attn_norm_w"].unsqueeze(1)),
                             (conv_w[:], t["L0_attn_conv_w"].rearrange("(c p) k -> p c k", p=P)),
                             (conv_b[:], t["L0_conv_b_T"]),
                             (w_bcdt[:], t["L0_bcdt_T"].rearrange("(c p) k -> p c k", p=P)),
                             (w_dt[:], t["L0_dt_proj_T"]),
                             (dt_b[:], t["L0_dt_b_T"]),
                             (a_log[:], t["L0_attn_A_log"].rearrange("(c p) n -> p c n", p=P)),
                             (skip[:], t["L0_D_T"]),
                             (w_out[:], t["L0_out_proj_T"].rearrange("(c p) k -> p c k", p=P)),
                             (onehot_f[:], t["onehot3"])):
                sp.dma_start(dst, src).then_inc(loaded, 16)

        @block.vector
        def _(dve):
            link = chained(dve, chain["dve"])
            link(dve.memset(xi_pad[:, :, 0:3], 0.0))
            normalise(dve, link, g["x"], stats, mv, rstd, var_ready, root_ready, xn, h_ready,
                      LN_EPS, h)
            dve.wait_ge(loaded, 16 * N_LOADS)
            link(dve.tensor_copy(onehot[:], onehot_f[:]))
            dve.wait_ge(xi_copied, 2 * NC)
            for c in range(NC):
                link(dve.tensor_scalar(conv[:, c, :], xi_pad[:, c, 0:S], conv_w[:, c, 0:1], None, ALU.mult))
                for k in range(1, 4):
                    ins = dve.scalar_tensor_tensor(out=conv[:, c, :], in0=xi_pad[:, c, k:k + S],
                                                   scalar=conv_w[:, c, k:k + 1], in1=conv[:, c, :],
                                                   op0=ALU.mult, op1=ALU.add)
                    if k < 3:
                        link(ins)
                ins.then_inc(conv_done, 1)
            dve.wait_ge(bc_done, 3)
            bc = ps[0:3 * BC, 0:2, :].rearrange("p b n -> p (b n)")
            link(dve.tensor_copy(hi[:], bc))
            link(dve.tensor_tensor(rest[:], bc, hi[:], ALU.subtract))
            link(dve.tensor_copy(mid[:], rest[:]))
            link(dve.tensor_tensor(rest[:], rest[:], mid[:], ALU.subtract))
            dve.tensor_copy(split[0:BC, :], hi[0:BC, :]).then_inc(split_ready, 1)
            dve.tensor_copy(split[BC:2 * BC, :], mid[BC:2 * BC, :]).then_inc(split_ready, 1)
            dve.tensor_copy(split[2 * BC:3 * BC, :], rest[2 * BC:3 * BC, :]).then_inc(split_ready, 1)
            dve.wait_ge(dt_done, 2 * NC)
            for c in range(NC):
                acc = ps[:, 4 + 2 * c:6 + 2 * c, :].rearrange("p b n -> p (b n)")
                link(dve.tensor_scalar(pre[:, c, :], acc, dt_b[:, c:c + 1], None, ALU.add))
            link(dve.tensor_scalar(soft[:], pre[:], -1.0, None, ALU.mult))
            dve.tensor_tensor(soft[:], soft[:], pre[:], ALU.min).then_inc(abs_ready, 1)
            dve.wait_ge(delta_ready, 1)
            link(dve.scalar_tensor_tensor(out=delta[:], in0=pre[:], scalar=0.0, in1=soft[:],
                                          op0=ALU.max, op1=ALU.add))
            dve.wait_ge(xi_ready, NC)
            dve.tensor_tensor(du[:], delta[:], xi[:], ALU.mult).then_inc(du_ready, 1)
            for s in range(NS):
                for c in range(NC):
                    n = NC * s + c
                    dve.wait_ge(decay_ready, n + 1)
                    dve.wait_ge(drive_ready, n + 1)
                    dve.tensor_tensor_scan(state[:, c, :], decay[:, c, :], drive[:, c, :], 0.0,
                                           ALU.mult, ALU.add).then_inc(scanned, 1)
                    dve.wait_ge(scanned, n + 1)
                    dve.wait_ge(c_bcast, s + 1)
                    if n >= 2:
                        dve.wait_ge(summed, n - 1)
                    dve.tensor_tensor(read[:, c, :], state[:, c, :],
                                      ps[:, 2:4, :].rearrange("p b n -> p (b n)"),
                                      ALU.mult).then_inc(read_ready, 1)
            dve.wait_ge(summed, NC * NS)
            dve.wait_ge(z_ready, 2 * NC)
            for c in range(NC):
                acc = ps[:, 4 + 2 * c:6 + 2 * c, :].rearrange("p b n -> p (b n)")
                link(dve.scalar_tensor_tensor(out=y[:, c, :], in0=xi[:, c, :], scalar=skip[:, c:c + 1],
                                              in1=acc, op0=ALU.mult, op1=ALU.add))
                dve.tensor_tensor(y[:, c, :], y[:, c, :], zs[:, c, :], ALU.mult).then_inc(y_ready, 1)
            link(dve.tensor_tensor(g["x"][:], g["x"][:], xn[:], ALU.add))
            dve.wait_ge(out_done, NT)
            dve.tensor_tensor(g["x"][:], g["x"][:],
                              ps[:, 0:2, :].rearrange("p b (i d) -> p (b i) d", d=D), ALU.add)

        @block.tensor
        def _(pe):
            transpose_tiles(pe, h, g["ident"][:], ps, h_ready, hT_psum)
            pe.wait_ge(loaded, 16 * N_LOADS)
            pe.wait_ge(hT_ready, 2)
            for e in range(2 * NC):
                for n in range(2):
                    bank = (4 + 2 * e + n) % 8
                    pe.matmul(ps[:, bank, :], w_in[:, e * P:(e + 1) * P], hT[:, n * HALF:(n + 1) * HALF],
                              start=True, stop=True).then_inc(in_done, 1)
            pe.wait_ge(xi_ready, NC)
            pe.wait_ge(z_ready, 2 * NC)
            for n in range(2):
                for c in range(NC):
                    last = pe.matmul(ps[0:3 * BC, n, :],
                                     w_bcdt[:, c, 0:BC3],
                                     xi[:, c, n * HALF:(n + 1) * HALF], start=c == 0, stop=c == NC - 1)
                last.then_inc(bc_done, 1)
                for c in range(NC):
                    last = pe.matmul(ps[0:DR, 2 + n, :], w_bcdt[:, c, BC3:BC3 + DR],
                                     xi[:, c, n * HALF:(n + 1) * HALF], start=c == 0, stop=c == NC - 1)
                last.then_inc(bc_done, 1)
            pe.wait_ge(dt_copied, 1)
            for c in range(NC):
                for n in range(2):
                    pe.matmul(ps[:, 4 + 2 * c + n, :], w_dt[:, c * P:(c + 1) * P],
                              dt_low[:, n * HALF:(n + 1) * HALF], start=True, stop=True).then_inc(dt_done, 1)
            pe.wait_ge(split_ready, 3)
            pe.wait_ge(abs_ready, 1)

            def broadcast(row, banks, done):
                sel = onehot[:, row:row + 1].to_broadcast([3 * BC, P])
                for n in range(2):
                    last = pe.matmul(ps[:, banks + n, :], sel, split[:, n * HALF:(n + 1) * HALF],
                                     start=True, stop=True)
                last.then_inc(done, 1)

            def add_state(n):
                c = n % NC
                pe.wait_ge(read_ready, n + 1)
                for q in range(2):
                    last = pe.matmul(ps[:, 4 + 2 * c + q, :], g["ident"][:],
                                     read[:, c, q * HALF:(q + 1) * HALF],
                                     start=n < NC, stop=n >= NC * (NS - 1))
                last.then_inc(summed, 1)

            for s in range(NS):
                if s >= 1:
                    pe.wait_ge(b_copied, s)
                broadcast(s, 0, b_bcast)
                if s >= 1:
                    pe.wait_ge(read_ready, NC * s)
                broadcast(NS + s, 2, c_bcast)
                if s >= 1:
                    for c in range(NC):
                        add_state(NC * (s - 1) + c)
            for c in range(NC):
                add_state(NC * (NS - 1) + c)
            pe.wait_ge(y_ready, NC)
            for i in range(NT):
                for c in range(NC):
                    last = pe.matmul(ps[:, i // 4, (i % 4) * D:(i % 4 + 1) * D],
                                     y[:, c, i * P:(i + 1) * P], w_out[:, c, :],
                                     start=c == 0, stop=c == NC - 1)
                last.then_inc(out_done, 1)

        @block.scalar
        def _(act):
            link = chained(act, chain["act"])
            root(act, rstd, 2, var_ready, root_ready)
            act.wait_ge(loaded, 16 * N_LOADS)
            link(act.activation(a_neg[:], a_log[:], ACT.Exp))
            link(act.mul(a_neg[:], a_neg[:], -1.0))
            for n in range(2):
                act.wait_ge(hT_psum, 4 * (n + 1))
                act.activation(hT[:, n * HALF:(n + 1) * HALF], ps[:, n, :], ACT.Copy,
                               scale=norm_w[:, 0:1]).then_inc(hT_ready, 1)
            for e in range(2 * NC):
                for n in range(2):
                    act.wait_ge(in_done, 2 * e + n + 1)
                    bank = (4 + 2 * e + n) % 8
                    if e < NC:
                        act.activation(xi_pad[:, e, 3 + n * HALF:3 + (n + 1) * HALF], ps[:, bank, :],
                                       ACT.Copy).then_inc(xi_copied, 1)
                    else:
                        act.activation(zs[:, e - NC, n * HALF:(n + 1) * HALF], ps[:, bank, :],
                                       ACT.Silu).then_inc(z_ready, 1)
            for c in range(NC):
                act.wait_ge(conv_done, c + 1)
                act.activation(xi[:, c, :], conv[:, c, :], ACT.Silu,
                               bias=conv_b[:, c:c + 1]).then_inc(xi_ready, 1)
            act.wait_ge(bc_done, 4)
            act.activation(dt_low[:], ps[0:DR, 2:4, :].rearrange("p b n -> p (b n)"),
                           ACT.Copy).then_inc(dt_copied, 1)
            act.wait_ge(abs_ready, 1)
            link(act.activation(soft[:], soft[:], ACT.Exp))
            act.activation(soft[:], soft[:], ACT.Ln, bias=1.0).then_inc(delta_ready, 1)
            act.wait_ge(du_ready, 1)
            for s in range(NS):
                act.wait_ge(b_bcast, s + 1)
                if s >= 2:
                    act.wait_ge(drive_ready, NC * (s - 1))
                act.activation(b_all[:, s % 2, :], ps[:, 0:2, :].rearrange("p b n -> p (b n)"),
                               ACT.Copy).then_inc(b_copied, 1)
                for c in range(NC):
                    n = NC * s + c
                    if n >= 2:
                        act.wait_ge(scanned, n - 1)
                    act.activation(decay[:, c, :], delta[:, c, :], ACT.Exp,
                                   scale=a_neg[:, c, s:s + 1]).then_inc(decay_ready, 1)

        @block.gpsimd
        def _(pool):
            pool.wait_ge(du_ready, 1)
            for s in range(NS):
                pool.wait_ge(b_copied, s + 1)
                for c in range(NC):
                    n = NC * s + c
                    if n >= 2:
                        pool.wait_ge(scanned, n - 1)
                    pool.tensor_tensor(drive[:, c, :], du[:, c, :], b_all[:, s % 2, :],
                                       ALU.mult).then_inc(drive_ready, 1)



ROUND = 1.5 * 2.0 ** 23
TURN = 6.2831850
NS = 64
GROUP = 8
NG = D // GROUP
RING_Q = 4


def s4d_buffers(g, m):
    k = {n: m.sb(f"s4d_{n}", [P, D]) for n in (
        "log_dt", "a_re", "a_im", "c_re", "c_im", "dt", "ar", "ai", "turns", "tanh", "grow", "er", "ei",
        "nr", "ni", "qr", "qi", "inv", "tmp", "on_c", "on_s")}
    for n in ("angle", "rounded"):
        k[n] = m.sb(f"s4d_{n}", [P, 3, D])
    k["index"] = m.sb("s4d_index", [P, P + NT])
    k["quarter"] = m.sb("s4d_quarter", [P, 1])
    k["j_angle"], k["j_round"] = m.sb("s4d_j_angle", [P, 2, D, NT]), m.sb("s4d_j_round", [P, 2, D, NT])
    k["j_decay"], k["left"] = m.sb("s4d_j_decay", [P, D, NT]), m.sb("s4d_left", [P, D, NT])
    for n in ("i_angle", "i_decay"):
        k[n] = m.sb(f"s4d_{n}", [P, RING_Q, GROUP, P])
    k["i_round"] = m.sb("s4d_i_round", [P, GROUP, P])
    k["d_skip"] = m.sb("s4d_d_skip", [1, D])
    k["sem"] = {n: m.sem(f"s4d_{n}") for n in (
        "loaded", "dt_ready", "parts_ready", "small_ready", "small_done", "j_ready", "j_done",
        "left_ready", "i_ready", "sin_done", "grown", "decayed", "powers", "k_psum", "k_ready")}
    k["k_tok"] = g["k_tok"]
    return k


def s4d_load(sp, t, k):
    loaded = k["sem"]["loaded"]
    sp.dma_start(k["log_dt"][:], t["L1_xattn_log_dt"].unsqueeze(0).to_broadcast([P, D])).then_inc(loaded, 16)
    for n in ("a_re", "a_im", "c_re", "c_im"):
        sp.dma_start(k[n][:], t[f"s4d_{n}"]).then_inc(loaded, 16)
    sp.dma_start(k["index"][:], t["s4d_index"]).then_inc(loaded, 16)
    sp.dma_start(k["quarter"][:], t["s4d_quarter"]).then_inc(loaded, 16)
    sp.dma_start(k["d_skip"][:], t["L1_xattn_D_skip"].unsqueeze(0)).then_inc(loaded, 16)


def s4d_vector(dve, link, k):
    sem = k["sem"]

    def tt(out, x, y, op):
        link(dve.tensor_tensor(out, x, y, op))

    dve.wait_ge(sem["dt_ready"], 1)
    tt(k["ar"][:], k["dt"][:], k["a_re"][:], ALU.mult)
    tt(k["ai"][:], k["dt"][:], k["a_im"][:], ALU.mult)
    dve.tensor_scalar(k["turns"][:], k["ai"][:], 1.0 / (2.0 * np.pi), None, ALU.mult).then_inc(sem["parts_ready"], 1)
    dve.wait_ge(sem["parts_ready"], 1)
    link(dve.tensor_scalar(k["angle"][:, 0, :], k["turns"][:], 0.25, None, ALU.add))
    link(dve.tensor_scalar(k["angle"][:, 1, :], k["turns"][:], 1.0, None, ALU.mult))
    link(dve.tensor_scalar(k["angle"][:, 2, :], k["turns"][:], 0.5, None, ALU.mult))
    link(dve.tensor_scalar(k["rounded"][:], k["angle"][:], ROUND, None, ALU.add))
    link(dve.tensor_scalar(k["rounded"][:], k["rounded"][:], ROUND, None, ALU.subtract))
    dve.tensor_tensor(k["angle"][:], k["angle"][:], k["rounded"][:], ALU.subtract).then_inc(sem["small_ready"], 1)
    dve.wait_ge(sem["small_done"], 2)
    link(dve.tensor_scalar(k["tmp"][:], k["tanh"][:], -1.0, 1.0, ALU.mult, ALU.add))
    link(dve.reciprocal(k["tmp"][:], k["tmp"][:]))
    link(dve.scalar_tensor_tensor(out=k["grow"][:], in0=k["tanh"][:], scalar=2.0, in1=k["tmp"][:],
                                  op0=ALU.mult, op1=ALU.mult))
    cos_b, sin_b, sin_half = k["angle"][:, 0, :], k["angle"][:, 1, :], k["angle"][:, 2, :]
    tt(k["er"][:], k["grow"][:], cos_b, ALU.mult)
    link(dve.scalar_tensor_tensor(out=k["tmp"][:], in0=sin_half, scalar=-2.0, in1=sin_half,
                                  op0=ALU.mult, op1=ALU.mult))
    tt(k["er"][:], k["er"][:], k["tmp"][:], ALU.add)
    link(dve.scalar_tensor_tensor(out=k["ei"][:], in0=k["grow"][:], scalar=1.0, in1=sin_b,
                                  op0=ALU.add, op1=ALU.mult))
    cr, ci, re, im = k["c_re"][:], k["c_im"][:], k["a_re"][:], k["a_im"][:]
    tt(k["nr"][:], cr, k["er"][:], ALU.mult)
    tt(k["tmp"][:], ci, k["ei"][:], ALU.mult)
    tt(k["nr"][:], k["nr"][:], k["tmp"][:], ALU.subtract)
    tt(k["ni"][:], cr, k["ei"][:], ALU.mult)
    tt(k["tmp"][:], ci, k["er"][:], ALU.mult)
    tt(k["ni"][:], k["ni"][:], k["tmp"][:], ALU.add)
    tt(k["inv"][:], re, re, ALU.mult)
    tt(k["tmp"][:], im, im, ALU.mult)
    tt(k["inv"][:], k["inv"][:], k["tmp"][:], ALU.add)
    link(dve.reciprocal(k["inv"][:], k["inv"][:]))
    tt(k["qr"][:], k["nr"][:], re, ALU.mult)
    tt(k["tmp"][:], k["ni"][:], im, ALU.mult)
    tt(k["qr"][:], k["qr"][:], k["tmp"][:], ALU.add)
    tt(k["qr"][:], k["qr"][:], k["inv"][:], ALU.mult)
    tt(k["qi"][:], k["ni"][:], re, ALU.mult)
    tt(k["tmp"][:], k["nr"][:], im, ALU.mult)
    tt(k["qi"][:], k["qi"][:], k["tmp"][:], ALU.subtract)
    tt(k["qi"][:], k["qi"][:], k["inv"][:], ALU.mult)
    link(dve.tensor_scalar(k["on_c"][0:NS, :], k["qr"][0:NS, :], 2.0, None, ALU.mult))
    link(dve.tensor_scalar(k["on_s"][0:NS, :], k["qi"][0:NS, :], -2.0, None, ALU.mult))
    link(dve.tensor_scalar(k["on_c"][NS:P, :], k["qi"][NS:P, :], -2.0, None, ALU.mult))
    link(dve.tensor_scalar(k["on_s"][NS:P, :], k["qr"][NS:P, :], -2.0, None, ALU.mult))

    def over(x, n):
        return x.unsqueeze(2).to_broadcast([P, x.shape[1], n])

    j_index = k["index"][:, P:P + NT].unsqueeze(1).to_broadcast([P, D, NT])
    tt(k["j_angle"][:, 1, :, :], over(k["turns"][:], NT), j_index, ALU.mult)
    link(dve.tensor_scalar(k["j_angle"][:, 0, :, :], k["j_angle"][:, 1, :, :], 0.25, None, ALU.add))
    link(dve.tensor_scalar(k["j_round"][:], k["j_angle"][:], ROUND, None, ALU.add))
    link(dve.tensor_scalar(k["j_round"][:], k["j_round"][:], ROUND, None, ALU.subtract))
    tt(k["j_angle"][:], k["j_angle"][:], k["j_round"][:], ALU.subtract)
    dve.tensor_tensor(k["j_decay"][:], over(k["ar"][:], NT), j_index, ALU.mult).then_inc(sem["j_ready"], 1)
    dve.wait_ge(sem["j_done"], 2)
    tt(k["left"][:], k["j_angle"][:, 0, :, :], over(k["on_c"][:], NT), ALU.mult)
    tt(k["j_angle"][:, 1, :, :], k["j_angle"][:, 1, :, :], over(k["on_s"][:], NT), ALU.mult)
    tt(k["left"][:], k["left"][:], k["j_angle"][:, 1, :, :], ALU.add)
    dve.tensor_tensor(k["left"][:], k["left"][:], k["j_decay"][:], ALU.mult).then_inc(sem["left_ready"], 1)

    def power(q):
        dve.wait_ge(sem["sin_done"], q + 1)
        dve.wait_ge(sem["decayed"], q + 1)
        b = q % RING_Q
        dve.tensor_tensor(k["i_angle"][:, b], k["i_angle"][:, b], k["i_decay"][:, b],
                          ALU.mult).then_inc(sem["powers"], 1)

    i_index = k["index"][:, 0:P].unsqueeze(1).to_broadcast([P, GROUP, P])
    for q in range(NG):
        b = q % RING_Q
        group = slice(q * GROUP, (q + 1) * GROUP)
        if q >= RING_Q:
            dve.wait_ge(sem["k_psum"], q - RING_Q + 1)
        if q >= 1:
            dve.wait_ge(sem["i_ready"], q)
        tt(k["i_angle"][:, b], over(k["turns"][:, group], P), i_index, ALU.mult)
        link(dve.tensor_scalar(k["i_round"][:], k["i_angle"][:, b], k["quarter"][:, 0:1], ROUND,
                               ALU.add, ALU.add))
        link(dve.tensor_scalar(k["i_round"][:], k["i_round"][:], ROUND, None, ALU.subtract))
        dve.scalar_tensor_tensor(out=k["i_angle"][:, b], in0=k["i_angle"][:, b], scalar=k["quarter"][:, 0:1],
                                 in1=k["i_round"][:], op0=ALU.add, op1=ALU.subtract).then_inc(sem["i_ready"], 1)
        if q >= 2:
            power(q - 2)
    power(NG - 2)
    power(NG - 1)
    dve.wait_ge(sem["k_ready"], 1)
    link(dve.tensor_tensor(k["k_tok"][0:1, 0, :], k["k_tok"][0:1, 0, :], k["d_skip"][:], ALU.add))


def s4d_pool(pool, k):
    sem = k["sem"]
    pool.wait_ge(sem["parts_ready"], 1)
    i_index = k["index"][:, 0:P].unsqueeze(1).to_broadcast([P, GROUP, P])
    for q in range(NG):
        group = slice(q * GROUP, (q + 1) * GROUP)
        if q >= RING_Q:
            pool.wait_ge(sem["powers"], q - RING_Q + 1)
        pool.tensor_tensor(k["i_decay"][:, q % RING_Q], k["ar"][:, group].unsqueeze(2).to_broadcast([P, GROUP, P]),
                           i_index, ALU.mult).then_inc(sem["grown"], 1)


S4D_STEPS = 3 + NG // 2


def s4d_scalar(act, k, step):
    sem = k["sem"]
    if step == 0:
        act.wait_ge(sem["loaded"], 16 * 8)
        act.activation(k["dt"][:], k["log_dt"][:], ACT.Exp).then_inc(sem["dt_ready"], 1)
    elif step == 1:
        act.wait_ge(sem["parts_ready"], 1)
        act.activation(k["tanh"][:], k["ar"][:], ACT.Tanh, scale=0.5).then_inc(sem["small_done"], 1)
        act.wait_ge(sem["small_ready"], 1)
        act.activation(k["angle"][:], k["angle"][:], ACT.Sin, scale=TURN).then_inc(sem["small_done"], 1)
    elif step == 2:
        act.wait_ge(sem["j_ready"], 1)
        act.activation(k["j_angle"][:], k["j_angle"][:], ACT.Sin, scale=TURN).then_inc(sem["j_done"], 1)
        act.activation(k["j_decay"][:], k["j_decay"][:], ACT.Exp).then_inc(sem["j_done"], 1)
    else:
        q = 2 * (step - 3)
        for b in range(2):
            act.wait_ge(sem["i_ready"], q + b + 1)
            angle = k["i_angle"][:, (q + b) % RING_Q]
            act.activation(angle, angle, ACT.Sin, scale=TURN).then_inc(sem["sin_done"], 1)
        for b in range(2):
            act.wait_ge(sem["grown"], q + b + 1)
            decay = k["i_decay"][:, (q + b) % RING_Q]
            act.activation(decay, decay, ACT.Exp).then_inc(sem["decayed"], 1)


def s4d_copy(act, k, banks):
    act.wait_ge(k["sem"]["k_psum"], NG)
    act.activation(k["k_tok"][:], banks.rearrange("p b (d j) -> p j (b d)", j=NT),
                   ACT.Copy).then_inc(k["sem"]["k_ready"], 1)


def s4d_tensor(pe, k, banks, q):
    sem = k["sem"]
    if q == 0:
        pe.wait_ge(sem["left_ready"], 1)
    pe.wait_ge(sem["powers"], q + 1)
    for c in range(GROUP):
        d = q * GROUP + c
        last = pe.matmul(banks[:, d // 64, (d % 64) * NT:(d % 64 + 1) * NT], k["i_angle"][:, q % RING_Q, c, :],
                         k["left"][:, d, :], start=True, stop=True)
    last.then_inc(sem["k_psum"], 1)



KT = -(-S2 // P)
K_LAST = S2 - (KT - 1) * P
CHUNK = 2 * HALF
N_CHUNK = -(-S2 // CHUNK)
S4D_AT = (2, 7) + tuple(range(12, 44, 4))
S4D_PE_AT, S4D_PE_EVERY = 17, 2


def cross_attention(nc, g, t, m):
    CA = DC + 1
    ps = g["psum"]
    ctx_T = m.sb("ctx_T", [CA, S2])
    w_q = m.sb("w_q", [P, D])
    b_q = m.sb("b_q", [P, 1])
    w_k = m.sb("w_k", [P, CA])
    w_v = m.sb("w_v", [CA, D + 1])
    stats = m.sb("stats", [P, NT, 6])
    mv = m.sb("mv", [P, NT, 2])
    rstd = m.sb("rstd", [P, NT, 1])
    xn = m.sb("xn", [P, NT, D])
    xT = m.sb("xT", [P, S])
    qT = m.sb("qT", [P, S])
    qc = m.sb("qc", [CA, S])
    qc_shifted = m.sb("qc_shifted", [CA, S])
    tops = m.sb("tops", [P, NT, N_CHUNK])
    top = m.sb("top", [P, NT])
    minus_top = m.sb("minus_top", [P, NT, CA])
    prob = m.sb("prob", [P, 3, S])
    summed_c = m.sb("summed_c", [CA, S])
    share = m.sb("share", [P, NT])

    loaded, ctx_loaded, ones_set = m.sem("loaded"), m.sem("ctx_loaded"), m.sem("ones_set")
    chain_dve, chain_pool = m.sem("chain_dve"), m.sem("chain_pool")
    var_ready, root_ready, xn_ready, xT_psum, xT_ready = (
        m.sem(n) for n in ("var_ready", "root_ready", "xn_ready", "xT_psum", "xT_ready"))
    q_done, q_ready, qc_done, qc_ready, score_done, max_read, top_ready = (
        m.sem(n) for n in ("q_done", "q_ready", "qc_done", "qc_ready", "score_done", "max_read",
                           "top_ready"))
    shift_done, shift_ready, prob_psum, prob_ready, pv_done, sum_ready, out_done = (
        m.sem(n) for n in ("shift_done", "shift_ready", "prob_psum", "prob_ready", "pv_done",
                           "sum_ready", "out_done"))
    N_LOADS, N_CTX = 5, 3
    ctx = g["ctx_rows"]
    s4d = s4d_buffers(g, m)
    s4d_banks = ps[:, 4:6, :]
    s4d_steps = dict(zip(S4D_AT, range(1, S4D_STEPS)))
    s4d_products = {S4D_PE_AT + S4D_PE_EVERY * q: q for q in range(NG)}

    def chunk_cols(c):
        return range(c * CHUNK, min((c + 1) * CHUNK, S2), HALF)

    def pair(n):
        return ps[:, n:n + 2, :].rearrange("p b n -> p (b n)")

    with nc.Block() as block:
        @block.sync
        def _(sp):
            sp.dma_start(w_q[:], t["L0_xattn_Wq"]).then_inc(loaded, 16)
            sp.dma_start(b_q[:], t["L0_xattn_bq"].unsqueeze(1)).then_inc(loaded, 16)
            sp.dma_start(w_k[:, 0:DC], t["L0_Wk_T"]).then_inc(loaded, 16)
            sp.dma_start(w_k[:, DC:CA], t["L0_xattn_bk"].unsqueeze(1)).then_inc(loaded, 16)
            sp.dma_start(ctx_T[0:DC, :], t["ctx_T"]).then_inc(loaded, 16)
            full = (KT - 1) * P
            sp.dma_start(ctx[:, 0:KT - 1, 0:DC],
                         t["ctx"][0:full, :].rearrange("(k p) c -> p k c", p=P)).then_inc(ctx_loaded, 16)
            sp.dma_start(ctx[0:K_LAST, KT - 1, 0:DC], t["ctx"][full:S2, :]).then_inc(ctx_loaded, 16)
            sp.wait_ge(ones_set, 1)
            sp.dma_start(w_v[0:DC, 0:D], t["L0_xattn_Wv"]).then_inc(ctx_loaded, 16)
            sp.dma_start(w_v[DC:CA, 0:D], t["L0_xattn_bv"].unsqueeze(0)).then_inc(ctx_loaded, 16)
            s4d_load(sp, t, s4d)

        @block.gpsimd
        def _(pool):
            link = chained(pool, chain_pool)
            link(pool.memset(w_v[:], 0.0))
            link(pool.memset(w_v[DC:CA, D:D + 1], 1.0))
            link(pool.memset(ctx_T[DC:CA, :], 1.0))
            link(pool.memset(ctx[:, :, DC:CA], 1.0))
            pool.memset(minus_top[:], 0.0).then_inc(ones_set, 1)
            s4d_pool(pool, s4d)

        @block.vector
        def _(dve):
            link = chained(dve, chain_dve)
            normalise(dve, link, g["x"], stats, mv, rstd, var_ready, root_ready, xn, xn_ready)
            dve.wait_ge(ones_set, 1)
            for i in range(NT):
                for c in range(N_CHUNK):
                    n = N_CHUNK * i + c
                    dve.wait_ge(score_done, n + 1)
                    width = min(CHUNK, S2 - c * CHUNK)
                    dve.reduce_max(tops[:, i, c:c + 1], pair(2 * (n % 4))[:, 0:width],
                                   AX).then_inc(max_read, 1)
            dve.wait_ge(max_read, NT * N_CHUNK)
            link(dve.reduce_max(top[:], tops[:], AX))
            dve.tensor_scalar(minus_top[:, :, DC], top[:], -1.0, None, ALU.mult).then_inc(top_ready, 1)
            s4d_vector(dve, link, s4d)
            dve.wait_ge(pv_done, KT)
            dve.tensor_copy(summed_c[:], pair(6)[0:CA, :]).then_inc(sum_ready, 1)
            for i in range(NT):
                dve.wait_ge(out_done, i + 1)
                bank = ps[:, i % 2, :]
                link(dve.reciprocal(share[:, i:i + 1], bank[:, D:D + 1]))
                dve.scalar_tensor_tensor(out=g["x"][:, i, :], in0=bank[:, 0:D], scalar=share[:, i:i + 1],
                                         in1=g["x"][:, i, :], op0=ALU.mult, op1=ALU.add).then_inc(sum_ready, 1)

        @block.tensor
        def _(pe):
            transpose_tiles(pe, xn, g["ident"][:], ps, xn_ready, xT_psum)
            pe.wait_ge(loaded, 16 * N_LOADS)
            for n in range(2):
                pe.wait_ge(xT_ready, n + 1)
                pe.matmul(ps[:, 2 + n, :], w_q[:], xT[:, n * HALF:(n + 1) * HALF],
                          start=True, stop=True).then_inc(q_done, 1)
            for n in range(2):
                pe.wait_ge(q_ready, n + 1)
                pe.matmul(ps[0:CA, 4 + n, :], w_k[:], qT[:, n * HALF:(n + 1) * HALF],
                          start=True, stop=True).then_inc(qc_done, 1)
            pe.wait_ge(ones_set, 1)
            pe.wait_ge(qc_ready, 2)
            for i in range(NT):
                for c in range(N_CHUNK):
                    n = N_CHUNK * i + c
                    if n >= 4:
                        pe.wait_ge(max_read, n - 3)
                    for b, k in enumerate(chunk_cols(c)):
                        width = min(HALF, S2 - k)
                        last = pe.matmul(ps[:, 2 * (n % 4) + b, 0:width], qc[:, i * P:(i + 1) * P],
                                         ctx_T[:, k:k + width], start=True, stop=True)
                    last.then_inc(score_done, 1)
            pe.wait_ge(top_ready, 1)
            for n in range(2):
                pe.matmul(ps[0:CA, n, :], w_k[:], qT[:, n * HALF:(n + 1) * HALF], start=True, stop=False)
                for q in range(4):
                    last = pe.matmul(ps[0:CA, n, q * P:(q + 1) * P], minus_top[:, 4 * n + q, :],
                                     g["ident"][:], start=False, stop=q == 3)
                last.then_inc(shift_done, 1)
            pe.wait_ge(ctx_loaded, 16 * 4)

            def weighted(k):
                rows = P if k < KT - 1 else K_LAST
                pe.wait_ge(prob_ready, k + 1)
                for n in range(2):
                    last = pe.matmul(ps[0:CA, 6 + n, :], ctx[0:rows, k, :],
                                     prob[0:rows, k % 3, n * HALF:(n + 1) * HALF],
                                     start=k == 0, stop=k == KT - 1)
                last.then_inc(pv_done, 1)

            pe.wait_ge(shift_ready, 2)
            for k in range(KT):
                rows = P if k < KT - 1 else K_LAST
                if k in s4d_products:
                    s4d_tensor(pe, s4d, s4d_banks, s4d_products[k])
                if k >= 2:
                    pe.wait_ge(prob_ready, k - 1)
                for n in range(2):
                    last = pe.matmul(ps[0:rows, 2 * (k % 2) + n, :], ctx_T[:, k * P:k * P + rows],
                                     qc_shifted[:, n * HALF:(n + 1) * HALF], start=True, stop=True)
                last.then_inc(prob_psum, 1)
                if k >= 1:
                    weighted(k - 1)
            weighted(KT - 1)
            pe.wait_ge(sum_ready, 1)
            for i in range(NT):
                if i >= 2:
                    pe.wait_ge(sum_ready, i)
                pe.matmul(ps[:, i % 2, 0:D + 1], summed_c[:, i * P:(i + 1) * P], w_v[:],
                          start=True, stop=True).then_inc(out_done, 1)

        @block.scalar
        def _(act):
            root(act, rstd, 1, var_ready, root_ready)
            act.wait_ge(loaded, 16 * N_LOADS)
            for n in range(2):
                act.wait_ge(xT_psum, 4 * (n + 1))
                act.activation(xT[:, n * HALF:(n + 1) * HALF], ps[:, n, :], ACT.Copy).then_inc(xT_ready, 1)
            for n in range(2):
                act.wait_ge(q_done, n + 1)
                act.activation(qT[:, n * HALF:(n + 1) * HALF], ps[:, 2 + n, :], ACT.Identity,
                               bias=b_q[:, 0:1]).then_inc(q_ready, 1)
            for n in range(2):
                act.wait_ge(qc_done, n + 1)
                act.activation(qc[:, n * HALF:(n + 1) * HALF], ps[0:CA, 4 + n, :],
                               ACT.Copy).then_inc(qc_ready, 1)
            s4d_scalar(act, s4d, 0)
            for n in range(2):
                act.wait_ge(shift_done, n + 1)
                act.activation(qc_shifted[:, n * HALF:(n + 1) * HALF], ps[0:CA, n, :],
                               ACT.Copy).then_inc(shift_ready, 1)
            for k in range(KT):
                rows = P if k < KT - 1 else K_LAST
                if k in s4d_steps:
                    s4d_scalar(act, s4d, s4d_steps[k])
                act.wait_ge(prob_psum, k + 1)
                if k >= 3:
                    act.wait_ge(pv_done, k - 2)
                act.activation(prob[0:rows, k % 3, :], pair(2 * (k % 2))[0:rows, :],
                               ACT.Exp).then_inc(prob_ready, 1)
            s4d_copy(act, s4d, s4d_banks)



def threshold_experts(nc, g, t, m):
    NE = 8
    THRESHOLD = 0.1
    ps = g["psum"]
    w_e = m.sb("w_e", [P, NE, D])
    b_e = m.sb("b_e", [1, NE * D])
    w_g = m.sb("w_g", [P, NE])
    b_g = m.sb("b_g", [1, NE])
    stats = m.sb("stats", [P, NT, 6])
    mv = m.sb("mv", [P, NT, 2])
    rstd = m.sb("rstd", [P, NT, 1])
    xn = m.sb("xn", [P, NT, D])
    xT = m.sb("xT", [P, S])
    gates = m.sb("gates", [P, NT, NE])
    kept = m.sb("kept", [P, NT, NE])
    best = m.sb("best", [P, NT])
    total = m.sb("total", [P, NT])
    none = m.sb("none", [P, NT])
    scaled = m.sb("scaled", [P, 2, NE, D])
    mixed = m.sb("mixed", [P, 2, D])

    loaded, chain_dve = m.sem("loaded"), m.sem("chain_dve")
    var_ready, root_ready, xn_ready, xT_psum, xT_ready = (
        m.sem(n) for n in ("var_ready", "root_ready", "xn_ready", "xT_psum", "xT_ready"))
    gate_done, shifted, exp_ready, expert_done, scaled_ready = (
        m.sem(n) for n in ("gate_done", "shifted", "exp_ready", "expert_done", "scaled_ready"))
    N_LOADS = 4

    def spread(v):
        return v.unsqueeze(2).to_broadcast([P, NT, NE])

    with nc.Block() as block:
        @block.sync
        def _(sp):
            sp.dma_start(w_e[:], t["L0_ffn_expert_w"].rearrange("e p d -> p e d")).then_inc(loaded, 16)
            sp.dma_start(b_e[:], t["L0_ffn_expert_b"].rearrange("e d -> (e d)").unsqueeze(0)).then_inc(loaded, 16)
            sp.dma_start(w_g[:], t["L0_ffn_gate_w"]).then_inc(loaded, 16)
            sp.dma_start(b_g[:], t["L0_ffn_gate_b"].unsqueeze(0)).then_inc(loaded, 16)

        @block.vector
        def _(dve):
            link = chained(dve, chain_dve)
            normalise(dve, link, g["x"], stats, mv, rstd, var_ready, root_ready, xn, xn_ready)
            dve.wait_ge(gate_done, 1)
            logits = ps[:, 6, 0:NT * NE].rearrange("p (i e) -> p i e", e=NE)
            link(dve.reduce_max(best[:], logits, AX))
            dve.tensor_tensor(gates[:], logits, spread(best[:]), ALU.subtract).then_inc(shifted, 1)
            dve.wait_ge(exp_ready, 1)
            link(dve.reduce_sum(total[:], gates[:], AX))
            link(dve.reciprocal(total[:], total[:]))
            link(dve.tensor_tensor(gates[:], gates[:], spread(total[:]), ALU.mult))
            link(dve.scalar_tensor_tensor(out=kept[:], in0=gates[:], scalar=THRESHOLD, in1=gates[:],
                                          op0=ALU.is_ge, op1=ALU.mult))
            link(dve.reduce_sum(total[:], kept[:], AX))
            link(dve.tensor_scalar(none[:], total[:], 0.0, None, ALU.is_equal))
            link(dve.tensor_tensor(total[:], total[:], none[:], ALU.add))
            link(dve.reciprocal(total[:], total[:]))
            link(dve.tensor_tensor(kept[:], kept[:], spread(total[:]), ALU.mult))
            for i in range(NT):
                dve.wait_ge(expert_done, i + 1)
                b = 2 * (i % 3)
                out = ps[:, b:b + 2, :].rearrange("p b (e d) -> p (b e) d", d=D)
                dve.tensor_tensor(scaled[:, i % 2, :, :], out,
                                  kept[:, i, :].unsqueeze(2).to_broadcast([P, NE, D]),
                                  ALU.mult).then_inc(scaled_ready, 1)
                dve.wait_ge(scaled_ready, i + 1)
                link(dve.reduce_sum(mixed[:, i % 2, :], scaled[:, i % 2, :, :].rearrange("p e d -> p d e"), AX))
                link(dve.tensor_tensor(g["x"][:, i, :], g["x"][:, i, :], mixed[:, i % 2, :], ALU.add))

        @block.tensor
        def _(pe):
            transpose_tiles(pe, xn, g["ident"][:], ps, xn_ready, xT_psum)
            pe.wait_ge(loaded, 16 * N_LOADS)
            for i in range(NT):
                pe.wait_ge(xT_ready, i // 4 + 1)
                cols = slice(i * NE, (i + 1) * NE)
                pe.matmul(ps[:, 6, cols], xT[:, i * P:(i + 1) * P], w_g[:], start=True, stop=False)
                last = pe.matmul(ps[:, 6, cols], g["ones"][:, 0:P], b_g[:], start=False, stop=True)
            last.then_inc(gate_done, 1)
            for i in range(NT):
                if i >= 3:
                    pe.wait_ge(scaled_ready, i - 2)
                for h in range(2):
                    bank = ps[:, 2 * (i % 3) + h, :]
                    pe.matmul(bank, xT[:, i * P:(i + 1) * P],
                              w_e[:, 4 * h:4 * h + 4, :].rearrange("p e d -> p (e d)"), start=True, stop=False)
                    last = pe.matmul(bank, g["ones"][:, 0:P], b_e[:, h * HALF:(h + 1) * HALF],
                                     start=False, stop=True)
                last.then_inc(expert_done, 1)

        @block.scalar
        def _(act):
            root(act, rstd, 1, var_ready, root_ready)
            for n in range(2):
                act.wait_ge(xT_psum, 4 * (n + 1))
                act.activation(xT[:, n * HALF:(n + 1) * HALF], ps[:, n, :], ACT.Copy).then_inc(xT_ready, 1)
            act.wait_ge(shifted, 1)
            act.activation(gates[:], gates[:], ACT.Exp).then_inc(exp_ready, 1)



def causal_attention(nc, g, t, m):
    SCALE = float(D) ** -0.5
    ps = g["psum"]
    w = m.sb("w", [P, 3, D])
    tri_f = m.sb("tri_f", [P, P])
    stats = m.sb("stats", [P, NT, 6])
    mv = m.sb("mv", [P, NT, 2])
    rstd = m.sb("rstd", [P, NT, 1])
    xn = m.sb("xn", [P, NT, D])
    xT = m.sb("xT", [P, S])
    qT = m.sb("qT", [P, S])
    kT = m.sb("kT", [P, S])
    v = m.sb("v", [P, NT, D])
    penalty = m.sb("penalty", [P, S])
    score = m.sb("score", [P, 2, S])
    low = m.sb("low", [P, NT])
    total = m.sb("total", [P, NT])
    share = m.sb("share", [P, NT])
    pT = m.sb("pT", [P, 2, S])

    loaded, chain_dve = m.sem("loaded"), m.sem("chain_dve")
    var_ready, root_ready, xn_ready, xT_psum, xT_ready = (
        m.sem(n) for n in ("var_ready", "root_ready", "xn_ready", "xT_psum", "xT_ready"))
    qkv_done, qkv_ready, score_done, low_ready, exp_ready, pT_psum, pT_ready, out_done, added = (
        m.sem(n) for n in ("qkv_done", "qkv_ready", "score_done", "low_ready", "exp_ready",
                           "pT_psum", "pT_ready", "out_done", "added"))
    N_LOADS = 4

    def wide(b, n):
        return ps[:, b:b + 2, :].rearrange("p b n -> p (b n)")[:, 0:n]

    with nc.Block() as block:
        @block.sync
        def _(sp):
            for k, name in enumerate(("L1_WQ_T", "L1_WK_T", "L1_WV_T")):
                sp.dma_start(w[:, k, :], t[name]).then_inc(loaded, 16)
            sp.dma_start(tri_f[:], t["above_diagonal"]).then_inc(loaded, 16)

        @block.vector
        def _(dve):
            link = chained(dve, chain_dve)
            normalise(dve, link, g["x"], stats, mv, rstd, var_ready, root_ready, xn, xn_ready)
            def finish(i):
                dve.wait_ge(exp_ready, i + 1)
                link(dve.reciprocal(share[:, i:i + 1], total[:, i:i + 1]))
                dve.wait_ge(out_done, i + 1)
                dve.scalar_tensor_tensor(out=g["x"][:, i, :], in0=ps[:, 6 + i % 2, 0:D],
                                         scalar=share[:, i:i + 1], in1=g["x"][:, i, :],
                                         op0=ALU.mult, op1=ALU.add).then_inc(added, 1)

            for i in range(NT):
                n = (i + 1) * P
                b = 2 * (i % 2)
                dve.wait_ge(score_done, i + 1)
                link(dve.tensor_scalar(penalty[:, 0:n], wide(b, n), 0.0, NEG, ALU.is_equal, ALU.mult))
                if i >= 2:
                    dve.wait_ge(pT_psum, i - 1)
                link(dve.tensor_tensor(score[:, i % 2, 0:n], wide(b, n), penalty[:, 0:n], ALU.add))
                link(dve.reduce_max(low[:, i:i + 1], score[:, i % 2, 0:n], AX))
                dve.tensor_scalar(low[:, i:i + 1], low[:, i:i + 1], -SCALE, None,
                                  ALU.mult).then_inc(low_ready, 1)
                if i >= 1:
                    finish(i - 1)
            finish(NT - 1)

        @block.tensor
        def _(pe):
            transpose_tiles(pe, xn, g["ident"][:], ps, xn_ready, xT_psum)
            pe.wait_ge(loaded, 16 * N_LOADS)
            pe.wait_ge(xT_ready, 2)
            for k in range(2):
                for n in range(2):
                    last = pe.matmul(ps[:, 2 + 2 * k + n, :], w[:, k, :], xT[:, n * HALF:(n + 1) * HALF],
                                     start=True, stop=True)
                last.then_inc(qkv_done, 1)
            for i in range(NT):
                last = pe.matmul(ps[:, 6 + i // 4, (i % 4) * D:(i % 4 + 1) * D], xT[:, i * P:(i + 1) * P],
                                 w[:, 2, :], start=True, stop=True)
            last.then_inc(qkv_done, 1)

            def scores(i):
                n = (i + 1) * P
                if i >= 2:
                    pe.wait_ge(low_ready, i - 1)
                for k in range(0, n, HALF):
                    width = min(HALF, n - k)
                    bank = 2 * (i % 2) + k // HALF
                    last = pe.matmul(ps[:, bank, 0:width], qT[:, i * P:(i + 1) * P], kT[:, k:k + width],
                                     start=True, stop=k + width < n)
                a = (i % 4) * P
                pe.matmul(ps[:, bank, a:a + P], g["ident"][:], tri_f[:], start=False,
                          stop=True).then_inc(score_done, 1)

            def values(i):
                n = i + 1
                pe.wait_ge(exp_ready, i + 1)
                if i >= 1:
                    pe.wait_ge(pT_ready, i)
                for k in range(n):
                    last = pe.transpose(ps[:, 4 + k // 4, (k % 4) * P:(k % 4 + 1) * P],
                                        score[:, i % 2, k * P:(k + 1) * P], g["ident"][:])
                last.then_inc(pT_psum, 1)
                if i >= 2:
                    pe.wait_ge(added, i - 1)
                pe.wait_ge(pT_ready, i + 1)
                for k in range(n):
                    last = pe.matmul(ps[:, 6 + i % 2, 0:D], pT[:, i % 2, k * P:(k + 1) * P], v[:, k, :],
                                     start=k == 0, stop=k == n - 1)
                last.then_inc(out_done, 1)

            pe.wait_ge(qkv_ready, 3)
            scores(0)
            for i in range(1, NT):
                scores(i)
                values(i - 1)
            values(NT - 1)

        @block.scalar
        def _(act):
            root(act, rstd, 1, var_ready, root_ready)
            for n in range(2):
                act.wait_ge(xT_psum, 4 * (n + 1))
                act.activation(xT[:, n * HALF:(n + 1) * HALF], ps[:, n, :], ACT.Copy).then_inc(xT_ready, 1)
            for k, dst in enumerate((qT[:], kT[:], v[:].rearrange("p i d -> p (i d)"))):
                act.wait_ge(qkv_done, k + 1)
                act.activation(dst, wide(2 + 2 * k, S), ACT.Copy).then_inc(qkv_ready, 1)

            def exps(i):
                n = (i + 1) * P
                act.wait_ge(low_ready, i + 1)
                act.activation(score[:, i % 2, 0:n], score[:, i % 2, 0:n], ACT.Exp, scale=SCALE,
                               bias=low[:, i:i + 1], accum_out=total[:, i:i + 1]).then_inc(exp_ready, 1)

            def copy_out(i):
                n = (i + 1) * P
                act.wait_ge(pT_psum, i + 1)
                if i >= 2:
                    act.wait_ge(out_done, i - 1)
                act.activation(pT[:, i % 2, 0:n], wide(4, n), ACT.Copy).then_inc(pT_ready, 1)

            exps(0)
            for i in range(1, NT):
                exps(i)
                copy_out(i - 1)
            copy_out(NT - 1)



NH, DH = 4, 32
TOP = 32
MASKED = 2.0 ** 50
GONE = -3e38
UNITS = [(c, min(CHUNK, S2 - c)) for c in range(0, S2, CHUNK)]


def segments(width):
    n = -(-width // 171)
    edges = [round(k * width / n) for k in range(n + 1)]
    return list(zip(edges[:-1], edges[1:]))


PIECES = [(c, min(HALF, S2 - c)) for c in range(0, S2, HALF)]
N_SEG = sum(len(segments(w)) for _, w in PIECES)


def film_context(nc, g, t, m):
    a = {"qa": m.sb("qa", [P, NT, NH, P], BF16), "qb": m.sb("qb", [P, NT, NH, P], BF16),
         "ka": m.sb("ka", [P, NH, S2], BF16), "kb": m.sb("kb", [P, NH, S2], BF16),
         "top": m.sb("top", [P, NT * NH, TOP]), "flags": m.sb("flags", [P, NT * NH]),
         "count": m.sb("count", [1, NT * NH + 1], mybir.dt.int32)}
    for part in (split_heads, search_and_weigh, search_general, weigh_again):
        with ExitStack() as ctx:
            part(nc, g, t, Memory(nc, ctx, part.__name__), a)


def split_heads(nc, g, t, m, a):
    ps = g["psum"]
    qa, qb, ka, kb = a["qa"], a["qb"], a["ka"], a["kb"]
    ROW = 3 * DH
    RING = 3
    w_q = m.sb("w_q", [P, NH, P])
    w_k = m.sb("w_k", [DC, NH, P])
    ctx_T = m.sb("ctx_T", [DC, RING, CHUNK])
    MR = 4
    mask = m.sb("mask", [MR, S2 // MR], U8)
    masking = m.sb("masking", [MR, S2 // MR], BF16)
    stats = m.sb("stats", [P, NT, 6])
    mv = m.sb("mv", [P, NT, 2])
    rstd = m.sb("rstd", [P, NT, 1])
    xT = m.sb("xT", [P, S])
    q = m.sb("q", [P, S])
    hi = m.sb("hi", [P, S], BF16)
    mid = m.sb("mid", [P, S], BF16)
    rest = m.sb("rest", [P, 2, S])
    k_mid = m.sb("k_mid", [2 * DH, 2, S], BF16)

    loaded, mask_loaded = m.sem("loaded"), m.sem("mask_loaded")
    masking_ready, masked = m.sem("masking_ready"), m.sem("masked")
    ctx_loaded = [m.sem(f"ctx_loaded_{r}") for r in range(RING)]
    chain_dve, chain_pool = m.sem("chain_dve"), m.sem("chain_pool")
    var_ready, root_ready, xn_ready, xT_psum, xT_ready = (
        m.sem(n) for n in ("var_ready", "root_ready", "xn_ready", "xT_psum", "xT_ready"))
    q_done, q_ready, q_split, k_done, k_hi, k_rest, k_mids, k_low = (
        m.sem(n) for n in ("q_done", "q_ready", "q_split", "k_done", "k_hi", "k_rest", "k_mids", "k_low"))
    xn = g["xn"]

    def pair(n):
        return ps[:, 2 * n:2 * n + 2, :].rearrange("p b n -> p (b n)")

    units = [(h, c, w) for c, w in UNITS for h in range(NH)]
    with nc.Block() as block:
        @block.sync
        def _(sp):
            def load_context(which):
                for u in which:
                    c, w = UNITS[u]
                    if u >= RING:
                        sp.wait_ge(k_done, NH * (u - RING + 1))
                    sp.dma_start(ctx_T[:, u % RING, 0:w], t["ctx_T"][:, c:c + w]
                                 ).then_inc(ctx_loaded[u % RING], 16)

            sp.dma_start(w_q[:], t["L1_Wq_rep"].rearrange("p (h c) -> p h c", c=P)).then_inc(loaded, 16)
            sp.dma_start(w_k[:], t["L1_Wk_rep"].rearrange("p (h c) -> p h c", c=P)).then_inc(loaded, 16)
            sp.dma_start(mask[:], t["vision_mask"].rearrange("o (r c) -> (o r) c", r=MR)).then_inc(mask_loaded, 16)
            load_context(range(RING))
            sp.wait_ge(masking_ready, 1)
            for h in range(NH):
                for r in range(MR):
                    cols = slice(r * (S2 // MR), (r + 1) * (S2 // MR))
                    sp.dma_start(kb[ROW:ROW + 1, h, cols], masking[r:r + 1, :]).then_inc(masked, 16)
            load_context(range(RING, len(UNITS)))
            sp.wait_ge(masked, 16 * NH * MR)

        @block.vector
        def _(dve):
            link = chained(dve, chain_dve)
            normalise(dve, link, g["x"], stats, mv, rstd, var_ready, root_ready, xn, xn_ready)
            for h in range(NH):
                dve.wait_ge(q_ready, h + 1)
                link(dve.tensor_copy(hi[:], q[:]))
                link(dve.tensor_tensor(rest[:, 0, :], q[:], hi[:], ALU.subtract))
                link(dve.tensor_copy(mid[:], rest[:, 0, :]))

                def rows(x):
                    return x.rearrange("p (i c) -> p i c", c=P)

                for k, src in enumerate((hi, mid, hi, mid)):
                    part = slice(k * DH, (k + 1) * DH)
                    dve.tensor_copy(qa[part, :, h, :], rows(src[part, :]))
                for k, src in enumerate((hi, mid)):
                    part = slice(k * DH, (k + 1) * DH)
                    dve.tensor_copy(qb[part, :, h, :], rows(src[part, :]))
                part = slice(2 * DH, 3 * DH)
                last = dve.tensor_tensor(qb[part, :, h, :], rows(rest[part, 0, :]), rows(mid[part, :]),
                                         ALU.subtract)
                link(last)
                dve.engine_nop().then_inc(q_split, 1)
            for n, (h, c, w) in enumerate(units):
                dve.wait_ge(k_hi, 2 * (n + 1))
                if n >= 2:
                    dve.wait_ge(k_low, n - 1)
                dve.tensor_tensor(rest[:, n % 2, 0:w], pair(n % 4)[:, 0:w], ka[:, h, c:c + w],
                                  ALU.subtract).then_inc(k_rest, 1)
                dve.wait_ge(k_rest, n + 1)
                dve.tensor_copy(k_mid[:, n % 2, 0:w], rest[0:2 * DH, n % 2, 0:w])
                dve.tensor_copy(ka[2 * DH:P, h, c:c + w], rest[2 * DH:P, n % 2, 0:w]).then_inc(k_mids, 1)

        @block.tensor
        def _(pe):
            transpose_tiles(pe, xn, g["ident"][:], ps, xn_ready, xT_psum)
            pe.wait_ge(loaded, 32)
            pe.wait_ge(xT_ready, 2)
            for h in range(NH):
                if h >= 2:
                    pe.wait_ge(q_ready, h - 1)
                for n in range(2):
                    last = pe.matmul(ps[:, 4 + 2 * (h % 2) + n, :], w_q[:, h, :],
                                     xT[:, n * HALF:(n + 1) * HALF], start=True, stop=True)
                last.then_inc(q_done, 1)
            pe.wait_ge(q_ready, NH)
            for n, (h, c, w) in enumerate(units):
                u = n // NH
                pe.wait_ge(ctx_loaded[u % RING], 16 * (u // RING + 1))
                if n >= 4:
                    pe.wait_ge(k_rest, n - 3)
                for b in range(0, w, HALF):
                    cols = min(HALF, w - b)
                    last = pe.matmul(ps[:, 2 * (n % 4) + b // HALF, 0:cols], w_k[:, h, :],
                                     ctx_T[:, u % RING, b:b + cols], start=True, stop=True)
                last.then_inc(k_done, 1)

        @block.scalar
        def _(act):
            root(act, rstd, 1, var_ready, root_ready)
            for n in range(2):
                act.wait_ge(xT_psum, 4 * (n + 1))
                act.activation(xT[:, n * HALF:(n + 1) * HALF], ps[:, n, :], ACT.Copy).then_inc(xT_ready, 1)
            for h in range(NH):
                act.wait_ge(q_done, h + 1)
                if h >= 1:
                    act.wait_ge(q_split, h)
                act.activation(q[:], pair(2 + h % 2), ACT.Copy,
                               scale=float(DH) ** -0.5).then_inc(q_ready, 1)
            part = slice(2 * DH, 3 * DH)
            for n, (h, c, w) in enumerate(units):
                act.wait_ge(k_done, n + 1)
                act.activation(ka[:, h, c:c + w], pair(n % 4)[:, 0:w], ACT.Copy).then_inc(k_hi, 1)
                act.activation(kb[part, h, c:c + w], pair(n % 4)[part, 0:w], ACT.Copy).then_inc(k_hi, 1)

        @block.gpsimd
        def _(pool):
            link = chained(pool, chain_pool)
            pool.wait_ge(mask_loaded, 16)
            pool.tensor_scalar(masking[:], mask[:], 1.0, MASKED, ALU.subtract,
                               ALU.mult).then_inc(masking_ready, 1)
            link(pool.memset(qb[ROW:ROW + 1, :, :, :], 1.0))
            for n, (h, c, w) in enumerate(units):
                pool.wait_ge(k_mids, n + 1)
                pool.tensor_tensor(kb[0:2 * DH, h, c:c + w], rest[0:2 * DH, n % 2, 0:w],
                                   k_mid[:, n % 2, 0:w], ALU.subtract).then_inc(k_low, 1)


def score_unit(pe, a, ps, bank, tile, h, c, w):
    ROWS = 3 * DH + 1
    for b in range(0, w, HALF):
        cols = min(HALF, w - b)
        out = ps[:, bank + b // HALF, 0:cols]
        pe.matmul(out, a["qa"][:, tile, h, :], a["ka"][:, h, c + b:c + b + cols], start=True, stop=False)
        last = pe.matmul(out, a["qb"][0:ROWS, tile, h, :], a["kb"][0:ROWS, h, c + b:c + b + cols],
                         start=False, stop=True)
    return last


def search_general(nc, g, t, m, a):
    ps = g["psum"]
    full = m.sb("full", [P, S2])
    best = m.sb("best", [P, TOP])
    column = m.sb("column", [P, 1])
    count = a["count"]
    in_all = m.sb("in_all", [1, 1])
    ones_set, counted, count_ready, score_done, copied, chain_dve, passed, passed_pe = (
        m.sem(n) for n in ("ones_set", "counted", "count_ready", "score_done", "copied", "chain_dve",
                           "passed", "passed_pe"))
    NU = len(UNITS)

    with nc.Block() as block:
        @block.tensor
        def _(pe):
            pe.wait_ge(ones_set, 1)
            pe.matmul(ps[0:1, 7, 0:NT * NH], column[:], a["flags"][:], start=True,
                      stop=True).then_inc(counted, 1)
            pe.wait_ge(count_ready, 1)
            any_flagged = pe.value_load(count[0:1, NT * NH:NT * NH + 1])
            with pe.If(any_flagged > 0):
                with pe.Fori(0, NT) as i:
                    for h in range(NH):
                        flagged = pe.value_load(count[0:1, bass.ds(i * NH + h, 1)])
                        base = i * NH * NU + h * NU
                        with pe.If(flagged > 0):
                            for u, (c, w) in enumerate(UNITS):
                                bank = 2 * (u % 2)
                                wait_in_loop(pe, copied, base + 1 + max(u - 1, 0), passed_pe)
                                score_unit(pe, a, ps, bank, i, h, c, w).then_inc(score_done, 1)
                        with pe.Else():
                            pe.sem_inc(score_done, NU)

        @block.vector
        def _(dve):
            dve.memset(column[:], 1.0).then_inc(ones_set, 1)
            dve.wait_ge(counted, 1)
            dve.tensor_copy(count[:, 0:NT * NH], ps[0:1, 7, 0:NT * NH]).then_inc(copied, 1)
            dve.reduce_sum(in_all[:], ps[0:1, 7, 0:NT * NH], AX).then_inc(copied, 1)
            dve.wait_ge(copied, 2)
            dve.sem_clear(copied)
            dve.tensor_copy(count[:, NT * NH:], in_all[:]).then_inc(count_ready, 1)
            dve.wait_ge(count_ready, 1)
            dve.engine_nop().then_inc(copied, 1)
            any_flagged = dve.value_load(count[0:1, NT * NH:NT * NH + 1])
            with dve.If(any_flagged > 0):
                with dve.Fori(0, NT) as i:
                    for h in range(NH):
                        flagged = dve.value_load(count[0:1, bass.ds(i * NH + h, 1)])
                        units = i * NH * NU + h * NU
                        with dve.If(flagged > 0):
                            for u, (c, w) in enumerate(UNITS):
                                bank = 2 * (u % 2)
                                wait_in_loop(dve, score_done, units + u + 1, passed)
                                dve.tensor_copy(full[:, c:c + w],
                                                ps[:, bank:bank + 2, :].rearrange("p b n -> p (b n)")[:, 0:w]
                                                ).then_inc(copied, 1)
                            wait_in_loop(dve, copied, units + NU + 1, passed)
                            dve.sem_clear(chain_dve)
                            link = chained(dve, chain_dve)
                            for r in range(TOP // 8):
                                eight = best[:, 8 * r:8 * r + 8]
                                link(dve.max(eight, full[:]))
                                if r < TOP // 8 - 1:
                                    link(dve.match_replace(full[:], eight, full[:], GONE))
                            link(dve.tensor_copy(a["top"][:, bass.ds(i * NH + h, 1), :], best[:].unsqueeze(1)))
                        with dve.Else():
                            dve.sem_inc(copied, NU)


def search_and_weigh(nc, g, t, m, a):
    weigh_program(nc, g, t, m, a, True)


def weigh_again(nc, g, t, m, a):
    weigh_program(nc, g, t, m, a, False)


def weigh_program(nc, g, t, m, a, searching):
    ps = g["psum"]
    NCH = len(PIECES)
    STEPS = NT * NCH
    LAG = NCH + 1 if searching else 1
    SEARCH_BANKS = WEIGH_BANKS = 3
    RING = 3
    MASK_LAG = 2
    TURN_LAG, CONTEXT_LAG = 2, 3
    kept = m.sb("kept", [P, 2, N_SEG, 8])
    eighth = m.sb("eighth", [P, 2])
    shifted = m.sb("shifted", [P, NH, TOP])
    total = m.sb("total", [P, NH])
    bias, least = m.sb("bias", [P, 2, NH]), m.sb("least", [P, 2, NH])
    e = m.sb("e", [P, RING, NH, HALF])
    mean = m.sb("mean", [P, RING, HALF])
    mean_T = m.sb("mean_T", [P, 2, HALF])
    mask8, mask = m.sb("mask8", [P, NT], U8), m.sb("mask", [P, NT])
    w_v = m.sb("w_v", [DC, D])
    c_tok, c_ctx = m.sb("c_tok", [P, NT, DC]), m.sb("c_ctx", [DC, S])
    loaded, chain_dve, chain_pool = m.sem("loaded"), m.sem("chain_dve"), m.sem("chain_pool")
    search_done, searched, found, flagged, exp_done, summed, ln_done, bias_ready, least_ready, mask_ready = (
        m.sem(n) for n in ("search_done", "searched", "found", "flagged", "exp_done", "summed", "ln_done",
                           "bias_ready", "least_ready", "mask_ready"))
    score_done, e_ready, w_ready, mean_ready, mT_psum, mT_ready, pv_done = (
        m.sem(n) for n in ("score_done", "e_ready", "w_ready", "mean_ready", "mT_psum", "mT_ready",
                           "pv_done"))
    tok_ready, cc_psum, cc_ready, c_done = (
        m.sem(n) for n in ("tok_ready", "cc_psum", "cc_ready", "c_done"))

    def tiles(w):
        return [(b, min(P, w - b)) for b in range(0, w, P)]

    def search_piece(r):
        if not searching or r >= STEPS * NH:
            return None
        i, s = divmod(r, NH * NCH)
        return i, s // NCH, s % NCH

    def limits_tile(G):
        i, u = divmod(G - LAG + 1, NCH)
        return i if u == 0 and 0 <= i < NT else None

    def vector(dve):
        link = chained(dve, chain_dve)

        def take_largest(i, h):
            j, k = i * NH + h, h % 2
            all_kept = kept[:, k, :, :].rearrange("p s e -> p (s e)")
            link(dve.reduce_max(eighth[:, k:k + 1], kept[:, k, :, 7], AX))
            for r in range(TOP // 8):
                eight = a["top"][:, j, 8 * r:8 * r + 8]
                link(dve.max(eight, all_kept))
                if r < TOP // 8 - 1:
                    link(dve.match_replace(all_kept, eight, all_kept, GONE))
            dve.tensor_tensor(a["flags"][:, j:j + 1], eighth[:, k:k + 1], a["top"][:, j, TOP - 1:TOP],
                              ALU.is_gt).then_inc(flagged, 1)

        dve.wait_ge(loaded, 32)
        dve.tensor_copy(mask[:], mask8[:]).then_inc(mask_ready, 1)
        for G in range(STEPS + LAG + 1):
            for sub in range(NH):
                r = NH * G + sub
                if search_piece(r):
                    i, h, u = search_piece(r)
                    dve.wait_ge(search_done, r + 1)
                    first = sum(len(segments(w)) for _, w in PIECES[:u])
                    bank = ps[:, r % SEARCH_BANKS, :]
                    for s, (lo, hi) in enumerate(segments(PIECES[u][1])):
                        last = dve.max(kept[:, h % 2, first + s, :], bank[:, lo:hi])
                    last.then_inc(searched, 1)
                    if u == NCH - 1:
                        dve.wait_ge(searched, r + 1)
                        take_largest(i, h)
                i = limits_tile(G)
                if i is not None:
                    top = a["top"][:, i * NH:(i + 1) * NH, :]
                    if sub == 0:
                        dve.tensor_tensor(shifted[:], top, top[:, :, 0:1].to_broadcast([P, NH, TOP]),
                                          ALU.subtract).then_inc(found, 1)
                    elif sub == 1:
                        dve.wait_ge(exp_done, i + 1)
                        dve.reduce_sum(total[:], shifted[:], AX).then_inc(summed, 1)
                    elif sub == 3:
                        b = bias[:, i % 2, :]
                        dve.wait_ge(ln_done, i + 1)
                        link(dve.tensor_tensor(b, total[:], top[:, :, 0], ALU.add))
                        link(dve.tensor_scalar(b, b, -1.0, None, ALU.mult))
                        dve.tensor_tensor(least[:, i % 2, :], top[:, :, TOP - 1], b,
                                          ALU.add).then_inc(bias_ready, 1)
                n, h = divmod(NH * (G - LAG) + sub - MASK_LAG, NH)
                if 0 <= n < STEPS:
                    i, u = divmod(n, NCH)
                    w = e[:, n % RING, h, 0:PIECES[u][1]]
                    if u == 0 and h == 0:
                        dve.wait_ge(least_ready, i + 1)
                    dve.wait_ge(e_ready, NH * n + h + 1)
                    dve.scalar_tensor_tensor(out=w, in0=w, scalar=least[:, i % 2, h:h + 1], in1=w,
                                             op0=ALU.is_ge, op1=ALU.mult).then_inc(w_ready, 1)
        if searching:
            dve.wait_ge(flagged, NT * NH)

    def pool_sums(pool):
        link = chained(pool, chain_pool)
        for n in range(STEPS):
            i, u = divmod(n, NCH)
            width = PIECES[u][1]
            w = [e[:, n % RING, h, 0:width] for h in range(NH)]
            out = mean[:, n % RING, 0:width]
            pool.wait_ge(w_ready, NH * n + 2)
            if n >= RING:
                pool.wait_ge(mT_psum, n - RING + 1)
            link(pool.tensor_tensor(out, w[0], w[1], ALU.add))
            pool.wait_ge(w_ready, NH * (n + 1))
            link(pool.tensor_tensor(w[2], w[2], w[3], ALU.add))
            pool.tensor_tensor(out, out, w[2], ALU.add).then_inc(mean_ready, 1)

    def tensor(pe):
        ctx = g["ctx_rows"]

        def turn(n):
            pe.wait_ge(mean_ready, n + 1)
            if n >= 1:
                pe.wait_ge(mT_ready, n)
            for b, r in tiles(PIECES[n % NCH][1]):
                last = pe.transpose(ps[0:r, 6, b:b + P], mean[:, n % RING, b:b + r], g["ident"][:])
            last.then_inc(mT_psum, 1)

        def add_context(n):
            i, u = divmod(n, NCH)
            c, wd = PIECES[u]
            pe.wait_ge(mT_ready, n + 1)
            if u == 0 and i >= 1:
                pe.wait_ge(tok_ready, i)
            for b, r in tiles(wd):
                last = pe.matmul(ps[:, 7, 0:DC], mean_T[0:r, n % 2, b:b + P],
                                 ctx[0:r, (c + b) // P, 0:DC], start=c + b == 0, stop=c + b + r == S2)
            last.then_inc(pv_done, 1)

        for G in range(STEPS + LAG + CONTEXT_LAG):
            n = G - LAG
            for sub in range(NH):
                r = NH * G + sub
                if search_piece(r):
                    i, h, u = search_piece(r)
                    if r >= SEARCH_BANKS:
                        pe.wait_ge(searched, r - SEARCH_BANKS + 1)
                    score_unit(pe, a, ps, r % SEARCH_BANKS, i, h, *PIECES[u]).then_inc(search_done, 1)
                if 0 <= n < STEPS:
                    q = NH * n + sub
                    if q >= WEIGH_BANKS:
                        pe.wait_ge(e_ready, q - WEIGH_BANKS + 1)
                    score_unit(pe, a, ps, SEARCH_BANKS + q % WEIGH_BANKS, n // NCH, sub,
                               *PIECES[n % NCH]).then_inc(score_done, 1)
                if sub == 1 and 0 <= n - TURN_LAG < STEPS:
                    turn(n - TURN_LAG)
                if sub == 3 and 0 <= n - CONTEXT_LAG < STEPS:
                    add_context(n - CONTEXT_LAG)
        pe.wait_ge(tok_ready, NT)
        for i in range(NT):
            last = pe.transpose(ps[0:DC, i // 4, (i % 4) * P:(i % 4 + 1) * P], c_tok[:, i, :],
                                g["ident"][:])
        last.then_inc(cc_psum, 1)
        pe.wait_ge(cc_ready, 1)
        pe.wait_ge(loaded, 32)
        for n in range(2):
            pe.matmul(ps[:, 2 + n, :], w_v[:], c_ctx[:, n * HALF:(n + 1) * HALF],
                      start=True, stop=True).then_inc(c_done, 1)

    def scalar(act):
        def copy_mean(n):
            wd = PIECES[n % NCH][1]
            act.wait_ge(mT_psum, n + 1)
            if n >= 2:
                act.wait_ge(pv_done, n - 1)
            full = wd // P * P
            last = act.activation(mean_T[:, n % 2, 0:full], ps[:, 6, 0:full], ACT.Copy)
            if wd > full:
                last = act.activation(mean_T[0:wd - full, n % 2, full:full + P],
                                      ps[0:wd - full, 6, full:full + P], ACT.Copy)
            last.then_inc(mT_ready, 1)

        for G in range(STEPS + LAG + CONTEXT_LAG + 1):
            n = G - LAG
            i, u = divmod(n - CONTEXT_LAG, NCH)
            if u == 0 and 1 <= i <= NT:
                if i == 1:
                    act.wait_ge(mask_ready, 1)
                act.wait_ge(pv_done, NCH * i)
                act.activation(c_tok[:, i - 1, :], ps[:, 7, 0:DC], ACT.Copy,
                               scale=mask[:, i - 1:i]).then_inc(tok_ready, 1)
            for sub in range(NH):
                if 0 <= n < STEPS:
                    i, u = divmod(n, NCH)
                    if sub == 0 and n >= RING:
                        act.wait_ge(mean_ready, n - RING + 1)
                    if sub == 0 and u == 0:
                        act.wait_ge(bias_ready, i + 1)
                    q = NH * n + sub
                    act.wait_ge(score_done, q + 1)
                    act.activation(e[:, n % RING, sub, 0:PIECES[u][1]],
                                   ps[:, SEARCH_BANKS + q % WEIGH_BANKS, 0:PIECES[u][1]], ACT.Exp,
                                   bias=bias[:, i % 2, sub:sub + 1]).then_inc(e_ready, 1)
                i = limits_tile(G)
                if i is not None and sub == 0:
                    act.wait_ge(found, i + 1)
                    act.activation(shifted[:], shifted[:], ACT.Exp).then_inc(exp_done, 1)
                elif i is not None and sub == 2:
                    act.wait_ge(summed, i + 1)
                    act.activation(total[:], total[:], ACT.Ln, scale=float(NH)).then_inc(ln_done, 1)
                elif i is not None and sub == 3:
                    act.wait_ge(bias_ready, i + 1)
                    act.activation(least[:, i % 2, :], least[:, i % 2, :], ACT.Exp).then_inc(least_ready, 1)
                if sub == 2 and 0 <= n - TURN_LAG < STEPS:
                    copy_mean(n - TURN_LAG)
        act.wait_ge(cc_psum, 1)
        act.activation(c_ctx[:], ps[0:DC, 0:2, :].rearrange("p b n -> p (b n)"),
                       ACT.Copy).then_inc(cc_ready, 1)
        for n in range(2):
            act.wait_ge(c_done, n + 1)
            act.activation(g["c_T"][:, n * HALF:(n + 1) * HALF], ps[:, 2 + n, :], ACT.Copy)

    def where_needed(eng, program):
        if searching:
            program(eng)
        else:
            any_flagged = eng.value_load(a["count"][0:1, NT * NH:NT * NH + 1])
            with eng.If(any_flagged > 0):
                program(eng)

    with nc.Block() as block:
        @block.sync
        def _(sp):
            sp.dma_start(mask8[:], t["text_mask"].rearrange("(i p) -> p i", p=P),
                         allow_slow_non_contiguous=True).then_inc(loaded, 16)
            sp.dma_start(w_v[:], t["L1_xattn_Wv"]).then_inc(loaded, 16)
            sp.wait_ge(loaded, 32)

        @block.vector
        def _(dve):
            where_needed(dve, vector)

        @block.gpsimd
        def _(pool):
            where_needed(pool, pool_sums)

        @block.tensor
        def _(pe):
            where_needed(pe, tensor)

        @block.scalar
        def _(act):
            where_needed(act, scalar)





NF = 2 * S


def film_s4d_ffn(nc, g, t, m):
    a = {"dft": m.sb("dft", [P, NT, NF]), "k_tok": g["k_tok"],
         "u": m.sb("u", [P, NT, D]), "y": m.sb("y", [P, NT, D]), "dft_loaded": [m.sem(f"dft_loaded_{j}") for j in range(NT)],
         "gate": m.sb("gate", [P, 1])}
    for part in (film_in, convolve, film_out_ffn):
        with ExitStack() as ctx:
            part(nc, g, t, Memory(nc, ctx, part.__name__), a)


def broadcast_row(name, t):
    return t[name].unsqueeze(0).to_broadcast([P, D])


def film(pe, g, w_f, b_f, ps, done):
    for i in range(NT):
        out = ps[:, i // 2, (i % 2) * 2 * D:(i % 2 + 1) * 2 * D]
        pe.matmul(out, g["c_T"][:, i * P:(i + 1) * P], w_f[:], start=True, stop=False)
        last = pe.matmul(out, g["ones"][:, 0:P], b_f[:], start=False, stop=True)
    last.then_inc(done, 1)


def film_apply(dve, link, ps, gate, x, scale, out):
    film_psum = ps[:, 0:4, :].rearrange("p b (i s d) -> p (b i) s d", s=2, d=D)
    link(dve.tensor_scalar(scale[:], film_psum[:, :, 0, :], gate[:, 0:1], 1.0, ALU.mult, ALU.add))
    link(dve.tensor_tensor(out, x, scale[:], ALU.mult))
    return dve.scalar_tensor_tensor(out=out, in0=film_psum[:, :, 1, :], scalar=gate[:, 0:1], in1=out,
                                    op0=ALU.mult, op1=ALU.add)


def film_in(nc, g, t, m, a):
    ps = g["psum"]
    gain, shift = m.sb("gain", [P, D]), m.sb("shift", [P, D])
    w_f, b_f = m.sb("w_f", [P, 2 * D]), m.sb("b_f", [1, 2 * D])
    stats = m.sb("stats", [P, NT, 6])
    mv = m.sb("mv", [P, NT, 2])
    rstd = m.sb("rstd", [P, NT, 1])
    scale = m.sb("scale", [P, NT, D])
    loaded, chain_dve, var_ready, root_ready, normed, film_done = (
        m.sem(n) for n in ("loaded", "chain_dve", "var_ready", "root_ready", "normed", "film_done"))
    N_LOADS = 5

    def tiles(v):
        return v.unsqueeze(1).to_broadcast([P, NT, D])

    with nc.Block() as block:
        @block.sync
        def _(sp):
            sp.dma_start(gain[:], broadcast_row("L1_xattn_g_norm_in", t)).then_inc(loaded, 16)
            sp.dma_start(shift[:], broadcast_row("L1_xattn_b_norm_in", t)).then_inc(loaded, 16)
            sp.dma_start(w_f[:], t["L1_xattn_W_film_in"]).then_inc(loaded, 16)
            sp.dma_start(b_f[:], t["L1_xattn_b_film_in"].unsqueeze(0)).then_inc(loaded, 16)
            sp.dma_start(a["gate"][:], t["mod_gate"].to_broadcast([P, 1])).then_inc(loaded, 16)
            for j in range(NT):
                sp.dma_start(a["dft"][:, j, :], t["dft"][j * P:(j + 1) * P, :]).then_inc(a["dft_loaded"][j], 16)

        @block.vector
        def _(dve):
            link = chained(dve, chain_dve)
            u = a["u"]
            normalise(dve, link, g["xn"], stats, mv, rstd, var_ready, root_ready, u, normed)
            dve.wait_ge(normed, NT)
            dve.wait_ge(loaded, 16 * N_LOADS)
            link(dve.tensor_tensor(u[:], u[:], tiles(gain[:]), ALU.mult))
            link(dve.tensor_tensor(u[:], u[:], tiles(shift[:]), ALU.add))
            dve.wait_ge(film_done, 1)
            link(film_apply(dve, link, ps, a["gate"], u[:], scale, u[:]))

        @block.scalar
        def _(act):
            root(act, rstd, 1, var_ready, root_ready)

        @block.tensor
        def _(pe):
            pe.wait_ge(loaded, 16 * N_LOADS)
            film(pe, g, w_f, b_f, ps, film_done)


def convolve(nc, g, t, m, a):
    ps = g["psum"]
    dft = a["dft"]
    kf = m.sb("kf", [P, NF])
    yf = m.sb("yf", [P, NF])
    cross = m.sb("cross", [P, S])
    ends = m.sb("ends", [P, 2])
    yt = m.sb("yt", [P, NF // P, D])
    sign = m.sb("sign", [1, S])
    sign_loaded, kf_done, kf_ready, uf_done, yf_ready, yt_psum, yt_ready, patched, y_done, chain_dve = (
        m.sem(n) for n in ("sign_loaded", "kf_done", "kf_ready", "uf_done", "yf_ready", "yt_psum",
                           "yt_ready", "patched", "y_done", "chain_dve"))

    def banks(b, n):
        return ps[:, b:b + n, :].rearrange("p b n -> p (b n)")

    with nc.Block() as block:
        @block.sync
        def _(sp):
            sp.dma_start(sign[:], t["alternating"]).then_inc(sign_loaded, 16)

        @block.tensor
        def _(pe):
            for src, first, done in ((a["k_tok"], 0, kf_done), (a["u"], 4, uf_done)):
                for n in range(4):
                    for j in range(NT):
                        if done is kf_done and n == 0:
                            pe.wait_ge(a["dft_loaded"][j], 16)
                        last = pe.matmul(ps[:, first + n, :], src[:, j, :], dft[:, j, n * HALF:(n + 1) * HALF],
                                         start=j == 0, stop=j == NT - 1)
                    last.then_inc(done, 1)
            for f in range(NF // P):
                pe.wait_ge(yf_ready, 1)
                pe.wait_ge(kf_ready, 4)
                pe.transpose(ps[:, f // 4, (f % 4) * P:(f % 4 + 1) * P], yf[:, f * P:(f + 1) * P],
                             g["ident"][:]).then_inc(yt_psum, 1)
            pe.wait_ge(patched, 1)
            pe.wait_ge(yt_ready, 4)
            for b in range(NT):
                for f in range(NF // P):
                    cols = (f // NT) * S + b * P
                    last = pe.matmul(ps[:, 4 + b // 4, (b % 4) * D:(b % 4 + 1) * D],
                                     dft[:, f % NT, cols:cols + P], yt[:, f, :],
                                     start=f == 0, stop=f == NF // P - 1)
            last.then_inc(y_done, 1)

        @block.scalar
        def _(act):
            for n in range(4):
                act.wait_ge(kf_done, n + 1)
                act.activation(kf[:, n * HALF:(n + 1) * HALF], ps[:, n, :], ACT.Copy,
                               scale=2.0 / NF).then_inc(kf_ready, 1)
            for n in range(4):
                act.wait_ge(yt_psum, 4 * (n + 1))
                act.activation(yt[:, 4 * n:4 * n + 4, :], ps[:, n, :].rearrange("p (f d) -> p f d", d=D),
                               ACT.Copy).then_inc(yt_ready, 1)
            act.wait_ge(y_done, 1)
            act.activation(a["y"][:], banks(4, 2).rearrange("p (i d) -> p i d", d=D), ACT.Copy)

        @block.vector
        def _(dve):
            link = chained(dve, chain_dve)
            dve.wait_ge(kf_ready, 4)
            dve.wait_ge(uf_done, 4)
            ur, ui, kr, ki = banks(4, 2), banks(6, 2), kf[:, 0:S], kf[:, S:NF]
            link(dve.scalar_tensor_tensor(out=ends[:], in0=banks(4, 4)[:, 0:NF:S], scalar=0.5,
                                          in1=kf[:, 0:NF:S], op0=ALU.mult, op1=ALU.mult))
            link(dve.tensor_tensor(yf[:, 0:S], ur, kr, ALU.mult))
            link(dve.tensor_tensor(cross[:], ui, ki, ALU.mult))
            link(dve.tensor_tensor(yf[:, 0:S], yf[:, 0:S], cross[:], ALU.subtract))
            link(dve.tensor_tensor(yf[:, S:NF], ur, ki, ALU.mult))
            link(dve.tensor_tensor(cross[:], ui, kr, ALU.mult))
            link(dve.tensor_tensor(yf[:, S:NF], yf[:, S:NF], cross[:], ALU.add))
            dve.tensor_copy(yf[:, 0:NF:S], ends[:]).then_inc(yf_ready, 1)
            link(dve.memset(dft[:, :, S:S + 1], 0.0))
            dve.wait_ge(sign_loaded, 16)
            dve.tensor_copy(dft[0:1, 0, S:NF], sign[:]).then_inc(patched, 1)


def film_out_ffn(nc, g, t, m, a):
    HID = 4 * D
    NH_ = HID // P
    ps = g["psum"]
    w_f, b_f = m.sb("w_f", [P, 2 * D]), m.sb("b_f", [1, 2 * D])
    w1, b1 = m.sb("w1", [P, HID]), m.sb("b1", [P, NH_])
    w2, b2 = m.sb("w2", [P, NH_, D]), m.sb("b2", [1, D])
    g_ffn, b_ffn = m.sb("g_ffn", [P, 1]), m.sb("b_ffn", [P, 1])
    gain, shift = m.sb("gain", [P, D]), m.sb("shift", [P, D])
    scale = m.sb("scale", [P, NT, D])
    xt = m.sb("xt", [P, NT, D])
    h = m.sb("h", [P, NT, D])
    hT = m.sb("hT", [P, S])
    act_T = m.sb("act_T", [P, NH_, S])
    norm = [{n: m.sb(f"{n}{k}", s) for n, s in (("stats", [P, NT, 6]), ("mv", [P, NT, 2]), ("rstd", [P, NT, 1]))}
            for k in range(2)]
    var_ready = [m.sem(f"var_ready{k}") for k in range(2)]
    root_ready = [m.sem(f"root_ready{k}") for k in range(2)]
    loaded, chain_dve, film_done, h_ready, hT_psum, hT_ready, u_done, act_ready, out_done, normed = (
        m.sem(n) for n in ("loaded", "chain_dve", "film_done", "h_ready", "hT_psum", "hT_ready",
                           "u_done", "act_ready", "out_done", "normed"))
    N_LOADS = 10

    def tiles(v):
        return v.unsqueeze(1).to_broadcast([P, NT, D])

    with nc.Block() as block:
        @block.sync
        def _(sp):
            for dst, src in ((w_f[:], t["L1_xattn_W_film_out"]),
                             (b_f[:], t["L1_xattn_b_film_out"].unsqueeze(0)),
                             (w1[:], t["L1_xattn_W1"]),
                             (b1[:], t["L1_b1_T"]),
                             (w2[:], t["L1_xattn_W2"].rearrange("(q p) d -> p q d", p=P)),
                             (b2[:], t["L1_xattn_b2"].unsqueeze(0)),
                             (g_ffn[:], t["L1_xattn_g_ffn"].unsqueeze(1)),
                             (b_ffn[:], t["L1_xattn_b_ffn"].unsqueeze(1)),
                             (gain[:], broadcast_row("L1_xattn_g_norm_out", t)),
                             (shift[:], broadcast_row("L1_xattn_b_norm_out", t))):
                sp.dma_start(dst, src).then_inc(loaded, 16)

        @block.vector
        def _(dve):
            link = chained(dve, chain_dve)
            dve.wait_ge(film_done, 1)
            link(film_apply(dve, link, ps, a["gate"], a["y"][:], scale, xt[:]))
            link(dve.tensor_tensor(xt[:], xt[:], g["xn"][:], ALU.add))
            normalise(dve, link, xt, norm[0]["stats"], norm[0]["mv"], norm[0]["rstd"], var_ready[0],
                      root_ready[0], h, h_ready)
            dve.wait_ge(out_done, 1)
            link(dve.tensor_tensor(xt[:], xt[:], ps[:, 4:6, :].rearrange("p b (i d) -> p (b i) d", d=D),
                                   ALU.add))
            normalise(dve, link, xt, norm[1]["stats"], norm[1]["mv"], norm[1]["rstd"], var_ready[1],
                      root_ready[1], h, normed)
            dve.wait_ge(normed, NT)
            link(dve.tensor_tensor(h[:], h[:], tiles(gain[:]), ALU.mult))
            link(dve.tensor_tensor(h[:], h[:], tiles(shift[:]), ALU.add))
            link(dve.tensor_tensor(g["x"][:], g["x"][:], h[:], ALU.add))

        @block.scalar
        def _(act):
            root(act, norm[0]["rstd"], 1, var_ready[0], root_ready[0])
            act.wait_ge(loaded, 16 * N_LOADS)
            for n in range(2):
                act.wait_ge(hT_psum, 4 * (n + 1))
                act.activation(hT[:, n * HALF:(n + 1) * HALF], ps[:, n, :], ACT.Identity,
                               scale=g_ffn[:, 0:1], bias=b_ffn[:, 0:1]).then_inc(hT_ready, 1)
            for q in range(NH_):
                act.wait_ge(u_done, q + 1)
                b = 2 * ((q + 1) % 4)
                act.activation(act_T[:, q, :], ps[:, b:b + 2, :].rearrange("p b n -> p (b n)"),
                               ACT.Gelu, bias=b1[:, q:q + 1]).then_inc(act_ready, 1)
            root(act, norm[1]["rstd"], 1, var_ready[1], root_ready[1])

        @block.tensor
        def _(pe):
            pe.wait_ge(loaded, 16 * N_LOADS)
            film(pe, g, w_f, b_f, ps, film_done)
            transpose_tiles(pe, h, g["ident"][:], ps, h_ready, hT_psum)
            pe.wait_ge(hT_ready, 2)
            for q in range(NH_):
                for n in range(2):
                    last = pe.matmul(ps[:, 2 * ((q + 1) % 4) + n, :], w1[:, q * P:(q + 1) * P],
                                     hT[:, n * HALF:(n + 1) * HALF], start=True, stop=True)
                last.then_inc(u_done, 1)
            pe.wait_ge(act_ready, NH_)
            for i in range(NT):
                out = ps[:, 4 + i // 4, (i % 4) * D:(i % 4 + 1) * D]
                for q in range(NH_):
                    pe.matmul(out, act_T[:, q, i * P:(i + 1) * P], w2[:, q, :], start=q == 0, stop=False)
                last = pe.matmul(out, g["ones"][:, 0:P], b2[:], start=False, stop=True)
            last.then_inc(out_done, 1)



HQ, HKV, HD = 16, 4, 8
HQK = HQ + HKV
PARTS9 = 9 * HD
SPLIT = PARTS9 + 3
OUT = HD + 1


def gqa_experts(nc, g, t, m):
    a = {"xn": m.sb("xn", [P, NT, D]), "stack": m.sb("stack", [P, HQ // 4, S])}
    with ExitStack() as ctx:
        mm = Memory(nc, ctx, "gqa")
        a["split"] = mm.sb("split", [P, NT, HQK, SPLIT], BF16)
        a["v"] = mm.sb("v", [P, NT, HKV, OUT])
        with ExitStack() as inner:
            gqa_project(nc, g, t, Memory(nc, inner, "gqa_project"), a)
        with ExitStack() as inner:
            gqa_attend(nc, g, t, Memory(nc, inner, "gqa_attend"), a)
    with ExitStack() as ctx:
        gqa_output(nc, g, t, Memory(nc, ctx, "gqa_output"), a)
    recycle(nc, Memory.used)
    with ExitStack() as ctx:
        top_expert(nc, g, t, Memory(nc, ctx, "top_expert"), a)


def gqa_project(nc, g, t, m, a):
    ps = g["psum"]
    WQKV = (HQ + 2 * HKV) * HD
    w, bias = m.sb("w", [P, WQKV]), m.sb("bias", [1, WQKV])
    ln_w = m.sb("ln_w", [P, 1])
    cos, sin = m.sb("cos", [P, NT, HD // 2]), m.sb("sin", [P, NT, HD // 2])
    qn_w, kn_w = m.sb("qn_w", [P, HD]), m.sb("kn_w", [P, HD])
    stats, mv, rstd = m.sb("stats", [P, NT, 6]), m.sb("mv", [P, NT, 2]), m.sb("rstd", [P, NT, 2])
    h, hT = m.sb("h", [P, NT, D]), m.sb("hT", [P, S])
    qkv = m.sb("qkv", [P, NT, HQ + 2 * HKV, HD])
    turned = m.sb("turned", [P, NT, HQK, HD])
    half = m.sb("half", [P, NT, HQK, HD // 2])
    square = m.sb("square", [P, NT * HQK, HD])
    scale = m.sb("scale", [P, NT * HQK])
    eps = m.sb("eps", [P, 1])
    part = m.sb("part", [P, 3, NT, HQK, HD], BF16)
    rest = m.sb("rest", [P, NT, HQK, HD])

    loaded, chain_dve, var_ready, root_ready, h_ready, hT_psum, hT_ready = (
        m.sem(n) for n in ("loaded", "chain_dve", "var_ready", "root_ready", "h_ready", "hT_psum", "hT_ready"))
    qkv_done, qkv_ready, square_ready, scale_ready, parts_ready, stacked = (
        m.sem(n) for n in ("qkv_done", "qkv_ready", "square_ready", "scale_ready", "parts_ready", "stacked"))
    N_LOADS = 7

    with nc.Block() as block:
        @block.sync
        def _(sp):
            for dst, src in ((w[:], t["L1_Wqkv"]), (bias[:], t["L1_bqkv"]),
                             (ln_w[:], t["L1_ffn_ln1_w"].unsqueeze(1)),
                             (cos[:], t["rope_cos"].rearrange("(i p) c -> p i c", p=P)),
                             (sin[:], t["rope_sin"].rearrange("(i p) c -> p i c", p=P)),
                             (qn_w[:], t["L1_ffn_qn_w"].unsqueeze(0).to_broadcast([P, HD])),
                             (kn_w[:], t["L1_ffn_kn_w"].unsqueeze(0).to_broadcast([P, HD]))):
                sp.dma_start(dst, src).then_inc(loaded, 16)

        @block.vector
        def _(dve):
            link = chained(dve, chain_dve)
            link(dve.memset(eps[:], 1e-6))
            normalise(dve, link, g["x"], stats, mv, rstd, var_ready, root_ready, a["xn"], h_ready,
                      1e-6, h)
            dve.wait_ge(qkv_ready, 4)
            HH = HD // 2
            x1, x2 = qkv[:, :, 0:HQK, 0:HH], qkv[:, :, 0:HQK, HH:HD]
            c = cos[:].unsqueeze(2).to_broadcast([P, NT, HQK, HH])
            s = sin[:].unsqueeze(2).to_broadcast([P, NT, HQK, HH])
            for out, one, two, op in ((turned[:, :, :, 0:HH], (x1, c), (x2, s), ALU.subtract),
                                      (turned[:, :, :, HH:HD], (x1, s), (x2, c), ALU.add)):
                link(dve.tensor_tensor(out, *one, ALU.mult))
                link(dve.tensor_tensor(half[:], *two, ALU.mult))
                link(dve.tensor_tensor(out, out, half[:], op))
            flat = turned[:].rearrange("p i h c -> p (i h) c")
            link(dve.tensor_tensor(square[:], flat, flat, ALU.mult))
            dve.reduce_sum(scale[:], square[:], AX).then_inc(square_ready, 1)
            dve.wait_ge(scale_ready, 1)
            link(dve.reciprocal(scale[:], scale[:]))
            link(dve.tensor_tensor(flat, flat, scale[:].unsqueeze(2).to_broadcast([P, NT * HQK, HD]), ALU.mult))
            for w_n, lo, hi in ((qn_w, 0, HQ), (kn_w, HQ, HQK)):
                v = turned[:, :, lo:hi, :]
                link(dve.tensor_tensor(v, v, w_n[:].unsqueeze(1).unsqueeze(1).to_broadcast(
                    [P, NT, hi - lo, HD]), ALU.mult))
            link(dve.tensor_copy(part[:, 0], turned[:]))
            link(dve.tensor_tensor(rest[:], turned[:], part[:, 0], ALU.subtract))
            link(dve.tensor_copy(part[:, 1], rest[:]))
            dve.tensor_tensor(part[:, 2], rest[:], part[:, 1], ALU.subtract).then_inc(parts_ready, 1)
            dve.wait_ge(parts_ready, 1)
            for n in range(9):
                cols = slice(n * HD, (n + 1) * HD)
                dve.tensor_copy(a["split"][:, :, HQ:HQK, cols], part[:, n % 3, :, HQ:HQK, :])
                last = dve.tensor_copy(a["split"][:, :, 0:HQ, cols], part[:, n // 3, :, 0:HQ, :])
            last.then_inc(stacked, 1)
            dve.wait_ge(stacked, 1)

        @block.gpsimd
        def _(pool):
            link = chained(pool, m.sem("chain_pool"))
            link(pool.memset(a["split"][:, :, HQ:HQK, PARTS9:SPLIT], 1.0))
            link(pool.memset(a["v"][:, :, :, HD:OUT], 1.0))
            link(pool.memset(a["stack"][:], 0.0))

        @block.scalar
        def _(act):
            root(act, rstd, 2, var_ready, root_ready)
            act.wait_ge(loaded, 16 * N_LOADS)
            for n in range(2):
                act.wait_ge(hT_psum, 4 * (n + 1))
                act.activation(hT[:, n * HALF:(n + 1) * HALF], ps[:, n, :], ACT.Copy,
                               scale=ln_w[:, 0:1]).then_inc(hT_ready, 1)
            for n in range(4):
                act.wait_ge(qkv_done, 2 * (n + 1))
                act.activation(qkv[:, 2 * n:2 * n + 2, :, :],
                               ps[:, 4 + n, 0:2 * WQKV].rearrange("p (i h c) -> p i h c", i=2, c=HD),
                               ACT.Copy).then_inc(qkv_ready, 1)
            act.wait_ge(qkv_ready, 4)
            act.activation(a["v"][:, :, :, 0:HD], qkv[:, :, HQK:, :], ACT.Copy)
            act.wait_ge(square_ready, 1)
            act.activation(scale[:], scale[:], ACT.Sqrt, scale=1.0 / HD, bias=eps[:, 0:1]).then_inc(scale_ready, 1)

        @block.tensor
        def _(pe):
            transpose_tiles(pe, h, g["ident"][:], ps, h_ready, hT_psum)
            pe.wait_ge(loaded, 16 * N_LOADS)
            for i in range(NT):
                pe.wait_ge(hT_ready, i // 4 + 1)
                out = ps[:, 4 + i // 2, (i % 2) * WQKV:(i % 2 + 1) * WQKV]
                pe.matmul(out, hT[:, i * P:(i + 1) * P], w[:], start=True, stop=False)
                pe.matmul(out, g["ones"][:, 0:P], bias[:], start=False, stop=True).then_inc(qkv_done, 1)


def gqa_attend(nc, g, t, m, a):
    SCALE = float(HD) ** -0.5
    ps = g["psum"]
    split = a["split"]
    ident = m.sb("ident", [P, P], BF16)
    above, below = m.sb("above", [P, P], BF16), m.sb("below", [P, P], BF16)
    masks_f = m.sb("masks_f", [P, 2, P])
    kT = m.sb("kT", [SPLIT, HKV, S], BF16)
    qT = m.sb("qT", [SPLIT, 2, S], BF16)
    sT = m.sb("sT", [SPLIT, 2, S], BF16)
    low = m.sb("low", [P, 2, NT])
    rest = m.sb("rest", [P, 2, NT])
    prob = m.sb("prob", [P, 2, NT, S])

    loaded, consts, chain_dve = m.sem("loaded"), m.sem("consts"), m.sem("chain_dve")
    k_psum, k_ready, q_psum, q_ready, score_done, max_read, shift_ready, s_psum, s_ready = (
        m.sem(n) for n in ("k_psum", "k_ready", "q_psum", "q_ready", "score_done", "max_read",
                           "shift_ready", "s_psum", "s_ready"))
    prob_psum, prob_ready, pv_done, o_ready = (
        m.sem(n) for n in ("prob_psum", "prob_ready", "pv_done", "o_ready"))

    def pair(n, cols):
        return ps[:, n:n + 2, :].rearrange("p b n -> p (b n)")[:, 0:cols]

    turned_bank = ps[0:SPLIT, 6, :].bitcast(BF16)

    def out_quadrant(h, half):
        q = 32 * (2 * (h % 2) + half)
        return ps[q:q + OUT, 7, :]

    Q_TURN, S_TURN, EXP_LAG, OUT_LAG = 5, NT + 2, NT + 3, NT + 5
    STEPS = HQ * NT + OUT_LAG

    with nc.Block() as block:
        @block.sync
        def _(sp):
            sp.dma_start(masks_f[:, 0, :], t["above_diagonal"]).then_inc(loaded, 16)
            sp.dma_start(masks_f[:, 1, :], t["below_diagonal"]).then_inc(loaded, 16)

        @block.tensor
        def _(pe):
            pe.wait_ge(consts, 3)

            def turn(head, rows, done):
                for i in range(NT):
                    last = pe.transpose(turned_bank[0:rows, i * P:(i + 1) * P], split[:, i, head, 0:rows],
                                        ident[:])
                last.then_inc(done, 1)

            def maxima(h, i):
                n = NT * h + i
                b = 2 * (n % 2)
                if i == 0:
                    pe.wait_ge(q_ready, h + 1)
                if n >= 2:
                    pe.wait_ge(max_read, n - 1)
                width = (i + 1) * P
                for k in range(0, width, HALF):
                    w = min(HALF, width - k)
                    pe.matmul(ps[:, b + k // HALF, 0:w], qT[0:PARTS9, h % 2, i * P:(i + 1) * P],
                              kT[0:PARTS9, h // (HQ // HKV), k:k + w], start=True, stop=k + w < width)
                col = (i % 4) * P
                pe.matmul(ps[:, b + i // 4, col:col + P], ident[:], above[:], start=False,
                          stop=True).then_inc(score_done, 1)

            def exponentials(h, k):
                n = NT * h + k
                if k == 0:
                    pe.wait_ge(s_ready, h + 1)
                if n >= 1:
                    pe.wait_ge(prob_ready, n)
                width = S - k * P
                for q in range(0, width, HALF):
                    w = min(HALF, width - q)
                    last = pe.matmul(ps[:, 4 + q // HALF, 0:w], kT[:, h // (HQ // HKV), k * P:(k + 1) * P],
                                     sT[:, h % 2, k * P + q:k * P + q + w], start=True, stop=q > 0)
                    if q == 0:
                        last = pe.matmul(ps[:, 4, 0:P], ident[:], below[:], start=False, stop=True)
                last.then_inc(prob_psum, 1)

            def outputs(h, k):
                pe.wait_ge(prob_ready, NT * h + k + 1)
                if k == 0 and h >= 2:
                    pe.wait_ge(o_ready, 2 * (h - 1))
                for half in range(2):
                    lo, hi = max(k * P, half * HALF), (half + 1) * HALF
                    if lo < hi:
                        last = pe.matmul(out_quadrant(h, half)[:, lo - half * HALF:HALF],
                                         a["v"][:, k, h // (HQ // HKV), :],
                                         prob[:, h % 2, k, lo - k * P:hi - k * P],
                                         start=k == 0, stop=hi == (k + 1) * P,
                                         tile_position=(0, 32 * (2 * (h % 2) + half)))
                if k == NT - 1:
                    last.then_inc(pv_done, 1)

            for k in range(HKV):
                if k >= 1:
                    pe.wait_ge(k_ready, k)
                turn(HQ + k, SPLIT, k_psum)
            pe.wait_ge(k_ready, HKV)
            turn(0, PARTS9, q_psum)
            for step in range(STEPS):
                h, k = divmod(step, NT)
                if k == Q_TURN and h + 1 < HQ:
                    pe.wait_ge(q_ready, 1) if h == 0 else pe.wait_ge(s_ready, h)
                    turn(h + 1, PARTS9, q_psum)
                h, k = divmod(step - S_TURN, NT)
                if k == 0 and 0 <= h < HQ:
                    pe.wait_ge(q_ready, min(h + 2, HQ))
                    pe.wait_ge(shift_ready, h + 1)
                    turn(h, SPLIT, s_psum)
                h, k = divmod(step, NT)
                if h < HQ:
                    maxima(h, k)
                h, k = divmod(step - EXP_LAG, NT)
                if 0 <= h < HQ:
                    exponentials(h, k)
                h, k = divmod(step - OUT_LAG, NT)
                if 0 <= h < HQ:
                    outputs(h, k)

        @block.vector
        def _(dve):
            link = chained(dve, chain_dve)
            dve.wait_ge(loaded, 32)
            dve.tensor_copy(ident[:], g["ident"][:]).then_inc(consts, 1)
            dve.tensor_copy(above[:], masks_f[:, 0, :]).then_inc(consts, 1)
            dve.tensor_copy(below[:], masks_f[:, 1, :]).then_inc(consts, 1)
            for step in range(STEPS + 1):
                h, k = divmod(step - OUT_LAG - NT, NT)
                if k == 0 and 0 <= h < HQ:
                    dve.wait_ge(pv_done, h + 1)
                    for half in range(2):
                        dve.tensor_copy(a["stack"][32 * (h % 4):32 * (h % 4) + OUT, h // 4,
                                                   half * HALF:(half + 1) * HALF],
                                        out_quadrant(h, half)).then_inc(o_ready, 1)
                h, i = divmod(step, NT)
                if h < HQ:
                    b = h % 2
                    dve.wait_ge(score_done, step + 1)
                    dve.tensor_reduce(low[:, b, i:i + 1], pair(2 * (step % 2), (i + 1) * P), AX, ALU.max,
                                      negate=True).then_inc(max_read, 1)
                    if i == NT - 1:
                        dve.wait_ge(max_read, NT * (h + 1))
                        parts = split[:, :, h, PARTS9:SPLIT]
                        link(dve.tensor_copy(parts[:, :, 0], low[:, b, :]))
                        link(dve.tensor_tensor(rest[:, b, :], low[:, b, :], parts[:, :, 0], ALU.subtract))
                        link(dve.tensor_copy(parts[:, :, 1], rest[:, b, :]))
                        dve.tensor_tensor(parts[:, :, 2], rest[:, b, :], parts[:, :, 1],
                                          ALU.subtract).then_inc(shift_ready, 1)

        @block.scalar
        def _(act):
            for k in range(HKV):
                act.wait_ge(k_psum, k + 1)
                act.activation(kT[:, k, :], turned_bank, ACT.Copy).then_inc(k_ready, 1)

            def copy_queries(h):
                act.wait_ge(q_psum, h + 1)
                act.activation(qT[0:PARTS9, h % 2, :], turned_bank[0:PARTS9, :], ACT.Copy).then_inc(q_ready, 1)

            copy_queries(0)
            for step in range(STEPS):
                h, k = divmod(step, NT)
                if k == Q_TURN and h + 1 < HQ:
                    copy_queries(h + 1)
                h, k = divmod(step - S_TURN, NT)
                if k == 0 and 0 <= h < HQ:
                    act.wait_ge(s_psum, h + 1)
                    act.activation(sT[:, h % 2, :], turned_bank, ACT.Copy).then_inc(s_ready, 1)
                h, k = divmod(step - EXP_LAG, NT)
                if 0 <= h < HQ:
                    act.wait_ge(prob_psum, NT * h + k + 1)
                    if h >= 2 and k == 0:
                        act.wait_ge(pv_done, h - 1)
                    act.activation(prob[:, h % 2, k, 0:S - k * P], pair(4, S - k * P), ACT.Exp,
                                   scale=SCALE).then_inc(prob_ready, 1)


def gqa_output(nc, g, t, m, a):
    ps = g["psum"]
    w_g, b_g = m.sb("w_g", [P, D]), m.sb("b_g", [1, D])
    w_o, b_o = m.sb("w_o", [P, D]), m.sb("b_o", [1, D])
    oT, gT = m.sb("oT", [P, S]), m.sb("gT", [P, S])
    gate = m.sb("gate", [P, NT, D])
    gated = m.sb("gated", [P, NT, D])
    zeroed, loaded, chain_dve, oT_psum, oT_ready, gate_done, gate_ready, gated_ready, gT_psum, gT_ready, out_done = (
        m.sem(n) for n in ("zeroed", "loaded", "chain_dve", "oT_psum", "oT_ready", "gate_done",
                           "gate_ready", "gated_ready", "gT_psum", "gT_ready", "out_done"))
    N_LOADS = 3 + HQ
    o4 = m.sb("o", [P, NT, HQ, HD])
    share = m.sb("share", [P, NT, HQ])
    o = o4[:].rearrange("p i h c -> p i (h c)")
    turned, o_ready = m.sem("turned"), m.sem("o_ready")

    def wide(b):
        return ps[:, b:b + 2, :].rearrange("p b (i d) -> p (b i) d", d=D)

    with nc.Block() as block:
        @block.sync
        def _(sp):
            sp.dma_start(b_g[:], t["L1_bg_rep"]).then_inc(loaded, 16)
            sp.dma_start(w_o[:], t["L1_ffn_Wo"]).then_inc(loaded, 16)
            sp.dma_start(b_o[:], t["L1_ffn_bo"].unsqueeze(0)).then_inc(loaded, 16)
            sp.wait_ge(zeroed, 1)
            for h in range(HQ):
                sp.dma_start(w_g[h * HD:(h + 1) * HD, h * HD:(h + 1) * HD], t["L1_ffn_Wg"]).then_inc(loaded, 16)

        @block.gpsimd
        def _(pool):
            pool.memset(w_g[:], 0.0).then_inc(zeroed, 1)

        @block.tensor
        def _(pe):
            for k in range(HQ // 4):
                for i in range(NT):
                    last = pe.transpose(ps[:, 2 * k + i // 4, (i % 4) * P:(i % 4 + 1) * P],
                                        a["stack"][:, k, i * P:(i + 1) * P], g["ident"][:])
                last.then_inc(turned, 1)
            pe.wait_ge(o_ready, HQ // 4)
            for i in range(NT):
                pe.transpose(ps[:, i // 4, (i % 4) * P:(i % 4 + 1) * P], o[:, i, :],
                             g["ident"][:]).then_inc(oT_psum, 1)
            pe.wait_ge(loaded, 16 * N_LOADS)
            for i in range(NT):
                pe.wait_ge(oT_ready, i // 4 + 1)
                out = ps[:, 2 + i // 4, (i % 4) * D:(i % 4 + 1) * D]
                pe.matmul(out, oT[:, i * P:(i + 1) * P], w_g[:], start=True, stop=False)
                pe.matmul(out, g["ones"][:, 0:P], b_g[:], start=False, stop=True).then_inc(gate_done, 1)
            transpose_tiles(pe, gated, g["ident"][:], ps[:, 4:6, :], gated_ready, gT_psum)
            for i in range(NT):
                pe.wait_ge(gT_ready, i // 4 + 1)
                out = ps[:, 6 + i // 4, (i % 4) * D:(i % 4 + 1) * D]
                pe.matmul(out, gT[:, i * P:(i + 1) * P], w_o[:], start=True, stop=False)
                last = pe.matmul(out, g["ones"][:, 0:P], b_o[:], start=False, stop=True)
            last.then_inc(out_done, 1)

        @block.scalar
        def _(act):
            for n in range(2):
                act.wait_ge(oT_psum, 4 * (n + 1))
                act.activation(oT[:, n * HALF:(n + 1) * HALF], ps[:, n, :], ACT.Copy).then_inc(oT_ready, 1)
            act.wait_ge(gate_done, NT)
            act.activation(gate[:], wide(2), ACT.Sigmoid).then_inc(gate_ready, 1)
            for n in range(2):
                act.wait_ge(gT_psum, 4 * (n + 1))
                act.activation(gT[:, n * HALF:(n + 1) * HALF], ps[:, 4 + n, :], ACT.Copy).then_inc(gT_ready, 1)

        @block.vector
        def _(dve):
            link = chained(dve, chain_dve)
            for k in range(HQ // 4):
                dve.wait_ge(turned, k + 1)
                out = wide(2 * k).rearrange("p i (h c) -> p i h c", c=32)
                heads = slice(4 * k, 4 * k + 4)
                link(dve.reciprocal(share[:, :, heads], out[:, :, :, HD]))
                dve.tensor_tensor(o4[:, :, heads, :], out[:, :, :, 0:HD],
                                  share[:, :, heads].unsqueeze(3).to_broadcast([P, NT, 4, HD]),
                                  ALU.mult).then_inc(o_ready, 1)
            dve.wait_ge(o_ready, HQ // 4)
            dve.wait_ge(gate_ready, 1)
            dve.tensor_tensor(gated[:], o, gate[:], ALU.mult).then_inc(gated_ready, NT)
            dve.wait_ge(out_done, 1)
            link(dve.tensor_tensor(a["xn"][:], a["xn"][:], wide(6), ALU.add))


def top_expert(nc, g, t, m, a):
    NE, HID = 8, 256
    ps = g["psum"]
    x1 = a["xn"]
    ln_w = m.sb("ln_w", [P, 1])
    w_r, b_r = m.sb("w_r", [P, NE]), m.sb("b_r", [1, NE])
    w1, b1 = m.sb("w1", [P, NE, 2 * HID]), m.sb("b1", [P, NE, 4])
    w2, b2 = m.sb("w2", [P, NE, 2, D]), m.sb("b2", [1, NE, D])
    order = m.sb("order", [P, NE])
    stats, mv = m.sb("stats", [P, NT, 6]), m.sb("mv", [P, NT, 2])
    scale = m.sb("scale", [P, NT])
    h, hT = m.sb("h", [P, NT, D]), m.sb("hT", [P, S])
    best = m.sb("best", [P, NT])
    rank = m.sb("rank", [P, NT, NE])
    own = m.sb("own", [P, NT, NE])
    sig = m.sb("sig", [P, 2, S])
    act_T = m.sb("act_T", [P, 2, 2, S])
    kept = m.sb("kept", [P, 2, NT, D])

    loaded, loaded_w, chain_dve, scale_sq, scale_ready, h_ready, hT_psum, hT_ready, logit_done = (
        m.sem(n) for n in ("loaded", "loaded_w", "chain_dve", "scale_sq", "scale_ready", "h_ready",
                           "hT_psum", "hT_ready", "logit_done"))
    u_done, sig_ready, act_ready, y_done, y_read, added, sum_ready = (
        m.sem(n) for n in ("u_done", "sig_ready", "act_ready", "y_done", "y_read", "added", "sum_ready"))
    N_LOADS = 4

    def pair(n):
        return ps[:, 2 * n:2 * n + 2, :].rearrange("p b n -> p (b n)")

    with nc.Block() as block:
        @block.sync
        def _(sp):
            sp.dma_start(ln_w[:], t["L1_ffn_ln2_w"].unsqueeze(1)).then_inc(loaded, 16)
            sp.dma_start(w_r[:], t["L1_ffn_Wr"]).then_inc(loaded, 16)
            sp.dma_start(b_r[:], t["L1_ffn_br"].unsqueeze(0)).then_inc(loaded, 16)
            sp.dma_start(order[:], t["order"]).then_inc(loaded, 16)
            sp.dma_start(b1[:], t["L1_eb1_T"].rearrange("(e q p) -> p e q", e=NE, p=P),
                         allow_slow_non_contiguous=True).then_inc(loaded_w, 16)
            sp.dma_start(w1[:], t["L1_ffn_W1"].rearrange("e p n -> p e n")).then_inc(loaded_w, 16)
            sp.dma_start(w2[:], t["L1_ffn_W2"].rearrange("e (q p) d -> p e q d", p=P)).then_inc(loaded_w, 16)
            sp.dma_start(b2[:], t["L1_ffn_b2"].unsqueeze(0)).then_inc(loaded_w, 16)

        @block.vector
        def _(dve):
            link = chained(dve, chain_dve)
            for i in range(NT):
                last = dve.bn_stats(stats[:, i, :], x1[:, i, :])
            link(last)
            for i in range(NT):
                last = dve.bn_aggr(mv[:, i, :], stats[:, i, :])
            link(last)
            link(dve.tensor_tensor(scale[:], mv[:, :, 0], mv[:, :, 0], ALU.mult))
            dve.scalar_tensor_tensor(out=scale[:], in0=scale[:], scalar=1e-6, in1=mv[:, :, 1],
                                     op0=ALU.add, op1=ALU.add).then_inc(scale_sq, 1)
            dve.wait_ge(scale_ready, 1)
            link(dve.reciprocal(scale[:], scale[:]))
            for i in range(NT):
                dve.tensor_scalar(h[:, i, :], x1[:, i, :], scale[:, i:i + 1], None,
                                  ALU.mult).then_inc(h_ready, 1)
            link(dve.tensor_tensor(g["x"][:], g["x"][:], x1[:], ALU.add))
            dve.wait_ge(logit_done, 1)
            dve.wait_ge(loaded, 16 * N_LOADS)
            logits = ps[:, 2, 0:NT * NE].rearrange("p (i e) -> p i e", e=NE)

            def spread(v):
                return v.unsqueeze(2).to_broadcast([P, NT, NE])

            link(dve.reduce_max(best[:], logits, AX))
            link(dve.tensor_tensor(rank[:], logits, spread(best[:]), ALU.is_equal))
            link(dve.tensor_tensor(rank[:], rank[:], order[:].unsqueeze(1).to_broadcast([P, NT, NE]), ALU.mult))
            link(dve.reduce_max(best[:], rank[:], AX))
            dve.tensor_tensor(own[:], rank[:], spread(best[:]), ALU.is_equal).then_inc(sum_ready, 1)
            dve.wait_ge(sum_ready, 1)

            def keep(e):
                dve.wait_ge(y_done, e + 1)
                if e >= 2:
                    dve.wait_ge(added, e - 1)
                dve.tensor_tensor(kept[:, e % 2], pair(3).rearrange("p (i d) -> p i d", d=D),
                                  own[:, :, e:e + 1].to_broadcast([P, NT, D]), ALU.mult).then_inc(y_read, 1)

            for e in range(NE):
                for q in range(2):
                    n = 2 * e + q
                    dve.wait_ge(u_done, 2 * n + 2)
                    dve.wait_ge(sig_ready, n + 1)
                    if e >= 2:
                        dve.wait_ge(y_done, e - 1)
                    dve.scalar_tensor_tensor(out=act_T[:, e % 2, q, :], in0=pair((2 * n + 1) % 3),
                                             scalar=b1[:, e, q:q + 1], in1=sig[:, q, :],
                                             op0=ALU.add, op1=ALU.mult).then_inc(act_ready, 1)
                if e >= 1:
                    keep(e - 1)
            keep(NE - 1)

        @block.gpsimd
        def _(pool):
            pool.wait_ge(sum_ready, 1)
            for e in range(NE):
                pool.wait_ge(y_read, e + 1)
                pool.tensor_tensor(g["x"][:], g["x"][:], kept[:, e % 2], ALU.add).then_inc(added, 1)
                pool.wait_ge(added, e + 1)

        @block.scalar
        def _(act):
            act.wait_ge(scale_sq, 1)
            act.activation(scale[:], scale[:], ACT.Sqrt).then_inc(scale_ready, 1)
            act.wait_ge(loaded, 16 * N_LOADS)
            for n in range(2):
                act.wait_ge(hT_psum, 4 * (n + 1))
                act.activation(hT[:, n * HALF:(n + 1) * HALF], ps[:, n, :], ACT.Copy,
                               scale=ln_w[:, 0:1]).then_inc(hT_ready, 1)
            act.wait_ge(loaded_w, 64)
            for e in range(NE):
                for q in range(2):
                    n = 2 * e + q
                    act.wait_ge(u_done, 2 * n + 1)
                    if n >= 2:
                        act.wait_ge(act_ready, n - 1)
                    act.activation(sig[:, q, :], pair((2 * n) % 3), ACT.Sigmoid,
                                   bias=b1[:, e, 2 + q:3 + q]).then_inc(sig_ready, 1)

        @block.tensor
        def _(pe):
            transpose_tiles(pe, h, g["ident"][:], ps, h_ready, hT_psum)
            pe.wait_ge(loaded, 16 * N_LOADS)
            for i in range(NT):
                pe.wait_ge(hT_ready, i // 4 + 1)
                out = ps[:, 2, i * NE:(i + 1) * NE]
                pe.matmul(out, hT[:, i * P:(i + 1) * P], w_r[:], start=True, stop=False)
                last = pe.matmul(out, g["ones"][:, 0:P], b_r[:], start=False, stop=True)
            last.then_inc(logit_done, 1)
            pe.wait_ge(loaded_w, 64)

            def expert_out(e):
                pe.wait_ge(act_ready, 2 * (e + 1))
                if e >= 1:
                    pe.wait_ge(y_read, e)
                for i in range(NT):
                    out = ps[:, 6 + i // 4, (i % 4) * D:(i % 4 + 1) * D]
                    for q in range(2):
                        pe.matmul(out, act_T[:, e % 2, q, i * P:(i + 1) * P], w2[:, e, q, :],
                                  start=q == 0, stop=False)
                    last = pe.matmul(out, g["ones"][:, 0:P], b2[:, e, :], start=False, stop=True)
                last.then_inc(y_done, 1)

            for e in range(NE):
                for q in range(2):
                    for k in (2 + q, q):
                        n = 2 * (2 * e + q) + (k < 2)
                        if n == 1:
                            pe.wait_ge(sum_ready, 1)
                        if n >= 3:
                            pe.wait_ge(sig_ready, (n - 3) // 2 + 1)
                            if (n - 3) % 2:
                                pe.wait_ge(act_ready, (n - 3) // 2 + 1)
                        for c in range(2):
                            last = pe.matmul(ps[:, 2 * (n % 3) + c, :], w1[:, e, k * P:(k + 1) * P],
                                             hT[:, c * HALF:(c + 1) * HALF], start=True, stop=True)
                        last.then_inc(u_done, 1)
                if e >= 1:
                    expert_out(e - 1)
            expert_out(NE - 1)



def shape_constants():
    onehot3 = np.tile(np.eye(32, dtype=np.float32), (3, 1))
    above = np.triu(np.full((P, P), NEG, np.float32), 1)
    turns = 2.0 * np.pi * (np.outer(np.arange(S), np.arange(S)) % NF) / NF
    dft = np.concatenate([np.cos(turns), -np.sin(turns)], 1)
    alternating = 1.0 - 2.0 * (np.arange(S) % 2)
    dft[:, S] = alternating
    index = np.concatenate([np.arange(P), P * np.arange(NT)]).astype(np.float32)
    quarter = np.where(np.arange(P) < P // 2, 0.25, 0.0).astype(np.float32).reshape(P, 1)
    freqs = np.outer(np.arange(S), 1.0 / 10000.0 ** (np.arange(0, HD, 2) / HD)).astype(np.float32)
    return {"rope_cos": np.cos(freqs), "rope_sin": np.sin(freqs), "below_diagonal": above.T,
            "order": np.tile(np.arange(8, 0, -1, dtype=np.float32), (P, 1)),
            "dft": dft.astype(np.float32), "alternating": alternating.astype(np.float32).reshape(1, S),
            "s4d_index": np.tile(index, (P, 1)), "s4d_quarter": quarter,
            "above_diagonal": above, "ident": np.eye(P, dtype=np.float32), "onehot3": onehot3}


def laid_out(a):
    w = {k: v for k, v in a.items() if k.startswith("L")}
    w["x"] = a["x"].reshape(S, D)
    w["ctx"] = a["ctx_768"].reshape(S2, DC)
    w["ctx_T"] = a["ctx_768"].reshape(S2, DC).T
    w["L0_in_proj_T"] = a["L0_attn_in_proj_w"].T
    w["L0_conv_b_T"] = a["L0_attn_conv_b"].reshape(2, P).T
    w["L0_dt_b_T"] = a["L0_attn_dt_proj_b"].reshape(2, P).T
    w["L0_D_T"] = a["L0_attn_D"].reshape(2, P).T
    xp = a["L0_attn_x_proj_w"]
    w["L0_bcdt_T"] = np.concatenate([xp[8:], xp[8:], xp[8:], xp[:8]], 0).T
    w["L0_dt_proj_T"] = a["L0_attn_dt_proj_w"].T
    w["L0_out_proj_T"] = a["L0_attn_out_proj_w"].T
    w["L0_Wk_T"] = a["L0_xattn_Wk"].T
    for k in ("WQ", "WK", "WV"):
        w[f"L1_{k}_T"] = a[f"L1_attn_{k}"].T
    w["L1_Wq_rep"] = np.concatenate([np.tile(a["L1_xattn_Wq"][:, 32 * h:32 * h + 32], 4) for h in range(4)], 1)
    w["L1_Wk_rep"] = np.concatenate([np.tile(a["L1_xattn_Wk"][:, 32 * h:32 * h + 32], 4) for h in range(4)], 1)
    w["vision_mask"] = a["mask_BxS2_bf1"].reshape(1, S2).view(np.uint8)
    w["text_mask"] = a["mask_BxS_bf1"].reshape(S).view(np.uint8)
    for n in ("A_re", "A_im", "C_re", "C_im"):
        w[f"s4d_{n.lower()}"] = np.tile(a[f"L1_xattn_{n}"].T, (2, 1))
    w["mod_gate"] = a["L1_xattn_mod_gate"].reshape(1, 1)
    w["L1_b1_T"] = a["L1_xattn_b1"].reshape(4, P).T
    w["L1_Wqkv"] = np.concatenate([a[f"L1_ffn_W{k}"] for k in "qkv"], 1)
    w["L1_bqkv"] = np.concatenate([a[f"L1_ffn_b{k}"] for k in "qkv"]).reshape(1, -1)
    w["L1_bg_rep"] = np.tile(a["L1_ffn_bg"], HQ).reshape(1, -1)
    w["L1_eb1_T"] = a["L1_ffn_b1"].reshape(-1)
    w.update(shape_constants())
    return w

PARTS = [mamba, cross_attention, threshold_experts, causal_attention, film_context, film_s4d_ffn,
         gqa_experts]



def decoder(nc, t):
    g = {}
    with ExitStack() as whole:
        g["psum"] = whole.enter_context(nc.psum_tensor("psum", [P, 8, HALF], F32))
        g["x"] = whole.enter_context(nc.sbuf_tensor("residual", [P, NT, D], F32))
        g["ident"] = whole.enter_context(nc.sbuf_tensor("ident", [P, P], F32))
        g["ones"] = whole.enter_context(nc.sbuf_tensor("ones", [1, HALF], F32))
        g["ctx_rows"] = whole.enter_context(nc.sbuf_tensor("ctx_rows", [P, KT, DC + 1], F32))
        g["xn"] = whole.enter_context(nc.sbuf_tensor("layer1_xn", [P, NT, D], F32))
        g["c_T"] = whole.enter_context(nc.sbuf_tensor("c_T", [P, S], F32))
        g["k_tok"] = whole.enter_context(nc.sbuf_tensor("s4d_k_tok", [P, NT, D], F32))
        Memory.used.clear()
        for part in [load_constants] + PARTS + [store_output]:
            with ExitStack() as ctx:
                part(nc, g, t, Memory(nc, ctx, part.__name__))
            if part in (causal_attention, film_context, film_s4d_ffn):
                recycle(nc, Memory.used)


def kernel(**inputs):
    import numpy as _np
    import concourse.bacc as _bacc
    from concourse import mybir as _mybir
    from concourse.bass_utils import run_bass_kernel_spmd as _run

    nc = _bacc.Bacc("TRN2", target_bir_lowering=False, num_devices=1)
    arrays = {k: v for k, v in laid_out({k: _np.asarray(v) for k, v in inputs.items()}).items()}
    t = {}
    feeds = {}
    for name, a in arrays.items():
        a = _np.ascontiguousarray(a)
        feeds[f"in_{name}"] = a
        t[name] = nc.dram_tensor(f"in_{name}", a.shape, _mybir.dt.from_np(a.dtype), kind="ExternalInput").ap()
    t["out"] = nc.dram_tensor("out_0", (S, D), _mybir.dt.float32, kind="ExternalOutput").ap()
    decoder(nc, t)
    r = _run(nc, [feeds], core_ids=[0])
    return r.results[0]["out_0"].reshape(1, S, D)
```

```python
from contextlib import ExitStack

import numpy as np

import concourse.bass as bass
from concourse import mybir

ALU = mybir.AluOpType
ACT = mybir.ActivationFunctionType
F32 = mybir.dt.float32
BF16 = mybir.dt.bfloat16
U8 = mybir.dt.uint8
AX = mybir.AxisListType.X

P = 128
S = 1024
D = 128
NT = S // P
S2 = 6404
DC = 96
HALF = 512
LN_EPS = 1e-5
NEG = -1e30


def recycle(nc, used):
    nc.clear_and_free_semaphores(list(used))
    used.clear()
    nc.all_engine_barrier()


class Memory:

    used = []

    def __init__(self, nc, ctx, name):
        self.nc, self.ctx, self.name = nc, ctx, name

    def sb(self, name, shape, dt=F32):
        return self.ctx.enter_context(self.nc.sbuf_tensor(f"{self.name}_{name}", shape, dt))

    def sem(self, name):
        handle = self.nc.alloc_semaphore(f"{self.name}_{name}")
        self.used.append(handle)
        return handle


def chained(eng, sem):
    count = [0]

    def link(ins):
        count[0] += 1
        ins.then_inc(sem, 1)
        eng.wait_ge(sem, count[0])

    return link


def wait_in_loop(eng, sem, value, passed):
    eng.wait_ge(sem, value)
    eng.sem_inc(passed, 1)


def normalise(dve, link, x, stats, mv, rstd, var_ready, root_ready, xn, ready, second_eps=None,
              second=None):
    for i in range(NT):
        ins = dve.bn_stats(stats[:, i, :], x[:, i, :])
    link(ins)
    for i in range(NT):
        ins = dve.bn_aggr(mv[:, i, :], stats[:, i, :])
    link(ins)
    ins = dve.tensor_scalar(rstd[:, :, 0], mv[:, :, 1], LN_EPS, None, ALU.add)
    n = 1
    if second is not None:
        n = 2
        ins = dve.tensor_scalar(rstd[:, :, 1], mv[:, :, 1], 1.0 + second_eps, LN_EPS * second_eps,
                                ALU.mult, ALU.add)
    ins.then_inc(var_ready, 1)
    dve.wait_ge(root_ready, 1)
    link(dve.reciprocal(rstd[:, :, 0:n], rstd[:, :, 0:n]))
    for k, dst in enumerate((xn, second)[:n]):
        for i in range(NT):
            ins = dve.tensor_scalar(dst[:, i, :], x[:, i, :], mv[:, i, 0:1], rstd[:, i, k:k + 1],
                                    ALU.subtract, ALU.mult)
            if k == n - 1:
                ins.then_inc(ready, 1)


def root(act, rstd, n, var_ready, root_ready):
    act.wait_ge(var_ready, 1)
    act.activation(rstd[:, :, 0:n], rstd[:, :, 0:n], ACT.Sqrt).then_inc(root_ready, 1)


def transpose_tiles(pe, src, ident, banks, ready, done):
    for i in range(NT):
        pe.wait_ge(ready, i + 1)
        pe.transpose(banks[:, i // 4, (i % 4) * P:(i % 4 + 1) * P], src[:, i, :],
                     ident).then_inc(done, 1)



def load_constants(nc, g, t, m):
    loaded = m.sem("loaded")
    g["ctx_loaded"] = m.sem("ctx_loaded")
    consts = m.sem("consts")
    with nc.Block() as block:
        @block.sync
        def _(sp):
            sp.dma_start(g["x"][:], t["x"].rearrange("(i p) d -> p i d", p=P)).then_inc(loaded, 16)
            sp.dma_start(g["ident"][:], t["ident"]).then_inc(loaded, 16)
            sp.wait_ge(loaded, 32)

        @block.vector
        def _(dve):
            dve.memset(g["ones"][:], 1.0).then_inc(consts, 1)
            dve.wait_ge(consts, 1)


def store_output(nc, g, t, m):
    stored = m.sem("stored")
    with nc.Block() as block:
        @block.sync
        def _(sp):
            sp.dma_start(t["out"].rearrange("(i p) d -> p i d", p=P), g["x"][:]).then_inc(stored, 16)
            sp.wait_ge(stored, 16)



def mamba(nc, g, t, m):
    DI, NS, DR = 2 * D, 16, D // 16
    NC = DI // P
    ps = g["psum"]
    w_in = m.sb("w_in", [P, 2 * DI])
    norm_w = m.sb("norm_w", [P, 1])
    conv_w = m.sb("conv_w", [P, NC, 4])
    conv_b = m.sb("conv_b", [P, NC])
    w_bcdt = m.sb("w_bcdt", [P, NC, 3 * 2 * NS + DR])
    w_dt = m.sb("w_dt", [DR, DI])
    dt_b = m.sb("dt_b", [P, NC])
    a_log = m.sb("a_log", [P, NC, NS])
    a_neg = m.sb("a_neg", [P, NC, NS])
    skip = m.sb("skip", [P, NC])
    w_out = m.sb("w_out", [P, NC, D])
    onehot = m.sb("onehot", [3 * 2 * NS, 2 * NS], BF16)
    onehot_f = m.sb("onehot_f", [3 * 2 * NS, 2 * NS])
    stats = m.sb("stats", [P, NT, 6])
    mv = m.sb("mv", [P, NT, 2])
    rstd = m.sb("rstd", [P, NT, 2])
    xn = m.sb("xn", [P, NT, D])
    h = m.sb("h", [P, NT, D])
    hT = m.sb("hT", [P, S])
    xi_pad = m.sb("xi_pad", [P, NC, S + 3])
    conv = m.sb("conv", [P, NC, S])
    xi = m.sb("xi", [P, NC, S])
    zs = m.sb("zs", [P, NC, S])
    dt_low = m.sb("dt_low", [DR, S])
    pre = m.sb("pre", [P, NC, S])
    soft = m.sb("soft", [P, NC, S])
    delta = m.sb("delta", [P, NC, S])
    du = pre
    rest = m.sb("rest", [3 * 2 * NS, S])
    hi = m.sb("hi", [3 * 2 * NS, S], BF16)
    mid = m.sb("mid", [3 * 2 * NS, S], BF16)
    split = m.sb("split", [3 * 2 * NS, S], BF16)
    b_all = m.sb("b_all", [P, 2, S])
    RING = 4
    decay = m.sb("decay", [P, RING, S])
    drive = m.sb("drive", [P, RING, S])
    state = m.sb("state", [P, 2, S])
    read = m.sb("read", [P, RING, S])
    y = conv

    loaded = m.sem("loaded")
    chain = {e: m.sem(f"chain_{e}") for e in ("dve", "act")}
    h_ready, hT_psum, hT_ready, in_done, xi_copied, z_ready, conv_done, xi_ready = (
        m.sem(n) for n in ("h_ready", "hT_psum", "hT_ready", "in_done", "xi_copied", "z_ready",
                           "conv_done", "xi_ready"))
    bc_done, dt_copied, split_ready, dt_done, pre_ready, delta_ready, du_ready = (
        m.sem(n) for n in ("bc_done", "dt_copied", "split_ready", "dt_done", "pre_ready",
                           "delta_ready", "du_ready"))
    b_bcast, c_bcast, b_copied, decay_ready, drive_ready, scanned, read_ready, summed = (
        m.sem(n) for n in ("b_bcast", "c_bcast", "b_copied", "decay_ready", "drive_ready",
                           "scanned", "read_ready", "summed"))
    y_ready, out_done, abs_ready, a_ready = (m.sem(n) for n in ("y_ready", "out_done", "abs_ready", "a_ready"))
    var_ready, root_ready = m.sem("var_ready"), m.sem("root_ready")
    N_LOADS = 11
    BC, BC3 = 2 * NS, 3 * 2 * NS

    with nc.Block() as block:
        @block.sync
        def _(sp):
            for dst, src in ((w_in[:], t["L0_in_proj_T"]),
                             (norm_w[:], t["L0_attn_norm_w"].unsqueeze(1)),
                             (conv_w[:], t["L0_attn_conv_w"].rearrange("(c p) k -> p c k", p=P)),
                             (conv_b[:], t["L0_conv_b_T"]),
                             (w_bcdt[:], t["L0_bcdt_T"].rearrange("(c p) k -> p c k", p=P)),
                             (w_dt[:], t["L0_dt_proj_T"]),
                             (dt_b[:], t["L0_dt_b_T"]),
                             (a_log[:], t["L0_attn_A_log"].rearrange("(c p) n -> p c n", p=P)),
                             (skip[:], t["L0_D_T"]),
                             (w_out[:], t["L0_out_proj_T"].rearrange("(c p) k -> p c k", p=P)),
                             (onehot_f[:], t["onehot3"])):
                sp.dma_start(dst, src).then_inc(loaded, 16)
            full = (KT - 1) * P
            ctx = g["ctx_rows"]
            sp.dma_start(g["ctx_T"][0:DC, :], t["ctx_T"]).then_inc(g["ctx_loaded"], 16)
            sp.dma_start(ctx[:, 0:KT - 1, 0:DC],
                         t["ctx"][0:full, :].rearrange("(k p) c -> p k c", p=P)).then_inc(g["ctx_loaded"], 16)
            sp.dma_start(ctx[0:K_LAST, KT - 1, 0:DC], t["ctx"][full:S2, :]).then_inc(g["ctx_loaded"], 16)

        @block.vector
        def _(dve):
            link = chained(dve, chain["dve"])
            link(dve.memset(xi_pad[:, :, 0:3], 0.0))
            normalise(dve, link, g["x"], stats, mv, rstd, var_ready, root_ready, xn, h_ready,
                      LN_EPS, h)
            dve.wait_ge(loaded, 16 * N_LOADS)
            link(dve.tensor_copy(onehot[:], onehot_f[:]))
            dve.wait_ge(xi_copied, 2 * NC)
            for c in range(NC):
                link(dve.tensor_scalar(conv[:, c, :], xi_pad[:, c, 0:S], conv_w[:, c, 0:1], None, ALU.mult))
                for k in range(1, 4):
                    ins = dve.scalar_tensor_tensor(out=conv[:, c, :], in0=xi_pad[:, c, k:k + S],
                                                   scalar=conv_w[:, c, k:k + 1], in1=conv[:, c, :],
                                                   op0=ALU.mult, op1=ALU.add)
                    if k < 3:
                        link(ins)
                ins.then_inc(conv_done, 1)
            dve.wait_ge(bc_done, 3)
            bc = ps[0:3 * BC, 0:2, :].rearrange("p b n -> p (b n)")
            link(dve.tensor_copy(hi[:], bc))
            link(dve.tensor_tensor(rest[:], bc, hi[:], ALU.subtract))
            link(dve.tensor_copy(mid[:], rest[:]))
            link(dve.tensor_tensor(rest[:], rest[:], mid[:], ALU.subtract))
            dve.tensor_copy(split[0:BC, :], hi[0:BC, :]).then_inc(split_ready, 1)
            dve.tensor_copy(split[BC:2 * BC, :], mid[BC:2 * BC, :]).then_inc(split_ready, 1)
            dve.tensor_copy(split[2 * BC:3 * BC, :], rest[2 * BC:3 * BC, :]).then_inc(split_ready, 1)
            dve.wait_ge(dt_done, 2 * NC)
            for c in range(NC):
                acc = ps[:, 4 + 2 * c:6 + 2 * c, :].rearrange("p b n -> p (b n)")
                link(dve.tensor_scalar(pre[:, c, :], acc, dt_b[:, c:c + 1], None, ALU.add))
            link(dve.tensor_scalar(soft[:], pre[:], -1.0, None, ALU.mult))
            dve.tensor_tensor(soft[:], soft[:], pre[:], ALU.min).then_inc(abs_ready, 1)
            dve.wait_ge(delta_ready, 1)
            link(dve.scalar_tensor_tensor(out=delta[:], in0=pre[:], scalar=0.0, in1=soft[:],
                                          op0=ALU.max, op1=ALU.add))
            dve.wait_ge(xi_ready, NC)
            dve.tensor_tensor(du[:], delta[:], xi[:], ALU.mult).then_inc(du_ready, 1)
            for s in range(NS):
                for c in range(NC):
                    n = NC * s + c
                    dve.wait_ge(decay_ready, n + 1)
                    dve.wait_ge(drive_ready, n + 1)
                    dve.tensor_tensor_scan(state[:, c, :], decay[:, n % RING, :], drive[:, n % RING, :], 0.0,
                                           ALU.mult, ALU.add).then_inc(scanned, 1)
                    dve.wait_ge(scanned, n + 1)
                    dve.wait_ge(c_bcast, s + 1)
                    if n >= RING:
                        dve.wait_ge(summed, n - RING + 1)
                    dve.tensor_tensor(read[:, n % RING, :], state[:, c, :],
                                      ps[:, 2:4, :].rearrange("p b n -> p (b n)"),
                                      ALU.mult).then_inc(read_ready, 1)
            dve.wait_ge(summed, NC * NS)
            dve.wait_ge(z_ready, 2 * NC)
            for c in range(NC):
                acc = ps[:, 4 + 2 * c:6 + 2 * c, :].rearrange("p b n -> p (b n)")
                link(dve.scalar_tensor_tensor(out=y[:, c, :], in0=xi[:, c, :], scalar=skip[:, c:c + 1],
                                              in1=acc, op0=ALU.mult, op1=ALU.add))
                dve.tensor_tensor(y[:, c, :], y[:, c, :], zs[:, c, :], ALU.mult).then_inc(y_ready, 1)
            link(dve.tensor_tensor(g["x"][:], g["x"][:], xn[:], ALU.add))
            dve.wait_ge(out_done, NT)
            dve.tensor_tensor(g["x"][:], g["x"][:],
                              ps[:, 0:2, :].rearrange("p b (i d) -> p (b i) d", d=D), ALU.add)

        @block.tensor
        def _(pe):
            transpose_tiles(pe, h, g["ident"][:], ps, h_ready, hT_psum)
            pe.wait_ge(loaded, 16 * N_LOADS)
            pe.wait_ge(hT_ready, 2)
            for e in range(2 * NC):
                for n in range(2):
                    bank = (4 + 2 * e + n) % 8
                    pe.matmul(ps[:, bank, :], w_in[:, e * P:(e + 1) * P], hT[:, n * HALF:(n + 1) * HALF],
                              start=True, stop=True).then_inc(in_done, 1)
            pe.wait_ge(xi_ready, NC)
            pe.wait_ge(z_ready, 2 * NC)
            for n in range(2):
                for c in range(NC):
                    last = pe.matmul(ps[0:3 * BC, n, :],
                                     w_bcdt[:, c, 0:BC3],
                                     xi[:, c, n * HALF:(n + 1) * HALF], start=c == 0, stop=c == NC - 1)
                last.then_inc(bc_done, 1)
                for c in range(NC):
                    last = pe.matmul(ps[0:DR, 2 + n, :], w_bcdt[:, c, BC3:BC3 + DR],
                                     xi[:, c, n * HALF:(n + 1) * HALF], start=c == 0, stop=c == NC - 1)
                last.then_inc(bc_done, 1)
            pe.wait_ge(dt_copied, 1)
            for c in range(NC):
                for n in range(2):
                    pe.matmul(ps[:, 4 + 2 * c + n, :], w_dt[:, c * P:(c + 1) * P],
                              dt_low[:, n * HALF:(n + 1) * HALF], start=True, stop=True).then_inc(dt_done, 1)
            pe.wait_ge(split_ready, 3)
            pe.wait_ge(abs_ready, 1)

            def broadcast(row, banks, done):
                sel = onehot[:, row:row + 1].to_broadcast([3 * BC, P])
                for n in range(2):
                    last = pe.matmul(ps[:, banks + n, :], sel, split[:, n * HALF:(n + 1) * HALF],
                                     start=True, stop=True)
                last.then_inc(done, 1)

            def add_state(n):
                c = n % NC
                pe.wait_ge(read_ready, n + 1)
                for q in range(2):
                    last = pe.matmul(ps[:, 4 + 2 * c + q, :], g["ident"][:],
                                     read[:, n % RING, q * HALF:(q + 1) * HALF],
                                     start=n < NC, stop=n >= NC * (NS - 1))
                last.then_inc(summed, 1)

            broadcast(0, 0, b_bcast)
            for s in range(NS):
                if s + 1 < NS:
                    pe.wait_ge(b_copied, s + 1)
                    broadcast(s + 1, 0, b_bcast)
                if s >= 1:
                    pe.wait_ge(read_ready, NC * s)
                broadcast(NS + s, 2, c_bcast)
                if s >= 1:
                    for c in range(NC):
                        add_state(NC * (s - 1) + c)
            for c in range(NC):
                add_state(NC * (NS - 1) + c)
            pe.wait_ge(y_ready, NC)
            for i in range(NT):
                for c in range(NC):
                    last = pe.matmul(ps[:, i // 4, (i % 4) * D:(i % 4 + 1) * D],
                                     y[:, c, i * P:(i + 1) * P], w_out[:, c, :],
                                     start=c == 0, stop=c == NC - 1)
                last.then_inc(out_done, 1)

        @block.scalar
        def _(act):
            link = chained(act, chain["act"])
            root(act, rstd, 2, var_ready, root_ready)
            act.wait_ge(loaded, 16 * N_LOADS)
            link(act.activation(a_neg[:], a_log[:], ACT.Exp))
            link(act.mul(a_neg[:], a_neg[:], -1.0))
            for n in range(2):
                act.wait_ge(hT_psum, 4 * (n + 1))
                act.activation(hT[:, n * HALF:(n + 1) * HALF], ps[:, n, :], ACT.Copy,
                               scale=norm_w[:, 0:1]).then_inc(hT_ready, 1)
            for e in range(2 * NC):
                for n in range(2):
                    act.wait_ge(in_done, 2 * e + n + 1)
                    bank = (4 + 2 * e + n) % 8
                    if e < NC:
                        act.activation(xi_pad[:, e, 3 + n * HALF:3 + (n + 1) * HALF], ps[:, bank, :],
                                       ACT.Copy).then_inc(xi_copied, 1)
                    else:
                        act.activation(zs[:, e - NC, n * HALF:(n + 1) * HALF], ps[:, bank, :],
                                       ACT.Silu).then_inc(z_ready, 1)
            for c in range(NC):
                act.wait_ge(conv_done, c + 1)
                act.activation(xi[:, c, :], conv[:, c, :], ACT.Silu,
                               bias=conv_b[:, c:c + 1]).then_inc(xi_ready, 1)
            act.wait_ge(bc_done, 4)
            act.activation(dt_low[:], ps[0:DR, 2:4, :].rearrange("p b n -> p (b n)"),
                           ACT.Copy).then_inc(dt_copied, 1)
            act.wait_ge(abs_ready, 1)
            link(act.activation(soft[:], soft[:], ACT.Exp))
            act.activation(soft[:], soft[:], ACT.Ln, bias=1.0).then_inc(delta_ready, 1)
            act.wait_ge(du_ready, 1)
            for s in range(NS):
                act.wait_ge(b_bcast, s + 1)
                if s >= 2:
                    act.wait_ge(drive_ready, NC * (s - 1))
                act.activation(b_all[:, s % 2, :], ps[:, 0:2, :].rearrange("p b n -> p (b n)"),
                               ACT.Copy).then_inc(b_copied, 1)
                for c in range(NC):
                    n = NC * s + c
                    if n >= RING:
                        act.wait_ge(scanned, n - RING + 1)
                    act.activation(decay[:, n % RING, :], delta[:, c, :], ACT.Exp,
                                   scale=a_neg[:, c, s:s + 1]).then_inc(decay_ready, 1)

        @block.gpsimd
        def _(pool):
            pool.wait_ge(du_ready, 1)
            for s in range(NS):
                pool.wait_ge(b_copied, s + 1)
                for c in range(NC):
                    n = NC * s + c
                    if n >= RING:
                        pool.wait_ge(scanned, n - RING + 1)
                    pool.tensor_tensor(drive[:, n % RING, :], du[:, c, :], b_all[:, s % 2, :],
                                       ALU.mult).then_inc(drive_ready, 1)



ROUND = 1.5 * 2.0 ** 23
TURN = 6.2831850
NS = 64
GROUP = 8
NG = D // GROUP
RING_Q = 4


def s4d_buffers(g, m):
    k = {n: m.sb(f"s4d_{n}", [P, D]) for n in (
        "log_dt", "a_re", "a_im", "c_re", "c_im", "dt", "ar", "ai", "turns", "tanh", "grow", "er", "ei",
        "nr", "ni", "qr", "qi", "inv", "tmp", "on_c", "on_s")}
    for n in ("angle", "rounded"):
        k[n] = m.sb(f"s4d_{n}", [P, 3, D])
    k["index"] = m.sb("s4d_index", [P, P + NT])
    k["quarter"] = m.sb("s4d_quarter", [P, 1])
    k["j_angle"], k["j_round"] = m.sb("s4d_j_angle", [P, 2, D, NT]), m.sb("s4d_j_round", [P, 2, D, NT])
    k["j_decay"], k["left"] = m.sb("s4d_j_decay", [P, D, NT]), m.sb("s4d_left", [P, D, NT])
    for n in ("i_angle", "i_decay"):
        k[n] = m.sb(f"s4d_{n}", [P, RING_Q, GROUP, P])
    k["i_round"] = m.sb("s4d_i_round", [P, GROUP, P])
    k["d_skip"] = m.sb("s4d_d_skip", [1, D])
    k["sem"] = {n: m.sem(f"s4d_{n}") for n in (
        "loaded", "dt_ready", "parts_ready", "small_ready", "small_done", "j_ready", "j_done",
        "left_ready", "i_ready", "sin_done", "grown", "decayed", "powers", "k_psum", "k_ready")}
    k["k_tok"] = g["k_tok"]
    return k


def s4d_load(sp, t, k):
    loaded = k["sem"]["loaded"]
    sp.dma_start(k["log_dt"][:], t["L1_xattn_log_dt"].unsqueeze(0).to_broadcast([P, D])).then_inc(loaded, 16)
    for n in ("a_re", "a_im", "c_re", "c_im"):
        sp.dma_start(k[n][:], t[f"s4d_{n}"]).then_inc(loaded, 16)
    sp.dma_start(k["index"][:], t["s4d_index"]).then_inc(loaded, 16)
    sp.dma_start(k["quarter"][:], t["s4d_quarter"]).then_inc(loaded, 16)
    sp.dma_start(k["d_skip"][:], t["L1_xattn_D_skip"].unsqueeze(0)).then_inc(loaded, 16)


def s4d_vector(dve, link, k):
    sem = k["sem"]

    def tt(out, x, y, op):
        link(dve.tensor_tensor(out, x, y, op))

    dve.wait_ge(sem["dt_ready"], 1)
    tt(k["ar"][:], k["dt"][:], k["a_re"][:], ALU.mult)
    tt(k["ai"][:], k["dt"][:], k["a_im"][:], ALU.mult)
    dve.tensor_scalar(k["turns"][:], k["ai"][:], 1.0 / (2.0 * np.pi), None, ALU.mult).then_inc(sem["parts_ready"], 1)
    dve.wait_ge(sem["parts_ready"], 1)
    link(dve.tensor_scalar(k["angle"][:, 0, :], k["turns"][:], 0.25, None, ALU.add))
    link(dve.tensor_scalar(k["angle"][:, 1, :], k["turns"][:], 1.0, None, ALU.mult))
    link(dve.tensor_scalar(k["angle"][:, 2, :], k["turns"][:], 0.5, None, ALU.mult))
    link(dve.tensor_scalar(k["rounded"][:], k["angle"][:], ROUND, None, ALU.add))
    link(dve.tensor_scalar(k["rounded"][:], k["rounded"][:], ROUND, None, ALU.subtract))
    dve.tensor_tensor(k["angle"][:], k["angle"][:], k["rounded"][:], ALU.subtract).then_inc(sem["small_ready"], 1)
    dve.wait_ge(sem["small_done"], 2)
    link(dve.tensor_scalar(k["tmp"][:], k["tanh"][:], -1.0, 1.0, ALU.mult, ALU.add))
    link(dve.reciprocal(k["tmp"][:], k["tmp"][:]))
    link(dve.scalar_tensor_tensor(out=k["grow"][:], in0=k["tanh"][:], scalar=2.0, in1=k["tmp"][:],
                                  op0=ALU.mult, op1=ALU.mult))
    cos_b, sin_b, sin_half = k["angle"][:, 0, :], k["angle"][:, 1, :], k["angle"][:, 2, :]
    tt(k["er"][:], k["grow"][:], cos_b, ALU.mult)
    link(dve.scalar_tensor_tensor(out=k["tmp"][:], in0=sin_half, scalar=-2.0, in1=sin_half,
                                  op0=ALU.mult, op1=ALU.mult))
    tt(k["er"][:], k["er"][:], k["tmp"][:], ALU.add)
    link(dve.scalar_tensor_tensor(out=k["ei"][:], in0=k["grow"][:], scalar=1.0, in1=sin_b,
                                  op0=ALU.add, op1=ALU.mult))
    cr, ci, re, im = k["c_re"][:], k["c_im"][:], k["a_re"][:], k["a_im"][:]
    tt(k["nr"][:], cr, k["er"][:], ALU.mult)
    tt(k["tmp"][:], ci, k["ei"][:], ALU.mult)
    tt(k["nr"][:], k["nr"][:], k["tmp"][:], ALU.subtract)
    tt(k["ni"][:], cr, k["ei"][:], ALU.mult)
    tt(k["tmp"][:], ci, k["er"][:], ALU.mult)
    tt(k["ni"][:], k["ni"][:], k["tmp"][:], ALU.add)
    tt(k["inv"][:], re, re, ALU.mult)
    tt(k["tmp"][:], im, im, ALU.mult)
    tt(k["inv"][:], k["inv"][:], k["tmp"][:], ALU.add)
    link(dve.reciprocal(k["inv"][:], k["inv"][:]))
    tt(k["qr"][:], k["nr"][:], re, ALU.mult)
    tt(k["tmp"][:], k["ni"][:], im, ALU.mult)
    tt(k["qr"][:], k["qr"][:], k["tmp"][:], ALU.add)
    tt(k["qr"][:], k["qr"][:], k["inv"][:], ALU.mult)
    tt(k["qi"][:], k["ni"][:], re, ALU.mult)
    tt(k["tmp"][:], k["nr"][:], im, ALU.mult)
    tt(k["qi"][:], k["qi"][:], k["tmp"][:], ALU.subtract)
    tt(k["qi"][:], k["qi"][:], k["inv"][:], ALU.mult)
    link(dve.tensor_scalar(k["on_c"][0:NS, :], k["qr"][0:NS, :], 2.0, None, ALU.mult))
    link(dve.tensor_scalar(k["on_s"][0:NS, :], k["qi"][0:NS, :], -2.0, None, ALU.mult))
    link(dve.tensor_scalar(k["on_c"][NS:P, :], k["qi"][NS:P, :], -2.0, None, ALU.mult))
    link(dve.tensor_scalar(k["on_s"][NS:P, :], k["qr"][NS:P, :], -2.0, None, ALU.mult))

    def over(x, n):
        return x.unsqueeze(2).to_broadcast([P, x.shape[1], n])

    j_index = k["index"][:, P:P + NT].unsqueeze(1).to_broadcast([P, D, NT])
    tt(k["j_angle"][:, 1, :, :], over(k["turns"][:], NT), j_index, ALU.mult)
    link(dve.tensor_scalar(k["j_angle"][:, 0, :, :], k["j_angle"][:, 1, :, :], 0.25, None, ALU.add))
    link(dve.tensor_scalar(k["j_round"][:], k["j_angle"][:], ROUND, None, ALU.add))
    link(dve.tensor_scalar(k["j_round"][:], k["j_round"][:], ROUND, None, ALU.subtract))
    tt(k["j_angle"][:], k["j_angle"][:], k["j_round"][:], ALU.subtract)
    dve.tensor_tensor(k["j_decay"][:], over(k["ar"][:], NT), j_index, ALU.mult).then_inc(sem["j_ready"], 1)
    dve.wait_ge(sem["j_done"], 2)
    tt(k["left"][:], k["j_angle"][:, 0, :, :], over(k["on_c"][:], NT), ALU.mult)
    tt(k["j_angle"][:, 1, :, :], k["j_angle"][:, 1, :, :], over(k["on_s"][:], NT), ALU.mult)
    tt(k["left"][:], k["left"][:], k["j_angle"][:, 1, :, :], ALU.add)
    dve.tensor_tensor(k["left"][:], k["left"][:], k["j_decay"][:], ALU.mult).then_inc(sem["left_ready"], 1)

    def power(q):
        dve.wait_ge(sem["sin_done"], q + 1)
        dve.wait_ge(sem["decayed"], q + 1)
        b = q % RING_Q
        dve.tensor_tensor(k["i_angle"][:, b], k["i_angle"][:, b], k["i_decay"][:, b],
                          ALU.mult).then_inc(sem["powers"], 1)

    i_index = k["index"][:, 0:P].unsqueeze(1).to_broadcast([P, GROUP, P])
    for q in range(NG):
        b = q % RING_Q
        group = slice(q * GROUP, (q + 1) * GROUP)
        if q >= RING_Q:
            dve.wait_ge(sem["k_psum"], q - RING_Q + 1)
        if q >= 1:
            dve.wait_ge(sem["i_ready"], q)
        tt(k["i_angle"][:, b], over(k["turns"][:, group], P), i_index, ALU.mult)
        link(dve.tensor_scalar(k["i_round"][:], k["i_angle"][:, b], k["quarter"][:, 0:1], ROUND,
                               ALU.add, ALU.add))
        link(dve.tensor_scalar(k["i_round"][:], k["i_round"][:], ROUND, None, ALU.subtract))
        dve.scalar_tensor_tensor(out=k["i_angle"][:, b], in0=k["i_angle"][:, b], scalar=k["quarter"][:, 0:1],
                                 in1=k["i_round"][:], op0=ALU.add, op1=ALU.subtract).then_inc(sem["i_ready"], 1)
        if q >= 2:
            power(q - 2)
    power(NG - 2)
    power(NG - 1)
    dve.wait_ge(sem["k_ready"], 1)
    link(dve.tensor_tensor(k["k_tok"][0:1, 0, :], k["k_tok"][0:1, 0, :], k["d_skip"][:], ALU.add))


def s4d_pool(pool, k):
    sem = k["sem"]
    pool.wait_ge(sem["parts_ready"], 1)
    i_index = k["index"][:, 0:P].unsqueeze(1).to_broadcast([P, GROUP, P])
    for q in range(NG):
        group = slice(q * GROUP, (q + 1) * GROUP)
        if q >= RING_Q:
            pool.wait_ge(sem["powers"], q - RING_Q + 1)
        pool.tensor_tensor(k["i_decay"][:, q % RING_Q], k["ar"][:, group].unsqueeze(2).to_broadcast([P, GROUP, P]),
                           i_index, ALU.mult).then_inc(sem["grown"], 1)


S4D_STEPS = 3 + NG // 2


def s4d_scalar(act, k, step):
    sem = k["sem"]
    if step == 0:
        act.wait_ge(sem["loaded"], 16 * 8)
        act.activation(k["dt"][:], k["log_dt"][:], ACT.Exp).then_inc(sem["dt_ready"], 1)
    elif step == 1:
        act.wait_ge(sem["parts_ready"], 1)
        act.activation(k["tanh"][:], k["ar"][:], ACT.Tanh, scale=0.5).then_inc(sem["small_done"], 1)
        act.wait_ge(sem["small_ready"], 1)
        act.activation(k["angle"][:], k["angle"][:], ACT.Sin, scale=TURN).then_inc(sem["small_done"], 1)
    elif step == 2:
        act.wait_ge(sem["j_ready"], 1)
        act.activation(k["j_angle"][:], k["j_angle"][:], ACT.Sin, scale=TURN).then_inc(sem["j_done"], 1)
        act.activation(k["j_decay"][:], k["j_decay"][:], ACT.Exp).then_inc(sem["j_done"], 1)
    else:
        q = 2 * (step - 3)
        for b in range(2):
            act.wait_ge(sem["i_ready"], q + b + 1)
            angle = k["i_angle"][:, (q + b) % RING_Q]
            act.activation(angle, angle, ACT.Sin, scale=TURN).then_inc(sem["sin_done"], 1)
        for b in range(2):
            act.wait_ge(sem["grown"], q + b + 1)
            decay = k["i_decay"][:, (q + b) % RING_Q]
            act.activation(decay, decay, ACT.Exp).then_inc(sem["decayed"], 1)


def s4d_copy(act, k, banks):
    act.wait_ge(k["sem"]["k_psum"], NG)
    act.activation(k["k_tok"][:], banks.rearrange("p b (d j) -> p j (b d)", j=NT),
                   ACT.Copy).then_inc(k["sem"]["k_ready"], 1)


def s4d_tensor(pe, k, banks, q):
    sem = k["sem"]
    if q == 0:
        pe.wait_ge(sem["left_ready"], 1)
    pe.wait_ge(sem["powers"], q + 1)
    for c in range(GROUP):
        d = q * GROUP + c
        last = pe.matmul(banks[:, d // 64, (d % 64) * NT:(d % 64 + 1) * NT], k["i_angle"][:, q % RING_Q, c, :],
                         k["left"][:, d, :], start=True, stop=True)
    last.then_inc(sem["k_psum"], 1)



KT = -(-S2 // P)
K_LAST = S2 - (KT - 1) * P
CHUNK = 2 * HALF
N_CHUNK = -(-S2 // CHUNK)
S4D_AT = (2, 7) + tuple(range(12, 44, 4))
S4D_PE_AT, S4D_PE_EVERY = 16, 2


def cross_attention(nc, g, t, m):
    CA = DC + 1
    ps = g["psum"]
    ctx_T = g["ctx_T"]
    w_q = m.sb("w_q", [P, D])
    b_q = m.sb("b_q", [P, 1])
    w_k = m.sb("w_k", [P, CA])
    w_v = m.sb("w_v", [CA, D + 1])
    stats = m.sb("stats", [P, NT, 6])
    mv = m.sb("mv", [P, NT, 2])
    rstd = m.sb("rstd", [P, NT, 1])
    xn = m.sb("xn", [P, NT, D])
    xT = m.sb("xT", [P, S])
    qT = m.sb("qT", [P, S])
    qc = m.sb("qc", [CA, S])
    qc_shifted = m.sb("qc_shifted", [CA, S])
    tops = m.sb("tops", [P, NT, N_CHUNK])
    top = m.sb("top", [P, NT])
    minus_top = m.sb("minus_top", [P, NT, CA])
    prob = m.sb("prob", [P, 3, S])
    summed_c = m.sb("summed_c", [CA, S])
    share = m.sb("share", [P, NT])

    loaded, w_v_loaded, ones_set = m.sem("loaded"), m.sem("w_v_loaded"), m.sem("ones_set")
    chain_dve, chain_pool = m.sem("chain_dve"), m.sem("chain_pool")
    var_ready, root_ready, xn_ready, xT_psum, xT_ready = (
        m.sem(n) for n in ("var_ready", "root_ready", "xn_ready", "xT_psum", "xT_ready"))
    q_done, q_ready, qc_done, qc_ready, score_done, max_read, top_ready = (
        m.sem(n) for n in ("q_done", "q_ready", "qc_done", "qc_ready", "score_done", "max_read",
                           "top_ready"))
    shift_done, shift_ready, prob_psum, prob_ready, pv_done, sum_ready, out_done = (
        m.sem(n) for n in ("shift_done", "shift_ready", "prob_psum", "prob_ready", "pv_done",
                           "sum_ready", "out_done"))
    N_LOADS = 4
    ctx = g["ctx_rows"]
    s4d = s4d_buffers(g, m)
    s4d_banks = ps[:, 4:6, :]
    s4d_steps = dict(zip(S4D_AT, range(1, S4D_STEPS)))
    s4d_products = {S4D_PE_AT + S4D_PE_EVERY * q: q for q in range(NG)}

    def chunk_cols(c):
        return range(c * CHUNK, min((c + 1) * CHUNK, S2), HALF)

    def pair(n):
        return ps[:, n:n + 2, :].rearrange("p b n -> p (b n)")

    with nc.Block() as block:
        @block.sync
        def _(sp):
            sp.dma_start(w_q[:], t["L0_xattn_Wq"]).then_inc(loaded, 16)
            sp.dma_start(b_q[:], t["L0_xattn_bq"].unsqueeze(1)).then_inc(loaded, 16)
            sp.dma_start(w_k[:, 0:DC], t["L0_Wk_T"]).then_inc(loaded, 16)
            sp.dma_start(w_k[:, DC:CA], t["L0_xattn_bk"].unsqueeze(1)).then_inc(loaded, 16)
            sp.wait_ge(ones_set, 1)
            sp.dma_start(w_v[0:DC, 0:D], t["L0_xattn_Wv"]).then_inc(w_v_loaded, 16)
            sp.dma_start(w_v[DC:CA, 0:D], t["L0_xattn_bv"].unsqueeze(0)).then_inc(w_v_loaded, 16)
            s4d_load(sp, t, s4d)

        @block.gpsimd
        def _(pool):
            link = chained(pool, chain_pool)
            link(pool.memset(w_v[:], 0.0))
            link(pool.memset(w_v[DC:CA, D:D + 1], 1.0))
            link(pool.memset(ctx_T[DC:CA, :], 1.0))
            link(pool.memset(ctx[:, :, DC:CA], 1.0))
            pool.memset(minus_top[:], 0.0).then_inc(ones_set, 1)
            s4d_pool(pool, s4d)

        @block.vector
        def _(dve):
            link = chained(dve, chain_dve)
            normalise(dve, link, g["x"], stats, mv, rstd, var_ready, root_ready, xn, xn_ready)
            dve.wait_ge(ones_set, 1)
            for i in range(NT):
                for c in range(N_CHUNK):
                    n = N_CHUNK * i + c
                    dve.wait_ge(score_done, n + 1)
                    width = min(CHUNK, S2 - c * CHUNK)
                    dve.reduce_max(tops[:, i, c:c + 1], pair(2 * (n % 4))[:, 0:width],
                                   AX).then_inc(max_read, 1)
            dve.wait_ge(max_read, NT * N_CHUNK)
            link(dve.reduce_max(top[:], tops[:], AX))
            dve.tensor_scalar(minus_top[:, :, DC], top[:], -1.0, None, ALU.mult).then_inc(top_ready, 1)
            s4d_vector(dve, link, s4d)
            dve.wait_ge(pv_done, KT)
            dve.tensor_copy(summed_c[:], pair(6)[0:CA, :]).then_inc(sum_ready, 1)
            for i in range(NT):
                dve.wait_ge(out_done, i + 1)
                bank = ps[:, i % 2, :]
                link(dve.reciprocal(share[:, i:i + 1], bank[:, D:D + 1]))
                dve.scalar_tensor_tensor(out=g["x"][:, i, :], in0=bank[:, 0:D], scalar=share[:, i:i + 1],
                                         in1=g["x"][:, i, :], op0=ALU.mult, op1=ALU.add).then_inc(sum_ready, 1)

        @block.tensor
        def _(pe):
            transpose_tiles(pe, xn, g["ident"][:], ps, xn_ready, xT_psum)
            pe.wait_ge(loaded, 16 * N_LOADS)
            for n in range(2):
                pe.wait_ge(xT_ready, n + 1)
                pe.matmul(ps[:, 2 + n, :], w_q[:], xT[:, n * HALF:(n + 1) * HALF],
                          start=True, stop=True).then_inc(q_done, 1)
            for n in range(2):
                pe.wait_ge(q_ready, n + 1)
                pe.matmul(ps[0:CA, 4 + n, :], w_k[:], qT[:, n * HALF:(n + 1) * HALF],
                          start=True, stop=True).then_inc(qc_done, 1)
            pe.wait_ge(ones_set, 1)
            pe.wait_ge(qc_ready, 2)
            pe.wait_ge(g["ctx_loaded"], 16 * 3)
            for i in range(NT):
                for c in range(N_CHUNK):
                    n = N_CHUNK * i + c
                    if n >= 4:
                        pe.wait_ge(max_read, n - 3)
                    for b, k in enumerate(chunk_cols(c)):
                        width = min(HALF, S2 - k)
                        last = pe.matmul(ps[:, 2 * (n % 4) + b, 0:width], qc[:, i * P:(i + 1) * P],
                                         ctx_T[:, k:k + width], start=True, stop=True)
                    last.then_inc(score_done, 1)
            pe.wait_ge(top_ready, 1)
            for n in range(2):
                pe.matmul(ps[0:CA, n, :], w_k[:], qT[:, n * HALF:(n + 1) * HALF], start=True, stop=False)
                for q in range(4):
                    last = pe.matmul(ps[0:CA, n, q * P:(q + 1) * P], minus_top[:, 4 * n + q, :],
                                     g["ident"][:], start=False, stop=q == 3)
                last.then_inc(shift_done, 1)
            pe.wait_ge(w_v_loaded, 16 * 2)

            def weighted(k):
                rows = P if k < KT - 1 else K_LAST
                pe.wait_ge(prob_ready, k + 1)
                for n in range(2):
                    last = pe.matmul(ps[0:CA, 6 + n, :], ctx[0:rows, k, :],
                                     prob[0:rows, k % 3, n * HALF:(n + 1) * HALF],
                                     start=k == 0, stop=k == KT - 1)
                last.then_inc(pv_done, 1)

            pe.wait_ge(shift_ready, 2)
            for k in range(KT):
                rows = P if k < KT - 1 else K_LAST
                if k in s4d_products:
                    s4d_tensor(pe, s4d, s4d_banks, s4d_products[k])
                if k >= 2:
                    pe.wait_ge(prob_ready, k - 1)
                for n in range(2):
                    last = pe.matmul(ps[0:rows, 2 * (k % 2) + n, :], ctx_T[:, k * P:k * P + rows],
                                     qc_shifted[:, n * HALF:(n + 1) * HALF], start=True, stop=True)
                last.then_inc(prob_psum, 1)
                if k >= 1:
                    weighted(k - 1)
            weighted(KT - 1)
            pe.wait_ge(sum_ready, 1)
            for i in range(NT):
                if i >= 2:
                    pe.wait_ge(sum_ready, i)
                pe.matmul(ps[:, i % 2, 0:D + 1], summed_c[:, i * P:(i + 1) * P], w_v[:],
                          start=True, stop=True).then_inc(out_done, 1)

        @block.scalar
        def _(act):
            root(act, rstd, 1, var_ready, root_ready)
            act.wait_ge(loaded, 16 * N_LOADS)
            for n in range(2):
                act.wait_ge(xT_psum, 4 * (n + 1))
                act.activation(xT[:, n * HALF:(n + 1) * HALF], ps[:, n, :], ACT.Copy).then_inc(xT_ready, 1)
            for n in range(2):
                act.wait_ge(q_done, n + 1)
                act.activation(qT[:, n * HALF:(n + 1) * HALF], ps[:, 2 + n, :], ACT.Identity,
                               bias=b_q[:, 0:1]).then_inc(q_ready, 1)
            for n in range(2):
                act.wait_ge(qc_done, n + 1)
                act.activation(qc[:, n * HALF:(n + 1) * HALF], ps[0:CA, 4 + n, :],
                               ACT.Copy).then_inc(qc_ready, 1)
            s4d_scalar(act, s4d, 0)
            for n in range(2):
                act.wait_ge(shift_done, n + 1)
                act.activation(qc_shifted[:, n * HALF:(n + 1) * HALF], ps[0:CA, n, :],
                               ACT.Copy).then_inc(shift_ready, 1)
            for k in range(KT):
                rows = P if k < KT - 1 else K_LAST
                if k in s4d_steps:
                    s4d_scalar(act, s4d, s4d_steps[k])
                act.wait_ge(prob_psum, k + 1)
                if k >= 3:
                    act.wait_ge(pv_done, k - 2)
                act.activation(prob[0:rows, k % 3, :], pair(2 * (k % 2))[0:rows, :],
                               ACT.Exp).then_inc(prob_ready, 1)
            s4d_copy(act, s4d, s4d_banks)



def threshold_experts(nc, g, t, m):
    NE = 8
    THRESHOLD = 0.1
    ps = g["psum"]
    w_e = m.sb("w_e", [P, NE, D])
    b_e = m.sb("b_e", [NE, D])
    w_g = m.sb("w_g", [P, NE])
    b_g = m.sb("b_g", [1, NE])
    stats = m.sb("stats", [P, NT, 6])
    mv = m.sb("mv", [P, NT, 2])
    rstd = m.sb("rstd", [P, NT, 1])
    xn = m.sb("xn", [P, NT, D])
    xT = m.sb("xT", [P, S])
    gates = m.sb("gates", [P, NT, NE])
    kept = m.sb("kept", [P, NT, NE])
    best = m.sb("best", [P, NT])
    total = m.sb("total", [P, NT])
    none = m.sb("none", [P, NT])
    scaled = m.sb("scaled", [P, 2, NE, D])
    mixed = m.sb("mixed", [P, 2, D])
    kept_T = m.sb("kept_T", [NE, S])
    kept_ready, kT_psum, kT_ready, bias_done = (
        m.sem(n) for n in ("kept_ready", "kT_psum", "kT_ready", "bias_done"))

    loaded, chain_dve = m.sem("loaded"), m.sem("chain_dve")
    var_ready, root_ready, xn_ready, xT_psum, xT_ready = (
        m.sem(n) for n in ("var_ready", "root_ready", "xn_ready", "xT_psum", "xT_ready"))
    gate_done, shifted, exp_ready, expert_done, scaled_ready = (
        m.sem(n) for n in ("gate_done", "shifted", "exp_ready", "expert_done", "scaled_ready"))
    N_LOADS = 4

    def spread(v):
        return v.unsqueeze(2).to_broadcast([P, NT, NE])

    with nc.Block() as block:
        @block.sync
        def _(sp):
            sp.dma_start(w_e[:], t["L0_ffn_expert_w"].rearrange("e p d -> p e d")).then_inc(loaded, 16)
            sp.dma_start(b_e[:], t["L0_ffn_expert_b"]).then_inc(loaded, 16)
            sp.dma_start(w_g[:], t["L0_ffn_gate_w"]).then_inc(loaded, 16)
            sp.dma_start(b_g[:], t["L0_ffn_gate_b"].unsqueeze(0)).then_inc(loaded, 16)

        @block.vector
        def _(dve):
            link = chained(dve, chain_dve)
            normalise(dve, link, g["x"], stats, mv, rstd, var_ready, root_ready, xn, xn_ready)
            dve.wait_ge(gate_done, 1)
            logits = ps[:, 6, 0:NT * NE].rearrange("p (i e) -> p i e", e=NE)
            link(dve.reduce_max(best[:], logits, AX))
            dve.tensor_tensor(gates[:], logits, spread(best[:]), ALU.subtract).then_inc(shifted, 1)
            dve.wait_ge(exp_ready, 1)
            link(dve.reduce_sum(total[:], gates[:], AX))
            link(dve.reciprocal(total[:], total[:]))
            link(dve.tensor_tensor(gates[:], gates[:], spread(total[:]), ALU.mult))
            link(dve.scalar_tensor_tensor(out=kept[:], in0=gates[:], scalar=THRESHOLD, in1=gates[:],
                                          op0=ALU.is_ge, op1=ALU.mult))
            link(dve.reduce_sum(total[:], kept[:], AX))
            link(dve.tensor_scalar(none[:], total[:], 0.0, None, ALU.is_equal))
            link(dve.tensor_tensor(total[:], total[:], none[:], ALU.add))
            link(dve.reciprocal(total[:], total[:]))
            dve.tensor_tensor(kept[:], kept[:], spread(total[:]), ALU.mult).then_inc(kept_ready, 1)
            dve.wait_ge(kept_ready, 1)
            for i in range(NT):
                dve.wait_ge(expert_done, i + 1)
                b = 2 * (i % 3)
                out = ps[:, b:b + 2, :].rearrange("p b (e d) -> p (b e) d", d=D)
                dve.tensor_tensor(scaled[:, i % 2, :, :], out,
                                  kept[:, i, :].unsqueeze(2).to_broadcast([P, NE, D]),
                                  ALU.mult).then_inc(scaled_ready, 1)
                dve.wait_ge(scaled_ready, i + 1)
                link(dve.reduce_sum(mixed[:, i % 2, :], scaled[:, i % 2, :, :].rearrange("p e d -> p d e"), AX))
                link(dve.tensor_tensor(g["x"][:, i, :], g["x"][:, i, :], mixed[:, i % 2, :], ALU.add))
            dve.wait_ge(bias_done, 1)
            link(dve.tensor_tensor(g["x"][:], g["x"][:],
                                   ps[:, 6:8, :].rearrange("p b (i d) -> p (b i) d", d=D), ALU.add))

        @block.tensor
        def _(pe):
            transpose_tiles(pe, xn, g["ident"][:], ps, xn_ready, xT_psum)
            pe.wait_ge(loaded, 16 * N_LOADS)
            for i in range(NT):
                pe.wait_ge(xT_ready, i // 4 + 1)
                cols = slice(i * NE, (i + 1) * NE)
                pe.matmul(ps[:, 6, cols], xT[:, i * P:(i + 1) * P], w_g[:], start=True, stop=False)
                last = pe.matmul(ps[:, 6, cols], g["ones"][:, 0:P], b_g[:], start=False, stop=True)
            last.then_inc(gate_done, 1)
            for i in range(NT):
                if i >= 3:
                    pe.wait_ge(scaled_ready, i - 2)
                for h in range(2):
                    bank = ps[:, 2 * (i % 3) + h, :]
                    last = pe.matmul(bank, xT[:, i * P:(i + 1) * P],
                                     w_e[:, 4 * h:4 * h + 4, :].rearrange("p e d -> p (e d)"),
                                     start=True, stop=True)
                last.then_inc(expert_done, 1)
                if i == 2:
                    pe.wait_ge(kept_ready, 1)
                    for k in range(NT):
                        last = pe.transpose(ps[0:NE, 6 + k // 4, (k % 4) * P:(k % 4 + 1) * P],
                                            kept[:, k, :], g["ident"][:])
                    last.then_inc(kT_psum, 1)
            pe.wait_ge(kT_ready, 1)
            for i in range(NT):
                last = pe.matmul(ps[:, 6 + i // 4, (i % 4) * D:(i % 4 + 1) * D], kept_T[:, i * P:(i + 1) * P],
                                 b_e[:], start=True, stop=True)
            last.then_inc(bias_done, 1)

        @block.scalar
        def _(act):
            root(act, rstd, 1, var_ready, root_ready)
            for n in range(2):
                act.wait_ge(xT_psum, 4 * (n + 1))
                act.activation(xT[:, n * HALF:(n + 1) * HALF], ps[:, n, :], ACT.Copy).then_inc(xT_ready, 1)
            act.wait_ge(shifted, 1)
            act.activation(gates[:], gates[:], ACT.Exp).then_inc(exp_ready, 1)
            act.wait_ge(kT_psum, 1)
            act.activation(kept_T[:], ps[0:NE, 6:8, :].rearrange("p b n -> p (b n)"),
                           ACT.Copy).then_inc(kT_ready, 1)




def causal_attention(nc, g, t, m):
    SCALE = float(D) ** -0.5
    ps = g["psum"]
    w = m.sb("w", [P, 3, D])
    tri_f = m.sb("tri_f", [P, P])
    stats = m.sb("stats", [P, NT, 6])
    mv = m.sb("mv", [P, NT, 2])
    rstd = m.sb("rstd", [P, NT, 1])
    xn = m.sb("xn", [P, NT, D])
    xT = m.sb("xT", [P, S])
    qT = m.sb("qT", [P, S])
    kT = m.sb("kT", [P, S])
    v = m.sb("v", [P, NT, D])
    penalty = m.sb("penalty", [P, S])
    score = m.sb("score", [P, 2, S])
    low = m.sb("low", [P, NT])
    total = m.sb("total", [P, NT])
    share = m.sb("share", [P, NT])
    pT = m.sb("pT", [P, 2, S])

    loaded, chain_dve = m.sem("loaded"), m.sem("chain_dve")
    var_ready, root_ready, xn_ready, xT_psum, xT_ready = (
        m.sem(n) for n in ("var_ready", "root_ready", "xn_ready", "xT_psum", "xT_ready"))
    qkv_done, qkv_ready, score_done, low_ready, exp_ready, pT_psum, pT_ready, out_done, added = (
        m.sem(n) for n in ("qkv_done", "qkv_ready", "score_done", "low_ready", "exp_ready",
                           "pT_psum", "pT_ready", "out_done", "added"))
    N_LOADS = 4

    def wide(b, n):
        return ps[:, b:b + 2, :].rearrange("p b n -> p (b n)")[:, 0:n]

    with nc.Block() as block:
        @block.sync
        def _(sp):
            for k, name in enumerate(("L1_WQ_T", "L1_WK_T", "L1_WV_T")):
                sp.dma_start(w[:, k, :], t[name]).then_inc(loaded, 16)
            sp.dma_start(tri_f[:], t["above_diagonal"]).then_inc(loaded, 16)

        @block.vector
        def _(dve):
            link = chained(dve, chain_dve)
            normalise(dve, link, g["x"], stats, mv, rstd, var_ready, root_ready, xn, xn_ready)
            def finish(i):
                dve.wait_ge(exp_ready, i + 1)
                link(dve.reciprocal(share[:, i:i + 1], total[:, i:i + 1]))
                dve.wait_ge(out_done, i + 1)
                dve.scalar_tensor_tensor(out=g["x"][:, i, :], in0=ps[:, 6 + i % 2, 0:D],
                                         scalar=share[:, i:i + 1], in1=g["x"][:, i, :],
                                         op0=ALU.mult, op1=ALU.add).then_inc(added, 1)

            for i in range(NT):
                n = (i + 1) * P
                b = 2 * (i % 2)
                dve.wait_ge(score_done, i + 1)
                link(dve.tensor_scalar(penalty[:, 0:n], wide(b, n), 0.0, NEG, ALU.is_equal, ALU.mult))
                if i >= 2:
                    dve.wait_ge(pT_psum, i - 1)
                link(dve.tensor_tensor(score[:, i % 2, 0:n], wide(b, n), penalty[:, 0:n], ALU.add))
                link(dve.reduce_max(low[:, i:i + 1], score[:, i % 2, 0:n], AX))
                dve.tensor_scalar(low[:, i:i + 1], low[:, i:i + 1], -SCALE, None,
                                  ALU.mult).then_inc(low_ready, 1)
                if i >= 2:
                    finish(i - 2)
            finish(NT - 2)
            finish(NT - 1)

        @block.tensor
        def _(pe):
            transpose_tiles(pe, xn, g["ident"][:], ps, xn_ready, xT_psum)
            pe.wait_ge(loaded, 16 * N_LOADS)
            pe.wait_ge(xT_ready, 2)
            for k in range(2):
                for n in range(2):
                    last = pe.matmul(ps[:, 2 + 2 * k + n, :], w[:, k, :], xT[:, n * HALF:(n + 1) * HALF],
                                     start=True, stop=True)
                last.then_inc(qkv_done, 1)
            for i in range(NT):
                last = pe.matmul(ps[:, 6 + i // 4, (i % 4) * D:(i % 4 + 1) * D], xT[:, i * P:(i + 1) * P],
                                 w[:, 2, :], start=True, stop=True)
            last.then_inc(qkv_done, 1)

            def scores(i):
                n = (i + 1) * P
                if i >= 2:
                    pe.wait_ge(low_ready, i - 1)
                for k in range(0, n, HALF):
                    width = min(HALF, n - k)
                    bank = 2 * (i % 2) + k // HALF
                    last = pe.matmul(ps[:, bank, 0:width], qT[:, i * P:(i + 1) * P], kT[:, k:k + width],
                                     start=True, stop=k + width < n)
                a = (i % 4) * P
                pe.matmul(ps[:, bank, a:a + P], g["ident"][:], tri_f[:], start=False,
                          stop=True).then_inc(score_done, 1)

            def turn(i):
                n = i + 1
                pe.wait_ge(exp_ready, i + 1)
                if i >= 1:
                    pe.wait_ge(pT_ready, i)
                for k in range(n):
                    last = pe.transpose(ps[:, 4 + k // 4, (k % 4) * P:(k % 4 + 1) * P],
                                        score[:, i % 2, k * P:(k + 1) * P], g["ident"][:])
                last.then_inc(pT_psum, 1)

            def values(i):
                n = i + 1
                if i >= 2:
                    pe.wait_ge(added, i - 1)
                pe.wait_ge(pT_ready, i + 1)
                for k in range(n):
                    last = pe.matmul(ps[:, 6 + i % 2, 0:D], pT[:, i % 2, k * P:(k + 1) * P], v[:, k, :],
                                     start=k == 0, stop=k == n - 1)
                last.then_inc(out_done, 1)

            pe.wait_ge(qkv_ready, 3)
            scores(0)
            scores(1)
            for i in range(NT):
                turn(i)
                if i + 2 < NT:
                    scores(i + 2)
                if i >= 1:
                    values(i - 1)
            values(NT - 1)

        @block.scalar
        def _(act):
            root(act, rstd, 1, var_ready, root_ready)
            for n in range(2):
                act.wait_ge(xT_psum, 4 * (n + 1))
                act.activation(xT[:, n * HALF:(n + 1) * HALF], ps[:, n, :], ACT.Copy).then_inc(xT_ready, 1)
            for k, dst in enumerate((qT[:], kT[:], v[:].rearrange("p i d -> p (i d)"))):
                act.wait_ge(qkv_done, k + 1)
                act.activation(dst, wide(2 + 2 * k, S), ACT.Copy).then_inc(qkv_ready, 1)

            def exps(i):
                n = (i + 1) * P
                act.wait_ge(low_ready, i + 1)
                act.activation(score[:, i % 2, 0:n], score[:, i % 2, 0:n], ACT.Exp, scale=SCALE,
                               bias=low[:, i:i + 1], accum_out=total[:, i:i + 1]).then_inc(exp_ready, 1)

            def copy_out(i):
                n = (i + 1) * P
                act.wait_ge(pT_psum, i + 1)
                if i >= 2:
                    act.wait_ge(out_done, i - 1)
                act.activation(pT[:, i % 2, 0:n], wide(4, n), ACT.Copy).then_inc(pT_ready, 1)

            exps(0)
            for i in range(1, NT):
                exps(i)
                copy_out(i - 1)
            copy_out(NT - 1)



NH, DH = 4, 32
TOP = 32
MASKED = 2.0 ** 50
GONE = -3e38
UNITS = [(c, min(CHUNK, S2 - c)) for c in range(0, S2, CHUNK)]


def segments(width):
    n = -(-width // 171)
    edges = [round(k * width / n) for k in range(n + 1)]
    return list(zip(edges[:-1], edges[1:]))


PIECES = [(c, min(HALF, S2 - c)) for c in range(0, S2, HALF)]
N_SEG = sum(len(segments(w)) for _, w in PIECES)


def film_context(nc, g, t, m):
    a = {"qa": m.sb("qa", [P, NT, NH, P], BF16), "qb": m.sb("qb", [P, NT, NH, P], BF16),
         "ka": m.sb("ka", [P, NH, S2], BF16), "kb": m.sb("kb", [P, NH, S2], BF16),
         "top": m.sb("top", [P, NT * NH, TOP]), "flags": m.sb("flags", [P, NT * NH]),
         "count": m.sb("count", [1, NT * NH + 1], mybir.dt.int32)}
    for part in (split_heads, search_and_weigh, search_general, weigh_again):
        with ExitStack() as ctx:
            part(nc, g, t, Memory(nc, ctx, part.__name__), a)


def split_heads(nc, g, t, m, a):
    ps = g["psum"]
    qa, qb, ka, kb = a["qa"], a["qb"], a["ka"], a["kb"]
    ROW = 3 * DH
    RING = 3
    w_q = m.sb("w_q", [P, NH, P])
    w_k = m.sb("w_k", [DC, NH, P])
    ctx_T = m.sb("ctx_T", [DC, RING, CHUNK])
    MR = 4
    mask = m.sb("mask", [MR, S2 // MR], U8)
    masking = m.sb("masking", [MR, S2 // MR], BF16)
    stats = m.sb("stats", [P, NT, 6])
    mv = m.sb("mv", [P, NT, 2])
    rstd = m.sb("rstd", [P, NT, 1])
    xT = m.sb("xT", [P, S])
    q = m.sb("q", [P, S])
    hi = m.sb("hi", [P, S], BF16)
    mid = m.sb("mid", [P, S], BF16)
    RESTS = 3
    rest = m.sb("rest", [P, RESTS, S])
    k_hi = m.sb("k_hi", [P, 2, S], BF16)

    loaded, mask_loaded = m.sem("loaded"), m.sem("mask_loaded")
    masking_ready, masked = m.sem("masking_ready"), m.sem("masked")
    ctx_loaded = [m.sem(f"ctx_loaded_{r}") for r in range(RING)]
    chain_dve, chain_pool = m.sem("chain_dve"), m.sem("chain_pool")
    var_ready, root_ready, xn_ready, xT_psum, xT_ready = (
        m.sem(n) for n in ("var_ready", "root_ready", "xn_ready", "xT_psum", "xT_ready"))
    q_done, q_ready, q_split, k_done, k_his, k_rest, k_mids, k_low, k_low_dve = (
        m.sem(n) for n in ("q_done", "q_ready", "q_split", "k_done", "k_his", "k_rest", "k_mids", "k_low",
                           "k_low_dve"))
    xn = g["xn"]

    def pair(n):
        return ps[:, 2 * n:2 * n + 2, :].rearrange("p b n -> p (b n)")

    units = [(h, c, w) for c, w in UNITS for h in range(NH)]

    def on_pool(n):
        return n % 7 != 6

    def lows_on_pool(n):
        return sum(on_pool(k) for k in range(n))

    def low(eng, n):
        h, c, w = units[n]
        part = kb[2 * DH:P, h, c:c + w]
        return eng.tensor_tensor(part, rest[2 * DH:P, n % RESTS, 0:w], part, ALU.subtract)

    with nc.Block() as block:
        @block.sync
        def _(sp):
            def load_context(which):
                for u in which:
                    c, w = UNITS[u]
                    if u >= RING:
                        sp.wait_ge(k_done, NH * (u - RING + 1))
                    sp.dma_start(ctx_T[:, u % RING, 0:w], t["ctx_T"][:, c:c + w]
                                 ).then_inc(ctx_loaded[u % RING], 16)

            sp.dma_start(w_q[:], t["L1_Wq_rep"].rearrange("p (h c) -> p h c", c=P)).then_inc(loaded, 16)
            sp.dma_start(w_k[:], t["L1_Wk_rep"].rearrange("p (h c) -> p h c", c=P)).then_inc(loaded, 16)
            sp.dma_start(mask[:], t["vision_mask"].rearrange("o (r c) -> (o r) c", r=MR)).then_inc(mask_loaded, 16)
            load_context(range(RING))
            sp.wait_ge(masking_ready, 1)
            for h in range(NH):
                for r in range(MR):
                    cols = slice(r * (S2 // MR), (r + 1) * (S2 // MR))
                    sp.dma_start(ka[ROW:ROW + 1, h, cols], masking[r:r + 1, :]).then_inc(masked, 16)
            load_context(range(RING, len(UNITS)))
            sp.wait_ge(masked, 16 * NH * MR)

        @block.vector
        def _(dve):
            link = chained(dve, chain_dve)
            normalise(dve, link, g["x"], stats, mv, rstd, var_ready, root_ready, xn, xn_ready)
            for h in range(NH):
                dve.wait_ge(q_ready, h + 1)
                link(dve.tensor_copy(hi[:], q[:]))
                link(dve.tensor_tensor(rest[:, 0, :], q[:], hi[:], ALU.subtract))
                link(dve.tensor_copy(mid[:], rest[:, 0, :]))

                def rows(x):
                    return x.rearrange("p (i c) -> p i c", c=P)

                for k, src in enumerate((hi, mid, hi, mid)):
                    part = slice(k * DH, (k + 1) * DH)
                    dve.tensor_copy(qb[part, :, h, :], rows(src[part, :]))
                for k, src in enumerate((hi, mid)):
                    part = slice(k * DH, (k + 1) * DH)
                    dve.tensor_copy(qa[part, :, h, :], rows(src[part, :]))
                part = slice(2 * DH, 3 * DH)
                last = dve.tensor_tensor(qa[part, :, h, :], rows(rest[part, 0, :]), rows(mid[part, :]),
                                         ALU.subtract)
                link(last)
                dve.engine_nop().then_inc(q_split, 1)
            for n, (h, c, w) in enumerate(units):
                dve.wait_ge(k_his, 2 * (n + 1))
                if n >= RESTS:
                    done = n - RESTS + 1
                    if on_pool(done - 1):
                        dve.wait_ge(k_low, lows_on_pool(done))
                    else:
                        dve.wait_ge(k_low_dve, done - lows_on_pool(done))
                dve.tensor_tensor(rest[:, n % RESTS, 0:w], pair(n % 4)[:, 0:w], k_hi[:, n % 2, 0:w],
                                  ALU.subtract).then_inc(k_rest, 1)
                dve.wait_ge(k_rest, n + 1)
                dve.tensor_copy(kb[:, h, c:c + w], rest[:, n % RESTS, 0:w]).then_inc(k_mids, 1)
                if not on_pool(n):
                    dve.wait_ge(k_mids, n + 1)
                    low(dve, n).then_inc(k_low_dve, 1)

        @block.tensor
        def _(pe):
            transpose_tiles(pe, xn, g["ident"][:], ps, xn_ready, xT_psum)
            pe.wait_ge(loaded, 32)
            pe.wait_ge(xT_ready, 2)
            for h in range(NH):
                if h >= 2:
                    pe.wait_ge(q_ready, h - 1)
                for n in range(2):
                    last = pe.matmul(ps[:, 4 + 2 * (h % 2) + n, :], w_q[:, h, :],
                                     xT[:, n * HALF:(n + 1) * HALF], start=True, stop=True)
                last.then_inc(q_done, 1)
            pe.wait_ge(q_ready, NH)
            for n, (h, c, w) in enumerate(units):
                u = n // NH
                pe.wait_ge(ctx_loaded[u % RING], 16 * (u // RING + 1))
                if n >= 4:
                    pe.wait_ge(k_rest, n - 3)
                for b in range(0, w, HALF):
                    cols = min(HALF, w - b)
                    last = pe.matmul(ps[:, 2 * (n % 4) + b // HALF, 0:cols], w_k[:, h, :],
                                     ctx_T[:, u % RING, b:b + cols], start=True, stop=True)
                last.then_inc(k_done, 1)

        @block.scalar
        def _(act):
            root(act, rstd, 1, var_ready, root_ready)
            for n in range(2):
                act.wait_ge(xT_psum, 4 * (n + 1))
                act.activation(xT[:, n * HALF:(n + 1) * HALF], ps[:, n, :], ACT.Copy).then_inc(xT_ready, 1)
            for h in range(NH):
                act.wait_ge(q_done, h + 1)
                if h >= 1:
                    act.wait_ge(q_split, h)
                act.activation(q[:], pair(2 + h % 2), ACT.Copy,
                               scale=float(DH) ** -0.5).then_inc(q_ready, 1)
            part = slice(0, 3 * DH)
            for n, (h, c, w) in enumerate(units):
                act.wait_ge(k_done, n + 1)
                if n >= 2:
                    act.wait_ge(k_rest, n - 1)
                act.activation(k_hi[:, n % 2, 0:w], pair(n % 4)[:, 0:w], ACT.Copy).then_inc(k_his, 1)
                act.activation(ka[part, h, c:c + w], pair(n % 4)[part, 0:w], ACT.Copy).then_inc(k_his, 1)

        @block.gpsimd
        def _(pool):
            link = chained(pool, chain_pool)
            pool.wait_ge(mask_loaded, 16)
            pool.tensor_scalar(masking[:], mask[:], 1.0, MASKED, ALU.subtract,
                               ALU.mult).then_inc(masking_ready, 1)
            link(pool.memset(qa[ROW:ROW + 1, :, :, :], 1.0))
            for n in range(len(units)):
                if on_pool(n):
                    pool.wait_ge(k_mids, n + 1)
                    low(pool, n).then_inc(k_low, 1)


def score_unit(pe, a, ps, bank, tile, h, c, w):
    ROWS = 3 * DH + 1
    for b in range(0, w, HALF):
        cols = min(HALF, w - b)
        out = ps[:, bank + b // HALF, 0:cols]
        pe.matmul(out, a["qa"][0:ROWS, tile, h, :], a["ka"][0:ROWS, h, c + b:c + b + cols],
                  start=True, stop=False)
        last = pe.matmul(out, a["qb"][:, tile, h, :], a["kb"][:, h, c + b:c + b + cols],
                         start=False, stop=True)
    return last


def search_general(nc, g, t, m, a):
    ps = g["psum"]
    full = m.sb("full", [P, S2])
    best = m.sb("best", [P, TOP])
    column = m.sb("column", [P, 1])
    count = a["count"]
    in_all = m.sb("in_all", [1, 1])
    ones_set, counted, count_ready, score_done, copied, chain_dve, passed, passed_pe = (
        m.sem(n) for n in ("ones_set", "counted", "count_ready", "score_done", "copied", "chain_dve",
                           "passed", "passed_pe"))
    NU = len(UNITS)

    with nc.Block() as block:
        @block.tensor
        def _(pe):
            pe.wait_ge(ones_set, 1)
            pe.matmul(ps[0:1, 7, 0:NT * NH], column[:], a["flags"][:], start=True,
                      stop=True).then_inc(counted, 1)
            pe.wait_ge(count_ready, 1)
            any_flagged = pe.value_load(count[0:1, NT * NH:NT * NH + 1])
            with pe.If(any_flagged > 0):
                with pe.Fori(0, NT) as i:
                    for h in range(NH):
                        flagged = pe.value_load(count[0:1, bass.ds(i * NH + h, 1)])
                        base = i * NH * NU + h * NU
                        with pe.If(flagged > 0):
                            for u, (c, w) in enumerate(UNITS):
                                bank = 2 * (u % 2)
                                wait_in_loop(pe, copied, base + 1 + max(u - 1, 0), passed_pe)
                                score_unit(pe, a, ps, bank, i, h, c, w).then_inc(score_done, 1)
                        with pe.Else():
                            pe.sem_inc(score_done, NU)

        @block.vector
        def _(dve):
            dve.memset(column[:], 1.0).then_inc(ones_set, 1)
            dve.wait_ge(counted, 1)
            dve.tensor_copy(count[:, 0:NT * NH], ps[0:1, 7, 0:NT * NH]).then_inc(copied, 1)
            dve.reduce_sum(in_all[:], ps[0:1, 7, 0:NT * NH], AX).then_inc(copied, 1)
            dve.wait_ge(copied, 2)
            dve.sem_clear(copied)
            dve.tensor_copy(count[:, NT * NH:], in_all[:]).then_inc(count_ready, 1)
            dve.wait_ge(count_ready, 1)
            dve.engine_nop().then_inc(copied, 1)
            any_flagged = dve.value_load(count[0:1, NT * NH:NT * NH + 1])
            with dve.If(any_flagged > 0):
                with dve.Fori(0, NT) as i:
                    for h in range(NH):
                        flagged = dve.value_load(count[0:1, bass.ds(i * NH + h, 1)])
                        units = i * NH * NU + h * NU
                        with dve.If(flagged > 0):
                            for u, (c, w) in enumerate(UNITS):
                                bank = 2 * (u % 2)
                                wait_in_loop(dve, score_done, units + u + 1, passed)
                                dve.tensor_copy(full[:, c:c + w],
                                                ps[:, bank:bank + 2, :].rearrange("p b n -> p (b n)")[:, 0:w]
                                                ).then_inc(copied, 1)
                            wait_in_loop(dve, copied, units + NU + 1, passed)
                            dve.sem_clear(chain_dve)
                            link = chained(dve, chain_dve)
                            for r in range(TOP // 8):
                                eight = best[:, 8 * r:8 * r + 8]
                                link(dve.max(eight, full[:]))
                                if r < TOP // 8 - 1:
                                    link(dve.match_replace(full[:], eight, full[:], GONE))
                            link(dve.tensor_copy(a["top"][:, bass.ds(i * NH + h, 1), :], best[:].unsqueeze(1)))
                        with dve.Else():
                            dve.sem_inc(copied, NU)


def search_and_weigh(nc, g, t, m, a):
    weigh_program(nc, g, t, m, a, True)


def weigh_again(nc, g, t, m, a):
    weigh_program(nc, g, t, m, a, False)


def weigh_program(nc, g, t, m, a, searching):
    ps = g["psum"]
    NCH = len(PIECES)
    STEPS = NT * NCH
    LAG = NCH + 1 if searching else 1
    SEARCH_BANKS = WEIGH_BANKS = 3
    RING, MEANS = 4, 3
    MASK_LAG = 2
    TURN_LAG, CONTEXT_LAG = 3, 4
    kept = m.sb("kept", [P, 2, N_SEG, 8])
    eighth = m.sb("eighth", [P, 2])
    shifted = m.sb("shifted", [P, NH, TOP])
    total = m.sb("total", [P, NH])
    bias, least = m.sb("bias", [P, 2, NH]), m.sb("least", [P, 2, NH])
    e = m.sb("e", [P, RING, NH, HALF])
    keep = m.sb("keep", [P, 2, HALF])
    below = m.sb("below", [P, 2])
    mean = m.sb("mean", [P, MEANS, HALF])
    mean_T = m.sb("mean_T", [P, 2, HALF])
    mask8, mask = m.sb("mask8", [P, NT], U8), m.sb("mask", [P, NT])
    w_v = m.sb("w_v", [DC, D])
    c_tok = g["c_T"][:, 0:NT * DC].rearrange("p (i c) -> p i c", c=DC)
    c_ctx = e[0:DC, 0, 0:2, :]
    loaded, chain_dve, chain_pool = m.sem("loaded"), m.sem("chain_dve"), m.sem("chain_pool")
    chain_act, keep_ready, summed_ready = m.sem("chain_act"), m.sem("keep_ready"), m.sem("summed_ready")
    search_done, searched, found, flagged, exp_done, summed, ln_done, bias_ready, least_ready, mask_ready = (
        m.sem(n) for n in ("search_done", "searched", "found", "flagged", "exp_done", "summed", "ln_done",
                           "bias_ready", "least_ready", "mask_ready"))
    score_done, e_ready, w_ready, mean_ready, mT_psum, mT_ready, pv_done = (
        m.sem(n) for n in ("score_done", "e_ready", "w_ready", "mean_ready", "mT_psum", "mT_ready",
                           "pv_done"))
    tok_ready, cc_psum, cc_ready, c_done = (
        m.sem(n) for n in ("tok_ready", "cc_psum", "cc_ready", "c_done"))

    def tiles(w):
        return [(b, min(P, w - b)) for b in range(0, w, P)]

    def masks_done(n):
        return (NH - 1) * n + max(0, n - (NT - 1) * NCH)

    def last_head_on_vector(n):
        return masks_done(n + 1) - masks_done(n) == NH

    def search_piece(r):
        if not searching or r >= STEPS * NH:
            return None
        i, s = divmod(r, NH * NCH)
        return i, s // NCH, s % NCH

    def limits_tile(G):
        i, u = divmod(G - LAG + 1, NCH)
        return i if u == 0 and 0 <= i < NT else None

    def vector(dve):
        link = chained(dve, chain_dve)

        def take_largest(i, h):
            j, k = i * NH + h, h % 2
            all_kept = kept[:, k, :, :].rearrange("p s e -> p (s e)")
            link(dve.reduce_max(eighth[:, k:k + 1], kept[:, k, :, 7], AX))
            for r in range(TOP // 8):
                eight = a["top"][:, j, 8 * r:8 * r + 8]
                link(dve.max(eight, all_kept))
                if r < TOP // 8 - 1:
                    link(dve.match_replace(all_kept, eight, all_kept, GONE))
            dve.tensor_tensor(a["flags"][:, j:j + 1], eighth[:, k:k + 1], a["top"][:, j, TOP - 1:TOP],
                              ALU.is_gt).then_inc(flagged, 1)

        dve.wait_ge(loaded, 32)
        dve.tensor_copy(mask[:], mask8[:]).then_inc(mask_ready, 1)
        for G in range(STEPS + LAG + 1):
            for sub in range(NH):
                r = NH * G + sub
                if search_piece(r):
                    i, h, u = search_piece(r)
                    dve.wait_ge(search_done, r + 1)
                    first = sum(len(segments(w)) for _, w in PIECES[:u])
                    bank = ps[:, r % SEARCH_BANKS, :]
                    for s, (lo, hi) in enumerate(segments(PIECES[u][1])):
                        last = dve.max(kept[:, h % 2, first + s, :], bank[:, lo:hi])
                    last.then_inc(searched, 1)
                    if u == NCH - 1:
                        dve.wait_ge(searched, r + 1)
                        take_largest(i, h)
                i = limits_tile(G)
                if i is not None:
                    top = a["top"][:, i * NH:(i + 1) * NH, :]
                    if sub == 0:
                        dve.tensor_tensor(shifted[:], top, top[:, :, 0:1].to_broadcast([P, NH, TOP]),
                                          ALU.subtract).then_inc(found, 1)
                    elif sub == 1:
                        dve.wait_ge(exp_done, i + 1)
                        dve.reduce_sum(total[:], shifted[:], AX).then_inc(summed, 1)
                    elif sub == 3:
                        b = bias[:, i % 2, :]
                        dve.wait_ge(ln_done, i + 1)
                        link(dve.tensor_tensor(b, total[:], top[:, :, 0], ALU.add))
                        link(dve.tensor_scalar(b, b, -1.0, None, ALU.mult))
                        dve.tensor_tensor(least[:, i % 2, :], top[:, :, TOP - 1], b,
                                          ALU.add).then_inc(bias_ready, 1)
                n, h = divmod(NH * (G - LAG) + sub - MASK_LAG, NH)
                if 0 <= n < STEPS and (h < NH - 1 or last_head_on_vector(n)):
                    i, u = divmod(n, NCH)
                    w = e[:, n % RING, h, 0:PIECES[u][1]]
                    if u == 0 and h == 0:
                        dve.wait_ge(least_ready, i + 1)
                    dve.wait_ge(e_ready, NH * n + h + 1)
                    dve.scalar_tensor_tensor(out=w, in0=w, scalar=least[:, i % 2, h:h + 1], in1=w,
                                             op0=ALU.is_ge, op1=ALU.mult).then_inc(w_ready, 1)
                    if h == NH - 1:
                        dve.wait_ge(w_ready, masks_done(n + 1))
                        other = e[:, n % RING, h - 1, 0:PIECES[u][1]]
                        dve.tensor_tensor(other, other, w, ALU.add).then_inc(summed_ready, 1)
        if searching:
            dve.wait_ge(flagged, NT * NH)

    def pool_sums(pool):
        link = chained(pool, chain_pool)
        for n in range(STEPS):
            width = PIECES[n % NCH][1]
            w = [e[:, n % RING, h, 0:width] for h in range(NH)]
            out = mean[:, n % MEANS, 0:width]
            if not last_head_on_vector(n):
                pool.wait_ge(keep_ready, n + 1)
                link(pool.tensor_tensor(w[3], w[3], keep[:, n % 2, 0:width], ALU.mult))
            pool.wait_ge(w_ready, masks_done(n + 1))
            if n >= MEANS:
                pool.wait_ge(mT_psum, n - MEANS + 1)
            link(pool.tensor_tensor(out, w[0], w[1], ALU.add))
            if last_head_on_vector(n):
                pool.wait_ge(summed_ready, n + 1 - (NT - 1) * NCH)
            else:
                link(pool.tensor_tensor(w[2], w[2], w[3], ALU.add))
            pool.tensor_tensor(out, out, w[2], ALU.add).then_inc(mean_ready, 1)

    def tensor(pe):
        ctx = g["ctx_rows"]

        def turn(n):
            pe.wait_ge(mean_ready, n + 1)
            if n >= 1:
                pe.wait_ge(mT_ready, n)
            for b, r in tiles(PIECES[n % NCH][1]):
                last = pe.transpose(ps[0:r, 6, b:b + P], mean[:, n % MEANS, b:b + r], g["ident"][:])
            last.then_inc(mT_psum, 1)

        def add_context(n):
            i, u = divmod(n, NCH)
            c, wd = PIECES[u]
            pe.wait_ge(mT_ready, n + 1)
            if u == 0 and i >= 1:
                pe.wait_ge(tok_ready, i)
            for b, r in tiles(wd):
                last = pe.matmul(ps[:, 7, 0:DC], mean_T[0:r, n % 2, b:b + P],
                                 ctx[0:r, (c + b) // P, 0:DC], start=c + b == 0, stop=c + b + r == S2)
            last.then_inc(pv_done, 1)

        for G in range(STEPS + LAG + CONTEXT_LAG):
            n = G - LAG
            for sub in range(NH):
                r = NH * G + sub
                if search_piece(r):
                    i, h, u = search_piece(r)
                    if r >= SEARCH_BANKS:
                        pe.wait_ge(searched, r - SEARCH_BANKS + 1)
                    score_unit(pe, a, ps, r % SEARCH_BANKS, i, h, *PIECES[u]).then_inc(search_done, 1)
                if 0 <= n < STEPS:
                    q = NH * n + sub
                    if q >= WEIGH_BANKS:
                        pe.wait_ge(e_ready, q - WEIGH_BANKS + 1)
                    score_unit(pe, a, ps, SEARCH_BANKS + q % WEIGH_BANKS, n // NCH, sub,
                               *PIECES[n % NCH]).then_inc(score_done, 1)
                if sub == 1 and 0 <= n - TURN_LAG < STEPS:
                    turn(n - TURN_LAG)
                if sub == 3 and 0 <= n - CONTEXT_LAG < STEPS:
                    add_context(n - CONTEXT_LAG)
        pe.wait_ge(tok_ready, NT)
        for i in range(NT):
            last = pe.transpose(ps[0:DC, i // 4, (i % 4) * P:(i % 4 + 1) * P], c_tok[:, i, :],
                                g["ident"][:])
        last.then_inc(cc_psum, 1)
        pe.wait_ge(cc_ready, 1)
        pe.wait_ge(loaded, 32)
        for n in range(2):
            pe.matmul(ps[:, 2 + n, :], w_v[:], c_ctx[:, n, :],
                      start=True, stop=True).then_inc(c_done, 1)

    def scalar(act):
        def copy_mean(n):
            wd = PIECES[n % NCH][1]
            act.wait_ge(mT_psum, n + 1)
            if n >= 2:
                act.wait_ge(pv_done, n - 1)
            full = wd // P * P
            last = act.activation(mean_T[:, n % 2, 0:full], ps[:, 6, 0:full], ACT.Copy)
            if wd > full:
                last = act.activation(mean_T[0:wd - full, n % 2, full:full + P],
                                      ps[0:wd - full, 6, full:full + P], ACT.Copy)
            last.then_inc(mT_ready, 1)

        link = chained(act, chain_act)

        def keep_last_head(n):
            i, u = divmod(n, NCH)
            width = PIECES[u][1]
            out = keep[:, n % 2, 0:width]
            if u == 0:
                act.wait_ge(least_ready, i + 1)
                link(act.activation(below[:, i % 2:i % 2 + 1], least[:, i % 2, NH - 1:NH], ACT.Copy,
                                    scale=2.0 ** -24 - 1.0))
            act.wait_ge(e_ready, NH * (n + 1))
            if n >= 2:
                act.wait_ge(mean_ready, n - 1)
            link(act.activation(out, e[:, n % RING, NH - 1, 0:width], ACT.Sign,
                                bias=below[:, i % 2:i % 2 + 1]))
            act.activation(out, out, ACT.Relu).then_inc(keep_ready, 1)

        for G in range(STEPS + LAG + CONTEXT_LAG + 1):
            n = G - LAG
            i, u = divmod(n - CONTEXT_LAG, NCH)
            if u == 0 and 1 <= i <= NT:
                if i == 1:
                    act.wait_ge(mask_ready, 1)
                act.wait_ge(pv_done, NCH * i)
                act.activation(c_tok[:, i - 1, :], ps[:, 7, 0:DC], ACT.Copy,
                               scale=mask[:, i - 1:i]).then_inc(tok_ready, 1)
            for sub in range(NH):
                if 0 <= n < STEPS:
                    i, u = divmod(n, NCH)
                    if sub == 0 and n >= RING:
                        act.wait_ge(mean_ready, n - RING + 1)
                    if sub == 0 and u == 0:
                        act.wait_ge(bias_ready, i + 1)
                    q = NH * n + sub
                    act.wait_ge(score_done, q + 1)
                    act.activation(e[:, n % RING, sub, 0:PIECES[u][1]],
                                   ps[:, SEARCH_BANKS + q % WEIGH_BANKS, 0:PIECES[u][1]], ACT.Exp,
                                   bias=bias[:, i % 2, sub:sub + 1]).then_inc(e_ready, 1)
                i = limits_tile(G)
                if i is not None and sub == 0:
                    act.wait_ge(found, i + 1)
                    act.activation(shifted[:], shifted[:], ACT.Exp).then_inc(exp_done, 1)
                elif i is not None and sub == 2:
                    act.wait_ge(summed, i + 1)
                    act.activation(total[:], total[:], ACT.Ln, scale=float(NH)).then_inc(ln_done, 1)
                elif i is not None and sub == 3:
                    act.wait_ge(bias_ready, i + 1)
                    act.activation(least[:, i % 2, :], least[:, i % 2, :], ACT.Exp).then_inc(least_ready, 1)
                if sub == 0 and 0 <= n - 1 < STEPS and not last_head_on_vector(n - 1):
                    keep_last_head(n - 1)
                if sub == 2 and 0 <= n - TURN_LAG < STEPS:
                    copy_mean(n - TURN_LAG)
        act.wait_ge(cc_psum, 1)
        act.activation(c_ctx, ps[0:DC, 0:2, :],
                       ACT.Copy).then_inc(cc_ready, 1)
        for n in range(2):
            act.wait_ge(c_done, n + 1)
            act.activation(g["c_T"][:, n * HALF:(n + 1) * HALF], ps[:, 2 + n, :], ACT.Copy)

    def where_needed(eng, program):
        if searching:
            program(eng)
        else:
            any_flagged = eng.value_load(a["count"][0:1, NT * NH:NT * NH + 1])
            with eng.If(any_flagged > 0):
                program(eng)

    with nc.Block() as block:
        @block.sync
        def _(sp):
            sp.dma_start(mask8[:], t["text_mask"].rearrange("(i p) -> p i", p=P),
                         allow_slow_non_contiguous=True).then_inc(loaded, 16)
            sp.dma_start(w_v[:], t["L1_xattn_Wv"]).then_inc(loaded, 16)
            sp.wait_ge(loaded, 32)

        @block.vector
        def _(dve):
            where_needed(dve, vector)

        @block.gpsimd
        def _(pool):
            where_needed(pool, pool_sums)

        @block.tensor
        def _(pe):
            where_needed(pe, tensor)

        @block.scalar
        def _(act):
            where_needed(act, scalar)





NF = 2 * S


def film_s4d_ffn(nc, g, t, m):
    a = {"dft": m.sb("dft", [P, NT, NF]), "k_tok": g["k_tok"],
         "u": m.sb("u", [P, NT, D]), "y": m.sb("y", [P, NT, D]),
         "dft_loaded": [m.sem(f"dft_loaded_{j}") for j in range(NT)],
         "gate": m.sb("gate", [P, 1]),
         "w_out": m.sb("w_out", [P, 2 * D]), "b_out": m.sb("b_out", [1, 2 * D]),
         "film_out": m.sb("film_out", [P, NT, 2, D]), "out_loaded": m.sem("out_loaded")}
    for part in (film_in, convolve, film_out_ffn):
        with ExitStack() as ctx:
            part(nc, g, t, Memory(nc, ctx, part.__name__), a)


def broadcast_row(name, t):
    return t[name].unsqueeze(0).to_broadcast([P, D])


def film(pe, g, w_f, b_f, ps, done):
    for i in range(NT):
        out = ps[:, i // 2, (i % 2) * 2 * D:(i % 2 + 1) * 2 * D]
        pe.matmul(out, g["c_T"][:, i * P:(i + 1) * P], w_f[:], start=True, stop=False)
        last = pe.matmul(out, g["ones"][:, 0:P], b_f[:], start=False, stop=True)
    last.then_inc(done, 1)


def film_banks(ps):
    return ps[:, 0:4, :].rearrange("p b (i s d) -> p (b i) s d", s=2, d=D)


def film_apply(dve, link, film_values, gate, x, scale, out):
    link(dve.tensor_scalar(scale[:], film_values[:, :, 0, :], gate[:, 0:1], 1.0, ALU.mult, ALU.add))
    link(dve.tensor_tensor(out, x, scale[:], ALU.mult))
    return dve.scalar_tensor_tensor(out=out, in0=film_values[:, :, 1, :], scalar=gate[:, 0:1], in1=out,
                                    op0=ALU.mult, op1=ALU.add)


def film_in(nc, g, t, m, a):
    ps = g["psum"]
    gain, shift = m.sb("gain", [P, D]), m.sb("shift", [P, D])
    w_f, b_f = m.sb("w_f", [P, 2 * D]), m.sb("b_f", [1, 2 * D])
    stats = m.sb("stats", [P, NT, 6])
    mv = m.sb("mv", [P, NT, 2])
    rstd = m.sb("rstd", [P, NT, 1])
    scale = m.sb("scale", [P, NT, D])
    loaded, chain_dve, var_ready, root_ready, normed, film_done = (
        m.sem(n) for n in ("loaded", "chain_dve", "var_ready", "root_ready", "normed", "film_done"))
    N_LOADS = 5

    def tiles(v):
        return v.unsqueeze(1).to_broadcast([P, NT, D])

    with nc.Block() as block:
        @block.sync
        def _(sp):
            sp.dma_start(gain[:], broadcast_row("L1_xattn_g_norm_in", t)).then_inc(loaded, 16)
            sp.dma_start(shift[:], broadcast_row("L1_xattn_b_norm_in", t)).then_inc(loaded, 16)
            sp.dma_start(w_f[:], t["L1_xattn_W_film_in"]).then_inc(loaded, 16)
            sp.dma_start(b_f[:], t["L1_xattn_b_film_in"].unsqueeze(0)).then_inc(loaded, 16)
            sp.dma_start(a["gate"][:], t["mod_gate"].to_broadcast([P, 1])).then_inc(loaded, 16)
            sp.dma_start(a["w_out"][:], t["L1_xattn_W_film_out"]).then_inc(a["out_loaded"], 16)
            sp.dma_start(a["b_out"][:], t["L1_xattn_b_film_out"].unsqueeze(0)).then_inc(a["out_loaded"], 16)
            for j in range(NT):
                sp.dma_start(a["dft"][:, j, :], t["dft"][j * P:(j + 1) * P, :]).then_inc(a["dft_loaded"][j], 16)

        @block.vector
        def _(dve):
            link = chained(dve, chain_dve)
            u = a["u"]
            normalise(dve, link, g["xn"], stats, mv, rstd, var_ready, root_ready, u, normed)
            dve.wait_ge(normed, NT)
            dve.wait_ge(loaded, 16 * N_LOADS)
            link(dve.tensor_tensor(u[:], u[:], tiles(gain[:]), ALU.mult))
            link(dve.tensor_tensor(u[:], u[:], tiles(shift[:]), ALU.add))
            dve.wait_ge(film_done, 1)
            link(film_apply(dve, link, film_banks(ps), a["gate"], u[:], scale, u[:]))

        @block.scalar
        def _(act):
            root(act, rstd, 1, var_ready, root_ready)

        @block.tensor
        def _(pe):
            pe.wait_ge(loaded, 16 * N_LOADS)
            film(pe, g, w_f, b_f, ps, film_done)


def convolve(nc, g, t, m, a):
    ps = g["psum"]
    dft = a["dft"]
    kf = m.sb("kf", [P, NF])
    yf = m.sb("yf", [P, NF])
    cross = m.sb("cross", [P, S])
    ends = m.sb("ends", [P, 2])
    yt = m.sb("yt", [P, NF // P, D])
    sign = m.sb("sign", [1, S])
    film_done, film_copied = m.sem("film_done"), m.sem("film_copied")
    sign_loaded, kf_done, kf_ready, uf_done, yf_ready, yt_psum, yt_ready, patched, y_done, chain_dve = (
        m.sem(n) for n in ("sign_loaded", "kf_done", "kf_ready", "uf_done", "yf_ready", "yt_psum",
                           "yt_ready", "patched", "y_done", "chain_dve"))

    def banks(b, n):
        return ps[:, b:b + n, :].rearrange("p b n -> p (b n)")

    with nc.Block() as block:
        @block.sync
        def _(sp):
            sp.dma_start(sign[:], t["alternating"]).then_inc(sign_loaded, 16)

        @block.tensor
        def _(pe):
            for src, first, done in ((a["k_tok"], 0, kf_done), (a["u"], 4, uf_done)):
                for j in range(NT):
                    if done is kf_done:
                        pe.wait_ge(a["dft_loaded"][j], 16)
                    for n in range(4):
                        last = pe.matmul(ps[:, first + n, :], src[:, j, :], dft[:, j, n * HALF:(n + 1) * HALF],
                                         start=j == 0, stop=j == NT - 1)
                        if j == NT - 1:
                            last.then_inc(done, 1)
            pe.wait_ge(kf_ready, 4)
            pe.wait_ge(a["out_loaded"], 32)
            film(pe, g, a["w_out"], a["b_out"], ps, film_done)
            pe.wait_ge(film_copied, 1)
            for f in range(NF // P):
                pe.wait_ge(yf_ready, 1)
                pe.transpose(ps[:, f // 4, (f % 4) * P:(f % 4 + 1) * P], yf[:, f * P:(f + 1) * P],
                             g["ident"][:]).then_inc(yt_psum, 1)
            pe.wait_ge(patched, 1)
            pe.wait_ge(yt_ready, 4)
            for b in range(NT):
                for f in range(NF // P):
                    cols = (f // NT) * S + b * P
                    last = pe.matmul(ps[:, 4 + b // 4, (b % 4) * D:(b % 4 + 1) * D],
                                     dft[:, f % NT, cols:cols + P], yt[:, f, :],
                                     start=f == 0, stop=f == NF // P - 1)
            last.then_inc(y_done, 1)

        @block.scalar
        def _(act):
            for n in range(4):
                act.wait_ge(kf_done, n + 1)
                act.activation(kf[:, n * HALF:(n + 1) * HALF], ps[:, n, :], ACT.Copy,
                               scale=2.0 / NF).then_inc(kf_ready, 1)
            act.wait_ge(film_done, 1)
            act.activation(a["film_out"][:], film_banks(ps), ACT.Copy).then_inc(film_copied, 1)
            for n in range(4):
                act.wait_ge(yt_psum, 4 * (n + 1))
                act.activation(yt[:, 4 * n:4 * n + 4, :], ps[:, n, :].rearrange("p (f d) -> p f d", d=D),
                               ACT.Copy).then_inc(yt_ready, 1)
            act.wait_ge(y_done, 1)
            act.activation(a["y"][:], banks(4, 2).rearrange("p (i d) -> p i d", d=D), ACT.Copy)

        @block.vector
        def _(dve):
            link = chained(dve, chain_dve)
            dve.wait_ge(kf_ready, 4)
            dve.wait_ge(uf_done, 4)
            ur, ui, kr, ki = banks(4, 2), banks(6, 2), kf[:, 0:S], kf[:, S:NF]
            link(dve.scalar_tensor_tensor(out=ends[:], in0=banks(4, 4)[:, 0:NF:S], scalar=0.5,
                                          in1=kf[:, 0:NF:S], op0=ALU.mult, op1=ALU.mult))
            link(dve.tensor_tensor(yf[:, 0:S], ur, kr, ALU.mult))
            link(dve.tensor_tensor(cross[:], ui, ki, ALU.mult))
            link(dve.tensor_tensor(yf[:, 0:S], yf[:, 0:S], cross[:], ALU.subtract))
            link(dve.tensor_tensor(yf[:, S:NF], ur, ki, ALU.mult))
            link(dve.tensor_tensor(cross[:], ui, kr, ALU.mult))
            link(dve.tensor_tensor(yf[:, S:NF], yf[:, S:NF], cross[:], ALU.add))
            dve.tensor_copy(yf[:, 0:NF:S], ends[:]).then_inc(yf_ready, 1)
            link(dve.memset(dft[:, :, S:S + 1], 0.0))
            dve.wait_ge(sign_loaded, 16)
            dve.tensor_copy(dft[0:1, 0, S:NF], sign[:]).then_inc(patched, 1)


def film_out_ffn(nc, g, t, m, a):
    HID = 4 * D
    NH_ = HID // P
    ps = g["psum"]
    w1, b1 = m.sb("w1", [P, HID]), m.sb("b1", [P, NH_])
    w2, b2 = m.sb("w2", [P, NH_, D]), m.sb("b2", [1, D])
    g_ffn, b_ffn = m.sb("g_ffn", [P, 1]), m.sb("b_ffn", [P, 1])
    gain, shift = m.sb("gain", [P, D]), m.sb("shift", [P, D])
    scale = m.sb("scale", [P, NT, D])
    xt = m.sb("xt", [P, NT, D])
    h = m.sb("h", [P, NT, D])
    hT = m.sb("hT", [P, S])
    act_T = m.sb("act_T", [P, NH_, S])
    norm = [{n: m.sb(f"{n}{k}", s) for n, s in (("stats", [P, NT, 6]), ("mv", [P, NT, 2]), ("rstd", [P, NT, 1]))}
            for k in range(2)]
    var_ready = [m.sem(f"var_ready{k}") for k in range(2)]
    root_ready = [m.sem(f"root_ready{k}") for k in range(2)]
    loaded, chain_dve, h_ready, hT_psum, hT_ready, u_done, act_ready, out_done, normed = (
        m.sem(n) for n in ("loaded", "chain_dve", "h_ready", "hT_psum", "hT_ready",
                           "u_done", "act_ready", "out_done", "normed"))
    N_LOADS = 8

    def tiles(v):
        return v.unsqueeze(1).to_broadcast([P, NT, D])

    with nc.Block() as block:
        @block.sync
        def _(sp):
            for dst, src in ((w1[:], t["L1_xattn_W1"]),
                             (b1[:], t["L1_b1_T"]),
                             (w2[:], t["L1_xattn_W2"].rearrange("(q p) d -> p q d", p=P)),
                             (b2[:], t["L1_xattn_b2"].unsqueeze(0)),
                             (g_ffn[:], t["L1_xattn_g_ffn"].unsqueeze(1)),
                             (b_ffn[:], t["L1_xattn_b_ffn"].unsqueeze(1)),
                             (gain[:], broadcast_row("L1_xattn_g_norm_out", t)),
                             (shift[:], broadcast_row("L1_xattn_b_norm_out", t))):
                sp.dma_start(dst, src).then_inc(loaded, 16)

        @block.vector
        def _(dve):
            link = chained(dve, chain_dve)
            link(film_apply(dve, link, a["film_out"][:], a["gate"], a["y"][:], scale, xt[:]))
            link(dve.tensor_tensor(xt[:], xt[:], g["xn"][:], ALU.add))
            normalise(dve, link, xt, norm[0]["stats"], norm[0]["mv"], norm[0]["rstd"], var_ready[0],
                      root_ready[0], h, h_ready)
            dve.wait_ge(out_done, 1)
            link(dve.tensor_tensor(xt[:], xt[:], ps[:, 4:6, :].rearrange("p b (i d) -> p (b i) d", d=D),
                                   ALU.add))
            normalise(dve, link, xt, norm[1]["stats"], norm[1]["mv"], norm[1]["rstd"], var_ready[1],
                      root_ready[1], h, normed)
            dve.wait_ge(normed, NT)
            dve.wait_ge(loaded, 16 * N_LOADS)
            link(dve.tensor_tensor(h[:], h[:], tiles(gain[:]), ALU.mult))
            link(dve.tensor_tensor(h[:], h[:], tiles(shift[:]), ALU.add))
            link(dve.tensor_tensor(g["x"][:], g["x"][:], h[:], ALU.add))

        @block.scalar
        def _(act):
            root(act, norm[0]["rstd"], 1, var_ready[0], root_ready[0])
            act.wait_ge(loaded, 16 * N_LOADS)
            for n in range(2):
                act.wait_ge(hT_psum, 4 * (n + 1))
                act.activation(hT[:, n * HALF:(n + 1) * HALF], ps[:, n, :], ACT.Identity,
                               scale=g_ffn[:, 0:1], bias=b_ffn[:, 0:1]).then_inc(hT_ready, 1)
            for q in range(NH_):
                act.wait_ge(u_done, q + 1)
                b = 2 * ((q + 1) % 4)
                act.activation(act_T[:, q, :], ps[:, b:b + 2, :].rearrange("p b n -> p (b n)"),
                               ACT.Gelu, bias=b1[:, q:q + 1]).then_inc(act_ready, 1)
            root(act, norm[1]["rstd"], 1, var_ready[1], root_ready[1])

        @block.tensor
        def _(pe):
            transpose_tiles(pe, h, g["ident"][:], ps, h_ready, hT_psum)
            pe.wait_ge(loaded, 16 * N_LOADS)
            pe.wait_ge(hT_ready, 2)
            for q in range(NH_):
                for n in range(2):
                    last = pe.matmul(ps[:, 2 * ((q + 1) % 4) + n, :], w1[:, q * P:(q + 1) * P],
                                     hT[:, n * HALF:(n + 1) * HALF], start=True, stop=True)
                last.then_inc(u_done, 1)
            pe.wait_ge(act_ready, NH_)
            for i in range(NT):
                out = ps[:, 4 + i // 4, (i % 4) * D:(i % 4 + 1) * D]
                for q in range(NH_):
                    pe.matmul(out, act_T[:, q, i * P:(i + 1) * P], w2[:, q, :], start=q == 0, stop=False)
                last = pe.matmul(out, g["ones"][:, 0:P], b2[:], start=False, stop=True)
            last.then_inc(out_done, 1)



HQ, HKV, HD = 16, 4, 8
HQK = HQ + HKV
PARTS9 = 9 * HD
SPLIT = PARTS9 + 3
OUT = HD + 1
NE, EH = 8, 256
N_PREFETCH = 11 + HQ


def gqa_experts(nc, g, t, m):
    a = {"xn": m.sb("xn", [P, NT, D]), "stack": m.sb("stack", [P, HQ // 4, S])}
    a["weights"] = {n: m.sb(n, s) for n, s in (
        ("w_g", [P, D]), ("b_g", [1, D]), ("w_o", [P, D]), ("b_o", [1, D]),
        ("ln_w", [P, 1]), ("w_r", [P, NE]), ("b_r", [1, NE]), ("order", [P, NE]),
        ("w1", [P, NE, 2 * EH]), ("b1", [P, NE, 4]), ("w2", [P, NE, 2, D]), ("b2", [NE, D]))}
    a["zeroed"], a["prefetched"] = m.sem("zeroed"), m.sem("prefetched")
    with ExitStack() as ctx:
        mm = Memory(nc, ctx, "gqa")
        a["split"] = mm.sb("split", [P, NT, HQK, SPLIT], BF16)
        a["v"] = mm.sb("v", [P, NT, HKV, OUT])
        for name in ("ident", "above", "below"):
            a[name] = mm.sb(name, [P, P], BF16)
        with ExitStack() as inner:
            gqa_project(nc, g, t, Memory(nc, inner, "gqa_project"), a)
        with ExitStack() as inner:
            gqa_attend(nc, g, t, Memory(nc, inner, "gqa_attend"), a)
    with ExitStack() as ctx:
        gqa_output(nc, g, t, Memory(nc, ctx, "gqa_output"), a)
    recycle(nc, Memory.used)
    with ExitStack() as ctx:
        top_expert(nc, g, t, Memory(nc, ctx, "top_expert"), a)


def gqa_project(nc, g, t, m, a):
    ps = g["psum"]
    WQKV = (HQ + 2 * HKV) * HD
    w, bias = m.sb("w", [P, WQKV]), m.sb("bias", [1, WQKV])
    ln_w = m.sb("ln_w", [P, 1])
    cos, sin = m.sb("cos", [P, NT, HD // 2]), m.sb("sin", [P, NT, HD // 2])
    qn_w, kn_w = m.sb("qn_w", [P, HD]), m.sb("kn_w", [P, HD])
    stats, mv, rstd = m.sb("stats", [P, NT, 6]), m.sb("mv", [P, NT, 2]), m.sb("rstd", [P, NT, 2])
    h, hT = m.sb("h", [P, NT, D]), m.sb("hT", [P, S])
    qkv = m.sb("qkv", [P, NT, HQ + 2 * HKV, HD])
    turned = m.sb("turned", [P, NT, HQK, HD])
    half = m.sb("half", [P, 2, NT, HQK, HD // 2])
    square = m.sb("square", [P, NT * HQK, HD])
    scale = m.sb("scale", [P, NT * HQK])
    eps = m.sb("eps", [P, 1])
    part = m.sb("part", [P, 3, NT, HQK, HD], BF16)
    rest = m.sb("rest", [P, NT, HQK, HD])

    loaded, chain_dve, var_ready, root_ready, h_ready, hT_psum, hT_ready = (
        m.sem(n) for n in ("loaded", "chain_dve", "var_ready", "root_ready", "h_ready", "hT_psum", "hT_ready"))
    qkv_done, qkv_ready, square_ready, scale_ready, parts_ready, stacked = (
        m.sem(n) for n in ("qkv_done", "qkv_ready", "square_ready", "scale_ready", "parts_ready", "stacked"))
    N_LOADS = 9
    masks_f = m.sb("masks_f", [P, 2, P])
    half_ready = m.sem("half_ready")

    with nc.Block() as block:
        @block.sync
        def _(sp):
            for dst, src in ((w[:], t["L1_Wqkv"]), (bias[:], t["L1_bqkv"]),
                             (ln_w[:], t["L1_ffn_ln1_w"].unsqueeze(1)),
                             (cos[:], t["rope_cos"].rearrange("(i p) c -> p i c", p=P)),
                             (sin[:], t["rope_sin"].rearrange("(i p) c -> p i c", p=P)),
                             (qn_w[:], t["L1_ffn_qn_w"].unsqueeze(0).to_broadcast([P, HD])),
                             (kn_w[:], t["L1_ffn_kn_w"].unsqueeze(0).to_broadcast([P, HD])),
                             (masks_f[:, 0, :], t["above_diagonal"]), (masks_f[:, 1, :], t["below_diagonal"])):
                sp.dma_start(dst, src).then_inc(loaded, 16)
            wt = a["weights"]
            for dst, src in ((wt["b_g"][:], t["L1_bg_rep"]), (wt["w_o"][:], t["L1_ffn_Wo"]),
                             (wt["b_o"][:], t["L1_ffn_bo"].unsqueeze(0)),
                             (wt["ln_w"][:], t["L1_ffn_ln2_w"].unsqueeze(1)),
                             (wt["w_r"][:], t["L1_ffn_Wr"]), (wt["b_r"][:], t["L1_ffn_br"].unsqueeze(0)),
                             (wt["order"][:], t["order"]),
                             (wt["w1"][:], t["L1_ffn_W1"].rearrange("e p n -> p e n")),
                             (wt["w2"][:], t["L1_ffn_W2"].rearrange("e (q p) d -> p e q d", p=P)),
                             (wt["b2"][:], t["L1_ffn_b2"])):
                sp.dma_start(dst, src).then_inc(a["prefetched"], 16)
            sp.dma_start(wt["b1"][:], t["L1_eb1_T"].rearrange("(e q p) -> p e q", e=NE, p=P),
                         allow_slow_non_contiguous=True).then_inc(a["prefetched"], 16)
            sp.wait_ge(a["zeroed"], 1)
            for h in range(HQ):
                sp.dma_start(wt["w_g"][h * HD:(h + 1) * HD, h * HD:(h + 1) * HD],
                             t["L1_ffn_Wg"]).then_inc(a["prefetched"], 16)

        @block.vector
        def _(dve):
            link = chained(dve, chain_dve)
            link(dve.memset(eps[:], 1e-6))
            normalise(dve, link, g["x"], stats, mv, rstd, var_ready, root_ready, a["xn"], h_ready,
                      1e-6, h)
            dve.wait_ge(qkv_ready, 4)
            HH = HD // 2
            x1 = qkv[:, :, 0:HQK, 0:HH]
            c = cos[:].unsqueeze(2).to_broadcast([P, NT, HQK, HH])
            s = sin[:].unsqueeze(2).to_broadcast([P, NT, HQK, HH])
            low, high = turned[:, :, :, 0:HH], turned[:, :, :, HH:HD]
            link(dve.tensor_tensor(low, x1, c, ALU.mult))
            link(dve.tensor_tensor(high, x1, s, ALU.mult))
            for n, (out, op) in enumerate(((low, ALU.subtract), (high, ALU.add))):
                dve.wait_ge(half_ready, n + 1)
                link(dve.tensor_tensor(out, out, half[:, n], op))
            flat = turned[:].rearrange("p i h c -> p (i h) c")
            link(dve.tensor_tensor(square[:], flat, flat, ALU.mult))
            dve.reduce_sum(scale[:], square[:], AX).then_inc(square_ready, 1)
            dve.wait_ge(scale_ready, 1)
            link(dve.reciprocal(scale[:], scale[:]))
            link(dve.tensor_tensor(flat, flat, scale[:].unsqueeze(2).to_broadcast([P, NT * HQK, HD]), ALU.mult))
            for w_n, lo, hi in ((qn_w, 0, HQ), (kn_w, HQ, HQK)):
                v = turned[:, :, lo:hi, :]
                link(dve.tensor_tensor(v, v, w_n[:].unsqueeze(1).unsqueeze(1).to_broadcast(
                    [P, NT, hi - lo, HD]), ALU.mult))
            link(dve.tensor_copy(part[:, 0], turned[:]))
            link(dve.tensor_tensor(rest[:], turned[:], part[:, 0], ALU.subtract))
            link(dve.tensor_copy(part[:, 1], rest[:]))
            dve.tensor_tensor(part[:, 2], rest[:], part[:, 1], ALU.subtract).then_inc(parts_ready, 1)
            dve.wait_ge(parts_ready, 1)
            for n in range(9):
                cols = slice(n * HD, (n + 1) * HD)
                last = dve.tensor_copy(a["split"][:, :, 0:HQ, cols], part[:, n // 3, :, 0:HQ, :])
            last.then_inc(stacked, 1)
            dve.wait_ge(stacked, 10)

        @block.gpsimd
        def _(pool):
            link = chained(pool, m.sem("chain_pool"))
            pool.memset(a["weights"]["w_g"][:], 0.0).then_inc(a["zeroed"], 1)
            link(pool.memset(a["split"][:, :, HQ:HQK, PARTS9:SPLIT], 1.0))
            link(pool.memset(a["v"][:, :, :, HD:OUT], 1.0))
            link(pool.memset(a["stack"][:], 0.0))
            link(pool.tensor_copy(a["ident"][:], g["ident"][:]))
            pool.wait_ge(loaded, 16 * N_LOADS)
            link(pool.tensor_copy(a["above"][:], masks_f[:, 0, :]))
            link(pool.tensor_copy(a["below"][:], masks_f[:, 1, :]))
            pool.wait_ge(qkv_ready, 4)
            x2 = qkv[:, :, 0:HQK, HD // 2:HD]
            for n, angle in enumerate((sin, cos)):
                pool.tensor_tensor(half[:, n], x2, angle[:].unsqueeze(2).to_broadcast([P, NT, HQK, HD // 2]),
                                   ALU.mult).then_inc(half_ready, 1)
            pool.wait_ge(parts_ready, 1)
            for n in range(9):
                pool.tensor_copy(a["split"][:, :, HQ:HQK, n * HD:(n + 1) * HD],
                                 part[:, n % 3, :, HQ:HQK, :]).then_inc(stacked, 1)
            pool.wait_ge(stacked, 10)

        @block.scalar
        def _(act):
            root(act, rstd, 2, var_ready, root_ready)
            act.wait_ge(loaded, 16 * N_LOADS)
            for n in range(2):
                act.wait_ge(hT_psum, 4 * (n + 1))
                act.activation(hT[:, n * HALF:(n + 1) * HALF], ps[:, n, :], ACT.Copy,
                               scale=ln_w[:, 0:1]).then_inc(hT_ready, 1)
            for n in range(4):
                act.wait_ge(qkv_done, 2 * (n + 1))
                act.activation(qkv[:, 2 * n:2 * n + 2, :, :],
                               ps[:, 4 + n, 0:2 * WQKV].rearrange("p (i h c) -> p i h c", i=2, c=HD),
                               ACT.Copy).then_inc(qkv_ready, 1)
            act.wait_ge(qkv_ready, 4)
            act.activation(a["v"][:, :, :, 0:HD], qkv[:, :, HQK:, :], ACT.Copy)
            act.wait_ge(square_ready, 1)
            act.activation(scale[:], scale[:], ACT.Sqrt, scale=1.0 / HD, bias=eps[:, 0:1]).then_inc(scale_ready, 1)

        @block.tensor
        def _(pe):
            transpose_tiles(pe, h, g["ident"][:], ps, h_ready, hT_psum)
            pe.wait_ge(loaded, 16 * N_LOADS)
            for i in range(NT):
                pe.wait_ge(hT_ready, i // 4 + 1)
                out = ps[:, 4 + i // 2, (i % 2) * WQKV:(i % 2 + 1) * WQKV]
                pe.matmul(out, hT[:, i * P:(i + 1) * P], w[:], start=True, stop=False)
                pe.matmul(out, g["ones"][:, 0:P], bias[:], start=False, stop=True).then_inc(qkv_done, 1)


def gqa_attend(nc, g, t, m, a):
    SCALE = float(HD) ** -0.5
    ps = g["psum"]
    split = a["split"]
    ident, above, below = a["ident"], a["above"], a["below"]
    kT = m.sb("kT", [SPLIT, HKV, S], BF16)
    qT = m.sb("qT", [SPLIT, 2, S], BF16)
    sT = m.sb("sT", [SPLIT, 2, S], BF16)
    low = m.sb("low", [P, 2, NT])
    rest = m.sb("rest", [P, 2, NT])
    prob = m.sb("prob", [P, 2, NT, S])

    chain_dve = m.sem("chain_dve")
    k_psum, k_ready, q_psum, q_ready, score_done, max_read, shift_ready, s_psum, s_ready = (
        m.sem(n) for n in ("k_psum", "k_ready", "q_psum", "q_ready", "score_done", "max_read",
                           "shift_ready", "s_psum", "s_ready"))
    prob_psum, prob_ready, pv_done, o_ready = (
        m.sem(n) for n in ("prob_psum", "prob_ready", "pv_done", "o_ready"))

    def pair(n, cols):
        return ps[:, n:n + 2, :].rearrange("p b n -> p (b n)")[:, 0:cols]

    turned_bank = ps[0:SPLIT, 6, :].bitcast(BF16)

    def key_bank(k):
        return ps[0:SPLIT, 6 + k % 2, :].bitcast(BF16)

    def pieces(h, k):
        def count(k):
            return -(-(S - k * P) // HALF)

        first = h * sum(map(count, range(NT))) + sum(map(count, range(k)))
        return [(first + n, n * HALF, min(HALF, S - k * P - n * HALF)) for n in range(count(k))]

    def out_quadrant(h, half):
        q = 32 * (2 * (h % 2) + half)
        return ps[q:q + OUT, 7, :]

    Q_TURN, S_TURN, EXP_LAG, OUT_LAG = 5, NT + 2, NT + 3, NT + 5
    STEPS = HQ * NT + OUT_LAG

    with nc.Block() as block:
        @block.tensor
        def _(pe):
            def turn(head, rows, done, bank=turned_bank):
                for i in range(NT):
                    last = pe.transpose(bank[0:rows, i * P:(i + 1) * P], split[:, i, head, 0:rows],
                                        ident[:])
                last.then_inc(done, 1)

            def maxima(h, i):
                n = NT * h + i
                b = 2 * (n % 2)
                if i == 0:
                    pe.wait_ge(q_ready, h + 1)
                if n >= 2:
                    pe.wait_ge(max_read, n - 1)
                width = (i + 1) * P
                for k in range(0, width, HALF):
                    w = min(HALF, width - k)
                    pe.matmul(ps[:, b + k // HALF, 0:w], qT[0:PARTS9, h % 2, i * P:(i + 1) * P],
                              kT[0:PARTS9, h // (HQ // HKV), k:k + w], start=True, stop=k + w < width)
                col = (i % 4) * P
                pe.matmul(ps[:, b + i // 4, col:col + P], ident[:], above[:], start=False,
                          stop=True).then_inc(score_done, 1)

            def exponentials(h, k):
                if k == 0:
                    pe.wait_ge(s_ready, h + 1)
                for n, q, w in pieces(h, k):
                    if n >= 2:
                        pe.wait_ge(prob_ready, n - 1)
                    last = pe.matmul(ps[:, 4 + n % 2, 0:w], kT[:, h // (HQ // HKV), k * P:(k + 1) * P],
                                     sT[:, h % 2, k * P + q:k * P + q + w], start=True, stop=q > 0)
                    if q == 0:
                        last = pe.matmul(ps[:, 4 + n % 2, 0:P], ident[:], below[:], start=False, stop=True)
                    last.then_inc(prob_psum, 1)

            def outputs(h, k):
                pe.wait_ge(prob_ready, pieces(h, k)[-1][0] + 1)
                if k == 0 and h >= 2:
                    pe.wait_ge(o_ready, 2 * (h - 1))
                for half in range(2):
                    lo, hi = max(k * P, half * HALF), (half + 1) * HALF
                    if lo < hi:
                        last = pe.matmul(out_quadrant(h, half)[:, lo - half * HALF:HALF],
                                         a["v"][:, k, h // (HQ // HKV), :],
                                         prob[:, h % 2, k, lo - k * P:hi - k * P],
                                         start=k == 0, stop=hi == (k + 1) * P,
                                         tile_position=(0, 32 * (2 * (h % 2) + half)))
                if k == NT - 1:
                    last.then_inc(pv_done, 1)

            for k in range(HKV):
                if k >= 2:
                    pe.wait_ge(k_ready, k - 1)
                turn(HQ + k, SPLIT, k_psum, key_bank(k))
            pe.wait_ge(k_ready, HKV)
            turn(0, PARTS9, q_psum)
            for step in range(STEPS):
                h, k = divmod(step, NT)
                if k == Q_TURN and h + 1 < HQ:
                    pe.wait_ge(q_ready, 1) if h == 0 else pe.wait_ge(s_ready, h)
                    turn(h + 1, PARTS9, q_psum)
                h, k = divmod(step - S_TURN, NT)
                if k == 0 and 0 <= h < HQ:
                    pe.wait_ge(q_ready, min(h + 2, HQ))
                    pe.wait_ge(shift_ready, h + 1)
                    turn(h, SPLIT, s_psum)
                h, k = divmod(step, NT)
                if h < HQ:
                    maxima(h, k)
                h, k = divmod(step - EXP_LAG, NT)
                if 0 <= h < HQ:
                    exponentials(h, k)
                h, k = divmod(step - OUT_LAG, NT)
                if 0 <= h < HQ:
                    outputs(h, k)

        @block.vector
        def _(dve):
            link = chained(dve, chain_dve)
            for step in range(STEPS + 1):
                h, k = divmod(step - OUT_LAG - NT, NT)
                if k == 0 and 0 <= h < HQ:
                    dve.wait_ge(pv_done, h + 1)
                    for half in range(2):
                        dve.tensor_copy(a["stack"][32 * (h % 4):32 * (h % 4) + OUT, h // 4,
                                                   half * HALF:(half + 1) * HALF],
                                        out_quadrant(h, half)).then_inc(o_ready, 1)
                h, i = divmod(step, NT)
                if h < HQ:
                    b = h % 2
                    dve.wait_ge(score_done, step + 1)
                    dve.tensor_reduce(low[:, b, i:i + 1], pair(2 * (step % 2), (i + 1) * P), AX, ALU.max,
                                      negate=True).then_inc(max_read, 1)
                    if i == NT - 1:
                        dve.wait_ge(max_read, NT * (h + 1))
                        parts = split[:, :, h, PARTS9:SPLIT]
                        link(dve.tensor_copy(parts[:, :, 0], low[:, b, :]))
                        link(dve.tensor_tensor(rest[:, b, :], low[:, b, :], parts[:, :, 0], ALU.subtract))
                        link(dve.tensor_copy(parts[:, :, 1], rest[:, b, :]))
                        dve.tensor_tensor(parts[:, :, 2], rest[:, b, :], parts[:, :, 1],
                                          ALU.subtract).then_inc(shift_ready, 1)

        @block.scalar
        def _(act):
            for k in range(HKV):
                act.wait_ge(k_psum, k + 1)
                act.activation(kT[:, k, :], key_bank(k), ACT.Copy).then_inc(k_ready, 1)

            def copy_queries(h):
                act.wait_ge(q_psum, h + 1)
                act.activation(qT[0:PARTS9, h % 2, :], turned_bank[0:PARTS9, :], ACT.Copy).then_inc(q_ready, 1)

            copy_queries(0)
            for step in range(STEPS):
                h, k = divmod(step, NT)
                if k == Q_TURN and h + 1 < HQ:
                    copy_queries(h + 1)
                h, k = divmod(step - S_TURN, NT)
                if k == 0 and 0 <= h < HQ:
                    act.wait_ge(s_psum, h + 1)
                    act.activation(sT[:, h % 2, :], turned_bank, ACT.Copy).then_inc(s_ready, 1)
                h, k = divmod(step - EXP_LAG, NT)
                if 0 <= h < HQ:
                    if h >= 2 and k == 0:
                        act.wait_ge(pv_done, h - 1)
                    for n, q, w in pieces(h, k):
                        act.wait_ge(prob_psum, n + 1)
                        act.activation(prob[:, h % 2, k, q:q + w], ps[:, 4 + n % 2, 0:w], ACT.Exp,
                                       scale=SCALE).then_inc(prob_ready, 1)


def gqa_output(nc, g, t, m, a):
    ps = g["psum"]
    w_g, b_g, w_o, b_o = (a["weights"][n] for n in ("w_g", "b_g", "w_o", "b_o"))
    oT, gT = m.sb("oT", [P, S]), m.sb("gT", [P, S])
    gate = m.sb("gate", [P, NT, D])
    gated = m.sb("gated", [P, NT, D])
    chain_dve, oT_psum, oT_ready, gate_done, gate_ready, gated_ready, gT_psum, gT_ready, out_done = (
        m.sem(n) for n in ("chain_dve", "oT_psum", "oT_ready", "gate_done",
                           "gate_ready", "gated_ready", "gT_psum", "gT_ready", "out_done"))
    o4 = m.sb("o", [P, NT, HQ, HD])
    share = m.sb("share", [P, NT, HQ])
    o = o4[:].rearrange("p i h c -> p i (h c)")
    turned, o_ready = m.sem("turned"), m.sem("o_ready")

    def wide(b):
        return ps[:, b:b + 2, :].rearrange("p b (i d) -> p (b i) d", d=D)

    with nc.Block() as block:
        @block.tensor
        def _(pe):
            for k in range(HQ // 4):
                for i in range(NT):
                    last = pe.transpose(ps[:, 2 * k + i // 4, (i % 4) * P:(i % 4 + 1) * P],
                                        a["stack"][:, k, i * P:(i + 1) * P], g["ident"][:])
                last.then_inc(turned, 1)
            pe.wait_ge(o_ready, HQ // 4)
            for i in range(NT):
                pe.transpose(ps[:, i // 4, (i % 4) * P:(i % 4 + 1) * P], o[:, i, :],
                             g["ident"][:]).then_inc(oT_psum, 1)
            pe.wait_ge(a["prefetched"], 16 * N_PREFETCH)
            for i in range(NT):
                pe.wait_ge(oT_ready, i // 4 + 1)
                out = ps[:, 2 + i // 4, (i % 4) * D:(i % 4 + 1) * D]
                pe.matmul(out, oT[:, i * P:(i + 1) * P], w_g[:], start=True, stop=False)
                pe.matmul(out, g["ones"][:, 0:P], b_g[:], start=False, stop=True).then_inc(gate_done, 1)
            transpose_tiles(pe, gated, g["ident"][:], ps[:, 4:6, :], gated_ready, gT_psum)
            for i in range(NT):
                pe.wait_ge(gT_ready, i // 4 + 1)
                out = ps[:, 6 + i // 4, (i % 4) * D:(i % 4 + 1) * D]
                pe.matmul(out, gT[:, i * P:(i + 1) * P], w_o[:], start=True, stop=False)
                last = pe.matmul(out, g["ones"][:, 0:P], b_o[:], start=False, stop=True)
            last.then_inc(out_done, 1)

        @block.scalar
        def _(act):
            for n in range(2):
                act.wait_ge(oT_psum, 4 * (n + 1))
                act.activation(oT[:, n * HALF:(n + 1) * HALF], ps[:, n, :], ACT.Copy).then_inc(oT_ready, 1)
            act.wait_ge(gate_done, NT)
            act.activation(gate[:], wide(2), ACT.Sigmoid).then_inc(gate_ready, 1)
            for n in range(2):
                act.wait_ge(gT_psum, 4 * (n + 1))
                act.activation(gT[:, n * HALF:(n + 1) * HALF], ps[:, 4 + n, :], ACT.Copy).then_inc(gT_ready, 1)

        @block.vector
        def _(dve):
            link = chained(dve, chain_dve)
            for k in range(HQ // 4):
                dve.wait_ge(turned, k + 1)
                out = wide(2 * k).rearrange("p i (h c) -> p i h c", c=32)
                heads = slice(4 * k, 4 * k + 4)
                link(dve.reciprocal(share[:, :, heads], out[:, :, :, HD]))
                dve.tensor_tensor(o4[:, :, heads, :], out[:, :, :, 0:HD],
                                  share[:, :, heads].unsqueeze(3).to_broadcast([P, NT, 4, HD]),
                                  ALU.mult).then_inc(o_ready, 1)
            dve.wait_ge(o_ready, HQ // 4)
            dve.wait_ge(gate_ready, 1)
            dve.tensor_tensor(gated[:], o, gate[:], ALU.mult).then_inc(gated_ready, NT)
            dve.wait_ge(out_done, 1)
            link(dve.tensor_tensor(a["xn"][:], a["xn"][:], wide(6), ALU.add))


def top_expert(nc, g, t, m, a):
    ps = g["psum"]
    x1 = a["xn"]
    ln_w, w_r, b_r, w1, b1, w2, b2, order = (
        a["weights"][n] for n in ("ln_w", "w_r", "b_r", "w1", "b1", "w2", "b2", "order"))
    stats, mv = m.sb("stats", [P, NT, 6]), m.sb("mv", [P, NT, 2])
    scale = m.sb("scale", [P, NT])
    h, hT = m.sb("h", [P, NT, D]), m.sb("hT", [P, S])
    best = m.sb("best", [P, NT])
    rank = m.sb("rank", [P, NT, NE])
    own = m.sb("own", [P, NT, NE])
    sig = m.sb("sig", [P, 2, S])
    act_T = m.sb("act_T", [P, 2, 2, S])
    kept = m.sb("kept", [P, 2, NT, D])
    own_T = m.sb("own_T", [NE, S])
    oT_psum, oT_ready, bias_done, bias_read = (
        m.sem(n) for n in ("oT_psum", "oT_ready", "bias_done", "bias_read"))

    chain_dve, scale_sq, scale_ready, h_ready, hT_psum, hT_ready, logit_done = (
        m.sem(n) for n in ("chain_dve", "scale_sq", "scale_ready", "h_ready",
                           "hT_psum", "hT_ready", "logit_done"))
    u_done, sig_ready, act_ready, y_done, y_read, added, sum_ready = (
        m.sem(n) for n in ("u_done", "sig_ready", "act_ready", "y_done", "y_read", "added", "sum_ready"))

    def pair(n):
        return ps[:, 2 * n:2 * n + 2, :].rearrange("p b n -> p (b n)")

    with nc.Block() as block:
        @block.vector
        def _(dve):
            link = chained(dve, chain_dve)
            for i in range(NT):
                last = dve.bn_stats(stats[:, i, :], x1[:, i, :])
            link(last)
            for i in range(NT):
                last = dve.bn_aggr(mv[:, i, :], stats[:, i, :])
            link(last)
            link(dve.tensor_tensor(scale[:], mv[:, :, 0], mv[:, :, 0], ALU.mult))
            dve.scalar_tensor_tensor(out=scale[:], in0=scale[:], scalar=1e-6, in1=mv[:, :, 1],
                                     op0=ALU.add, op1=ALU.add).then_inc(scale_sq, 1)
            dve.wait_ge(scale_ready, 1)
            link(dve.reciprocal(scale[:], scale[:]))
            for i in range(NT):
                dve.tensor_scalar(h[:, i, :], x1[:, i, :], scale[:, i:i + 1], None,
                                  ALU.mult).then_inc(h_ready, 1)
            link(dve.tensor_tensor(g["x"][:], g["x"][:], x1[:], ALU.add))
            dve.wait_ge(logit_done, 1)
            logits = ps[:, 2, 0:NT * NE].rearrange("p (i e) -> p i e", e=NE)

            def spread(v):
                return v.unsqueeze(2).to_broadcast([P, NT, NE])

            link(dve.reduce_max(best[:], logits, AX))
            link(dve.tensor_tensor(rank[:], logits, spread(best[:]), ALU.is_equal))
            link(dve.tensor_tensor(rank[:], rank[:], order[:].unsqueeze(1).to_broadcast([P, NT, NE]), ALU.mult))
            link(dve.reduce_max(best[:], rank[:], AX))
            dve.tensor_tensor(own[:], rank[:], spread(best[:]), ALU.is_equal).then_inc(sum_ready, 1)
            dve.wait_ge(sum_ready, 1)

            def keep(e):
                dve.wait_ge(y_done, e + 1)
                if e >= 2:
                    dve.wait_ge(added, e - 1)
                dve.tensor_tensor(kept[:, e % 2], pair(3).rearrange("p (i d) -> p i d", d=D),
                                  own[:, :, e:e + 1].to_broadcast([P, NT, D]), ALU.mult).then_inc(y_read, 1)

            dve.wait_ge(bias_done, 1)
            dve.tensor_tensor(g["x"][:], g["x"][:], pair(3).rearrange("p (i d) -> p i d", d=D),
                              ALU.add).then_inc(bias_read, 1)
            for e in range(NE):
                for q in range(2):
                    n = 2 * e + q
                    dve.wait_ge(u_done, 2 * n + 2)
                    dve.wait_ge(sig_ready, n + 1)
                    if e >= 2:
                        dve.wait_ge(y_done, e - 1)
                    dve.scalar_tensor_tensor(out=act_T[:, e % 2, q, :], in0=pair((2 * n + 1) % 3),
                                             scalar=b1[:, e, q:q + 1], in1=sig[:, q, :],
                                             op0=ALU.add, op1=ALU.mult).then_inc(act_ready, 1)
                if e >= 1:
                    keep(e - 1)
            keep(NE - 1)

        @block.gpsimd
        def _(pool):
            pool.wait_ge(bias_read, 1)
            for e in range(NE):
                pool.wait_ge(y_read, e + 1)
                pool.tensor_tensor(g["x"][:], g["x"][:], kept[:, e % 2], ALU.add).then_inc(added, 1)
                pool.wait_ge(added, e + 1)

        @block.scalar
        def _(act):
            act.wait_ge(scale_sq, 1)
            act.activation(scale[:], scale[:], ACT.Sqrt).then_inc(scale_ready, 1)
            for n in range(2):
                act.wait_ge(hT_psum, 4 * (n + 1))
                act.activation(hT[:, n * HALF:(n + 1) * HALF], ps[:, n, :], ACT.Copy,
                               scale=ln_w[:, 0:1]).then_inc(hT_ready, 1)
            act.wait_ge(oT_psum, 1)
            act.activation(own_T[:], pair(3)[0:NE, :], ACT.Copy).then_inc(oT_ready, 1)
            for e in range(NE):
                for q in range(2):
                    n = 2 * e + q
                    act.wait_ge(u_done, 2 * n + 1)
                    if n >= 2:
                        act.wait_ge(act_ready, n - 1)
                    act.activation(sig[:, q, :], pair((2 * n) % 3), ACT.Sigmoid,
                                   bias=b1[:, e, 2 + q:3 + q]).then_inc(sig_ready, 1)

        @block.tensor
        def _(pe):
            transpose_tiles(pe, h, g["ident"][:], ps, h_ready, hT_psum)
            for i in range(NT):
                pe.wait_ge(hT_ready, i // 4 + 1)
                out = ps[:, 2, i * NE:(i + 1) * NE]
                pe.matmul(out, hT[:, i * P:(i + 1) * P], w_r[:], start=True, stop=False)
                last = pe.matmul(out, g["ones"][:, 0:P], b_r[:], start=False, stop=True)
            last.then_inc(logit_done, 1)
            def own_bias():
                pe.wait_ge(sum_ready, 1)
                for i in range(NT):
                    last = pe.transpose(ps[0:NE, 6 + i // 4, (i % 4) * P:(i % 4 + 1) * P], own[:, i, :],
                                        g["ident"][:])
                last.then_inc(oT_psum, 1)
                pe.wait_ge(oT_ready, 1)
                for i in range(NT):
                    last = pe.matmul(ps[:, 6 + i // 4, (i % 4) * D:(i % 4 + 1) * D],
                                     own_T[:, i * P:(i + 1) * P], b2[:], start=True, stop=True)
                last.then_inc(bias_done, 1)

            own_bias()
            def expert_out(e):
                pe.wait_ge(act_ready, 2 * (e + 1))
                if e >= 1:
                    pe.wait_ge(y_read, e)
                else:
                    pe.wait_ge(bias_read, 1)
                for i in range(NT):
                    out = ps[:, 6 + i // 4, (i % 4) * D:(i % 4 + 1) * D]
                    for q in range(2):
                        last = pe.matmul(out, act_T[:, e % 2, q, i * P:(i + 1) * P], w2[:, e, q, :],
                                         start=q == 0, stop=q == 1)
                last.then_inc(y_done, 1)

            for e in range(NE):
                for q in range(2):
                    for k in (2 + q, q):
                        n = 2 * (2 * e + q) + (k < 2)
                        if n >= 3:
                            pe.wait_ge(sig_ready, (n - 3) // 2 + 1)
                            if (n - 3) % 2:
                                pe.wait_ge(act_ready, (n - 3) // 2 + 1)
                        for c in range(2):
                            last = pe.matmul(ps[:, 2 * (n % 3) + c, :], w1[:, e, k * P:(k + 1) * P],
                                             hT[:, c * HALF:(c + 1) * HALF], start=True, stop=True)
                        last.then_inc(u_done, 1)
                if e >= 1:
                    expert_out(e - 1)
            expert_out(NE - 1)



def shape_constants():
    onehot3 = np.tile(np.eye(32, dtype=np.float32), (3, 1))
    above = np.triu(np.full((P, P), NEG, np.float32), 1)
    turns = 2.0 * np.pi * (np.outer(np.arange(S), np.arange(S)) % NF) / NF
    dft = np.concatenate([np.cos(turns), -np.sin(turns)], 1)
    alternating = 1.0 - 2.0 * (np.arange(S) % 2)
    dft[:, S] = alternating
    index = np.concatenate([np.arange(P), P * np.arange(NT)]).astype(np.float32)
    quarter = np.where(np.arange(P) < P // 2, 0.25, 0.0).astype(np.float32).reshape(P, 1)
    freqs = np.outer(np.arange(S), 1.0 / 10000.0 ** (np.arange(0, HD, 2) / HD)).astype(np.float32)
    return {"rope_cos": np.cos(freqs), "rope_sin": np.sin(freqs), "below_diagonal": above.T,
            "order": np.tile(np.arange(8, 0, -1, dtype=np.float32), (P, 1)),
            "dft": dft.astype(np.float32), "alternating": alternating.astype(np.float32).reshape(1, S),
            "s4d_index": np.tile(index, (P, 1)), "s4d_quarter": quarter,
            "above_diagonal": above, "ident": np.eye(P, dtype=np.float32), "onehot3": onehot3}


def laid_out(a):
    w = {k: v for k, v in a.items() if k.startswith("L")}
    w["x"] = a["x"].reshape(S, D)
    w["ctx"] = a["ctx_768"].reshape(S2, DC)
    w["ctx_T"] = a["ctx_768"].reshape(S2, DC).T
    w["L0_in_proj_T"] = a["L0_attn_in_proj_w"].T
    w["L0_conv_b_T"] = a["L0_attn_conv_b"].reshape(2, P).T
    w["L0_dt_b_T"] = a["L0_attn_dt_proj_b"].reshape(2, P).T
    w["L0_D_T"] = a["L0_attn_D"].reshape(2, P).T
    xp = a["L0_attn_x_proj_w"]
    w["L0_bcdt_T"] = np.concatenate([xp[8:], xp[8:], xp[8:], xp[:8]], 0).T
    w["L0_dt_proj_T"] = a["L0_attn_dt_proj_w"].T
    w["L0_out_proj_T"] = a["L0_attn_out_proj_w"].T
    w["L0_Wk_T"] = a["L0_xattn_Wk"].T
    for k in ("WQ", "WK", "WV"):
        w[f"L1_{k}_T"] = a[f"L1_attn_{k}"].T
    w["L1_Wq_rep"] = np.concatenate([np.tile(a["L1_xattn_Wq"][:, 32 * h:32 * h + 32], 4) for h in range(4)], 1)
    w["L1_Wk_rep"] = np.concatenate([np.tile(a["L1_xattn_Wk"][:, 32 * h:32 * h + 32], 4) for h in range(4)], 1)
    w["vision_mask"] = a["mask_BxS2_bf1"].reshape(1, S2).view(np.uint8)
    w["text_mask"] = a["mask_BxS_bf1"].reshape(S).view(np.uint8)
    for n in ("A_re", "A_im", "C_re", "C_im"):
        w[f"s4d_{n.lower()}"] = np.tile(a[f"L1_xattn_{n}"].T, (2, 1))
    w["mod_gate"] = a["L1_xattn_mod_gate"].reshape(1, 1)
    w["L1_b1_T"] = a["L1_xattn_b1"].reshape(4, P).T
    w["L1_Wqkv"] = np.concatenate([a[f"L1_ffn_W{k}"] for k in "qkv"], 1)
    w["L1_bqkv"] = np.concatenate([a[f"L1_ffn_b{k}"] for k in "qkv"]).reshape(1, -1)
    w["L1_bg_rep"] = np.tile(a["L1_ffn_bg"], HQ).reshape(1, -1)
    w["L1_eb1_T"] = a["L1_ffn_b1"].reshape(-1)
    w.update(shape_constants())
    return w

PARTS = [mamba, cross_attention, threshold_experts, causal_attention, film_context, film_s4d_ffn,
         gqa_experts]



def decoder(nc, t):
    g = {}
    with ExitStack() as whole:
        g["psum"] = whole.enter_context(nc.psum_tensor("psum", [P, 8, HALF], F32))
        g["x"] = whole.enter_context(nc.sbuf_tensor("residual", [P, NT, D], F32))
        g["ident"] = whole.enter_context(nc.sbuf_tensor("ident", [P, P], F32))
        g["ones"] = whole.enter_context(nc.sbuf_tensor("ones", [1, HALF], F32))
        g["ctx_rows"] = whole.enter_context(nc.sbuf_tensor("ctx_rows", [P, KT, DC + 1], F32))
        g["k_tok"] = whole.enter_context(nc.sbuf_tensor("s4d_k_tok", [P, NT, D], F32))
        first = whole.enter_context(ExitStack())
        g["ctx_T"] = first.enter_context(nc.sbuf_tensor("ctx_T", [DC + 1, S2], F32))
        Memory.used.clear()
        for part in [load_constants] + PARTS + [store_output]:
            with ExitStack() as ctx:
                part(nc, g, t, Memory(nc, ctx, part.__name__))
            if part is cross_attention:
                first.close()
                g["xn"] = whole.enter_context(nc.sbuf_tensor("layer1_xn", [P, NT, D], F32))
                g["c_T"] = whole.enter_context(nc.sbuf_tensor("c_T", [P, S], F32))
            if part in (causal_attention, film_context, film_s4d_ffn):
                recycle(nc, Memory.used)


def kernel(**inputs):
    import numpy as _np
    import concourse.bacc as _bacc
    from concourse import mybir as _mybir
    from concourse.bass_utils import run_bass_kernel_spmd as _run

    nc = _bacc.Bacc("TRN2", target_bir_lowering=False, num_devices=1)
    arrays = {k: v for k, v in laid_out({k: _np.asarray(v) for k, v in inputs.items()}).items()}
    t = {}
    feeds = {}
    for name, a in arrays.items():
        a = _np.ascontiguousarray(a)
        feeds[f"in_{name}"] = a
        t[name] = nc.dram_tensor(f"in_{name}", a.shape, _mybir.dt.from_np(a.dtype), kind="ExternalInput").ap()
    t["out"] = nc.dram_tensor("out_0", (S, D), _mybir.dt.float32, kind="ExternalOutput").ap()
    decoder(nc, t)
    r = _run(nc, [feeds], core_ids=[0])
    return r.results[0]["out_0"].reshape(1, S, D)
```
